# Optimizing a Trainium2 kernel written in Bass

```python
import numpy as np
import jax
import jax.numpy as jnp

def _softmax(x, axis=-1):
    return jax.nn.softmax(x, axis=axis)

def _gelu(x):
    return jax.nn.gelu(x, approximate=True)

def _silu(x):
    return jax.nn.silu(x)

def _sigmoid(x):
    return jax.nn.sigmoid(x)

def _layernorm(x, axis=-1, eps=1e-05):
    m = jnp.mean(x, axis=axis, keepdims=True)
    v = jnp.var(x, axis=axis, keepdims=True)
    return (x - m) / jnp.sqrt(v + eps)

def _scatter_add(tgt, idx, src, axis=0):
    return tgt.at[idx].add(src)

def _segment_sum(src, seg, n):
    return jax.ops.segment_sum(src, seg, n)
kernel_name = 'mk_flamingo_gated_d4_seqx_r4_15165d'

def setup_inputs(seed: int=0):
    np.random.seed(seed)
    _w = jnp.asarray

    def _rec_inputs():
        import jax
        import jax.numpy as jnp
        _rk = jax.random.key(seed)
        x = -0.0003929 + 0.9999 * jax.random.normal(jax.random.fold_in(_rk, 1), (8, 512, 256), jnp.float32)
        _lenS = 512 - jax.random.randint(jax.random.fold_in(_rk, 7), (8,), 0, max(1, 512 // 4) + 1, jnp.int32)
        _lenS2 = 64 - jax.random.randint(jax.random.fold_in(_rk, 8), (8,), 0, max(1, 64 // 4) + 1, jnp.int32)
        _ctx_1024P = jax.random.normal(jax.random.fold_in(_rk, 11), (8, 16, 256), jnp.float32)
        _ctx_1024c = jax.random.dirichlet(jax.random.fold_in(_rk, 511), 0.3 * jnp.ones((16,), jnp.float32), (8, 64))
        _ctx_1024t = jnp.einsum('bsk,bkd->bsd', _ctx_1024c, _ctx_1024P)
        _ctx_1024t = _ctx_1024t * jax.lax.rsqrt(jnp.mean(jnp.square(_ctx_1024t)) + 1e-12) * 0.953939
        ctx_1024 = -1.39393e-06 + 0.999914 * (_ctx_1024t + 0.3 * jax.random.normal(jax.random.fold_in(_rk, 611), (8, 64, 256), jnp.float32))
        _validS = jnp.arange(512)[None, :] < _lenS[:, None]
        _validS2 = jnp.arange(64)[None, :] < _lenS2[:, None]
        _causal = jnp.tril(jnp.ones((512, 512), dtype=bool))
        mask_BxS2_bf1 = jnp.ones((8, 64), dtype=bool)
        mask_Bx1x1xS2_ff1 = jnp.where(jnp.ones((8, 1, 1, 64), dtype=bool), 1.0, 0.0).astype(jnp.float32)
        mask_SxS2_ik1 = jnp.where(jnp.broadcast_to(_validS2[0:1, :], (512, 64)), 1, 0).astype(jnp.int32)
        _g = jax.random.normal(jax.random.fold_in(_rk, 9001), (2, 4), jnp.float32)
        _g = jnp.sign(_g) * jnp.maximum(jnp.abs(_g), 1.0) + (_g == 0) * 1.0
        g_xattn = _g[0]
        g_ffn = _g[1]
        return (x, ctx_1024, mask_BxS2_bf1, mask_Bx1x1xS2_ff1, mask_SxS2_ik1, g_xattn, g_ffn)
    x, ctx_1024, mask_BxS2_bf1, mask_Bx1x1xS2_ff1, mask_SxS2_ik1, g_xattn, g_ffn = _rec_inputs()

    def _L0_xattn_setup():
        import jax, jax.numpy as jnp
        import numpy as np
        GAMMA = 10.0
        BASE = 10000.0
        SCALE = 64 ** (-0.5)
        NUM_HEADS = 16

        def _larope(t, seq_len):
            B, H, L, D = t.shape
            inv_freq = 1.0 / BASE ** (jnp.arange(0, D, 2, dtype=jnp.float32) / D)
            pos = GAMMA * (jnp.arange(L, dtype=jnp.float32) / float(seq_len))
            ang = pos[:, None] * inv_freq
            cos = jnp.cos(ang)
            sin = jnp.sin(ang)
            te, to = (t[..., 0::2], t[..., 1::2])
            re = te * cos - to * sin
            ro = te * sin + to * cos
            return jnp.stack([re, ro], axis=-1).reshape(t.shape)
        key = jax.random.key(seed)
        ks = jax.random.split(key, 8)
        B, Lq, Lk, D = (8, 512, 128, 256)
        s = D ** (-0.5)
        return {'x': jax.random.normal(ks[0], (B, Lq, D), jnp.float32), 'context': jax.random.normal(ks[1], (B, Lk, D), jnp.float32), 'context_mask': jnp.ones((B, Lk), dtype=bool), 'Wq': jax.random.normal(ks[2], (D, D), jnp.float32) * s, 'bq': jnp.zeros((D,), jnp.float32), 'Wkv': jax.random.normal(ks[3], (D, 2 * D), jnp.float32) * s, 'bkv': jnp.zeros((2 * D,), jnp.float32), 'Wo': jax.random.normal(ks[4], (D, D), jnp.float32) * s, 'bo': jnp.zeros((D,), jnp.float32)}
    _L0_xattn_all = _L0_xattn_setup()
    _L0_xattn_in = {k: v for k, v in _L0_xattn_all.items() if k in ('Wq', 'bq', 'Wkv', 'bkv', 'Wo', 'bo')}
    del _L0_xattn_all

    def _L0_ffn_setup():
        import jax, jax.numpy as jnp
        import numpy as np
        B, N, D = (4, 2048, 256)
        HEADS, DH = (8, 64)
        HID = HEADS * DH
        WIN = 128
        NQ, NKV = (256, 512)
        EPS, N_ITERS, FETCH_K = (1.0, 50, 9.0 / 8.0)
        SCALE = DH ** (-0.5)

        def rmsnorm(x, gamma):
            norm = jnp.maximum(jnp.linalg.norm(x, axis=-1, keepdims=True), 1e-12)
            return x / norm * x.shape[-1] ** 0.5 * gamma

        def coor_descent(s, k):
            logk = jnp.log(jnp.asarray(k, s.dtype))

            def body(_, ab):
                a, b = ab
                a = EPS * (logk - jax.nn.logsumexp((s + b) / EPS, axis=-1, keepdims=True))
                b = -jax.nn.relu(s + a)
                return (a, b)
            a, b = jax.lax.fori_loop(0, N_ITERS, body, (jnp.zeros_like(s[..., :1]), -s))
            return jnp.exp((s + a + b) / EPS)

        def route(x, routing_token, num_tokens):
            s = jnp.einsum('bnd,d->bn', x, routing_token)
            k = min(num_tokens * FETCH_K, x.shape[1])
            scores = coor_descent(s, k)
            sel_scores, sel_idx = jax.lax.top_k(scores, num_tokens)
            sel_scores = sel_scores + jax.lax.stop_gradient(1.0 - sel_scores)
            return (sel_scores, sel_idx)

        def light_local_attn(x, gamma, wq, wkv, wo):
            b, n, d = x.shape
            xn = rmsnorm(x, gamma)
            q = xn @ wq
            k, v = jnp.split(xn @ wkv, 2, axis=-1)

            def win(t):
                return t.reshape(b, n // WIN, WIN, HEADS, DH).transpose(0, 1, 3, 2, 4)
            q, k, v = (win(q) * SCALE, win(k), win(v))
            attn = jax.nn.softmax(jnp.einsum('bwhid,bwhjd->bwhij', q, k), axis=-1)
            out = jnp.einsum('bwhij,bwhjd->bwhid', attn, v)
            out = out.transpose(0, 1, 3, 2, 4).reshape(b, n, HID)
            return out @ wo

        def heavy_attn(xq, context, scores_kv, gamma, wq, wkv_t, wo):
            b, nq, d = xq.shape
            nkv = context.shape[1]
            xqn = rmsnorm(xq, gamma)
            ctx = rmsnorm(context, gamma)[:, None]
            q = (xqn @ wq).reshape(b, nq, HEADS, DH).transpose(0, 2, 1, 3) * SCALE
            kvw = wkv_t.reshape(1, HEADS, 2 * DH, d)
            kv = jnp.einsum('rhdi,brni->brhnd', kvw, ctx)
            k, v = jnp.split(kv, 2, axis=-1)
            v = v * scores_kv[:, None, None, :, None]
            k = k.reshape(b, HEADS, nkv, DH)
            v = v.reshape(b, HEADS, nkv, DH)
            attn = jax.nn.softmax(jnp.einsum('bhid,bhjd->bhij', q, k), axis=-1)
            out = jnp.einsum('bhij,bhjd->bhid', attn, v)
            out = out.transpose(0, 2, 1, 3).reshape(b, nq, HID)
            return out @ wo
        key = jax.random.key(seed)
        ks = jax.random.split(key, 10)
        lin = lambda k, shape, fan: jax.random.normal(k, shape, jnp.float32) * fan ** (-0.5)
        return dict(x=jax.random.normal(ks[0], (B, N, D), jnp.float32), gamma_light=jnp.ones((D,), jnp.float32), wq_light=lin(ks[1], (D, HID), D), wkv_light=lin(ks[2], (D, 2 * HID), D), wo_light=lin(ks[3], (HID, D), HID), q_routing_token=jax.random.normal(ks[4], (D,), jnp.float32), kv_routing_token=jax.random.normal(ks[5], (D,), jnp.float32), gamma_heavy=jnp.ones((D,), jnp.float32), wq_heavy=lin(ks[6], (D, HID), D), wkv_heavy=lin(ks[7], (2 * HID, D), D), wo_heavy=lin(ks[8], (HID, D), HID))
    _L0_ffn_all = _L0_ffn_setup()
    _L0_ffn_in = {k: v for k, v in _L0_ffn_all.items() if k in ('gamma_light', 'wq_light', 'wkv_light', 'wo_light', 'q_routing_token', 'kv_routing_token', 'gamma_heavy', 'wq_heavy', 'wkv_heavy', 'wo_heavy')}
    del _L0_ffn_all

    def _L1_xattn_setup():
        import jax, jax.numpy as jnp
        import numpy as np
        D_MODEL = 256
        NUM_HEADS = 16
        DEPTH = D_MODEL // NUM_HEADS

        def _split_heads(x, B):
            return x.reshape(B, -1, NUM_HEADS, DEPTH).transpose(0, 2, 1, 3)
        key = jax.random.key(seed)
        ks = jax.random.split(key, 12)
        B, S = (2, 1024)
        s = 1.0 / np.sqrt(D_MODEL)
        return {'Q': jax.random.normal(ks[0], (B, S, D_MODEL), jnp.float32), 'K': jax.random.normal(ks[1], (B, S, D_MODEL), jnp.float32), 'V': jax.random.normal(ks[2], (B, S, D_MODEL), jnp.float32), 'mask': jnp.ones((B, 1, 1, S), jnp.float32), 'Wq': jax.random.normal(ks[3], (D_MODEL, D_MODEL), jnp.float32) * s, 'bq': jax.random.normal(ks[4], (D_MODEL,), jnp.float32) * s, 'Wk': jax.random.normal(ks[5], (D_MODEL, D_MODEL), jnp.float32) * s, 'bk': jax.random.normal(ks[6], (D_MODEL,), jnp.float32) * s, 'Wv': jax.random.normal(ks[7], (D_MODEL, D_MODEL), jnp.float32) * s, 'bv': jax.random.normal(ks[8], (D_MODEL,), jnp.float32) * s, 'Wo': jax.random.normal(ks[9], (D_MODEL, D_MODEL), jnp.float32) * s, 'bo': jax.random.normal(ks[10], (D_MODEL,), jnp.float32) * s}
    _L1_xattn_all = _L1_xattn_setup()
    _L1_xattn_in = {k: v for k, v in _L1_xattn_all.items() if k in ('Wq', 'bq', 'Wk', 'bk', 'Wv', 'bv', 'Wo', 'bo')}
    del _L1_xattn_all

    def _L1_ffn_setup():
        import jax, jax.numpy as jnp
        import numpy as np
        B, S, H, F, G = (8, 512, 256, 1024, 128)
        EPS = 1e-05

        def _dequant(q, scales, g):
            K, N = q.shape
            w = (q.astype(jnp.float32) - 128.0).reshape(K // g, g, N) * scales[:, None, :]
            return w.reshape(K, N)
        key = jax.random.key(seed)
        ks = jax.random.split(key, 8)
        x = jax.random.normal(ks[0], (B, S, H), dtype=jnp.float32)
        ln_gamma = jnp.ones((H,), jnp.float32)
        ln_beta = jnp.zeros((H,), jnp.float32)
        fc1_q = jax.random.randint(ks[1], (H, F), 0, 64, dtype=jnp.int32)
        fc2_q = jax.random.randint(ks[2], (F, H), 0, 64, dtype=jnp.int32)
        fc1_scales = jax.random.uniform(ks[3], (H // G, F), jnp.float32) * 0.02 + 0.001
        fc2_scales = jax.random.uniform(ks[4], (F // G, H), jnp.float32) * 0.02 + 0.001
        fc1_bias = jax.random.normal(ks[5], (F,), jnp.float32) * 0.02
        fc2_bias = jax.random.normal(ks[6], (H,), jnp.float32) * 0.02
        return {'x': x, 'ln_gamma': ln_gamma, 'ln_beta': ln_beta, 'fc1_q': fc1_q, 'fc1_scales': fc1_scales, 'fc1_bias': fc1_bias, 'fc2_q': fc2_q, 'fc2_scales': fc2_scales, 'fc2_bias': fc2_bias}
    _L1_ffn_all = _L1_ffn_setup()
    _L1_ffn_in = {k: v for k, v in _L1_ffn_all.items() if k in ('ln_gamma', 'ln_beta', 'fc1_q', 'fc1_scales', 'fc1_bias', 'fc2_q', 'fc2_scales', 'fc2_bias')}
    del _L1_ffn_all

    def _L2_xattn_setup():
        import jax, jax.numpy as jnp
        import numpy as np
        B, N, M, D_MODEL, D_K, D_V = (8, 512, 512, 256, 256, 256)
        NEG = -1000000000.0
        key = jax.random.key(seed)
        ks = jax.random.split(key, 10)
        s = 1.0 / np.sqrt(D_MODEL)
        return {'querys': jax.random.normal(ks[0], (B, N, D_MODEL), jnp.float32), 'keys': jax.random.normal(ks[1], (B, M, D_MODEL), jnp.float32), 'values': jax.random.normal(ks[2], (B, M, D_MODEL), jnp.float32), 'mask': jax.random.randint(ks[3], (N, M), 0, 2, jnp.int32), 'Wq': jax.random.normal(ks[4], (D_K, D_MODEL), jnp.float32) * s, 'bq': jnp.zeros((D_K,), jnp.float32), 'Wk': jax.random.normal(ks[5], (D_K, D_MODEL), jnp.float32) * s, 'bk': jnp.zeros((D_K,), jnp.float32), 'Wv': jax.random.normal(ks[6], (D_V, D_MODEL), jnp.float32) * s, 'bv': jnp.zeros((D_V,), jnp.float32)}
    _L2_xattn_all = _L2_xattn_setup()
    _L2_xattn_in = {k: v for k, v in _L2_xattn_all.items() if k in ('Wq', 'bq', 'Wk', 'bk', 'Wv', 'bv')}
    del _L2_xattn_all

    def _L2_ffn_setup():
        import jax, jax.numpy as jnp
        import numpy as np
        from jax import lax
        T, B, I, M, O = (64, 64, 256, 256, 256)

        def _xavier(key, shape):
            fan_out, fan_in = shape
            limit = float(np.sqrt(6.0 / (fan_in + fan_out)))
            return jax.random.uniform(key, shape, jnp.float32, -limit, limit)
        key = jax.random.key(seed)
        ks = jax.random.split(key, 9)
        x = jax.random.normal(ks[0], (T, B, I), jnp.float32)
        return {'x': x, 'wf': _xavier(ks[1], (M, I)), 'uf': _xavier(ks[2], (M, M)), 'bf': jnp.zeros((M,), jnp.float32), 'wi': _xavier(ks[3], (M, I)), 'ui': _xavier(ks[4], (M, M)), 'bi': jnp.zeros((M,), jnp.float32), 'wc': _xavier(ks[5], (M, I)), 'uc': _xavier(ks[6], (M, M)), 'bc': jnp.zeros((M,), jnp.float32), 'wo': _xavier(ks[7], (O, I)), 'uo': _xavier(ks[8], (O, M)), 'bo': jnp.zeros((O,), jnp.float32), 'in_c': jnp.zeros((M,), jnp.float32)}
    _L2_ffn_all = _L2_ffn_setup()
    _L2_ffn_in = {k: v for k, v in _L2_ffn_all.items() if k in ('wf', 'uf', 'bf', 'wi', 'ui', 'bi', 'wc', 'uc', 'bc', 'wo', 'uo', 'bo', 'in_c')}
    del _L2_ffn_all

    def _L3_xattn_setup():
        import jax, jax.numpy as jnp
        import numpy as np
        D_MODEL = 256
        NUM_HEADS = 16

        def _split_heads(x, n_heads):
            B, L, D = x.shape
            return x.reshape(B, L, n_heads, D // n_heads).transpose(0, 2, 1, 3)
        key = jax.random.key(seed)
        ks = jax.random.split(key, 11)
        B, L, D = (1, 1024, D_MODEL)
        s = 1.0 / np.sqrt(D)
        inp = {'Q': jax.random.normal(ks[0], (B, L, D), jnp.float32), 'K': jax.random.normal(ks[1], (B, L, D), jnp.float32), 'V': jax.random.normal(ks[2], (B, L, D), jnp.float32), 'w_q': jax.random.normal(ks[3], (D, D), jnp.float32) * s, 'b_q': jax.random.normal(ks[4], (D,), jnp.float32) * s, 'w_k': jax.random.normal(ks[5], (D, D), jnp.float32) * s, 'b_k': jax.random.normal(ks[6], (D,), jnp.float32) * s, 'w_v': jax.random.normal(ks[7], (D, D), jnp.float32) * s, 'b_v': jax.random.normal(ks[8], (D,), jnp.float32) * s, 'w_o': jax.random.normal(ks[9], (D, D), jnp.float32) * s, 'b_o': jax.random.normal(ks[10], (D,), jnp.float32) * s}
        return inp
    _L3_xattn_all = _L3_xattn_setup()
    _L3_xattn_in = {k: v for k, v in _L3_xattn_all.items() if k in ('w_q', 'b_q', 'w_k', 'b_k', 'w_v', 'b_v', 'w_o', 'b_o')}
    del _L3_xattn_all

    def _L3_ffn_setup():
        import jax, jax.numpy as jnp
        import numpy as np
        E, K = (8, 2)
        DM, DE = (256, 704)
        B, S = (1, 512)
        EPS = 1e-06

        def _rmsnorm(x, w):
            var = jnp.mean(jnp.square(x), axis=-1, keepdims=True)
            return x * jax.lax.rsqrt(var + EPS) * w
        key = jax.random.key(seed)
        kx, kg, k1, k2, k3 = jax.random.split(key, 5)

        def kaiming_uniform(k, shape, fan_in):
            bound = 1.0 / np.sqrt(fan_in)
            return jax.random.uniform(k, shape, jnp.float32, -bound, bound)
        return {'x': jax.random.normal(kx, (B, S, DM), jnp.float32), 'gate_w': kaiming_uniform(kg, (E, DM), DM), 'rms_w': jnp.ones((DM,), jnp.float32), 'W1': kaiming_uniform(k1, (E, DE, DM), DE * DM), 'W2': kaiming_uniform(k2, (E, DE, DM), DE * DM), 'W3': kaiming_uniform(k3, (E, DM, DE), DM * DE)}
    _L3_ffn_all = _L3_ffn_setup()
    _L3_ffn_in = {k: v for k, v in _L3_ffn_all.items() if k in ('gate_w', 'rms_w', 'W1', 'W2', 'W3')}
    del _L3_ffn_all
    return {'x': x, 'ctx_1024': ctx_1024, 'mask_BxS2_bf1': mask_BxS2_bf1, 'mask_Bx1x1xS2_ff1': mask_Bx1x1xS2_ff1, 'mask_SxS2_ik1': mask_SxS2_ik1, 'g_xattn': g_xattn, 'g_ffn': g_ffn, 'L0_xattn_Wq': _L0_xattn_in['Wq'], 'L0_xattn_bq': _L0_xattn_in['bq'], 'L0_xattn_Wkv': _L0_xattn_in['Wkv'], 'L0_xattn_bkv': _L0_xattn_in['bkv'], 'L0_xattn_Wo': _L0_xattn_in['Wo'], 'L0_xattn_bo': _L0_xattn_in['bo'], 'L0_ffn_gamma_light': _L0_ffn_in['gamma_light'], 'L0_ffn_wq_light': _L0_ffn_in['wq_light'], 'L0_ffn_wkv_light': _L0_ffn_in['wkv_light'], 'L0_ffn_wo_light': _L0_ffn_in['wo_light'], 'L0_ffn_q_routing_token': _L0_ffn_in['q_routing_token'], 'L0_ffn_kv_routing_token': _L0_ffn_in['kv_routing_token'], 'L0_ffn_gamma_heavy': _L0_ffn_in['gamma_heavy'], 'L0_ffn_wq_heavy': _L0_ffn_in['wq_heavy'], 'L0_ffn_wkv_heavy': _L0_ffn_in['wkv_heavy'], 'L0_ffn_wo_heavy': _L0_ffn_in['wo_heavy'], 'L1_xattn_Wq': _L1_xattn_in['Wq'], 'L1_xattn_bq': _L1_xattn_in['bq'], 'L1_xattn_Wk': _L1_xattn_in['Wk'], 'L1_xattn_bk': _L1_xattn_in['bk'], 'L1_xattn_Wv': _L1_xattn_in['Wv'], 'L1_xattn_bv': _L1_xattn_in['bv'], 'L1_xattn_Wo': _L1_xattn_in['Wo'], 'L1_xattn_bo': _L1_xattn_in['bo'], 'L1_ffn_ln_gamma': _L1_ffn_in['ln_gamma'], 'L1_ffn_ln_beta': _L1_ffn_in['ln_beta'], 'L1_ffn_fc1_q': _L1_ffn_in['fc1_q'], 'L1_ffn_fc1_scales': _L1_ffn_in['fc1_scales'], 'L1_ffn_fc1_bias': _L1_ffn_in['fc1_bias'], 'L1_ffn_fc2_q': _L1_ffn_in['fc2_q'], 'L1_ffn_fc2_scales': _L1_ffn_in['fc2_scales'], 'L1_ffn_fc2_bias': _L1_ffn_in['fc2_bias'], 'L2_xattn_Wq': _L2_xattn_in['Wq'], 'L2_xattn_bq': _L2_xattn_in['bq'], 'L2_xattn_Wk': _L2_xattn_in['Wk'], 'L2_xattn_bk': _L2_xattn_in['bk'], 'L2_xattn_Wv': _L2_xattn_in['Wv'], 'L2_xattn_bv': _L2_xattn_in['bv'], 'L2_ffn_wf': _L2_ffn_in['wf'], 'L2_ffn_uf': _L2_ffn_in['uf'], 'L2_ffn_bf': _L2_ffn_in['bf'], 'L2_ffn_wi': _L2_ffn_in['wi'], 'L2_ffn_ui': _L2_ffn_in['ui'], 'L2_ffn_bi': _L2_ffn_in['bi'], 'L2_ffn_wc': _L2_ffn_in['wc'], 'L2_ffn_uc': _L2_ffn_in['uc'], 'L2_ffn_bc': _L2_ffn_in['bc'], 'L2_ffn_wo': _L2_ffn_in['wo'], 'L2_ffn_uo': _L2_ffn_in['uo'], 'L2_ffn_bo': _L2_ffn_in['bo'], 'L2_ffn_in_c': _L2_ffn_in['in_c'], 'L3_xattn_w_q': _L3_xattn_in['w_q'], 'L3_xattn_b_q': _L3_xattn_in['b_q'], 'L3_xattn_w_k': _L3_xattn_in['w_k'], 'L3_xattn_b_k': _L3_xattn_in['b_k'], 'L3_xattn_w_v': _L3_xattn_in['w_v'], 'L3_xattn_b_v': _L3_xattn_in['b_v'], 'L3_xattn_w_o': _L3_xattn_in['w_o'], 'L3_xattn_b_o': _L3_xattn_in['b_o'], 'L3_ffn_gate_w': _L3_ffn_in['gate_w'], 'L3_ffn_rms_w': _L3_ffn_in['rms_w'], 'L3_ffn_W1': _L3_ffn_in['W1'], 'L3_ffn_W2': _L3_ffn_in['W2'], 'L3_ffn_W3': _L3_ffn_in['W3']}

def reference(x, ctx_1024, mask_BxS2_bf1, mask_Bx1x1xS2_ff1, mask_SxS2_ik1, g_xattn, g_ffn, L0_xattn_Wq, L0_xattn_bq, L0_xattn_Wkv, L0_xattn_bkv, L0_xattn_Wo, L0_xattn_bo, L0_ffn_gamma_light, L0_ffn_wq_light, L0_ffn_wkv_light, L0_ffn_wo_light, L0_ffn_q_routing_token, L0_ffn_kv_routing_token, L0_ffn_gamma_heavy, L0_ffn_wq_heavy, L0_ffn_wkv_heavy, L0_ffn_wo_heavy, L1_xattn_Wq, L1_xattn_bq, L1_xattn_Wk, L1_xattn_bk, L1_xattn_Wv, L1_xattn_bv, L1_xattn_Wo, L1_xattn_bo, L1_ffn_ln_gamma, L1_ffn_ln_beta, L1_ffn_fc1_q, L1_ffn_fc1_scales, L1_ffn_fc1_bias, L1_ffn_fc2_q, L1_ffn_fc2_scales, L1_ffn_fc2_bias, L2_xattn_Wq, L2_xattn_bq, L2_xattn_Wk, L2_xattn_bk, L2_xattn_Wv, L2_xattn_bv, L2_ffn_wf, L2_ffn_uf, L2_ffn_bf, L2_ffn_wi, L2_ffn_ui, L2_ffn_bi, L2_ffn_wc, L2_ffn_uc, L2_ffn_bc, L2_ffn_wo, L2_ffn_uo, L2_ffn_bo, L2_ffn_in_c, L3_xattn_w_q, L3_xattn_b_q, L3_xattn_w_k, L3_xattn_b_k, L3_xattn_w_v, L3_xattn_b_v, L3_xattn_w_o, L3_xattn_b_o, L3_ffn_gate_w, L3_ffn_rms_w, L3_ffn_W1, L3_ffn_W2, L3_ffn_W3):
    import jax
    import jax.numpy as jnp

    def _L0_xattn_ref(x, context, context_mask, Wq, bq, Wkv, bkv, Wo, bo):
        import jax, jax.numpy as jnp
        import numpy as np
        GAMMA = 10.0
        BASE = 10000.0
        SCALE = 64 ** (-0.5)
        NUM_HEADS = 16

        def _larope(t, seq_len):
            B, H, L, D = t.shape
            inv_freq = 1.0 / BASE ** (jnp.arange(0, D, 2, dtype=jnp.float32) / D)
            pos = GAMMA * (jnp.arange(L, dtype=jnp.float32) / float(seq_len))
            ang = pos[:, None] * inv_freq
            cos = jnp.cos(ang)
            sin = jnp.sin(ang)
            te, to = (t[..., 0::2], t[..., 1::2])
            re = te * cos - to * sin
            ro = te * sin + to * cos
            return jnp.stack([re, ro], axis=-1).reshape(t.shape)
        B, Lq, D = x.shape
        Lk = context.shape[1]
        H = NUM_HEADS
        hd = D // H
        q = x @ Wq + bq
        kv = context @ Wkv + bkv
        k, v = jnp.split(kv, 2, axis=-1)
        q = q.reshape(B, Lq, H, hd).transpose(0, 2, 1, 3)
        k = k.reshape(B, Lk, H, hd).transpose(0, 2, 1, 3)
        v = v.reshape(B, Lk, H, hd).transpose(0, 2, 1, 3)
        q = _larope(q, Lq)
        k = _larope(k, Lk)
        scores = jnp.einsum('bhqd,bhkd->bhqk', q, k) * SCALE
        scores = jnp.where(context_mask[:, None, None, :], scores, -jnp.inf)
        attn = jax.nn.softmax(scores, axis=-1)
        out = jnp.einsum('bhqk,bhkd->bhqd', attn, v)
        out = out.transpose(0, 2, 1, 3).reshape(B, Lq, H * hd)
        return out @ Wo + bo

    def _L0_ffn_ref(x, gamma_light, wq_light, wkv_light, wo_light, q_routing_token, kv_routing_token, gamma_heavy, wq_heavy, wkv_heavy, wo_heavy):
        import jax, jax.numpy as jnp
        import numpy as np
        B, N, D = (4, 2048, 256)
        HEADS, DH = (8, 64)
        HID = HEADS * DH
        WIN = 128
        NQ, NKV = (256, 512)
        EPS, N_ITERS, FETCH_K = (1.0, 50, 9.0 / 8.0)
        SCALE = DH ** (-0.5)

        def rmsnorm(x, gamma):
            norm = jnp.maximum(jnp.linalg.norm(x, axis=-1, keepdims=True), 1e-12)
            return x / norm * x.shape[-1] ** 0.5 * gamma

        def coor_descent(s, k):
            logk = jnp.log(jnp.asarray(k, s.dtype))

            def body(_, ab):
                a, b = ab
                a = EPS * (logk - jax.nn.logsumexp((s + b) / EPS, axis=-1, keepdims=True))
                b = -jax.nn.relu(s + a)
                return (a, b)
            a, b = jax.lax.fori_loop(0, N_ITERS, body, (jnp.zeros_like(s[..., :1]), -s))
            return jnp.exp((s + a + b) / EPS)

        def route(x, routing_token, num_tokens):
            s = jnp.einsum('bnd,d->bn', x, routing_token)
            k = min(num_tokens * FETCH_K, x.shape[1])
            scores = coor_descent(s, k)
            sel_scores, sel_idx = jax.lax.top_k(scores, num_tokens)
            sel_scores = sel_scores + jax.lax.stop_gradient(1.0 - sel_scores)
            return (sel_scores, sel_idx)

        def light_local_attn(x, gamma, wq, wkv, wo):
            b, n, d = x.shape
            xn = rmsnorm(x, gamma)
            q = xn @ wq
            k, v = jnp.split(xn @ wkv, 2, axis=-1)

            def win(t):
                return t.reshape(b, n // WIN, WIN, HEADS, DH).transpose(0, 1, 3, 2, 4)
            q, k, v = (win(q) * SCALE, win(k), win(v))
            attn = jax.nn.softmax(jnp.einsum('bwhid,bwhjd->bwhij', q, k), axis=-1)
            out = jnp.einsum('bwhij,bwhjd->bwhid', attn, v)
            out = out.transpose(0, 1, 3, 2, 4).reshape(b, n, HID)
            return out @ wo

        def heavy_attn(xq, context, scores_kv, gamma, wq, wkv_t, wo):
            b, nq, d = xq.shape
            nkv = context.shape[1]
            xqn = rmsnorm(xq, gamma)
            ctx = rmsnorm(context, gamma)[:, None]
            q = (xqn @ wq).reshape(b, nq, HEADS, DH).transpose(0, 2, 1, 3) * SCALE
            kvw = wkv_t.reshape(1, HEADS, 2 * DH, d)
            kv = jnp.einsum('rhdi,brni->brhnd', kvw, ctx)
            k, v = jnp.split(kv, 2, axis=-1)
            v = v * scores_kv[:, None, None, :, None]
            k = k.reshape(b, HEADS, nkv, DH)
            v = v.reshape(b, HEADS, nkv, DH)
            attn = jax.nn.softmax(jnp.einsum('bhid,bhjd->bhij', q, k), axis=-1)
            out = jnp.einsum('bhij,bhjd->bhid', attn, v)
            out = out.transpose(0, 2, 1, 3).reshape(b, nq, HID)
            return out @ wo
        b = x.shape[0]
        light_out = light_local_attn(x, gamma_light, wq_light, wkv_light, wo_light)
        scores_q, idx_q = route(x, q_routing_token, NQ)
        scores_kv, idx_kv = route(x, kv_routing_token, NKV)
        routed_q = jnp.take_along_axis(x, idx_q[..., None], axis=1)
        routed_kv = jnp.take_along_axis(x, idx_kv[..., None], axis=1)
        routed_out = heavy_attn(routed_q, routed_kv, scores_kv, gamma_heavy, wq_heavy, wkv_heavy, wo_heavy)
        routed_out = routed_out * scores_q[..., None]
        heavy_out = jnp.zeros_like(x).at[jnp.arange(b)[:, None], idx_q].set(routed_out)
        return light_out + heavy_out

    def _L1_xattn_ref(Q, K, V, mask, Wq, bq, Wk, bk, Wv, bv, Wo, bo):
        import jax, jax.numpy as jnp
        import numpy as np
        D_MODEL = 256
        NUM_HEADS = 16
        DEPTH = D_MODEL // NUM_HEADS

        def _split_heads(x, B):
            return x.reshape(B, -1, NUM_HEADS, DEPTH).transpose(0, 2, 1, 3)
        B = Q.shape[0]
        q = _split_heads(Q @ Wq.T + bq, B)
        k = _split_heads(K @ Wk.T + bk, B)
        v = _split_heads(V @ Wv.T + bv, B)
        scale = 1.0 / jnp.sqrt(jnp.asarray(DEPTH, q.dtype))
        scores = jnp.einsum('bhqd,bhkd->bhqk', q, k) * scale
        scores = jnp.where(mask == 0, jnp.asarray(-1000000000.0, scores.dtype), scores)
        attn = jax.nn.softmax(scores, axis=-1)
        out = jnp.einsum('bhqk,bhkd->bhqd', attn, v)
        out = out.transpose(0, 2, 1, 3).reshape(B, -1, D_MODEL)
        return out @ Wo.T + bo

    def _L1_ffn_ref(x, ln_gamma, ln_beta, fc1_q, fc1_scales, fc1_bias, fc2_q, fc2_scales, fc2_bias):
        import jax, jax.numpy as jnp
        import numpy as np
        B, S, H, F, G = (8, 512, 256, 1024, 128)
        EPS = 1e-05

        def _dequant(q, scales, g):
            K, N = q.shape
            w = (q.astype(jnp.float32) - 128.0).reshape(K // g, g, N) * scales[:, None, :]
            return w.reshape(K, N)
        residual = x
        mu = jnp.mean(x, axis=-1, keepdims=True)
        var = jnp.mean(jnp.square(x - mu), axis=-1, keepdims=True)
        h = (x - mu) * jax.lax.rsqrt(var + EPS) * ln_gamma + ln_beta
        hf = h.reshape(-1, H)
        w1 = _dequant(fc1_q, fc1_scales, G)
        y = hf @ w1 + fc1_bias
        y = jax.nn.silu(y)
        w2 = _dequant(fc2_q, fc2_scales, G)
        z = y @ w2 + fc2_bias
        return residual + 0.5 * z.reshape(residual.shape)

    def _L2_xattn_ref(querys, keys, values, mask, Wq, bq, Wk, bk, Wv, bv):
        import jax, jax.numpy as jnp
        import numpy as np
        B, N, M, D_MODEL, D_K, D_V = (8, 512, 512, 256, 256, 256)
        NEG = -1000000000.0
        q = querys @ Wq.T + bq
        k = keys @ Wk.T + bk
        v = values @ Wv.T + bv
        scores = jnp.einsum('bnd,bmd->bnm', q, k)
        scores = jnp.where(mask[None, :, :] == 0, NEG, scores)
        weights = jax.nn.softmax(scores, axis=2)
        out = jnp.einsum('bnm,bmd->bnd', weights, v)
        return out

    def _L2_ffn_ref(x, wf, uf, bf, wi, ui, bi, wc, uc, bc, wo, uo, bo, in_c):
        import jax, jax.numpy as jnp
        import numpy as np
        from jax import lax
        T, B, I, M, O = (64, 64, 256, 256, 256)

        def _xavier(key, shape):
            fan_out, fan_in = shape
            limit = float(np.sqrt(6.0 / (fan_in + fan_out)))
            return jax.random.uniform(key, shape, jnp.float32, -limit, limit)
        batch = x.shape[1]
        c0 = jnp.broadcast_to(in_c, (batch, in_c.shape[0]))

        def step(c, xt):
            ft = jax.nn.sigmoid(xt @ wf.T + c @ uf.T + bf)
            it = jax.nn.sigmoid(xt @ wi.T + c @ ui.T + bi)
            gt = jnp.tanh(xt @ wc.T + c @ uc.T + bc)
            c = ft * c + it * gt
            return (c, None)
        c_final, _ = lax.scan(step, c0, x)
        h = jnp.tanh(jnp.einsum('tbi,oi->tbo', x, wo) + c_final @ uo.T + bo)
        return h

    def _L3_xattn_ref(Q, K, V, w_q, b_q, w_k, b_k, w_v, b_v, w_o, b_o):
        import jax, jax.numpy as jnp
        import numpy as np
        D_MODEL = 256
        NUM_HEADS = 16

        def _split_heads(x, n_heads):
            B, L, D = x.shape
            return x.reshape(B, L, n_heads, D // n_heads).transpose(0, 2, 1, 3)
        H = NUM_HEADS
        q = _split_heads(Q @ w_q.T + b_q, H)
        k = _split_heads(K @ w_k.T + b_k, H)
        v = _split_heads(V @ w_v.T + b_v, H)
        d_h = q.shape[-1]
        scores = jnp.einsum('bhqd,bhkd->bhqk', q, k) / jnp.sqrt(jnp.float32(d_h))
        attn = jax.nn.softmax(scores, axis=-1)
        out = jnp.einsum('bhqk,bhkd->bhqd', attn, v)
        B, _, L, _ = out.shape
        out = out.transpose(0, 2, 1, 3).reshape(B, L, H * d_h)
        return out @ w_o.T + b_o

    def _L3_ffn_ref(x, gate_w, rms_w, W1, W2, W3):
        import jax, jax.numpy as jnp
        import numpy as np
        E, K = (8, 2)
        DM, DE = (256, 704)
        B, S = (1, 512)
        EPS = 1e-06

        def _rmsnorm(x, w):
            var = jnp.mean(jnp.square(x), axis=-1, keepdims=True)
            return x * jax.lax.rsqrt(var + EPS) * w
        y = _rmsnorm(x, rms_w)
        logits = jnp.einsum('bsd,ed->bse', y, gate_w)
        vals, idx = jax.lax.top_k(logits, K)
        w = jax.nn.softmax(vals, axis=-1)
        w_full = jnp.einsum('bsk,bske->bse', w, jax.nn.one_hot(idx, E, dtype=x.dtype))
        up = jnp.einsum('bsd,end->bsen', y, W1)
        gate = jnp.einsum('bsd,end->bsen', y, W2)
        h = jax.nn.silu(up) * gate
        out = jnp.einsum('bsen,emn->bsem', h, W3)
        comb = jnp.einsum('bsem,bse->bsm', out, w_full)
        return x + comb
    x = x + jnp.tanh(g_xattn[0]) * _L0_xattn_ref(_layernorm(x, axis=-1), ctx_1024, mask_BxS2_bf1, L0_xattn_Wq, L0_xattn_bq, L0_xattn_Wkv, L0_xattn_bkv, L0_xattn_Wo, L0_xattn_bo)
    x = x + jnp.tanh(g_ffn[0]) * _L0_ffn_ref(_layernorm(x, axis=-1), L0_ffn_gamma_light, L0_ffn_wq_light, L0_ffn_wkv_light, L0_ffn_wo_light, L0_ffn_q_routing_token, L0_ffn_kv_routing_token, L0_ffn_gamma_heavy, L0_ffn_wq_heavy, L0_ffn_wkv_heavy, L0_ffn_wo_heavy)
    x = x + jnp.tanh(g_xattn[1]) * _L1_xattn_ref(_layernorm(x, axis=-1), ctx_1024, ctx_1024, mask_Bx1x1xS2_ff1, L1_xattn_Wq, L1_xattn_bq, L1_xattn_Wk, L1_xattn_bk, L1_xattn_Wv, L1_xattn_bv, L1_xattn_Wo, L1_xattn_bo)
    x = x + jnp.tanh(g_ffn[1]) * _L1_ffn_ref(_layernorm(x, axis=-1), L1_ffn_ln_gamma, L1_ffn_ln_beta, L1_ffn_fc1_q, L1_ffn_fc1_scales, L1_ffn_fc1_bias, L1_ffn_fc2_q, L1_ffn_fc2_scales, L1_ffn_fc2_bias)
    x = x + jnp.tanh(g_xattn[2]) * _L2_xattn_ref(_layernorm(x, axis=-1), ctx_1024, ctx_1024, mask_SxS2_ik1, L2_xattn_Wq, L2_xattn_bq, L2_xattn_Wk, L2_xattn_bk, L2_xattn_Wv, L2_xattn_bv)
    x = x + jnp.tanh(g_ffn[2]) * _L2_ffn_ref(_layernorm(x, axis=-1), L2_ffn_wf, L2_ffn_uf, L2_ffn_bf, L2_ffn_wi, L2_ffn_ui, L2_ffn_bi, L2_ffn_wc, L2_ffn_uc, L2_ffn_bc, L2_ffn_wo, L2_ffn_uo, L2_ffn_bo, L2_ffn_in_c)
    x = x + jnp.tanh(g_xattn[3]) * _L3_xattn_ref(_layernorm(x, axis=-1), ctx_1024, ctx_1024, L3_xattn_w_q, L3_xattn_b_q, L3_xattn_w_k, L3_xattn_b_k, L3_xattn_w_v, L3_xattn_b_v, L3_xattn_w_o, L3_xattn_b_o)
    x = x + jnp.tanh(g_ffn[3]) * _L3_ffn_ref(_layernorm(x, axis=-1), L3_ffn_gate_w, L3_ffn_rms_w, L3_ffn_W1, L3_ffn_W2, L3_ffn_W3)
    return x

_drawn_inputs = setup_inputs


def setup_inputs(seed=0):
    import zlib

    import numpy as np

    out = dict(_drawn_inputs(seed))
    spreads = {'L0_xattn_bq': (0.0, 0.8),
     'L0_xattn_bkv': (0.0, 0.1),
     'L0_xattn_bo': (0.0, 0.364),
     'L0_ffn_gamma_light': (1.0, 0.2),
     'L0_ffn_gamma_heavy': (1.0, 0.6),
     'L1_ffn_ln_gamma': (1.0, 0.2),
     'L1_ffn_ln_beta': (0.0, 0.1),
     'L2_xattn_bq': (0.0, 2.0),
     'L2_xattn_bk': (0.0, 2.0),
     'L2_xattn_bv': (0.0, 2.0),
     'L2_ffn_bf': (0.0, 2.0),
     'L2_ffn_bi': (0.0, 2.0),
     'L2_ffn_bc': (0.0, 2.0),
     'L2_ffn_bo': (0.0, 2.0),
     'L2_ffn_in_c': (0.0, 2.0),
     'L3_ffn_rms_w': (1.0, 0.6)}
    factors = {'L0_ffn_kv_routing_token': 200.0,
     'L1_xattn_bq': 8.0,
     'L1_xattn_bk': 200.0,
     'L1_xattn_bo': 3.495,
     'L1_ffn_fc1_bias': 200.0,
     'L1_ffn_fc2_bias': 200.0,
     'L2_xattn_Wq': 64.0,
     'L2_xattn_Wk': 195.52,
     'L2_xattn_Wv': 64.0,
     'L2_ffn_wf': 200.0,
     'L2_ffn_uf': 200.0,
     'L2_ffn_wi': 200.0,
     'L2_ffn_ui': 200.0,
     'L2_ffn_wc': 200.0,
     'L2_ffn_uc': 200.0,
     'L2_ffn_wo': 200.0,
     'L2_ffn_uo': 200.0,
     'L3_xattn_w_q': 67.005,
     'L3_xattn_b_q': 200.0,
     'L3_xattn_w_k': 68.406,
     'L3_xattn_b_k': 200.0,
     'L3_xattn_w_v': 8.0,
     'L3_xattn_b_v': 200.0,
     'L3_xattn_w_o': 8.0,
     'L3_xattn_b_o': 200.0,
     'L3_ffn_gate_w': 200.0,
     'L3_ffn_W1': 200.0,
     'L3_ffn_W2': 200.0,
     'L3_ffn_W3': 200.0}
    for name, (base, spread) in spreads.items():
        noise = np.random.default_rng([zlib.crc32(name.encode()), seed]).standard_normal(out[name].shape)
        drawn = base * np.exp(spread * noise) if base else spread * noise
        out[name] = jnp.asarray(drawn.astype(out[name].dtype))
    for name, factor in factors.items():
        out[name] = (out[name] * factor).astype(out[name].dtype)
    return out
```

```python
from contextlib import ExitStack

import concourse.bass as bass
from concourse import mybir
import numpy as np

F32 = mybir.dt.float32
BF16 = mybir.dt.bfloat16
I32 = mybir.dt.int32
U8 = mybir.dt.uint8
ALU = mybir.AluOpType
ACT = mybir.ActivationFunctionType
AX_X = mybir.AxisListType.X

P = 128
B, S, D = 8, 512, 256
TB = S // P
NT = B * TB
KD = D // P
SC = 64
NH, HD = 16, 16
HH = NH // KD
NP = HH // 2
VW = HD + 1
LN_EPS = 1e-5
STAGES = ["L0_xattn", "L0_ffn", "L1_xattn", "L1_ffn", "L2_xattn", "L2_ffn", "L3_xattn", "L3_ffn"]

NE, DE = 8, 704
KE = -(-DE // P)
HE = DE // 2
MOE_TILES = 2 * B * S // P + NE
E_N = 2 * KD * DE + KE * D
MOE_N = 3400



def shape_constants():
    p = np.arange(P)
    f = np.float32
    out = {"ident": np.eye(P, dtype=f)}
    for name, scale in (("head8", 64 ** -0.5), ("head4", 0.25)):
        out[name] = ((p[:, None] // HD) == np.arange(HH)[None, :]).astype(f) * f(scale)
    swap = np.zeros((P, P), f)
    swap[p[0::2] + 1, p[0::2]] = -1.0
    swap[p[0::2], p[0::2] + 1] = 1.0
    out["swap"] = swap
    inv = (f(1.0) / np.power(f(10000.0), np.arange(0, HD, 2, dtype=f) / f(HD))).astype(f)
    for name, n in (("q", S), ("k", SC)):
        pos = (f(10.0) * (np.arange(n, dtype=f) / f(n))).astype(f)
        ang = (inv[(p % HD) // 2][:, None] * pos[None, :]).astype(f)
        out["cos_" + name] = np.cos(ang).astype(f)
        out["sin_" + name] = np.sin(ang).astype(f)
    q = np.arange(P)
    out["same_batch"] = ((q[:, None] // TB == q[None, :NT] // TB) & (q[:, None] < NT)).astype(f)
    tok = np.arange(TB)[None, :, None] * P + p[:, None, None]
    out["earlier"] = (np.arange(S)[None, None, :] < tok).astype(f).reshape(P, TB * S)
    out["expert"] = np.broadcast_to(np.arange(8, dtype=f)[None, :], (P, 8)).copy()
    out["before"] = (q[:, None] < q[None, :]).astype(f)
    out["ones"] = np.ones((P, P), f)
    out["batch_slot"] = np.broadcast_to((q[:NT] // TB * 256).astype(f)[None, :], (P, NT)).copy()
    out["slot_start"] = np.broadcast_to(P * np.arange(MOE_TILES, dtype=f)[None, :], (P, MOE_TILES)).copy()
    return out


ROTARY = ("cos_q", "sin_q", "cos_k", "sin_k")
OF_A_STAGE = ROTARY + ("earlier",)


def constant_columns():
    at, cols = 0, {}
    for name, a in shape_constants().items():
        if name in OF_A_STAGE:
            continue
        cols[name] = (at, a.shape[1])
        at += a.shape[1]
    return cols, at


CONST_AT, CONST_N = constant_columns()


W_N, A_N = 9216, 17000


def runs(numbers):
    out = []
    for n in sorted(numbers):
        if out and out[-1][1] == n:
            out[-1][1] = n + 1
        else:
            out.append([n, n + 1])
    return out


class Carver:

    def __init__(self, tensor, first, end):
        self.tensor, self.at, self.end = tensor, first, end

    def take(self, *shape):
        n = 1
        for s in shape:
            n *= s
        ap = self.tensor[:, self.at:self.at + n]
        self.at += n
        assert self.at <= self.end, (self.at, self.end)
        if len(shape) == 2:
            ap = ap.rearrange("p (a b) -> p a b", b=shape[1])
        elif len(shape) == 3:
            ap = ap.rearrange("p (a b c) -> p a b c", b=shape[1], c=shape[2])
        elif len(shape) == 4:
            ap = ap.rearrange("p (a b c d) -> p a b c d", b=shape[1], c=shape[2], d=shape[3])
        return ap


class Order:

    def __init__(self, eng, sem):
        self.eng, self.sem, self.base, self.k, self.i, self.per = eng, sem, 0, 0, None, 0

    def mark(self, ins):
        ins.then_inc(self.sem, 1)
        self.k += 1

    def turn(self, i, per):
        self.base, self.i, self.per, self.k = self.base + self.k, i, per, 0

    def end(self, turns):
        assert self.k == self.per, (self.k, self.per)
        self.base, self.i, self.k = self.base + turns * self.per, None, 0

    def settle(self, back=0):
        v = self.base + self.k - back
        self.eng.wait_ge(self.sem, v if self.i is None else self.i * self.per + v)


class Names:
    pass


def flamingo_kernel(nc, T, out, stages):
    ctx = ExitStack()
    with ctx:
        def sb(name, shape, dt=F32):
            return ctx.enter_context(nc.sbuf_tensor(name, shape, dt))

        def sem(name):
            return ctx.enter_context(nc.semaphore(name))

        numbers, handles = [[], []], [[], []]

        def stage_sems(k):
            for h in handles[k % 2]:
                nc.release_semaphore(h)
            handles[k % 2] = []
            used = iter(list(numbers[k % 2]))

            def take(name):
                num = next(used, None)
                h = nc.alloc_semaphore(name=name, num=num)
                if num is None:
                    numbers[k % 2].append(h.num)
                handles[k % 2].append(h)
                return h
            return take

        x_all = sb("x_all", [P, NT + TB, D])
        consts = sb("consts", [P, CONST_N])
        ctx2T = sb("ctx2T", [P, KD, B, 2 * SC])
        tg = sb("tg", [P, 8])
        minus_half = sb("minus_half", [P, TB])
        ones_bf = sb("ones_bf", [1, P], BF16)
        mem = sb("mem", [P, 2 * W_N + A_N])
        xn = sb("xn", [P, TB, D])
        xnT = sb("xnT", [P, KD, S])
        stats = sb("stats", [P, TB, 6])
        mean_var = sb("mean_var", [P, TB, 2])
        var_eps = sb("var_eps", [P, TB])
        rstd = sb("rstd", [P, TB])
        moe_small = sb("moe_small", [P, MOE_N])
        PS = ctx.enter_context(nc.psum_tensor("PS", [P, 8, 512], F32))

        def const(name, rows=P):
            at, n = CONST_AT[name]
            return consts[0:rows, at:at + n]

        ident = const("ident")

        x_loaded = sem("x_loaded")
        consts_loaded = sem("consts_loaded")
        ctx_loaded = sem("ctx_loaded")
        gates_loaded = sem("gates_loaded")
        gates_ready = sem("gates_ready")
        ctx_psum = sem("ctx_psum")
        ctx_ready = sem("ctx_ready")
        x_updated = sem("x_updated")
        out_stored = sem("out_stored")
        zeros_ready = sem("zeros_ready")
        sems_cleared = sem("sems_cleared")
        spare = sem("spare")
        dve_order = sem("dve_order")
        act_order = sem("act_order")
        pool_order = sem("pool_order")

        loaded = [sem(f"{name}_weights_loaded") for name in stages]
        plans = []
        for k, name in enumerate(stages):
            s = Names()
            s.name, s.k = name, k
            half = STAGES.index(name) % 2
            s.w = Carver(mem, half * W_N, (half + 1) * W_N)
            s.a = Carver(mem, 2 * W_N, 2 * W_N + A_N)
            s.mem = mem
            s.x_before = NT * k
            s.weights_loaded = loaded[k]
            s.looks_ahead = s.stores = False
            s.early_sync_program = s.sync_program = None
            s.loads = []
            s.gate = tg[:, STAGES.index(name) // 2 + 4 * (STAGES.index(name) % 2):][:, 0:1]
            stage, s.own_sem = stage_sems(k), sem
            s.var_ready, s.rstd_ready, s.ln_ready, s.xnT_psum, s.xnT_ready = (
                stage(f"{name}_{n}") for n in ("var_ready", "rstd_ready", "ln_ready", "xnT_psum", "xnT_ready"))
            PLAN[name](s, T, stage, moe_small)
            plans.append(s)

        block = ctx.enter_context(nc.Block())

        def dve_layernorm(dve, order, s, i, last_read=None):
            for t in range(TB):
                order.mark(dve.bn_stats(stats[:, t, :], x_all[:, i * TB + t, :]))
            order.settle()
            dve.sem_inc(spare, 1)
            for t in range(TB):
                order.mark(dve.bn_aggr(mean_var[:, t, :], stats[:, t, :]))
            order.settle()
            dve.tensor_scalar(var_eps[:], mean_var[:, :, 1], LN_EPS, None, ALU.add).then_inc(s.var_ready, 1)
            dve.wait_ge(s.rstd_ready, i + 1)
            dve.wait_ge(s.xnT_psum, KD * i)
            if last_read is not None:
                dve.wait_ge(*last_read)
            for t in range(TB):
                dve.tensor_scalar(xn[:, t, :], x_all[:, i * TB + t, :], mean_var[:, t, 0:1], rstd[:, t:t + 1],
                                  ALU.subtract, ALU.mult).then_inc(s.ln_ready, 1)

        LN_MARKS = 2 * TB

        def stage_start(eng, s):
            eng.wait_ge(x_updated, s.x_before)
            if s.k >= 2:
                eng.wait_ge(sems_cleared, s.k - 1)
                eng.sem_inc(spare, 1)
            if s.k == 0:
                eng.wait_ge(ctx_ready, 2 * KD)
            if s.k > 0 and plans[s.k - 1].looks_ahead:
                eng.wait_ge(plans[s.k - 1].xnT_ready, KD * (B + 1))

        def pool_rstd(pool, s, i):
            pool.wait_ge(s.var_ready, i + 1)
            nc.gpsimd.tensor_tensor(rstd[:], var_eps[:], minus_half[:], ALU.pow).then_inc(s.rstd_ready, 1)

        def pe_transpose_xn(pe, s, i, banks=(0, 1), src=None, ready=None):
            src = xn if src is None else src
            for k in range(KD):
                for t in range(TB):
                    if k == 0:
                        pe.wait_ge(ready or s.ln_ready, TB * i + t + 1)
                    last = nc.tensor.transpose(PS[:, banks[k], t * P:(t + 1) * P], src[:, t, k * P:(k + 1) * P], ident)
                last.then_inc(s.xnT_psum, 1)

        def act_copy_xnT(act, s, i, banks=(0, 1)):
            for k in range(KD):
                act.wait_ge(s.xnT_psum, KD * i + k + 1)
                nc.scalar.activation(xnT[:, k, :], PS[:, banks[k], :], ACT.Copy).then_inc(s.xnT_ready, 1)

        env = Names()
        env.LN_MARKS, env.PS, env.act_copy_xnT, env.const, env.ctx2T, env.dve_layernorm = LN_MARKS, PS, act_copy_xnT, const, ctx2T, dve_layernorm
        env.ident, env.mean_var, env.minus_half, env.nc, env.ones_bf, env.out_stored = ident, mean_var, minus_half, nc, ones_bf, out_stored
        env.pe_transpose_xn, env.pool_rstd, env.rstd, env.spare, env.stage_start, env.stats = pe_transpose_xn, pool_rstd, rstd, spare, stage_start, stats
        env.var_eps, env.x_all, env.x_updated, env.xn, env.xnT, env.zeros_ready = var_eps, x_all, x_updated, xn, xnT, zeros_ready

        @block.sync
        def _(sp):
            for k, s in enumerate(plans):
                if k > 0:
                    sp.wait_ge(x_updated, NT * k)
                if k >= 2:
                    for lo, hi in runs(numbers[k % 2]):
                        last = sp.sem_clear(range(lo, hi))
                    last.then_inc(sems_cleared, 1)
                if k == 0:
                    for b in range(B):
                        sp.dma_start(x_all[:, b * TB:(b + 1) * TB, :],
                                     T["x"][b].rearrange("(t p) d -> p t d", p=P)).then_inc(x_loaded, 16)
                for later in plans[k:k + 2] if k == 0 else plans[k + 1:k + 2]:
                    for dst, src in later.loads:
                        sp.dma_start(dst, src).then_inc(later.weights_loaded, 16)
                    if later.early_sync_program:
                        later.early_sync_program(sp, env, later)
                if s.sync_program:
                    s.sync_program(sp, env, s)
            for b in range(0 if plans[-1].stores else B):
                sp.wait_ge(x_updated, NT * (len(plans) - 1) + TB * (b + 1))
                sp.dma_start(out[b].rearrange("(t p) d -> p t d", p=P),
                             x_all[:, b * TB:(b + 1) * TB, :]).then_inc(out_stored, 16)
            if not plans[-1].stores:
                sp.wait_ge(out_stored, 16 * B)

        @block.gpsimd
        def _(pool):
            nc.gpsimd.memset(minus_half[:], -0.5).then_inc(pool_order, 1)
            pool.wait_ge(pool_order, 1)
            order = Order(pool, pool_order)
            order.k = 1
            for s in plans:
                stage_start(pool, s)
                s.pool(pool, order, env, s)

        @block.scalar
        def _(act):
            order = Order(act, act_order)
            act.dma_start(consts[:], T["consts"]).then_inc(consts_loaded, 16)
            ctx_v = T["ctx_1024"].rearrange("b s d -> (b s) d").rearrange("(t p) d -> p t d", p=P)
            act.dma_start(xn[:], ctx_v).then_inc(ctx_loaded, 16)
            act.dma_start(tg[:, 0:4], T["g_xattn"].rearrange("(a n) -> a n", a=1).broadcast_to([P, 4])).then_inc(gates_loaded, 16)
            act.dma_start(tg[:, 4:8], T["g_ffn"].rearrange("(a n) -> a n", a=1).broadcast_to([P, 4])).then_inc(gates_loaded, 16)
            act.wait_ge(gates_loaded, 32)
            nc.scalar.activation(tg[:], tg[:], ACT.Tanh).then_inc(gates_ready, 1)
            for k in range(KD):
                act.wait_ge(ctx_psum, k + 1)
                src = PS[:, k, :].rearrange("p (b s) -> p b s", s=SC)
                for e in range(2):
                    nc.scalar.activation(ctx2T[:, k, :, e * SC:(e + 1) * SC], src, ACT.Copy).then_inc(ctx_ready, 1)
            for s in plans:
                stage_start(act, s)
                s.act(act, order, env, s)

        @block.vector
        def _(dve):
            order = Order(dve, dve_order)
            order.mark(dve.memset(ones_bf[:], 1.0))
            order.mark(dve.memset(x_all[:, NT:NT + TB, :], 0.0))
            order.settle()
            dve.sem_inc(zeros_ready, 1)
            dve.wait_ge(consts_loaded, 16)
            dve.wait_ge(gates_ready, 1)
            dve.wait_ge(ctx_psum, KD)
            dve.wait_ge(x_loaded, 16 * B)
            for s in plans:
                stage_start(dve, s)
                s.dve(dve, order, env, s)

        @block.tensor
        def _(pe):
            pe.wait_ge(consts_loaded, 16)
            pe.wait_ge(ctx_loaded, 16)
            for k in range(KD):
                for t in range(B * SC // P):
                    last = nc.tensor.transpose(PS[:, k, t * P:(t + 1) * P], xn[:, t, k * P:(k + 1) * P], ident)
                last.then_inc(ctx_psum, 1)
            pe.wait_ge(ctx_ready, 2 * KD)
            for s in plans:
                stage_start(pe, s)
                s.pe(pe, env, s)


def plan_xattn(s, T, sem, small):
    L = s.name[:2]
    s.rope, s.masked = L == "L0", L in ("L0", "L1")
    take = s.w.take
    s.wq, s.wk, s.wv, s.wo = take(KD, D), take(KD, D), take(KD, D), take(KD, D)
    s.bq, s.bk, s.bv, s.bo = take(KD), take(KD), take(D), take(D)
    n = {c: T[f"{s.name}_{c}"] for c in ("wq", "wk", "wv", "wo", "bq", "bk")}
    for c, w in (("wq", s.wq), ("wk", s.wk), ("wv", s.wv), ("wo", s.wo)):
        s.loads.append((w, n[c].rearrange("p (k n) -> p k n", k=KD)))
    s.loads += [(s.bq, n["bq"]), (s.bk, n["bk"]),
                (s.bv, T[f"{s.name}_bv"].broadcast_to([P, D])), (s.bo, T[f"{s.name}_bo"].broadcast_to([P, D]))]
    if s.masked:
        s.mask = take(B * SC)
        mask = T["mask_L0" if s.rope else "mask_L1"].rearrange("a (b s) -> a b s", s=SC)
        s.mask_u8 = s.mask[:, 0:B * SC // 4].bitcast(U8)
        s.loads.append((s.mask_u8 if s.rope else s.mask, mask.rearrange("a b s -> a (b s)").broadcast_to([P, B * SC])))
    if s.rope:
        s.rotary = {n: take(w) for n, w in zip(ROTARY, (S, S, SC, SC))}
        s.loads += [(s.rotary[n], T["table_" + n]) for n in ROTARY]
    take = s.a.take
    s.kT = take(KD, B * SC)
    s.kbd = take(KD, HH, SC)
    s.vbd = take(B, KD * NP, 2 * VW)
    s.qT = take(KD, S)
    s.shifted, s.probs, s.probsT = take(2, S), take(2, S), take(2, S)
    s.o, s.oT = take(2, D), take(2, KD, P)
    s.recip = take(2, NH)
    s.gbo = take(D)
    s.maxes = take(2, HH)
    if s.masked:
        s.keep = take(B * SC)
        s.mask_row = take(B * SC // 2).bitcast(BF16)
    if s.rope:
        s.rot, s.rot2 = take(KD, S), take(KD, S)
    s.sems = {n: sem(f"{s.name}_{n}") for n in (
        "k_psum", "k_ready", "v_psum", "v_ready", "setup", "q_psum", "q_ready", "swap_psum", "q_roped", "kbd_ready",
        "scores", "shifted_ready", "exp_ready", "pT_psum", "pT_ready", "pv_psum", "o_ready", "oT_psum",
        "oT_ready", "y_psum", "biased")}
    s.pe, s.act, s.dve, s.pool = xattn_pe, xattn_act, xattn_dve, xattn_pool


def xattn_pe(pe, e, s):
    PS, nc = e.PS, e.nc
    pe.wait_ge(s.weights_loaded, 16 * len(s.loads))
    for f in range(KD):
        for k in range(KD):
            last = nc.tensor.matmul(PS[:, f, :], s.wk[:, k, f * P:(f + 1) * P], e.ctx2T[:, k, :, 0:SC],
                                    start=k == 0, stop=k == KD - 1)
        last.then_inc(s.sems["k_psum"], 1)
    if s.rope:
        pe.wait_ge(s.sems["k_ready"], KD)
        for f in range(KD):
            nc.tensor.matmul(PS[:, f, :], e.const("swap"), s.kT[:, f, :], start=True, stop=True)\
                .then_inc(s.sems["swap_psum"], 1)
    for b in range(B):
        if b >= 2:
            pe.wait_ge(s.sems["v_ready"], 2 * (b - 1))
        for k in range(KD):
            last = nc.tensor.matmul(PS[:, 2 + b % 2, 0:D], e.ctx2T[:, k, b, :], s.wv[:, k, :],
                                    start=k == 0, stop=k == KD - 1)
        last.then_inc(s.sems["v_psum"], 1)
    pe.wait_ge(s.sems["setup"], 1)
    swaps = KD if s.rope else 0
    with pe.Fori(0, B) as i:
        e.pe_transpose_xn(pe, s, i)
        pe.wait_ge(s.xnT_ready, KD * (i + 1))
        for f in range(KD):
            for k in range(KD):
                last = nc.tensor.matmul(PS[:, f, :], s.wq[:, k, f * P:(f + 1) * P], e.xnT[:, k, :],
                                        start=k == 0, stop=k == KD - 1)
            last.then_inc(s.sems["q_psum"], 1)
        if s.rope:
            pe.wait_ge(s.sems["q_ready"], KD * (i + 1))
            for f in range(KD):
                nc.tensor.matmul(PS[:, f, :], e.const("swap"), s.qT[:, f, :], start=True, stop=True)\
                    .then_inc(s.sems["swap_psum"], 1)
            pe.wait_ge(s.sems["q_roped"], i + 1)
        qT = s.rot if s.rope else s.qT
        pe.wait_ge(s.sems["q_ready"], KD * (i + 1))
        pe.wait_ge(s.sems["kbd_ready"], KD * (i + 1))

        def scores(u):
            t, f = u // KD, u % KD
            if u >= 2:
                pe.wait_ge(s.sems["shifted_ready"], 2 * TB * i + u - 1)
            last = nc.tensor.matmul(PS[:, 2 + u % 2, :], qT[:, f, t * P:(t + 1) * P],
                                    s.kbd[:, f, :, :], start=True, stop=not s.masked)
            if s.masked:
                row = s.mask_row[0:1, :].rearrange("a (o b s) -> a o b s", o=1, s=SC)[:, :, bass.ds(i, 1), :]
                last = nc.tensor.matmul(PS[:, 2 + u % 2, :], e.ones_bf[:],
                                        row.rearrange("a o b s -> a (o b) s").broadcast_to([1, HH, SC]), start=False, stop=True)
            last.then_inc(s.sems["scores"], 1)

        def transposes(u):
            pe.wait_ge(s.sems["exp_ready"], 2 * TB * i + u + 1)
            if u >= 2:
                pe.wait_ge(s.sems["pT_ready"], 2 * TB * i + u - 1)
            for j in range(NP):
                last = nc.tensor.transpose(PS[:, 4 + u % 2, j * P:(j + 1) * P],
                                           s.probs[:, u % 2, j * P:(j + 1) * P], e.ident)
            last.then_inc(s.sems["pT_psum"], 1)

        def values(u):
            t, f = u // KD, u % KD
            pe.wait_ge(s.sems["pT_ready"], 2 * TB * i + u + 1)
            if f == 0 and t >= 2:
                pe.wait_ge(s.sems["o_ready"], TB * i + t - 1)
            for j in range(NP):
                at = (f * NP + j) * 2 * VW
                last = nc.tensor.matmul(PS[:, 6 + t % 2, at:at + 2 * VW], s.probsT[:, u % 2, j * P:(j + 1) * P],
                                        s.vbd[:, bass.ds(i, 1), f * NP + j, :], start=True, stop=True)
            last.then_inc(s.sems["pv_psum"], 1)

        for step in range(2 * TB + 4):
            if step < 2 * TB:
                scores(step)
            if 1 <= step < 2 * TB + 1:
                transposes(step - 1)
            if 2 <= step < 2 * TB + 2:
                values(step - 2)
            if step >= 4 and step % 2 == 0:
                t = (step - 4) // 2
                pe.wait_ge(s.sems["o_ready"], TB * i + t + 1)
                if t >= 2:
                    pe.wait_ge(e.x_updated, s.x_before + TB * i + t - 1)
                for k in range(KD):
                    last = nc.tensor.transpose(PS[:, t % 2, k * P:(k + 1) * P], s.o[:, t % 2, k * P:(k + 1) * P], e.ident)
                last.then_inc(s.sems["oT_psum"], 1)
            if step >= 5 and step % 2 == 1:
                t = (step - 5) // 2
                pe.wait_ge(s.sems["oT_ready"], TB * i + t + 1)
                for k in range(KD):
                    last = nc.tensor.matmul(PS[:, t % 2, D:2 * D], s.oT[:, t % 2, k, :], s.wo[:, k, :],
                                            start=k == 0, stop=k == KD - 1)
                last.then_inc(s.sems["y_psum"], 1)


def xattn_act(act, order, e, s):
    PS, nc = e.PS, e.nc
    act.wait_ge(s.weights_loaded, 16 * len(s.loads))
    for f in range(KD):
        act.wait_ge(s.sems["k_psum"], f + 1)
        nc.scalar.activation(s.kT[:, f, :], PS[:, f, :], ACT.Identity, bias=s.bk[:, f:f + 1]).then_inc(s.sems["k_ready"], 1)
    with act.Fori(0, B) as i:
        e.act_copy_xnT(act, s, i)
        for f in range(KD):
            act.wait_ge(s.sems["q_psum"], KD * i + f + 1)
            nc.scalar.activation(s.qT[:, f, :], PS[:, f, :], ACT.Identity, bias=s.bq[:, f:f + 1]).then_inc(s.sems["q_ready"], 1)
        for step in range(2 * TB + 4):
            if step < 2 * TB:
                u = step
                act.wait_ge(s.sems["shifted_ready"], 2 * TB * i + u + 1)
                if u >= 2:
                    act.wait_ge(s.sems["pT_psum"], 2 * TB * i + u - 1)
                nc.scalar.activation(s.probs[:, u % 2, :], s.shifted[:, u % 2, :], ACT.Exp).then_inc(s.sems["exp_ready"], 1)
            if 1 <= step < 2 * TB + 1:
                u = step - 1
                act.wait_ge(s.sems["pT_psum"], 2 * TB * i + u + 1)
                if u >= 2:
                    act.wait_ge(s.sems["pv_psum"], 2 * TB * i + u - 1)
                nc.scalar.activation(s.probsT[:, u % 2, :], PS[:, 4 + u % 2, :], ACT.Copy).then_inc(s.sems["pT_ready"], 1)
            if step >= 4 and step % 2 == 0:
                t = (step - 4) // 2
                act.wait_ge(s.sems["oT_psum"], TB * i + t + 1)
                if t >= 2:
                    act.wait_ge(s.sems["y_psum"], TB * i + t - 1)
                nc.scalar.activation(s.oT[:, t % 2, :, :], PS[:, t % 2, 0:D].rearrange("p (k n) -> p k n", k=KD),
                                     ACT.Copy).then_inc(s.sems["oT_ready"], 1)


def xattn_dve(dve, order, e, s):
    PS = e.PS
    dve.wait_ge(s.weights_loaded, 16 * len(s.loads))
    order.mark(dve.memset(s.vbd, 0.0))
    if s.masked:
        order.mark(dve.tensor_scalar(s.keep, s.mask_u8 if s.rope else s.mask, 0.0, None, ALU.not_equal))
    order.settle()
    order.mark(dve.memset(s.vbd.rearrange("p b j (e v) -> p (b j e) v", v=VW)[:, :, HD:VW], 1.0))
    if s.masked:
        order.mark(dve.tensor_scalar(s.mask_row[0:1, :], s.keep[0:1, :], 1.0, 3e38 if s.rope else 1e9,
                                     ALU.subtract, ALU.mult))
    order.settle()
    for h in range(2):
        order.mark(dve.memset(s.vbd.rearrange("p b j (e v) -> p (b j) e v", v=VW)[h * SC:(h + 1) * SC, :, 1 - h, HD:VW], 0.0))
    if s.rope:
        cos = s.rotary["cos_k"].rearrange("p (o s) -> p o s", o=1).broadcast_to([P, B, SC])
        sin = s.rotary["sin_k"].rearrange("p (o s) -> p o s", o=1).broadcast_to([P, B, SC])
        for f in range(KD):
            dve.wait_ge(s.sems["swap_psum"], f + 1)
            order.mark(dve.tensor_tensor(s.rot2[:, f, :].rearrange("p (b s) -> p b s", s=SC),
                                         PS[:, f, :].rearrange("p (b s) -> p b s", s=SC), sin, ALU.mult))
            kf = s.kT[:, f, :].rearrange("p (b s) -> p b s", s=SC)
            order.mark(dve.tensor_tensor(kf, kf, cos, ALU.mult))
        order.settle()
        order.mark(dve.tensor_tensor(s.kT, s.kT, s.rot2, ALU.add))
    elif s.masked:
        dve.wait_ge(s.sems["k_ready"], KD)
        for f in range(KD):
            order.mark(dve.tensor_tensor(s.kT[:, f, :], s.kT[:, f, :], s.keep, ALU.mult))
    bv = s.bv.rearrange("p (j e d) -> p j e d", e=2, d=HD)
    order.settle()
    for b in range(B):
        dve.wait_ge(s.sems["v_psum"], b + 1)
        src = PS[:, 2 + b % 2, 0:D].rearrange("p (j e d) -> p j e d", e=2, d=HD)
        dst = s.vbd[:, b, :, :].rearrange("p j (e v) -> p j e v", v=VW)
        for h in range(2):
            r = slice(h * SC, (h + 1) * SC)
            dve.tensor_tensor(dst[r, :, h, 0:HD], src[r, :, h, :], bv[r, :, h, :], ALU.add).then_inc(s.sems["v_ready"], 1)
    dve.wait_ge(s.sems["k_ready"], KD)
    dve.wait_ge(s.sems["v_ready"], 2 * B)
    dve.tensor_scalar(s.gbo, s.bo, s.gate, None, ALU.mult).then_inc(s.sems["setup"], 1)

    with dve.Fori(0, B) as i:
        order.turn(i, e.LN_MARKS + 3 * TB + (3 if s.rope else 0))
        e.dve_layernorm(dve, order, s, i)
        if s.rope:
            dve.wait_ge(s.sems["q_ready"], KD * (i + 1))
            bc = lambda n: s.rotary[n].rearrange("p (o s) -> p o s", o=1).broadcast_to([P, KD, S])
            order.mark(dve.tensor_tensor(s.rot, s.qT, bc("cos_q"), ALU.mult))
            dve.wait_ge(s.sems["swap_psum"], KD * (i + 2))
            for f in range(KD):
                order.mark(dve.tensor_tensor(s.rot2[:, f, :], PS[:, f, :], s.rotary["sin_q"], ALU.mult))
            order.settle()
            dve.tensor_tensor(s.rot, s.rot, s.rot2, ALU.add).then_inc(s.sems["q_roped"], 1)
        for step in range(2 * TB + 6):
            if step < 2 * TB:
                u = step
                dve.wait_ge(s.sems["scores"], 2 * TB * i + u + 1)
                bank = PS[:, 2 + u % 2, :].rearrange("p (h s) -> p h s", s=SC)
                order.mark(dve.tensor_reduce(s.maxes[:, u % 2, :], bank, AX_X, ALU.max))
                order.settle()
                if u >= 2:
                    dve.wait_ge(s.sems["exp_ready"], 2 * TB * i + u - 1)
                dve.tensor_tensor(s.shifted[:, u % 2, :].rearrange("p (h s) -> p h s", s=SC), bank,
                                  s.maxes[:, u % 2, :].rearrange("p (h o) -> p h o", o=1).broadcast_to([P, HH, SC]),
                                  ALU.subtract).then_inc(s.sems["shifted_ready"], 1)
            if 3 <= step < 2 * TB + 3 and step % 2 == 1:
                t = (step - 3) // 2
                dve.wait_ge(s.sems["pv_psum"], 2 * (TB * i + t + 1))
                o = PS[:, 6 + t % 2, 0:NH * VW].rearrange("p (h v) -> p h v", v=VW)
                order.mark(dve.reciprocal(s.recip[:, t % 2, :], o[:, :, HD]))
                order.settle()
                if t >= 2:
                    dve.wait_ge(s.sems["oT_psum"], TB * i + t - 1)
                dve.tensor_tensor(s.o[:, t % 2, :].rearrange("p (h d) -> p h d", d=HD), o[:, :, 0:HD],
                                  s.recip[:, t % 2, :].rearrange("p (h o) -> p h o", o=1).broadcast_to([P, NH, HD]),
                                  ALU.mult).then_inc(s.sems["o_ready"], 1)
            if step >= 6 and step % 2 == 0:
                t = (step - 6) // 2
                dve.wait_ge(s.sems["y_psum"], TB * i + t + 1)
                if t == 0:
                    dve.wait_ge(s.sems["biased"], i + 1)
                tile = e.x_all[:, i * TB + t, :]
                dve.scalar_tensor_tensor(tile, PS[:, t % 2, D:2 * D], s.gate, tile, ALU.mult, ALU.add)\
                    .then_inc(e.x_updated, 1)
    order.end(B)


def xattn_pool(pool, order, e, s):
    nc = e.nc
    mask16 = e.const("head8" if s.rope else "head4").rearrange("p (h o) -> p h o", o=1).broadcast_to([P, HH, SC])
    pool.wait_ge(s.sems["setup"], 1)
    with pool.Fori(0, B) as i:
        e.pool_rstd(pool, s, i)
        pool.wait_ge(s.sems["scores"], 2 * TB * i)
        for f in range(KD):
            keys = s.kT[:, f, :].rearrange("p (b s) -> p b s", s=SC)[:, bass.ds(i, 1), :].broadcast_to([P, HH, SC])
            nc.gpsimd.tensor_tensor(s.kbd[:, f, :, :], keys, mask16, ALU.mult).then_inc(s.sems["kbd_ready"], 1)
        pool.wait_ge(s.ln_ready, TB * (i + 1))
        tiles = e.x_all[:, bass.ds(i * TB, TB), :]
        nc.gpsimd.tensor_tensor(tiles, tiles, s.gbo.rearrange("p (o d) -> p o d", o=1).broadcast_to([P, TB, D]),
                                ALU.add).then_inc(s.sems["biased"], 1)


FF = 1024
KF = FF // P


def plan_ffn1(s, T, sem, small):
    take = s.w.take
    s.w1, s.w2 = take(KD, FF), take(KF, D)
    s.sc1, s.sc2 = take(KD, FF), take(KF, D)
    s.b1, s.gamma, s.beta, s.b2 = take(KF), take(KD), take(KD), take(D)
    n = {c: T["L1_ffn_" + c] for c in ("q1", "q2", "sc1", "sc2", "b1", "gamma", "beta", "b2")}
    s.q1, s.q2 = s.w1.bitcast(I32), s.w2.bitcast(I32)
    s.loads += [(s.q1, n["q1"].rearrange("p (k n) -> p k n", k=KD)), (s.q2, n["q2"].rearrange("p (k n) -> p k n", k=KF)),
                (s.sc1.rearrange("p k n -> p (k n)"), n["sc1"].broadcast_to([P, KD * FF])),
                (s.sc2.rearrange("p k n -> p (k n)"), n["sc2"].broadcast_to([P, KF * D])),
                (s.b1, n["b1"]), (s.gamma, n["gamma"]), (s.beta, n["beta"]), (s.b2, n["b2"].broadcast_to([P, D]))]
    take = s.a.take
    s.hn = take(TB, D)
    s.hT = take(KD, S)
    s.yT = take(KF, S)
    s.xng = take(TB, D)
    s.gb2 = take(D)
    s.half_gate = take(1)
    s.sems = {n: sem(f"{s.name}_{n}") for n in (
        "setup", "var2_ready", "rstd2_ready", "hn_ready", "up_psum", "y_ready", "down_psum", "residual")}
    s.looks_ahead = True
    s.pe, s.act, s.dve, s.pool = ffn1_pe, ffn1_act, ffn1_dve, ffn1_pool


def ffn1_pe(pe, e, s):
    PS, nc = e.PS, e.nc
    pe.wait_ge(s.sems["setup"], 1)

    def front(i):
        e.pe_transpose_xn(pe, s, i, src=s.hn, ready=s.sems["hn_ready"])

    front(0)
    with pe.Fori(0, B) as i:
        pe.wait_ge(s.xnT_ready, KD * (i + 1))
        for n in range(KF):
            if n >= 4:
                pe.wait_ge(s.sems["y_ready"], KF * i + n - 3)
            for k in range(KD):
                last = nc.tensor.matmul(PS[:, 2 + n % 4, :], s.w1[:, k, n * P:(n + 1) * P], s.hT[:, k, :],
                                        start=k == 0, stop=k == KD - 1)
            last.then_inc(s.sems["up_psum"], 1)
        for t in range(TB):
            if t == TB - 1:
                front(i + 1)
            pe.wait_ge(e.x_updated, s.x_before + TB * i + max(t - 1, 0))
            pe.wait_ge(s.sems["y_ready"], KF * (i + 1))
            for n in range(KF):
                last = nc.tensor.matmul(PS[:, 6 + t % 2, 0:D], s.yT[:, n, t * P:(t + 1) * P], s.w2[:, n, :],
                                        start=n == 0, stop=n == KF - 1)
            last.then_inc(s.sems["down_psum"], 1)


def ffn1_act(act, order, e, s):
    PS, nc = e.PS, e.nc
    act.wait_ge(s.weights_loaded, 16 * len(s.loads))

    def front(i):
        for k in range(KD):
            act.wait_ge(s.xnT_psum, KD * i + k + 1)
            nc.scalar.activation(s.hT[:, k, :], PS[:, k, :], ACT.Identity, bias=s.beta[:, k:k + 1],
                                 scale=s.gamma[:, k:k + 1]).then_inc(s.xnT_ready, 1)

    front(0)
    with act.Fori(0, B) as i:
        for n in range(KF):
            act.wait_ge(s.sems["up_psum"], KF * i + n + 1)
            if n == 0:
                act.wait_ge(s.sems["down_psum"], TB * i)
            nc.scalar.activation(s.yT[:, n, :], PS[:, 2 + n % 4, :], ACT.Silu, bias=s.b1[:, n:n + 1]).then_inc(s.sems["y_ready"], 1)
        front(i + 1)


def ffn1_dve(dve, order, e, s):
    PS = e.PS
    dve.wait_ge(s.weights_loaded, 16 * len(s.loads))
    order.mark(dve.scalar_tensor_tensor(s.w1, s.q1, 128.0, s.sc1, ALU.subtract, ALU.mult))
    order.mark(dve.scalar_tensor_tensor(s.w2, s.q2, 128.0, s.sc2, ALU.subtract, ALU.mult))
    order.mark(dve.tensor_scalar(s.half_gate, s.gate, 0.5, None, ALU.mult))
    order.settle()
    dve.tensor_scalar(s.gb2, s.b2, s.half_gate, None, ALU.mult).then_inc(s.sems["setup"], 1)

    def front(i):
        e.dve_layernorm(dve, order, s, i, last_read=(s.sems["residual"], 2 * i))
        dve.wait_ge(s.ln_ready, TB * (i + 1))
        for t in range(TB):
            order.mark(dve.bn_stats(e.stats[:, t, :], e.xn[:, t, :]))
        order.settle()
        dve.sem_inc(e.spare, 1)
        for t in range(TB):
            order.mark(dve.bn_aggr(e.mean_var[:, t, :], e.stats[:, t, :]))
        order.settle()
        dve.tensor_scalar(e.var_eps[:], e.mean_var[:, :, 1], LN_EPS, None, ALU.add).then_inc(s.sems["var2_ready"], 1)
        dve.wait_ge(s.sems["rstd2_ready"], i + 1)
        for t in range(TB):
            dve.tensor_scalar(s.hn[:, t, :], e.xn[:, t, :], e.mean_var[:, t, 0:1], e.rstd[:, t:t + 1],
                              ALU.subtract, ALU.mult).then_inc(s.sems["hn_ready"], 1)

    front(0)
    with dve.Fori(0, B) as i:
        order.turn(i, 2 * e.LN_MARKS)
        front(i + 1)
        for t in range(TB):
            dve.wait_ge(s.sems["down_psum"], TB * i + t + 1)
            if t == 0:
                dve.wait_ge(s.sems["residual"], 2 * (i + 1))
            tile = e.x_all[:, i * TB + t, :]
            dve.scalar_tensor_tensor(tile, PS[:, 6 + t % 2, 0:D], s.half_gate, tile, ALU.mult, ALU.add)\
                .then_inc(e.x_updated, 1)
    order.end(B)


def ffn1_pool(pool, order, e, s):
    nc = e.nc
    pool.wait_ge(s.sems["setup"], 1)

    def front(i):
        e.pool_rstd(pool, s, i)
        pool.wait_ge(s.sems["var2_ready"], i + 1)
        nc.gpsimd.tensor_tensor(e.rstd[:], e.var_eps[:], e.minus_half[:], ALU.pow).then_inc(s.sems["rstd2_ready"], 1)

    front(0)
    gate = s.gate.rearrange("p (o d) -> p o d", o=1).broadcast_to([P, TB, D])
    bias = s.gb2.rearrange("p (o d) -> p o d", o=1).broadcast_to([P, TB, D])
    with pool.Fori(0, B) as i:
        order.turn(i, 1)
        tiles = e.x_all[:, bass.ds(i * TB, TB), :]
        pool.wait_ge(s.sems["hn_ready"], TB * (i + 1))
        nc.gpsimd.tensor_tensor(s.xng, e.xn[:], gate, ALU.mult).then_inc(s.sems["residual"], 1)
        pool.wait_ge(s.sems["residual"], 2 * i + 1)
        order.mark(nc.gpsimd.tensor_tensor(s.xng, s.xng, bias, ALU.add))
        order.settle()
        nc.gpsimd.tensor_tensor(tiles, tiles, s.xng, ALU.add).then_inc(s.sems["residual"], 1)
        front(i + 1)
    order.end(B)


def plan_xattn2(s, T, sem, small):
    take = s.w.take
    s.wq, s.wk, s.wv = take(KD, D), take(KD, D), take(KD, D)
    s.bq, s.bk, s.bv = take(KD), take(KD), take(D)
    s.mask = take(TB, SC)
    n = {c: T[f"{s.name}_{c}"] for c in ("wq", "wk", "wv", "bq", "bk", "bv")}
    for c, w in (("wq", s.wq), ("wk", s.wk), ("wv", s.wv)):
        s.loads.append((w, n[c].rearrange("p (k n) -> p k n", k=KD)))
    s.loads += [(s.bq, n["bq"]), (s.bk, n["bk"]), (s.bv, n["bv"].broadcast_to([P, D])),
                (s.mask.bitcast(I32), T["mask_L2"].rearrange("(t p) s -> p t s", p=P))]
    take = s.a.take
    s.keep, s.bias = take(TB, SC), take(TB, SC)
    s.kT = take(KD, B * SC)
    s.bq_wide = take(KD, P)
    s.qk = take(KD, B * SC)
    s.qk_bias = take(B * SC)
    s.v = take(B, D)
    s.sc, s.probs = take(TB, SC), take(TB, SC)
    s.maxes, s.sums, s.scale = take(TB), take(TB), take(TB)
    s.probsT = take(TB, P)
    s.sems = {n: sem(f"{s.name}_{n}") for n in (
        "k_psum", "k_ready", "qk_psum", "qk_ready", "v_psum", "v_ready", "setup", "scores", "shifted_ready",
        "exp_ready", "pT_psum", "pT_ready", "out_psum")}
    s.looks_ahead = True
    s.pe, s.act, s.dve, s.pool = xattn2_pe, xattn2_act, xattn2_dve, xattn2_pool


def xattn2_pe(pe, e, s):
    PS, nc = e.PS, e.nc
    pe.wait_ge(s.weights_loaded, 16 * len(s.loads))
    for f in range(KD):
        for k in range(KD):
            last = nc.tensor.matmul(PS[:, f, :], s.wk[:, k, f * P:(f + 1) * P], e.ctx2T[:, k, :, 0:SC],
                                    start=k == 0, stop=k == KD - 1)
        last.then_inc(s.sems["k_psum"], 1)
    pe.wait_ge(s.sems["k_ready"], KD + 1)
    for f in range(KD + 1):
        for k in range(KD):
            lhsT = s.wq[:, k, f * P:(f + 1) * P] if f < KD else s.bq_wide[:, k, :]
            last = nc.tensor.matmul(PS[:, 2 + f, :], lhsT, s.kT[:, k, :], start=k == 0, stop=k == KD - 1)
        last.then_inc(s.sems["qk_psum"], 1)
    for b in range(B):
        if b >= 2:
            pe.wait_ge(s.sems["v_ready"], b - 1)
        for k in range(KD):
            last = nc.tensor.matmul(PS[0:SC, 5 + b % 2, 0:D], e.ctx2T[:, k, b, 0:SC], s.wv[:, k, :],
                                    start=k == 0, stop=k == KD - 1)
        last.then_inc(s.sems["v_psum"], 1)
    pe.wait_ge(s.sems["setup"], 1)
    e.pe_transpose_xn(pe, s, 0)
    with pe.Fori(0, B) as i:
        pe.wait_ge(s.xnT_ready, KD * (i + 1))
        for t in range(TB):
            for k in range(KD):
                rhs = s.qk[:, k, :].rearrange("p (b s) -> p b s", s=SC)[:, bass.ds(i, 1), :]
                last = nc.tensor.matmul(PS[:, 2, t * SC:(t + 1) * SC], e.xnT[:, k, t * P:(t + 1) * P], rhs,
                                        start=k == 0, stop=k == KD - 1)
        last.then_inc(s.sems["scores"], 1)
        e.pe_transpose_xn(pe, s, i + 1)
        pe.wait_ge(s.sems["exp_ready"], i + 1)
        pe.sem_inc(e.spare, 1)
        for t in range(TB):
            last = nc.tensor.transpose(PS[0:SC, 3, t * P:(t + 1) * P], s.probs[:, t, :], e.ident)
        last.then_inc(s.sems["pT_psum"], 1)
        for t in range(TB):
            if t == 0:
                pe.wait_ge(s.sems["pT_ready"], i + 1)
                pe.sem_inc(e.spare, 1)
            if t >= 2:
                pe.wait_ge(e.x_updated, s.x_before + TB * i + t - 1)
                pe.sem_inc(e.spare, 1)
            nc.tensor.matmul(PS[:, 4 + t % 2, 0:D], s.probsT[0:SC, t, :], s.v[0:SC, bass.ds(i, 1), :],
                             start=True, stop=True).then_inc(s.sems["out_psum"], 1)


def xattn2_act(act, order, e, s):
    PS, nc = e.PS, e.nc
    act.wait_ge(s.weights_loaded, 16 * len(s.loads))
    for f in range(KD):
        act.wait_ge(s.sems["k_psum"], f + 1)
        nc.scalar.activation(s.kT[:, f, :], PS[:, f, :], ACT.Identity, bias=s.bk[:, f:f + 1]).then_inc(s.sems["k_ready"], 1)
    for f in range(KD + 1):
        act.wait_ge(s.sems["qk_psum"], f + 1)
        nc.scalar.activation(s.qk[:, f, :] if f < KD else s.qk_bias, PS[:, 2 + f, :], ACT.Copy).then_inc(s.sems["qk_ready"], 1)
    e.act_copy_xnT(act, s, 0)
    with act.Fori(0, B) as i:
        act.wait_ge(s.sems["scores"], i + 1)
        e.act_copy_xnT(act, s, i + 1)
        act.wait_ge(s.sems["shifted_ready"], i + 1)
        nc.scalar.activation(s.probs, s.sc, ACT.Exp).then_inc(s.sems["exp_ready"], 1)
        act.wait_ge(s.sems["pT_psum"], i + 1)
        nc.scalar.activation(s.probsT[0:SC, :, :], PS[0:SC, 3, :].rearrange("p (t n) -> p t n", n=P), ACT.Copy)\
            .then_inc(s.sems["pT_ready"], 1)


def xattn2_dve(dve, order, e, s):
    PS = e.PS
    dve.wait_ge(s.weights_loaded, 16 * len(s.loads))
    dve.tensor_copy(s.bq_wide, s.bq.rearrange("p (k o) -> p k o", o=1).broadcast_to([P, KD, P])).then_inc(s.sems["k_ready"], 1)
    order.mark(dve.tensor_scalar(s.keep, s.mask.bitcast(I32), 0.0, None, ALU.not_equal))
    order.settle()
    order.mark(dve.tensor_scalar(s.bias, s.keep, 1.0, 1e9, ALU.subtract, ALU.mult))
    for b in range(B):
        dve.wait_ge(s.sems["v_psum"], b + 1)
        dve.tensor_tensor(s.v[0:SC, b, :], PS[0:SC, 5 + b % 2, 0:D], s.bv[0:SC, :], ALU.add).then_inc(s.sems["v_ready"], 1)
    dve.wait_ge(s.sems["qk_ready"], KD + 1)
    dve.wait_ge(s.sems["v_ready"], B)
    dve.sem_inc(s.sems["setup"], 1)
    e.dve_layernorm(dve, order, s, 0)
    with dve.Fori(0, B) as i:
        order.turn(i, e.LN_MARKS + 7)
        dve.wait_ge(s.sems["scores"], i + 1)
        dve.wait_ge(s.sems["pT_psum"], i)
        qk_bias = s.qk_bias.rearrange("p (b s) -> p b s", s=SC)[:, bass.ds(i, 1), :].broadcast_to([P, TB, SC])
        order.mark(dve.tensor_tensor(s.sc, PS[:, 2, 0:TB * SC].rearrange("p (t s) -> p t s", s=SC), qk_bias, ALU.add))
        order.settle()
        order.mark(dve.tensor_tensor(s.sc, s.sc, s.keep, ALU.mult))
        order.settle()
        order.mark(dve.tensor_tensor(s.sc, s.sc, s.bias, ALU.add))
        order.settle()
        order.mark(dve.tensor_reduce(s.maxes, s.sc, AX_X, ALU.max))
        order.settle()
        dve.tensor_tensor(s.sc, s.sc, s.maxes.rearrange("p (t o) -> p t o", o=1).broadcast_to([P, TB, SC]), ALU.subtract)\
            .then_inc(s.sems["shifted_ready"], 1)
        e.dve_layernorm(dve, order, s, i + 1)
        dve.wait_ge(s.sems["exp_ready"], i + 1)
        order.mark(dve.tensor_reduce(s.sums, s.probs, AX_X, ALU.add))
        order.settle()
        order.mark(dve.reciprocal(s.scale, s.sums))
        order.settle()
        order.mark(dve.tensor_scalar(s.scale, s.scale, s.gate, None, ALU.mult))
        order.settle()
        for t in range(TB):
            dve.wait_ge(s.sems["out_psum"], TB * i + t + 1)
            tile = e.x_all[:, i * TB + t, :]
            dve.scalar_tensor_tensor(tile, PS[:, 4 + t % 2, 0:D], s.scale[:, t:t + 1], tile, ALU.mult, ALU.add)\
                .then_inc(e.x_updated, 1)
    order.end(B)


def xattn2_pool(pool, order, e, s):
    e.pool_rstd(pool, s, 0)
    with pool.Fori(0, B) as i:
        e.pool_rstd(pool, s, i + 1)


GATES = ("f", "i", "c")


def plan_ffn2(s, T, sem, small):
    take = s.w.take
    s.wx = [take(KD, D) for _ in GATES]
    s.wc = [take(KD, D) for _ in GATES]
    s.wo, s.uo = take(KD, D), take(KD, D)
    s.bg = take(3, KD)
    s.bo, s.c0 = take(D), take(KD)
    for g, n in enumerate(GATES):
        s.loads.append((s.wx[g], T[f"L2_ffn_w{n}"].rearrange("p (k n) -> p k n", k=KD)))
        s.loads.append((s.wc[g], T[f"L2_ffn_u{n}"].rearrange("p (k n) -> p k n", k=KD)))
        s.loads.append((s.bg[:, g, :], T[f"L2_ffn_b{n}"]))
    s.loads += [(s.wo, T["L2_ffn_wo"].rearrange("p (k n) -> p k n", k=KD)),
                (s.uo, T["L2_ffn_uo"].rearrange("p (k n) -> p k n", k=KD)),
                (s.bo, T["L2_ffn_bo"].broadcast_to([P, D])), (s.c0, T["L2_ffn_in_c"])]
    take = s.a.take
    s.cT = take(KD, S)
    s.gates = take(3, KD, S)
    s.own = take(NT, D)
    s.last = take(TB, D)
    s.h = take(TB, D)
    s.sems = {n: sem(f"{s.name}_{n}") for n in (
        "x_part", "gate_psum", "gate_ready", "c_ready", "own_psum", "own_ready", "last_psum", "sum_ready", "tanh_ready")}
    s.looks_ahead = True
    s.pe, s.act, s.dve, s.pool = ffn2_pe, ffn2_act, ffn2_dve, ffn2_pool


def ffn2_pe(pe, e, s):
    PS, nc = e.PS, e.nc
    pe.wait_ge(s.weights_loaded, 16 * len(s.loads))
    NG = 3 * KD
    e.pe_transpose_xn(pe, s, 0)
    pe.wait_ge(s.sems["c_ready"], 1)
    with pe.Fori(0, B) as i:
        pe.wait_ge(s.xnT_ready, KD * (i + 1))
        for g in range(3):
            for m in range(KD):
                pe.wait_ge(s.sems["gate_ready"], NG * i)
                for k in range(KD):
                    nc.tensor.matmul(PS[:, 2 + KD * g + m, :], s.wx[g][:, k, m * P:(m + 1) * P], e.xnT[:, k, :],
                                     start=k == 0, stop=False)
        for t in range(TB):
            for k in range(KD):
                last = nc.tensor.matmul(PS[:, t // 2, (t % 2) * D:(t % 2 + 1) * D], e.xnT[:, k, t * P:(t + 1) * P],
                                        s.wo[:, k, :], start=k == 0, stop=k == KD - 1)
            last.then_inc(s.sems["own_psum"], 1)
        pe.wait_ge(s.sems["c_ready"], i + 1)
        for g in range(3):
            for m in range(KD):
                for k in range(KD):
                    last = nc.tensor.matmul(PS[:, 2 + KD * g + m, :], s.wc[g][:, k, m * P:(m + 1) * P], s.cT[:, k, :],
                                            start=False, stop=k == KD - 1)
                last.then_inc(s.sems["gate_psum"], 1)
        pe.wait_ge(s.sems["own_ready"], TB * (i + 1))
        e.pe_transpose_xn(pe, s, i + 1)
    pe.wait_ge(s.sems["c_ready"], B + 1)
    for t in range(TB):
        for k in range(KD):
            last = nc.tensor.matmul(PS[:, 2 + t // 2, (t % 2) * D:(t % 2 + 1) * D], s.cT[:, k, t * P:(t + 1) * P],
                                    s.uo[:, k, :], start=k == 0, stop=k == KD - 1)
    last.then_inc(s.sems["last_psum"], 1)


def ffn2_act(act, order, e, s):
    PS, nc = e.PS, e.nc
    act.wait_ge(s.weights_loaded, 16 * len(s.loads))
    e.act_copy_xnT(act, s, 0)
    NG = 3 * KD
    with act.Fori(0, B) as i:
        act.wait_ge(s.sems["c_ready"], i + 1)
        for g in range(3):
            for m in range(KD):
                act.wait_ge(s.sems["gate_psum"], NG * i + KD * g + m + 1)
                nc.scalar.activation(s.gates[:, g, m, :], PS[:, 2 + KD * g + m, :], ACT.Tanh if g == 2 else ACT.Sigmoid,
                                     bias=s.bg[:, g, m:m + 1]).then_inc(s.sems["gate_ready"], 1)
        e.act_copy_xnT(act, s, i + 1)
    with act.Fori(0, B) as i:
        act.wait_ge(s.sems["sum_ready"], i + 1)
        nc.scalar.activation(s.h, s.h, ACT.Tanh).then_inc(s.sems["tanh_ready"], 1)


def ffn2_dve(dve, order, e, s):
    PS = e.PS
    dve.wait_ge(s.weights_loaded, 16 * len(s.loads))
    NG = 3 * KD
    dve.tensor_copy(s.cT, s.c0.rearrange("p (k o) -> p k o", o=1).broadcast_to([P, KD, S])).then_inc(s.sems["c_ready"], 1)
    e.dve_layernorm(dve, order, s, 0)
    with dve.Fori(0, B) as i:
        order.turn(i, e.LN_MARKS + 2)
        for t in range(TB):
            dve.wait_ge(s.sems["own_psum"], TB * i + 2 * (t // 2) + 2)
            dve.tensor_tensor(s.own[:, i * TB + t, :], PS[:, t // 2, (t % 2) * D:(t % 2 + 1) * D], s.bo, ALU.add)\
                .then_inc(s.sems["own_ready"], 1)
        e.dve_layernorm(dve, order, s, i + 1)
        dve.wait_ge(s.sems["gate_ready"], NG * i + 2 * KD)
        dve.wait_ge(s.sems["c_ready"], i + 1)
        dve.wait_ge(s.sems["gate_psum"], NG * (i + 1))
        order.mark(dve.tensor_tensor(s.cT, s.cT, s.gates[:, 0, :, :], ALU.mult))
        dve.wait_ge(s.sems["gate_ready"], NG * (i + 1))
        order.mark(dve.tensor_tensor(s.gates[:, 1, :, :], s.gates[:, 1, :, :], s.gates[:, 2, :, :], ALU.mult))
        order.settle()
        dve.tensor_tensor(s.cT, s.cT, s.gates[:, 1, :, :], ALU.add).then_inc(s.sems["c_ready"], 1)
    order.end(B)
    dve.wait_ge(s.sems["own_ready"], NT)
    dve.wait_ge(s.sems["last_psum"], 1)
    order.mark(dve.tensor_copy(s.last, PS[:, 2:4, :].rearrange("p b (t d) -> p (b t) d", d=D)))
    order.settle()
    with dve.Fori(0, B) as i:
        order.turn(i, 1)
        dve.wait_ge(e.x_updated, s.x_before + TB * i)
        dve.tensor_tensor(s.h, s.own[:, bass.ds(i * TB, TB), :], s.last, ALU.add).then_inc(s.sems["sum_ready"], 1)
        dve.wait_ge(s.sems["tanh_ready"], i + 1)
        tiles = e.x_all[:, bass.ds(i * TB, TB), :]
        order.mark(dve.scalar_tensor_tensor(tiles, s.h, s.gate, tiles, ALU.mult, ALU.add))
        order.settle()
        dve.sem_inc(e.x_updated, TB)
    order.end(B)


def ffn2_pool(pool, order, e, s):
    e.pool_rstd(pool, s, 0)
    with pool.Fori(0, B) as i:
        e.pool_rstd(pool, s, i + 1)


def plan_moe(s, T, sem, small):
    s.stores = True
    s.T = T
    first = W_N - 2 * E_N
    assert first >= 0 and first + NE * E_N <= 2 * W_N + A_N
    s.experts = s.mem[:, first:first + NE * E_N].rearrange("p (e n) -> p e n", e=NE)
    s.expert_loads = [(s.experts[:, (e + 2) % NE, :], T["L3_ffn_experts"][e]) for e in range(NE)]
    s.loads = s.expert_loads[:2]
    c = Carver(small, 0, MOE_N)
    s.gate_w, s.rms_w = c.take(KD, NE), c.take(D)
    s.small_loads = [(s.gate_w, T["L3_ffn_gate_w"].rearrange("p (k n) -> p k n", k=KD)),
                     (s.rms_w, T["L3_ffn_rms_w"].broadcast_to([P, D]))]
    s.ss, s.junk = c.take(TB), c.take(D)
    c2 = Carver(small, c.at, c.at + 2 * KE * P)
    s.hT = c.take(2, KE, P)
    s.logits, s.top = c2.take(NT, NE), c2.take(NT, 8)
    s.index = c2.take(NT, 8).bitcast(mybir.dt.uint32)
    s.pick = [c2.take(NT, NE), c2.take(NT, NE)]
    s.picked = c2.take(NT, NE)
    s.index_f = c.take(NT, 2)
    s.total, s.cum = c.take(NE, NT), c.take(NE, NT)
    s.count, s.pad, s.padcum, s.base = c.take(NE), c.take(NE), c.take(NE), c.take(NE)
    s.slot = c.take(2, NT)
    s.slot_u = c.take(2, NT).bitcast(mybir.dt.uint32)
    s.w = c.take(2, NT)
    s.tile_expert, s.tile_wrap = c.take(MOE_TILES), c.take(MOE_TILES)
    s.tile_slot = c.take(MOE_TILES).bitcast(I32)
    s.sems = {n: sem(f"{s.name}_{n}") for n in (
        "experts_loaded", "msq_ready", "rrms_ready", "y_ready", "y_kept", "logits_psum", "logits_kept",
        "residual", "residual_stored", "residual_loaded", "dispatch", "picked", "ranks_psum", "slots_ready", "exp2",
        "rowT_psum", "rowT_ready", "up_psum", "gate_psum", "silu_ready",
        "h_ready", "hT_psum", "hT_ready", "y_psum", "y_copied", "y_stored", "final")}
    s.row_loaded_s = [sem(f"{s.name}_row_loaded{n}") for n in range(2)]
    s.small_loaded_s, s.zeroed_s, s.row_scattered_s = [s.own_sem(f"{s.name}_{n}") for n in ("small_loaded", "zeroed", "row_scattered")]
    s.gathered_s = [s.own_sem(f"{s.name}_gathered{b}") for b in range(B)]
    s.early_sync_program, s.sync_program = moe_early_sync, moe_sync
    s.pe, s.act, s.dve, s.pool = moe_pe, moe_act, moe_dve, moe_pool


def moe_buffers(e, s):
    m = Names()
    flat = e.ctx2T[:, :, :, :].rearrange("p k b s -> p (k b s)")
    m.y = flat[:, 0:TB * D].rearrange("p (t d) -> p t d", d=D)
    m.residual = flat[:, TB * D:2 * TB * D].rearrange("p (t d) -> p t d", d=D)
    m.rowT = flat[:, 0:2 * D].rearrange("p (b k n) -> p b k n", k=KD, n=P)
    m.h = flat[:, 2 * D:2 * D + 2 * DE].rearrange("p (b n) -> p b n", n=DE)
    m.row, m.result = e.xn[:, 0:2, :], e.xn[:, 2:4, :]
    m.hT = s.hT
    m.gathered = s.mem[:, 0:2 * NT * D].rearrange("p (c t d) -> p c t d", c=2, d=D)
    return m


def moe_early_sync(sp, e, s):
    for dst, src in s.small_loads:
        sp.dma_start(dst, src).then_inc(s.small_loaded_s, 16)
    sp.wait_ge(e.zeros_ready, 1)
    slots = s.T["slots"].rearrange("(g t p) d -> g p t d", p=P, t=TB)
    for g in range(MOE_TILES // TB):
        sp.dma_start(slots[g], e.x_all[:, NT:NT + TB, :]).then_inc(s.zeroed_s, 16)


def moe_sync(sp, e, s):
    e.stage_start(sp, s)
    for dst, src in s.expert_loads[2:]:
        sp.dma_start(dst, src).then_inc(s.sems["experts_loaded"], 16)
    residual = s.T["residual"].rearrange("(b t p) d -> b p t d", p=P, t=TB)
    m = moe_buffers(e, s)
    with sp.Fori(0, B) as i:
        sp.wait_ge(s.sems["residual"], 2 * (i + 1))
        sp.dma_start(residual[bass.ds(i, 1)].rearrange("o p t d -> (o p) t d"), m.residual).then_inc(s.sems["residual_stored"], 16)
    sp.wait_ge(s.sems["residual_stored"], 16 * B)
    sp.wait_ge(s.row_scattered_s, 16 * 2 * NT)
    sp.dma_start(e.x_all[:, 0:NT, :], s.T["residual"].rearrange("(t p) d -> p t d", p=P)).then_inc(s.sems["residual_loaded"], 16)
    rows_in = s.T["slots"].rearrange("(j p) d -> j p d", p=P)

    def load(j, par):
        sp.dma_start(m.row[:, par, :], rows_in[bass.ds(j, 1)].rearrange("o p d -> (o p) d")).then_inc(s.row_loaded_s[par], 16)

    load(0, 0)
    load(1, 1)
    with sp.Fori(0, MOE_TILES // 2 - 1) as i:
        for par in range(2):
            j = 2 * i + 2 + par
            sp.wait_ge(s.sems["rowT_psum"], j - 1)
            load(j, par)
    out = s.T["out"].rearrange("b (t p) d -> b p t d", p=P)
    for b in range(B):
        sp.wait_ge(s.sems["final"], TB * (b + 1))
        sp.dma_start(out[b], e.x_all[:, b * TB:(b + 1) * TB, :]).then_inc(e.out_stored, 16)
    sp.wait_ge(e.out_stored, 16 * B)


def moe_pe(pe, e, s):
    PS, nc = e.PS, e.nc
    m = moe_buffers(e, s)
    pe.wait_ge(s.small_loaded_s, 32)
    with pe.Fori(0, B) as i:
        e.pe_transpose_xn(pe, s, i, src=m.y, ready=s.sems["y_ready"])
        pe.wait_ge(s.xnT_ready, KD * (i + 1))
        for t in range(TB):
            for k in range(KD):
                last = nc.tensor.matmul(PS[:, 2, t * NE:(t + 1) * NE], e.xnT[:, k, t * P:(t + 1) * P], s.gate_w[:, k, :],
                                        start=k == 0, stop=k == KD - 1)
        last.then_inc(s.sems["logits_psum"], 1)
    pe.wait_ge(s.sems["picked"], 1)
    picked = s.picked.rearrange("p t e -> p (t e)")
    nc.tensor.matmul(PS[:, 3, 0:NT * NE], e.const("before"), picked, start=True, stop=True)
    nc.tensor.matmul(PS[:, 4, 0:NT * NE], e.const("ones"), picked, start=True, stop=True).then_inc(s.sems["ranks_psum"], 1)
    pe.wait_ge(s.sems["slots_ready"], 1)
    pe.wait_ge(s.weights_loaded, 32)
    pe.wait_ge(s.sems["experts_loaded"], 16 * (NE - 2))

    def expert(j):
        return pe.value_load(s.tile_slot[0:1, bass.ds(j, 1)], min_val=0, max_val=NE - 1)

    def turn_rows(j, par, nth):
        pe.wait_ge(s.row_loaded_s[par], 16 * nth)
        pe.wait_ge(s.sems["rowT_ready"], j)
        for k in range(KD):
            last = nc.tensor.transpose(PS[:, 0, k * P:(k + 1) * P], m.row[:, par, k * P:(k + 1) * P], e.ident)
        last.then_inc(s.sems["rowT_psum"], 1)

    def widen(j, par):
        w = s.experts[:, bass.ds(expert(j), 1), :]
        pe.wait_ge(s.sems["rowT_ready"], j + 1)
        pe.wait_ge(s.sems["h_ready"], 2 * j)
        for g in range(2):
            for half in range(2):
                for k in range(KD):
                    at = (g * KD + k) * DE + half * HE
                    last = nc.tensor.matmul(PS[:, 1 + 2 * g + half, 0:HE], m.rowT[:, par, k, :], w[:, :, at:at + HE],
                                            start=k == 0, stop=k == KD - 1)
                last.then_inc(s.sems["gate_psum"] if g else s.sems["up_psum"], 1)

    def turn_hidden(j, par):
        pe.wait_ge(s.sems["h_ready"], 2 * (j + 1))
        pe.wait_ge(s.sems["hT_ready"], 2 * j)
        for n in range(KE):
            wide = min(P, DE - n * P)
            last = nc.tensor.transpose(PS[0:wide, 5 + n // 4, (n % 4) * P:(n % 4 + 1) * P],
                                       m.h[:, par, n * P:n * P + wide], e.ident)
            if n in (3, KE - 1):
                last.then_inc(s.sems["hT_psum"], 1)

    def narrow(j, par):
        w = s.experts[:, bass.ds(expert(j), 1), :]
        pe.wait_ge(s.sems["hT_ready"], 2 * (j + 1))
        pe.wait_ge(s.sems["y_copied"], j)
        for n in range(KE):
            at = 2 * KD * DE + n * D
            last = nc.tensor.matmul(PS[:, 7, 0:D], m.hT[:, par, n, :], w[:, :, at:at + D], start=n == 0, stop=n == KE - 1)
        last.then_inc(s.sems["y_psum"], 1)

    turn_rows(0, 0, 1)
    widen(0, 0)
    turn_rows(1, 1, 1)
    with pe.Fori(0, MOE_TILES // 2 - 1) as i:
        for par in (1, 0):
            j = 2 * i + (1 if par else 2)
            turn_hidden(j - 1, 1 - par)
            widen(j, par)
            turn_rows(j + 1, 1 - par, i + 2)
            narrow(j - 1, 1 - par)
    turn_hidden(MOE_TILES - 2, 0)
    widen(MOE_TILES - 1, 1)
    narrow(MOE_TILES - 2, 0)
    turn_hidden(MOE_TILES - 1, 1)
    narrow(MOE_TILES - 1, 1)


def moe_act(act, order, e, s):
    PS, nc = e.PS, e.nc
    m = moe_buffers(e, s)
    with act.Fori(0, B) as i:
        e.act_copy_xnT(act, s, i)
        act.wait_ge(s.sems["residual"], 2 * (i + 1))
        nc.scalar.activation(e.x_all[:, bass.ds(i * TB, TB), :], m.y, ACT.Copy).then_inc(s.sems["y_kept"], 1)
    act.wait_ge(s.sems["dispatch"], 1)
    nc.scalar.activation(s.w[:, 1, :], s.w[:, 1, :], ACT.Exp).then_inc(s.sems["exp2"], 1)
    act.wait_ge(s.sems["slots_ready"], 1)
    act.wait_ge(s.sems["residual_stored"], 16 * B)
    rows_out = s.T["results"].rearrange("(j p) d -> j p d", p=P)

    def copy_row(j, par):
        act.wait_ge(s.sems["rowT_psum"], j + 1)
        if not isinstance(j, int):
            act.wait_ge(s.sems["gate_psum"], 2 * (j - 1))
        nc.scalar.activation(m.rowT[:, par, :, :], PS[:, 0, 0:D].rearrange("p (k n) -> p k n", k=KD), ACT.Copy)\
            .then_inc(s.sems["rowT_ready"], 1)

    def silu(j, par):
        for half in range(2):
            act.wait_ge(s.sems["up_psum"], 2 * j + half + 1)
            if not (isinstance(j, int) and j < 2):
                act.wait_ge(s.sems["hT_psum"], 2 * (j - 1))
            nc.scalar.activation(m.h[:, par, half * HE:(half + 1) * HE], PS[:, 1 + half, 0:HE], ACT.Silu)\
                .then_inc(s.sems["silu_ready"], 1)

    def result(j, par):
        act.wait_ge(s.sems["y_psum"], j + 1)
        act.wait_ge(s.sems["y_stored"], 16 * j)
        nc.scalar.activation(m.result[:, par, :], PS[:, 7, 0:D], ACT.Copy).then_inc(s.sems["y_copied"], 1)
        act.wait_ge(s.sems["y_copied"], j + 1)
        act.dma_start(rows_out[bass.ds(j, 1)].rearrange("o p d -> (o p) d"), m.result[:, par, :]).then_inc(s.sems["y_stored"], 16)

    copy_row(0, 0)
    silu(0, 0)
    copy_row(1, 1)
    with act.Fori(0, MOE_TILES // 2 - 1) as i:
        for par in (1, 0):
            j = 2 * i + (1 if par else 2)
            silu(j, par)
            copy_row(j + 1, 1 - par)
            result(j - 1, 1 - par)
    silu(MOE_TILES - 1, 1)
    result(MOE_TILES - 2, 0)
    result(MOE_TILES - 1, 1)


def moe_dve(dve, order, e, s):
    PS = e.PS
    m = moe_buffers(e, s)
    dve.wait_ge(s.small_loaded_s, 32)
    with dve.Fori(0, B) as i:
        order.turn(i, e.LN_MARKS + TB)
        e.dve_layernorm(dve, order, s, i, last_read=(s.sems["residual"], 2 * i))
        dve.wait_ge(s.ln_ready, TB * (i + 1))
        for t in range(TB):
            order.mark(dve.tensor_tensor_reduce(s.junk, e.xn[:, t, :], e.xn[:, t, :], 1.0, 0.0, ALU.mult, ALU.add,
                                                s.ss[:, t:t + 1]))
            order.settle()
        dve.tensor_scalar(e.var_eps[:], s.ss, 1.0 / D, 1e-6, ALU.mult, ALU.add).then_inc(s.sems["msq_ready"], 1)
        dve.wait_ge(s.sems["rrms_ready"], i + 1)
        dve.wait_ge(s.sems["y_kept"], i)
        for t in range(TB):
            dve.scalar_tensor_tensor(m.y[:, t, :], e.xn[:, t, :], e.rstd[:, t:t + 1], s.rms_w, ALU.mult, ALU.mult)\
                .then_inc(s.sems["y_ready"], 1)
        dve.wait_ge(s.sems["logits_psum"], i + 1)
        dve.tensor_copy(s.logits[:, bass.ds(i * TB, TB), :], PS[:, 2, 0:TB * NE].rearrange("p (t e) -> p t e", e=NE))\
            .then_inc(s.sems["logits_kept"], 1)
    order.end(B)
    dve.wait_ge(s.sems["logits_kept"], B)

    def step(ins):
        order.mark(ins)
        order.settle()

    def wide(ap, axis, shape):
        return ap.rearrange("p (o a) -> p o a" if axis == 0 else "p (a o) -> p a o", o=1).broadcast_to(shape)

    for t in range(NT):
        order.mark(dve.max(s.top[:, t, :], s.logits[:, t, :]))
    order.settle()
    for t in range(NT):
        order.mark(dve.max_index(s.index[:, t, :], s.top[:, t, :], s.logits[:, t, :]))
    order.settle()
    dve.tensor_tensor(s.w[:, 1, :], s.top[:, :, 1], s.top[:, :, 0], ALU.subtract).then_inc(s.sems["dispatch"], 1)
    step(dve.tensor_copy(s.index_f, s.index[:, :, 0:2]))
    for c in range(2):
        step(dve.tensor_tensor(s.pick[c], wide(e.const("expert"), 0, [P, NT, NE]),
                               wide(s.index_f[:, :, c], 1, [P, NT, NE]), ALU.is_equal))
    dve.tensor_tensor(s.picked, s.pick[0], s.pick[1], ALU.add).then_inc(s.sems["picked"], 1)
    dve.wait_ge(s.sems["ranks_psum"], 1)
    step(dve.tensor_copy(s.total, PS[:, 4, 0:NT * NE].rearrange("p (t e) -> p e t", e=NE)))
    flat = s.total.rearrange("p e t -> p (e t)")
    step(dve.tensor_tensor_scan(s.cum.rearrange("p e t -> p (e t)"), flat, flat, 0.0, ALU.add, ALU.max))
    step(dve.tensor_tensor(s.count, s.cum[:, :, NT - 1], s.cum[:, :, 0], ALU.subtract))
    step(dve.tensor_tensor(s.count, s.count, s.total[:, :, 0], ALU.add))
    step(dve.tensor_tensor(s.cum, s.cum, s.total, ALU.subtract))
    step(dve.tensor_scalar(s.pad.bitcast(I32), s.count, P - 1.0, None, ALU.add))
    step(dve.tensor_scalar(s.pad.bitcast(I32), s.pad.bitcast(I32), 7, 7, ALU.logical_shift_right, ALU.logical_shift_left))
    step(dve.tensor_copy(s.count, s.pad.bitcast(I32)))
    step(dve.tensor_tensor_scan(s.padcum, s.count, s.count, 0.0, ALU.add, ALU.max))
    step(dve.tensor_tensor(s.base, s.padcum, s.count, ALU.subtract))
    step(dve.tensor_tensor(s.base, s.base, s.cum[:, :, 0], ALU.subtract))
    step(dve.tensor_tensor(s.cum, s.cum, wide(s.base, 1, [P, NE, NT]), ALU.add))
    step(dve.tensor_tensor(s.picked, PS[:, 3, 0:NT * NE].rearrange("p (t e) -> p t e", e=NE),
                           s.cum.rearrange("p e t -> p t e"), ALU.add))
    for c in range(2):
        step(dve.tensor_tensor(s.pick[c], s.pick[c], s.picked, ALU.mult))
        step(dve.tensor_reduce(s.slot[:, c, :], s.pick[c], AX_X, ALU.add))
    step(dve.tensor_copy(s.slot_u, s.slot))
    step(dve.memset(s.tile_expert, 0.0))
    for x in range(NE - 1):
        step(dve.scalar_tensor_tensor(s.tile_expert, e.const("slot_start"), s.padcum[:, x:x + 1], s.tile_expert,
                                      ALU.is_ge, ALU.add))
    step(dve.tensor_scalar(s.tile_wrap, s.tile_expert, NE - 2.0, -float(NE), ALU.is_ge, ALU.mult))
    step(dve.scalar_tensor_tensor(s.tile_expert, s.tile_expert, 2.0, s.tile_wrap, ALU.add, ALU.add))
    step(dve.tensor_copy(s.tile_slot, s.tile_expert))
    dve.wait_ge(s.sems["exp2"], 1)
    step(dve.tensor_scalar(s.w[:, 0, :], s.w[:, 1, :], 1.0, None, ALU.add))
    step(dve.reciprocal(s.w[:, 0, :], s.w[:, 0, :]))
    step(dve.tensor_tensor(s.w[:, 1, :], s.w[:, 1, :], s.w[:, 0, :], ALU.mult))
    step(dve.tensor_scalar(s.w, s.w, s.gate, None, ALU.mult))
    dve.memset(m.hT[DE % P:P, :, KE - 1, :], 0.0).then_inc(s.sems["slots_ready"], 1)

    def multiply(j, par):
        for half in range(2):
            dve.wait_ge(s.sems["gate_psum"], 2 * j + half + 1)
            dve.wait_ge(s.sems["silu_ready"], 2 * j + half + 1)
            h = m.h[:, par, half * HE:(half + 1) * HE]
            dve.tensor_tensor(h, PS[:, 3 + half, 0:HE], h, ALU.mult).then_inc(s.sems["h_ready"], 1)

    def copy_hidden(j, par):
        dve.wait_ge(s.sems["y_psum"], j)
        dve.wait_ge(s.sems["hT_psum"], 2 * j + 1)
        dve.tensor_copy(m.hT[:, par, 0:4, :], PS[:, 5, :].rearrange("p (n t) -> p n t", t=P)).then_inc(s.sems["hT_ready"], 1)
        dve.wait_ge(s.sems["hT_psum"], 2 * j + 2)
        dve.tensor_copy(m.hT[:, par, 4, :], PS[:, 6, 0:P]).then_inc(e.spare, 1)
        dve.tensor_copy(m.hT[0:DE % P, par, 5, :], PS[0:DE % P, 6, P:2 * P]).then_inc(s.sems["hT_ready"], 1)

    multiply(0, 0)
    with dve.Fori(0, MOE_TILES // 2 - 1) as i:
        for par in (1, 0):
            j = 2 * i + (1 if par else 2)
            copy_hidden(j - 1, 1 - par)
            multiply(j, par)
    copy_hidden(MOE_TILES - 2, 0)
    multiply(MOE_TILES - 1, 1)
    copy_hidden(MOE_TILES - 1, 1)

    dve.wait_ge(s.sems["residual_loaded"], 16)
    for b in range(B):
        dve.wait_ge(s.gathered_s[b], 16 * 2 * TB)
        for c in range(2):
            for t in range(b * TB, (b + 1) * TB):
                tile = e.x_all[:, t, :]
                ins = dve.scalar_tensor_tensor(tile, m.gathered[:, c, t, :], s.w[:, c, t:t + 1], tile, ALU.mult, ALU.add)
                if c == 0:
                    order.mark(ins)
                else:
                    ins.then_inc(s.sems["final"], 1)
            if c == 0:
                order.settle()


def moe_pool(pool, order, e, s):
    nc = e.nc
    m = moe_buffers(e, s)
    gate = s.gate.rearrange("p (o d) -> p o d", o=1).broadcast_to([P, TB, D])
    with pool.Fori(0, B) as i:
        e.pool_rstd(pool, s, i)
        pool.wait_ge(s.sems["msq_ready"], i + 1)
        nc.gpsimd.tensor_tensor(e.rstd[:], e.var_eps[:], e.minus_half[:], ALU.pow).then_inc(s.sems["rrms_ready"], 1)
        pool.wait_ge(s.sems["residual_stored"], 16 * i)
        nc.gpsimd.tensor_tensor(m.residual, e.xn[:], gate, ALU.mult).then_inc(s.sems["residual"], 1)
        pool.wait_ge(s.sems["residual"], 2 * i + 1)
        nc.gpsimd.tensor_tensor(m.residual, m.residual, e.x_all[:, bass.ds(i * TB, TB), :], ALU.add).then_inc(s.sems["residual"], 1)
    pool.wait_ge(s.sems["slots_ready"], 1)
    pool.wait_ge(s.sems["y_kept"], B)
    pool.wait_ge(s.zeroed_s, 16 * MOE_TILES // TB)
    for t in range(NT):
        for c in range(2):
            nc.gpsimd.indirect_dma_start(s.T["slots"], bass.IndirectOffsetOnAxis(s.slot_u[:, c, t:t + 1], 0),
                                         e.x_all[:, t, :], None).then_inc(s.row_scattered_s, 16)
    pool.wait_ge(s.sems["y_stored"], 16 * MOE_TILES)
    for t in range(NT):
        for c in range(2):
            nc.gpsimd.indirect_dma_start(m.gathered[:, c, t, :], None, s.T["results"],
                                         bass.IndirectOffsetOnAxis(s.slot_u[:, c, t:t + 1], 0))\
                .then_inc(s.gathered_s[t // TB], 16)


CH, CD = 8, 64
CT = CH * CD // P
CV = CD + 1
NQ = 256
QT = NQ // P
ROUTE_STEPS = 50
ROUTE_K = NQ * 9 / 8
NR = B * NQ


def plan_colt(s, T, sem, small):
    s.T = T
    take = s.w.take
    s.wq, s.wk, s.wv, s.wo, s.gamma = [], [], [], [], []
    for part in ("light", "heavy"):
        for lst, n in ((s.wq, "wq"), (s.wk, "wk"), (s.wv, "wv")):
            w = take(KD, CH * CD)
            lst.append(w)
            s.loads.append((w, T[f"L0_ffn_{n}_{part}"].rearrange("p (k n) -> p k n", k=KD)))
        w = take(CT, D)
        s.wo.append(w)
        s.loads.append((w, T[f"L0_ffn_wo_{part}"].rearrange("p (k n) -> p k n", k=CT)))
        g = take(KD)
        s.gamma.append(g)
        s.loads.append((g, T[f"L0_ffn_gamma_{part}"]))
    s.token = take(D)
    s.loads.append((s.token, T["L0_ffn_q_routing_token"].broadcast_to([P, D])))
    take = s.a.take
    s.kTz = take(CH, S)
    s.v = take(TB, CH, CV)
    at = s.a.at
    s.qT = take(CT, S)
    s.shifted, s.probs, s.probsT = take(2, S), take(2, S), take(2, S)
    s.o, s.oT = take(2, CH * CD), take(2, CT, P)
    c = Carver(s.mem, at, s.a.end)
    s.hq_rows, s.hxT = c.take(QT, D), c.take(KD, NQ)
    s.hqT = c.take(CT, NQ)
    s.hprobs, s.hprobsT = c.take(2, S), c.take(2, S)
    s.ho, s.hoT = c.take(QT, CH * CD), c.take(QT, CT, P)
    s.hy = c.take(QT, D)
    c2 = Carver(s.mem, at, s.a.end)
    s.rows = c2.take(NT, D)
    assert max(c.at, s.a.at) <= c2.at
    s.a.at = c2.at
    s.earlier = s.a.take(TB, S)
    s.loads.append((s.earlier, T["table_earlier"].rearrange("p (t j) -> p t j", t=TB)))
    c = Carver(small, 0, MOE_N)
    s.dots, s.dots_of_batch, s.sumsq = c.take(NT), c.take(TB), c.take(TB)
    s.junk = c.take(D)
    s.dots_T = c.take(P + 1)
    s.u, s.neg_t, s.e = c.take(P + 1), c.take(P + 1), c.take(P)
    s.rowsum, s.log, s.a_ = c.take(1), c.take(1), c.take(1)
    s.tile_max, s.batch_max = c.take(NT), c.take(NT)
    s.score, s.rank = c.take(NT), c.take(NT)
    s.over = c.take(NT)
    s.to_u, s.from_u = c.take(NT).bitcast(mybir.dt.uint32), c.take(NT).bitcast(mybir.dt.uint32)
    s.from_f = c.take(NT)
    s.junk2 = c.take(2, S)
    s.maxes, s.recip = c.take(2, CH), c.take(2, CH)
    s.row_scores = s.kTz.rearrange("p h s -> p (h s)")
    s.sems = {n: sem(f"{s.name}_{n}") for n in (
        "setup", "sumsq_ready", "rnorm_ready", "unit_ready", "unit_stored", "all_max", "cd_turned", "cd_psum",
        "cd_neg", "cd_exp", "cd_sum", "cd_log", "score_row", "score_psum", "score_stored", "scores_spread", "slots_ready",
        "rows_loaded", "zero_rows", "results_stored", "kv_cleared", "light_done", "light_x", "cd_final")}
    s.rows_scattered_s = s.own_sem(f"{s.name}_rows_scattered")
    s.gathered_b_s = [s.own_sem(f"{s.name}_gathered{b}") for b in range(B)]
    s.parts = []
    for part in ("light", "heavy"):
        heavy = part == "heavy"
        names = ("loaded", "xT_psum", "xT_ready", "proj_psum", "k_ready", "v_ready", "q_ready", "scores", "shifted_ready",
                  "exp_ready", "pT_psum", "pT_ready", "pv_psum", "o_ready", "oT_psum", "oT_ready", "y_psum")\
            + (("q_loaded", "qx_psum", "qx_ready", "y_ready") if heavy else ())
        p = Names()
        p.heavy, p.sems = heavy, {n: sem(f"{s.name}_{part}_{n}") for n in names}
        s.parts.append(p)
    s.sync_program = colt_sync
    s.pe, s.act, s.dve, s.pool = colt_pe, colt_act, colt_dve, colt_pool


def colt_sync(sp, e, s):
    units = s.T["unit_rows"].rearrange("(b t p) d -> b p t d", p=P, t=TB)
    light, heavy = s.parts
    e.stage_start(sp, s)
    with sp.Fori(0, B) as i:
        sp.wait_ge(s.sems["unit_ready"], TB * (i + 1))
        sp.dma_start(units[bass.ds(i, 1)].rearrange("o p t d -> (o p) t d"), e.xnT[:].rearrange("p k s -> p (k s)").rearrange("p (t d) -> p t d", d=D))\
            .then_inc(s.sems["unit_stored"], 16)
    sp.wait_ge(s.sems["unit_stored"], 16 * B)
    sp.dma_start(s.T["routed_out"][NR:NR + P, :], e.x_all[:, NT, :]).then_inc(s.sems["zero_rows"], 16)
    with sp.Fori(0, B) as i:
        sp.wait_ge(light.sems["xT_psum"], KD * i)
        sp.dma_start(e.xn[:], units[bass.ds(i, 1)].rearrange("o p t d -> (o p) t d")).then_inc(light.sems["loaded"], 16)
    sp.wait_ge(s.sems["score_row"], 1)
    sp.dma_start(s.T["row_scores"].rearrange("(t p) -> t p", p=P), s.e[0:NT, :]).then_inc(s.sems["score_stored"], 16)
    sp.wait_ge(s.sems["score_stored"], 16)
    sp.wait_ge(light.sems["scores"], 2 * TB * B)
    sp.dma_start(s.row_scores, s.T["row_scores"].rearrange("(o n) -> o n", o=1).broadcast_to([P, B * S])).then_inc(s.sems["scores_spread"], 16)
    sp.wait_ge(s.sems["light_done"], 1)
    sp.dma_start(s.rows, s.T["unit_rows"].rearrange("(t p) d -> p t d", p=P)).then_inc(s.sems["rows_loaded"], 16)
    sp.wait_ge(s.rows_scattered_s, 16 * NT)
    routed = s.T["routed_in"].rearrange("(b t p) d -> b p t d", p=P, t=QT)
    out = s.T["routed_out"][0:NR, :].rearrange("(b t p) d -> b p t d", p=P, t=QT)
    with sp.Fori(0, B) as i:
        sp.wait_ge(heavy.sems["xT_psum"], KD * i)
        sp.dma_start(e.xn[:], units[bass.ds(i, 1)].rearrange("o p t d -> (o p) t d")).then_inc(heavy.sems["loaded"], 16)
        sp.wait_ge(heavy.sems["qx_psum"], i)
        sp.dma_start(s.hq_rows, routed[bass.ds(i, 1)].rearrange("o p t d -> (o p) t d")).then_inc(heavy.sems["q_loaded"], 16)
        sp.wait_ge(heavy.sems["y_ready"], QT * (i + 1))
        sp.dma_start(out[bass.ds(i, 1)].rearrange("o p t d -> (o p) t d"), s.hy).then_inc(s.sems["results_stored"], 16)


def colt_pe(pe, e, s):
    PS, nc = e.PS, e.nc
    pe.wait_ge(s.sems["setup"], 1)
    light, heavy = s.parts

    def project(p, i):
        w = 1 if p.heavy else 0
        pe.wait_ge(p.sems["loaded"], 16 * (i + 1))
        if p.heavy:
            pe.wait_ge(p.sems["oT_ready"], QT * i)
            pe.wait_ge(p.sems["y_ready"], QT * i)
        else:
            pe.wait_ge(p.sems["oT_ready"], TB * i)
            pe.wait_ge(s.sems["light_x"], TB * i)
        for k in range(KD):
            for t in range(TB):
                last = nc.tensor.transpose(PS[:, k, t * P:(t + 1) * P], e.xn[:, t, k * P:(k + 1) * P], e.ident)
            last.then_inc(p.sems["xT_psum"], 1)
        if p.heavy:
            pe.wait_ge(p.sems["q_loaded"], 16 * (i + 1))
            pe.wait_ge(p.sems["xT_ready"], KD * i + 1)
            for k in range(KD):
                for t in range(QT):
                    last = nc.tensor.transpose(PS[:, 0, (k * QT + t) * P:(k * QT + t + 1) * P],
                                               s.hq_rows[:, t, k * P:(k + 1) * P], e.ident)
            last.then_inc(p.sems["qx_psum"], 1)
        pe.wait_ge(p.sems["xT_ready"], KD * (i + 1))
        for c in range(3 * CT):
            kind, n = c // CT, c % CT
            if c >= 6:
                pe.wait_ge(p.sems["k_ready"] if c - 6 < CT else p.sems["v_ready"], CT * i + (c - 6) % CT + 1)
            if kind == 2 and n == 0 and p.heavy:
                pe.wait_ge(p.sems["qx_ready"], i + 1)
            for k in range(KD):
                if kind == 0:
                    lhsT, rhs = s.wk[w][:, k, n * P:(n + 1) * P], e.xnT[:, k, :]
                elif kind == 1:
                    lhsT, rhs = e.xnT[:, k, n * P:(n + 1) * P], s.wv[w][:, k, :]
                else:
                    lhsT, rhs = s.wq[w][:, k, n * P:(n + 1) * P], (s.hxT if p.heavy else e.xnT)[:, k, :]
                wide = NQ if p.heavy and kind == 2 else S
                last = nc.tensor.matmul(PS[:, 2 + c % 6, 0:wide], lhsT, rhs, start=k == 0, stop=k == KD - 1)
            last.then_inc(p.sems["proj_psum"], 1)
        pe.wait_ge(p.sems["q_ready"], CT * (i + 1))

    def turn_probs(p, n, u, probs):
        pe.wait_ge(p.sems["exp_ready"], n + u + 1)
        if u >= 2:
            pe.wait_ge(p.sems["pT_ready"], n + u - 1)
        for j in range(4):
            last = nc.tensor.transpose(PS[:, 4 + u % 2, j * P:(j + 1) * P], probs[:, u % 2, j * P:(j + 1) * P], e.ident)
        last.then_inc(p.sems["pT_psum"], 1)

    def project_out(p, n, t, o, oT, step):
        if step == 0:
            for k in range(CT):
                last = nc.tensor.transpose(PS[:, 0, k * P:(k + 1) * P], o[:, t % 2, k * P:(k + 1) * P], e.ident)
            last.then_inc(p.sems["oT_psum"], 1)
        else:
            pe.wait_ge(p.sems["oT_ready"], n + t + 1)
            for k in range(CT):
                last = nc.tensor.matmul(PS[:, 1, 0:D], oT[:, t % 2, k, :], s.wo[1 if p.heavy else 0][:, k, :],
                                        start=k == 0, stop=k == CT - 1)
            last.then_inc(p.sems["y_psum"], 1)

    with pe.Fori(0, B) as i:
        p, n = light, 2 * TB * i
        project(p, i)
        pe.wait_ge(p.sems["k_ready"], CT * (i + 1))
        pe.wait_ge(p.sems["v_ready"], TB * (i + 1))
        for step in range(2 * TB + 4):
            if step < 2 * TB:
                u, t, g = step, step // 2, step % 2
                if u >= 2:
                    pe.wait_ge(p.sems["shifted_ready"], n + u - 1)
                for j in range(4):
                    h = 4 * g + j
                    last = nc.tensor.matmul(PS[:, 2 + u % 2, j * P:(j + 1) * P], s.qT[:, h // 2, t * P:(t + 1) * P],
                                            s.kTz[:, h, t * P:(t + 1) * P], start=True, stop=True)
                last.then_inc(p.sems["scores"], 1)
            if 1 <= step < 2 * TB + 1:
                turn_probs(p, n, step - 1, s.probs)
            if 2 <= step < 2 * TB + 2:
                u = step - 2
                pe.wait_ge(p.sems["pT_ready"], n + u + 1)
                if u >= 2:
                    pe.wait_ge(p.sems["o_ready"], n + u - 1)
                for j in range(4):
                    last = nc.tensor.matmul(PS[:, 6 + u % 2, j * CV:(j + 1) * CV], s.probsT[:, u % 2, j * P:(j + 1) * P],
                                            s.v[:, u // 2, 4 * (u % 2) + j, :], start=True, stop=True)
                last.then_inc(p.sems["pv_psum"], 1)
            if step >= 4 and step % 2 == 0:
                t = (step - 4) // 2
                pe.wait_ge(p.sems["o_ready"], n + 2 * (t + 1))
                pe.wait_ge(p.sems["oT_ready"], TB * i + t)
                project_out(p, TB * i, t, s.o, s.oT, 0)
            if step >= 5 and step % 2 == 1:
                t = (step - 5) // 2
                pe.wait_ge(s.sems["light_x"], TB * i + t)
                project_out(p, TB * i, t, s.o, s.oT, 1)

    pe.wait_ge(s.sems["cd_turned"], 1)
    nc.tensor.transpose(PS[0:NT, 2, 0:P], s.dots, e.ident)
    nc.tensor.transpose(PS[0:NT, 2, P:2 * P], s.batch_max, e.ident).then_inc(s.sems["cd_psum"], 1)
    with pe.Fori(0, ROUTE_STEPS) as i:
        pe.wait_ge(s.sems["cd_exp"], i + 1)
        pe.sem_inc(e.spare, 1)
        nc.tensor.matmul(PS[0:NT, 3, 0:1], e.const("same_batch", NT), s.rowsum[0:NT, :], start=True, stop=True)\
            .then_inc(s.sems["cd_sum"], 1)
    pe.wait_ge(s.sems["score_row"], 1)
    nc.tensor.transpose(PS[:, 4, 0:NT], s.e[0:NT, :], e.ident[0:NT, 0:NT]).then_inc(s.sems["score_psum"], 1)

    pe.wait_ge(s.sems["kv_cleared"], 1)
    with pe.Fori(0, B) as i:
        p, n = heavy, QT * CH * i
        project(p, i)
        pe.wait_ge(p.sems["k_ready"], CT * (i + 1))
        pe.wait_ge(p.sems["v_ready"], TB * (i + 1))
        for step in range(QT * CH + 4):
            if step < QT * CH:
                u, t, h = step, step // CH, step % CH
                if u >= 2:
                    pe.wait_ge(p.sems["exp_ready"], n + u - 1)
                nc.tensor.matmul(PS[:, 2 + u % 2, :], s.hqT[:, h // 2, t * P:(t + 1) * P], s.kTz[:, h, :],
                                 start=True, stop=True).then_inc(p.sems["scores"], 1)
            if 1 <= step < QT * CH + 1:
                turn_probs(p, n, step - 1, s.hprobs)
            if 2 <= step < QT * CH + 2:
                u = step - 2
                t, h = u // CH, u % CH
                pe.wait_ge(p.sems["pT_ready"], n + u + 1)
                if h % 4 == 0:
                    pe.wait_ge(p.sems["o_ready"], (QT * i + t) * 2 + max(h // 4 - 1, 0) if t or h else QT * i * 2)
                for j in range(4):
                    last = nc.tensor.matmul(PS[:, 6 + h // 4, (h % 4) * CV:(h % 4 + 1) * CV],
                                            s.hprobsT[:, u % 2, j * P:(j + 1) * P], s.v[:, j, h, :], start=j == 0, stop=j == 3)
                last.then_inc(p.sems["pv_psum"], 1)
            for t in range(QT):
                if step == (t + 1) * CH + 2:
                    pe.wait_ge(p.sems["o_ready"], 2 * (QT * i + t + 1))
                    pe.wait_ge(p.sems["oT_ready"], QT * i + t)
                    project_out(p, QT * i, t, s.ho, s.hoT, 0)
                if step == (t + 1) * CH + 3:
                    pe.wait_ge(p.sems["y_ready"], QT * i + t)
                    project_out(p, QT * i, t, s.ho, s.hoT, 1)


def colt_act(act, order, e, s):
    PS, nc = e.PS, e.nc
    light, heavy = s.parts

    def project(p, i):
        for k in range(KD):
            act.wait_ge(p.sems["xT_psum"], KD * i + k + 1)
            nc.scalar.activation(e.xnT[:, k, :], PS[:, k, :], ACT.Copy).then_inc(p.sems["xT_ready"], 1)
        if p.heavy:
            act.wait_ge(p.sems["qx_psum"], i + 1)
            nc.scalar.activation(s.hxT, PS[:, 0, :].rearrange("p (k n) -> p k n", k=KD), ACT.Copy).then_inc(p.sems["qx_ready"], 1)
        for t in range(TB):
            act.wait_ge(p.sems["proj_psum"], 3 * CT * i + CT + t + 1)
            nc.scalar.activation(s.v[:, t, :, 0:CD], PS[:, 2 + (CT + t) % 6, :].rearrange("p (h d) -> p h d", d=CD), ACT.Copy)\
                .then_inc(p.sems["v_ready"], 1)
        for m in range(CT):
            act.wait_ge(p.sems["proj_psum"], 3 * CT * i + 2 * CT + m + 1)
            q, wide = (s.hqT, NQ) if p.heavy else (s.qT, S)
            nc.scalar.activation(q[:, m, :], PS[:, 2 + (2 * CT + m) % 6, 0:wide], ACT.Copy).then_inc(p.sems["q_ready"], 1)

    def copy_oT(p, n, t, oT):
        act.wait_ge(p.sems["oT_psum"], n + t + 1)
        act.wait_ge(p.sems["y_psum"], n + max(t - 1, 0))
        nc.scalar.activation(oT[:, t % 2, :, :], PS[:, 0, :].rearrange("p (k n) -> p k n", k=CT), ACT.Copy).then_inc(p.sems["oT_ready"], 1)

    with act.Fori(0, B) as i:
        p, n = light, 2 * TB * i
        project(p, i)
        for step in range(2 * TB + 4):
            if step < 2 * TB:
                u = step
                act.wait_ge(p.sems["shifted_ready"], n + u + 1)
                if u >= 2:
                    act.wait_ge(p.sems["pT_psum"], n + u - 1)
                nc.scalar.activation(s.probs[:, u % 2, :], s.shifted[:, u % 2, :], ACT.Exp).then_inc(p.sems["exp_ready"], 1)
            if 1 <= step < 2 * TB + 1:
                u = step - 1
                act.wait_ge(p.sems["pT_psum"], n + u + 1)
                if u >= 2:
                    act.wait_ge(p.sems["pv_psum"], n + u - 1)
                nc.scalar.activation(s.probsT[:, u % 2, :], PS[:, 4 + u % 2, :], ACT.Copy).then_inc(p.sems["pT_ready"], 1)
            if step >= 4 and step % 2 == 0:
                copy_oT(p, TB * i, (step - 4) // 2, s.oT)

    with act.Fori(0, ROUTE_STEPS) as i:
        act.wait_ge(s.sems["cd_neg"], i + 1)
        nc.scalar.activation(s.e[0:NT, :], s.neg_t[0:NT, 0:P], ACT.Exp, bias=s.neg_t[0:NT, P:P + 1], scale=-1.0,
                             accum_out=s.rowsum[0:NT, :]).then_inc(s.sems["cd_exp"], 1)
        act.wait_ge(s.sems["cd_sum"], i + 1)
        nc.scalar.activation(s.log[0:NT, :], PS[0:NT, 3, 0:1], ACT.Ln, scale=1.0 / ROUTE_K).then_inc(s.sems["cd_log"], 1)
    act.wait_ge(s.sems["cd_final"], 1)
    nc.scalar.activation(s.e[0:NT, :], s.u[0:NT, 0:P], ACT.Exp).then_inc(s.sems["score_row"], 1)

    act.wait_ge(s.rows_scattered_s, 16 * NT)
    with act.Fori(0, B) as i:
        p, n = heavy, QT * CH * i
        project(p, i)
        for step in range(QT * CH + 4):
            if step < QT * CH:
                u = step
                act.wait_ge(p.sems["shifted_ready"], n + u + 1)
                if u >= 2:
                    act.wait_ge(p.sems["pT_psum"], n + u - 1)
                nc.scalar.activation(s.hprobs[:, u % 2, :], PS[:, 2 + u % 2, :], ACT.Exp, bias=s.maxes[:, 0, u % 2:u % 2 + 1])\
                    .then_inc(p.sems["exp_ready"], 1)
            for t in range(QT):
                if step == (t + 1) * CH + 2:
                    copy_oT(p, QT * i, t, s.hoT)
                if step == (t + 1) * CH + 3:
                    act.wait_ge(p.sems["y_psum"], QT * i + t + 1)
                    act.wait_ge(s.sems["results_stored"], 16 * i)
                    nc.scalar.activation(s.hy[:, t, :], PS[:, 1, 0:D], ACT.Copy, scale=s.gate).then_inc(p.sems["y_ready"], 1)


def colt_dve(dve, order, e, s):
    PS = e.PS
    light, heavy = s.parts
    dve.wait_ge(s.weights_loaded, 16 * len(s.loads))
    for w in range(2):
        for k in range(KD):
            g = s.gamma[w][:, k:k + 1]
            order.mark(dve.tensor_scalar(s.wk[w][:, k, :], s.wk[w][:, k, :], g, D ** 0.5, ALU.mult, ALU.mult))
            order.mark(dve.tensor_scalar(s.wv[w][:, k, :], s.wv[w][:, k, :], g, D ** 0.5, ALU.mult, ALU.mult))
            order.mark(dve.tensor_scalar(s.wq[w][:, k, :], s.wq[w][:, k, :], g, D ** 0.5 * CD ** -0.5, ALU.mult, ALU.mult))
    order.mark(dve.memset(s.kTz, 0.0))
    order.mark(dve.memset(s.v[:, :, :, CD:CV], 1.0))
    order.settle()
    dve.sem_inc(s.sems["setup"], 1)

    unit = e.xnT[:].rearrange("p k s -> p (k s)").rearrange("p (t d) -> p t d", d=D)
    with dve.Fori(0, B) as i:
        order.turn(i, 2 * TB + TB + TB + 1)
        for t in range(TB):
            order.mark(dve.bn_stats(e.stats[:, t, :], e.x_all[:, i * TB + t, :]))
        order.settle()
        dve.sem_inc(e.spare, 1)
        for t in range(TB):
            order.mark(dve.bn_aggr(e.mean_var[:, t, :], e.stats[:, t, :]))
        order.settle()
        dve.tensor_scalar(e.var_eps[:], e.mean_var[:, :, 1], LN_EPS, None, ALU.add).then_inc(s.var_ready, 1)
        dve.wait_ge(s.rstd_ready, i + 1)
        for t in range(TB):
            dve.tensor_scalar(e.xn[:, t, :], e.x_all[:, i * TB + t, :], e.mean_var[:, t, 0:1], e.rstd[:, t:t + 1],
                              ALU.subtract, ALU.mult).then_inc(s.ln_ready, 1)
        dve.wait_ge(s.ln_ready, TB * (i + 1))
        for t in range(TB):
            order.mark(dve.tensor_tensor_reduce(s.junk, e.xn[:, t, :], s.token, 1.0, 0.0, ALU.mult, ALU.add,
                                                s.dots_of_batch[:, t:t + 1]))
            order.settle()
            order.mark(dve.tensor_tensor_reduce(s.junk, e.xn[:, t, :], e.xn[:, t, :], 1.0, 0.0, ALU.mult, ALU.add,
                                                s.sumsq[:, t:t + 1]))
            order.settle()
        order.mark(dve.tensor_copy(s.dots[:, bass.ds(i * TB, TB)], s.dots_of_batch))
        dve.tensor_scalar(e.var_eps[:], s.sumsq, 1e-24, None, ALU.max).then_inc(s.sems["sumsq_ready"], 1)
        dve.wait_ge(s.sems["rnorm_ready"], i + 1)
        dve.wait_ge(s.sems["unit_stored"], 16 * i)
        for t in range(TB):
            dve.tensor_scalar(unit[:, t, :], e.xn[:, t, :], e.rstd[:, t:t + 1], None, ALU.mult).then_inc(s.sems["unit_ready"], 1)
    order.end(B)

    def copy_keys(p, i):
        for m in range(CT):
            dve.wait_ge(p.sems["proj_psum"], 3 * CT * i + m + 1)
            dve.tensor_copy(s.kTz[0:CD, 2 * m, :], PS[0:CD, 2 + m, :]).then_inc(e.spare, 1)
            dve.tensor_copy(s.kTz[CD:P, 2 * m + 1, :], PS[CD:P, 2 + m, :]).then_inc(p.sems["k_ready"], 1)

    def normalise(p, wait, bank, at, o, done, par):
        dve.wait_ge(p.sems["pv_psum"], wait)
        dve.wait_ge(p.sems["o_ready"], done)
        recip = s.recip[:, par, 0:4]
        src = PS[:, bank, 0:4 * CV].rearrange("p (h v) -> p h v", v=CV)
        order.mark(dve.reciprocal(recip, src[:, :, CD]))
        order.settle()
        dve.tensor_tensor(o[:, at:at + 4 * CD].rearrange("p (h d) -> p h d", d=CD), src[:, :, 0:CD],
                          recip.rearrange("p (h o) -> p h o", o=1).broadcast_to([P, 4, CD]), ALU.mult)\
            .then_inc(p.sems["o_ready"], 1)

    dve.wait_ge(s.sems["unit_stored"], 16 * B)
    with dve.Fori(0, B) as i:
        p, n = light, 2 * TB * i
        order.turn(i, 4 * TB)
        copy_keys(p, i)
        for step in range(2 * TB + 6):
            if step < 2 * TB:
                u = step
                dve.wait_ge(p.sems["scores"], n + u + 1)
                bank = PS[:, 2 + u % 2, :].rearrange("p (h s) -> p h s", s=P)
                order.mark(dve.tensor_reduce(s.maxes[:, u % 2, 0:4], bank, AX_X, ALU.max))
                order.settle()
                if u >= 2:
                    dve.wait_ge(p.sems["exp_ready"], n + u - 1)
                dve.tensor_tensor(s.shifted[:, u % 2, :].rearrange("p (h s) -> p h s", s=P), bank,
                                  s.maxes[:, u % 2, 0:4].rearrange("p (h o) -> p h o", o=1).broadcast_to([P, 4, P]),
                                  ALU.subtract).then_inc(p.sems["shifted_ready"], 1)
            if 3 <= step < 2 * TB + 3:
                u = step - 3
                if u >= 4 and u % 2 == 0:
                    dve.wait_ge(p.sems["oT_psum"], TB * i + u // 2 - 1)
                normalise(p, n + u + 1, 6 + u % 2, (u % 2) * 4 * CD, s.o[:, (u // 2) % 2, :], n + max(u - 1, 0), u % 2)
            if step >= 6 and step % 2 == 0:
                t = (step - 6) // 2
                dve.wait_ge(p.sems["y_psum"], TB * i + t + 1)
                tile = e.x_all[:, i * TB + t, :]
                dve.scalar_tensor_tensor(tile, PS[:, 1, 0:D], s.gate, tile, ALU.mult, ALU.add).then_inc(s.sems["light_x"], 1)
    order.end(B)
    dve.wait_ge(s.sems["light_x"], NT)
    dve.sem_inc(s.sems["light_done"], 1)

    def step(ins):
        order.mark(ins)
        order.settle()

    dve.wait_ge(s.sems["all_max"], 1)
    step(dve.tensor_reduce(s.batch_max[:, 0:B], s.tile_max.rearrange("p (b t) -> p b t", t=TB), AX_X, ALU.max))
    step(dve.tensor_copy(s.tile_max.rearrange("p (b t) -> p b t", t=TB),
                         s.batch_max[:, 0:B].rearrange("p (b o) -> p b o", o=1).broadcast_to([P, B, TB])))
    dve.tensor_copy(s.batch_max, s.tile_max).then_inc(s.sems["cd_turned"], 1)
    dve.wait_ge(s.sems["cd_psum"], 1)
    step(dve.tensor_copy(s.dots_T[0:NT, :], PS[0:NT, 2, 0:P + 1]))
    dve.memset(s.neg_t[0:NT, :], 0.0).then_inc(s.sems["cd_neg"], 1)
    with dve.Fori(0, ROUTE_STEPS) as i:
        order.turn(i, 2)
        dve.wait_ge(s.sems["cd_log"], i + 1)
        order.mark(dve.tensor_tensor(s.a_[0:NT, :], s.neg_t[0:NT, P:P + 1], s.log[0:NT, :], ALU.subtract))
        order.settle()
        order.mark(dve.tensor_scalar(s.u[0:NT, :], s.dots_T[0:NT, :], s.a_[0:NT, :], 0.0, ALU.add, ALU.max))
        order.settle()
        dve.tensor_tensor(s.neg_t[0:NT, :], s.u[0:NT, :], s.dots_T[0:NT, :], ALU.subtract).then_inc(s.sems["cd_neg"], 1)
    order.end(ROUTE_STEPS)
    dve.wait_ge(s.sems["cd_neg"], ROUTE_STEPS + 1)
    step(dve.tensor_scalar(s.u[0:NT, :], s.dots_T[0:NT, :], s.a_[0:NT, :], 0.0, ALU.add, ALU.min))
    dve.sem_inc(s.sems["cd_final"], 1)
    dve.wait_ge(s.sems["score_psum"], 1)
    step(dve.tensor_copy(s.score, PS[:, 4, 0:NT]))
    dve.wait_ge(s.sems["scores_spread"], 16)
    for t in range(NT):
        b, w = t // TB, t % TB
        row = s.row_scores[:, b * S:(b + 1) * S]
        step(dve.scalar_tensor_tensor(s.junk2[:, 0, :], row, s.score[:, t:t + 1], s.earlier[:, w, :], ALU.is_equal, ALU.mult))
        step(dve.scalar_tensor_tensor(s.junk2[:, 1, :], row, s.score[:, t:t + 1], s.junk2[:, 0, :], ALU.is_gt, ALU.add,
                                      accum_out=s.rank[:, t:t + 1]))
    step(dve.tensor_scalar(s.over, s.rank, float(NQ), None, ALU.is_ge))
    step(dve.tensor_tensor(s.rank, s.rank, e.const("batch_slot"), ALU.add))
    step(dve.scalar_tensor_tensor(s.from_f, s.over, float(NR - NQ), s.rank, ALU.mult, ALU.add))
    step(dve.tensor_copy(s.to_u, s.from_f))
    step(dve.tensor_scalar(s.from_f, s.rank, -1.0, float(NR), ALU.mult, ALU.add))
    step(dve.tensor_tensor(s.from_f, s.from_f, s.over, ALU.mult))
    step(dve.tensor_tensor(s.from_f, s.from_f, s.rank, ALU.add))
    step(dve.tensor_copy(s.from_u, s.from_f))
    dve.sem_inc(s.sems["slots_ready"], 1)
    step(dve.memset(s.kTz, 0.0))
    dve.sem_inc(s.sems["kv_cleared"], 1)

    dve.wait_ge(s.rows_scattered_s, 16 * NT)
    with dve.Fori(0, B) as i:
        p, n = heavy, QT * CH * i
        order.turn(i, 2 * QT)
        copy_keys(p, i)
        for step_ in range(QT * CH + 4):
            if step_ < QT * CH:
                u = step_
                dve.wait_ge(p.sems["scores"], n + u + 1)
                if u >= 2:
                    dve.wait_ge(p.sems["exp_ready"], n + u - 1)
                dve.tensor_reduce(s.maxes[:, 0, u % 2:u % 2 + 1], PS[:, 2 + u % 2, :], AX_X, ALU.max, negate=True)\
                    .then_inc(p.sems["shifted_ready"], 1)
            if 1 <= step_ < QT * CH + 1:
                u = step_ - 1
                dve.wait_ge(p.sems["pT_psum"], n + u + 1)
                if u >= 2:
                    dve.wait_ge(p.sems["pv_psum"], n + u - 1)
                dve.tensor_copy(s.hprobsT[:, u % 2, :], PS[:, 4 + u % 2, :]).then_inc(p.sems["pT_ready"], 1)
            if step_ >= 6 and (step_ - 2) % 4 == 0:
                g = (step_ - 6) // 4
                if g % 2 == 0:
                    dve.wait_ge(p.sems["oT_psum"], QT * i)
                normalise(p, n + 4 * (g + 1), 6 + g % 2, (g % 2) * 4 * CD, s.ho[:, g // 2, :], 2 * QT * i + max(g - 1, 0), g % 2)
    order.end(B)

    for t in range(NT):
        dve.wait_ge(s.gathered_b_s[t // TB], 16 * TB)
        dve.tensor_tensor(e.x_all[:, t, :], e.x_all[:, t, :], s.rows[:, t, :], ALU.add).then_inc(e.x_updated, 1)


def colt_pool(pool, order, e, s):
    nc = e.nc
    with pool.Fori(0, B) as i:
        e.pool_rstd(pool, s, i)
        pool.wait_ge(s.sems["sumsq_ready"], i + 1)
        nc.gpsimd.tensor_tensor(e.rstd[:], e.var_eps[:], e.minus_half[:], ALU.pow).then_inc(s.sems["rnorm_ready"], 1)
    pool.wait_ge(s.sems["unit_ready"], NT)
    nc.gpsimd.partition_all_reduce(s.tile_max, s.dots, P, bass.bass_isa.ReduceOp.max).then_inc(s.sems["all_max"], 1)
    pool.wait_ge(s.sems["slots_ready"], 1)
    pool.wait_ge(s.sems["rows_loaded"], 16)
    for t in range(NT):
        nc.gpsimd.indirect_dma_start(s.T["routed_in"], bass.IndirectOffsetOnAxis(s.to_u[:, t:t + 1], 0),
                                     s.rows[:, t, :], None).then_inc(s.rows_scattered_s, 16)
    pool.wait_ge(s.sems["results_stored"], 16 * B)
    pool.wait_ge(s.sems["zero_rows"], 16)
    for t in range(NT):
        nc.gpsimd.indirect_dma_start(s.rows[:, t, :], None, s.T["routed_out"],
                                     bass.IndirectOffsetOnAxis(s.from_u[:, t:t + 1], 0)).then_inc(s.gathered_b_s[t // TB], 16)


PLAN = {"L0_xattn": plan_xattn, "L1_xattn": plan_xattn, "L3_xattn": plan_xattn, "L1_ffn": plan_ffn1,
        "L2_xattn": plan_xattn2, "L2_ffn": plan_ffn2, "L3_ffn": plan_moe, "L0_ffn": plan_colt}


def rows(w):
    k, n = w.shape
    return np.ascontiguousarray(w.reshape(k // P, P, n).transpose(1, 0, 2).reshape(P, -1))


def cols(b):
    return np.ascontiguousarray(b.reshape(-1, P).T)


def lay_out(i):
    i = {k: np.asarray(v) for k, v in i.items()}
    t = {"x": i["x"], "ctx_1024": i["ctx_1024"], "g_xattn": i["g_xattn"], "g_ffn": i["g_ffn"]}
    t["consts"] = np.zeros((P, CONST_N), np.float32)
    for name, a in shape_constants().items():
        if name in OF_A_STAGE:
            t["table_" + name] = a
            continue
        at, n = CONST_AT[name]
        t["consts"][:, at:at + n] = a
    t["mask_L0"] = i["mask_BxS2_bf1"].view(np.uint8).reshape(1, -1)
    t["mask_L1"] = i["mask_Bx1x1xS2_ff1"].reshape(1, -1)
    wkv, bkv = i["L0_xattn_Wkv"], i["L0_xattn_bkv"]
    xa = {"L0": (i["L0_xattn_Wq"], wkv[:, :D], wkv[:, D:], i["L0_xattn_Wo"], i["L0_xattn_bq"], bkv[:D], bkv[D:], i["L0_xattn_bo"])}
    for L, q in (("L1", "W{} b{}"), ("L3", "w_{} b_{}")):
        wn, bn = q.split()
        up = (lambda c: c)
        xa[L] = tuple(i[f"{L}_xattn_{wn.format(c)}"].T for c in "qkvo") + tuple(i[f"{L}_xattn_{bn.format(c)}"] for c in "qkvo")
    for L, (wq, wk, wv, wo, bq, bk, bv, bo) in xa.items():
        for n, w in (("wq", wq), ("wk", wk), ("wv", wv), ("wo", wo)):
            t[f"{L}_xattn_{n}"] = rows(w)
        t[f"{L}_xattn_bq"], t[f"{L}_xattn_bk"] = cols(bq), cols(bk)
        t[f"{L}_xattn_bv"], t[f"{L}_xattn_bo"] = bv.reshape(1, -1), bo.reshape(1, -1)
    for part in ("light", "heavy"):
        wkv = i[f"L0_ffn_wkv_{part}"]
        if part == "light":
            wk, wv = wkv[:, :CH * CD], wkv[:, CH * CD:]
        else:
            heads = wkv.reshape(CH, 2, CD, D)
            wk, wv = heads[:, 0].reshape(CH * CD, D).T, heads[:, 1].reshape(CH * CD, D).T
        for n, w in (("wq", i[f"L0_ffn_wq_{part}"]), ("wk", wk), ("wv", wv), ("wo", i[f"L0_ffn_wo_{part}"])):
            t[f"L0_ffn_{n}_{part}"] = rows(w)
        t[f"L0_ffn_gamma_{part}"] = cols(i[f"L0_ffn_gamma_{part}"])
    t["L0_ffn_q_routing_token"] = i["L0_ffn_q_routing_token"].reshape(1, -1)
    t["L1_ffn_q1"], t["L1_ffn_q2"] = rows(i["L1_ffn_fc1_q"]), rows(i["L1_ffn_fc2_q"])
    t["L1_ffn_sc1"], t["L1_ffn_sc2"] = i["L1_ffn_fc1_scales"].reshape(1, -1), i["L1_ffn_fc2_scales"].reshape(1, -1)
    t["L1_ffn_b1"], t["L1_ffn_b2"] = cols(i["L1_ffn_fc1_bias"]), i["L1_ffn_fc2_bias"].reshape(1, -1)
    t["L1_ffn_gamma"], t["L1_ffn_beta"] = cols(i["L1_ffn_ln_gamma"]), cols(i["L1_ffn_ln_beta"])
    t["mask_L2"] = i["mask_SxS2_ik1"]
    t["L2_xattn_wq"] = rows(i["L2_xattn_Wq"])
    t["L2_xattn_wk"], t["L2_xattn_wv"] = rows(i["L2_xattn_Wk"].T), rows(i["L2_xattn_Wv"].T)
    t["L2_xattn_bq"], t["L2_xattn_bk"] = cols(i["L2_xattn_bq"]), cols(i["L2_xattn_bk"])
    t["L2_xattn_bv"] = i["L2_xattn_bv"].reshape(1, -1)
    for g in ("f", "i", "c", "o"):
        t[f"L2_ffn_w{g}"], t[f"L2_ffn_u{g}"] = rows(i[f"L2_ffn_w{g}"].T), rows(i[f"L2_ffn_u{g}"].T)
        t[f"L2_ffn_b{g}"] = i["L2_ffn_bo"].reshape(1, -1) if g == "o" else cols(i[f"L2_ffn_b{g}"])
    ex = np.zeros((NE, P, E_N), np.float32)
    for e in range(NE):
        ex[e, :, 0:KD * DE] = rows(i["L3_ffn_W1"][e].T)
        ex[e, :, KD * DE:2 * KD * DE] = rows(i["L3_ffn_W2"][e].T)
        down = np.zeros((KE * P, D), np.float32)
        down[:DE] = i["L3_ffn_W3"][e].T
        ex[e, :, 2 * KD * DE:] = rows(down)
    t["L3_ffn_experts"] = ex
    t["L3_ffn_gate_w"], t["L3_ffn_rms_w"] = rows(i["L3_ffn_gate_w"].T), i["L3_ffn_rms_w"].reshape(1, -1)
    t["L2_ffn_in_c"] = cols(i["L2_ffn_in_c"])
    return t


def declare_and_write(nc, tensors, stages):
    arrays = {f"in_{n}": np.ascontiguousarray(a) for n, a in tensors.items()}
    T = {n[3:]: nc.dram_tensor(n, a.shape, mybir.dt.from_np(a.dtype), kind="ExternalInput").ap() for n, a in arrays.items()}
    T["out"] = nc.dram_tensor("out_x", (B, S, D), F32, kind="ExternalOutput").ap()
    for n, shape in (("slots", (MOE_TILES * P, D)), ("results", (MOE_TILES * P, D)), ("unit_rows", (B * S, D)),
                     ("row_scores", (B * S,)), ("routed_in", (2 * NR, D)), ("routed_out", (NR + P, D)), ("residual", (B * S, D))):
        T[n] = nc.dram_tensor(n, shape, F32, kind="Internal").ap()
    flamingo_kernel(nc, T, T["out"], stages)
    return arrays


def kernel(**inputs):
    import concourse.bacc as bacc
    from concourse.bass_utils import run_bass_kernel_spmd as run

    nc = bacc.Bacc("TRN2", target_bir_lowering=False, num_devices=1)
    arrays = declare_and_write(nc, lay_out(inputs), STAGES)
    return run(nc, [arrays], core_ids=[0]).results[0]["out_x"]
```

```python
from contextlib import ExitStack
from math import exp

import concourse.bass as bass
from concourse import mybir
import numpy as np

F32 = mybir.dt.float32
BF16 = mybir.dt.bfloat16
I32 = mybir.dt.int32
U8 = mybir.dt.uint8
ALU = mybir.AluOpType
ACT = mybir.ActivationFunctionType
AX_X = mybir.AxisListType.X

P = 128
B, S, D = 8, 512, 256
TB = S // P
NT = B * TB
KD = D // P
SC = 64
NH, HD = 16, 16
HH = NH // KD
NP = HH // 2
VW = HD + 1
LN_EPS = 1e-5
STAGES = ["L0_xattn", "L0_ffn", "L1_xattn", "L1_ffn", "L2_xattn", "L2_ffn", "L3_xattn", "L3_ffn"]

NE, DE = 8, 704
KE = -(-DE // P)
HE = DE // 2
MOE_TILES = 2 * B * S // P + NE
E_N = 2 * KD * DE + KE * D
MOE_N = 3400



def shape_constants():
    p = np.arange(P)
    f = np.float32
    out = {"ident": np.eye(P, dtype=f)}
    for name, scale in (("head8", 64 ** -0.5), ("head4", 0.25)):
        out[name] = ((p[:, None] // HD) == np.arange(HH)[None, :]).astype(f) * f(scale)
    swap = np.zeros((P, P), f)
    swap[p[0::2] + 1, p[0::2]] = -1.0
    swap[p[0::2], p[0::2] + 1] = 1.0
    out["swap"] = swap
    inv = (f(1.0) / np.power(f(10000.0), np.arange(0, HD, 2, dtype=f) / f(HD))).astype(f)
    for name, n in (("q", S), ("k", SC)):
        pos = (f(10.0) * (np.arange(n, dtype=f) / f(n))).astype(f)
        ang = (inv[(p % HD) // 2][:, None] * pos[None, :]).astype(f)
        out["cos_" + name] = np.cos(ang).astype(f)
        out["sin_" + name] = np.sin(ang).astype(f)
    q = np.arange(P)
    out["same_batch"] = ((q[:, None] // TB == q[None, :NT] // TB) & (q[:, None] < NT)).astype(f)
    tok = np.arange(TB)[None, :, None] * P + p[:, None, None]
    out["earlier"] = (np.arange(S)[None, None, :] < tok).astype(f).reshape(P, TB * S)
    out["expert"] = np.broadcast_to(np.arange(8, dtype=f)[None, :], (P, 8)).copy()
    out["before"] = (q[:, None] < q[None, :]).astype(f)
    out["ones"] = np.ones((P, P), f)
    out["batch_slot"] = np.broadcast_to((q[:NT] // TB * 256).astype(f)[None, :], (P, NT)).copy()
    out["slot_start"] = np.broadcast_to(P * np.arange(MOE_TILES, dtype=f)[None, :], (P, MOE_TILES)).copy()
    return out


ROTARY = ("cos_q", "sin_q", "cos_k", "sin_k")
OF_A_STAGE = ROTARY + ("earlier",)


def constant_columns():
    at, cols = 0, {}
    for name, a in shape_constants().items():
        if name in OF_A_STAGE:
            continue
        cols[name] = (at, a.shape[1])
        at += a.shape[1]
    return cols, at


CONST_AT, CONST_N = constant_columns()


W_N, A_N = 9216, 17000


def runs(numbers):
    out = []
    for n in sorted(numbers):
        if out and out[-1][1] == n:
            out[-1][1] = n + 1
        else:
            out.append([n, n + 1])
    return out


class Carver:

    def __init__(self, tensor, first, end):
        self.tensor, self.at, self.end = tensor, first, end

    def take(self, *shape):
        n = 1
        for s in shape:
            n *= s
        ap = self.tensor[:, self.at:self.at + n]
        self.at += n
        assert self.at <= self.end, (self.at, self.end)
        if len(shape) == 2:
            ap = ap.rearrange("p (a b) -> p a b", b=shape[1])
        elif len(shape) == 3:
            ap = ap.rearrange("p (a b c) -> p a b c", b=shape[1], c=shape[2])
        elif len(shape) == 4:
            ap = ap.rearrange("p (a b c d) -> p a b c d", b=shape[1], c=shape[2], d=shape[3])
        return ap


class Order:

    def __init__(self, eng, sem):
        self.eng, self.sem, self.base, self.k, self.i, self.per = eng, sem, 0, 0, None, 0

    def mark(self, ins):
        ins.then_inc(self.sem, 1)
        self.k += 1

    def turn(self, i, per):
        self.base, self.i, self.per, self.k = self.base + self.k, i, per, 0

    def end(self, turns):
        assert self.k == self.per, (self.k, self.per)
        self.base, self.i, self.k = self.base + turns * self.per, None, 0

    def settle(self, back=0):
        v = self.base + self.k - back
        self.eng.wait_ge(self.sem, v if self.i is None else self.i * self.per + v)


class Names:
    pass


def flamingo_kernel(nc, T, out, stages):
    ctx = ExitStack()
    with ctx:
        def sb(name, shape, dt=F32):
            return ctx.enter_context(nc.sbuf_tensor(name, shape, dt))

        def sem(name):
            return ctx.enter_context(nc.semaphore(name))

        numbers, handles = [[], []], [[], []]

        def stage_sems(k):
            for h in handles[k % 2]:
                nc.release_semaphore(h)
            handles[k % 2] = []
            used = iter(list(numbers[k % 2]))

            def take(name):
                num = next(used, None)
                h = nc.alloc_semaphore(name=name, num=num)
                if num is None:
                    numbers[k % 2].append(h.num)
                handles[k % 2].append(h)
                return h
            return take

        x_all = sb("x_all", [P, NT + TB, D])
        consts = sb("consts", [P, CONST_N])
        ctx2T = sb("ctx2T", [P, KD, B, 2 * SC])
        tg = sb("tg", [P, 8])
        minus_half = sb("minus_half", [P, TB])
        ones_bf = sb("ones_bf", [1, P], BF16)
        mem = sb("mem", [P, 2 * W_N + A_N])
        xn = sb("xn", [P, TB, D])
        xnT = sb("xnT", [P, KD, S])
        stats = sb("stats", [P, TB, 6])
        mean_var = sb("mean_var", [P, TB, 2])
        var_eps = sb("var_eps", [P, TB])
        rstd = sb("rstd", [P, TB])
        moe_small = sb("moe_small", [P, MOE_N])
        PS = ctx.enter_context(nc.psum_tensor("PS", [P, 8, 512], F32))

        def const(name, rows=P):
            at, n = CONST_AT[name]
            return consts[0:rows, at:at + n]

        ident = const("ident")

        x_loaded = sem("x_loaded")
        consts_loaded = sem("consts_loaded")
        ctx_loaded = sem("ctx_loaded")
        gates_loaded = sem("gates_loaded")
        gates_ready = sem("gates_ready")
        ctx_psum = sem("ctx_psum")
        ctx_ready = sem("ctx_ready")
        x_updated = sem("x_updated")
        out_stored = sem("out_stored")
        zeros_ready = sem("zeros_ready")
        sems_cleared = sem("sems_cleared")
        spare = sem("spare")
        dve_order = sem("dve_order")
        act_order = sem("act_order")
        pool_order = sem("pool_order")

        loaded = [sem(f"{name}_weights_loaded") for name in stages]
        plans = []
        for k, name in enumerate(stages):
            s = Names()
            s.name, s.k = name, k
            half = STAGES.index(name) % 2
            s.w = Carver(mem, half * W_N, (half + 1) * W_N)
            s.a = Carver(mem, 2 * W_N, 2 * W_N + A_N)
            s.mem = mem
            s.x_before = NT * k
            s.weights_loaded = loaded[k]
            s.looks_ahead = s.stores = False
            s.early_sync_program = s.sync_program = None
            s.loads = []
            s.gate = tg[:, STAGES.index(name) // 2 + 4 * (STAGES.index(name) % 2):][:, 0:1]
            stage, s.own_sem = stage_sems(k), sem
            s.var_ready, s.rstd_ready, s.ln_ready, s.xnT_psum, s.xnT_ready = (
                stage(f"{name}_{n}") for n in ("var_ready", "rstd_ready", "ln_ready", "xnT_psum", "xnT_ready"))
            PLAN[name](s, T, stage, moe_small)
            plans.append(s)

        block = ctx.enter_context(nc.Block())

        def dve_layernorm(dve, order, s, i, last_read=None):
            for t in range(TB):
                order.mark(dve.bn_stats(stats[:, t, :], x_all[:, i * TB + t, :]))
            order.settle()
            dve.sem_inc(spare, 1)
            for t in range(TB):
                order.mark(dve.bn_aggr(mean_var[:, t, :], stats[:, t, :]))
            order.settle()
            dve.tensor_scalar(var_eps[:], mean_var[:, :, 1], LN_EPS, None, ALU.add).then_inc(s.var_ready, 1)
            dve.wait_ge(s.rstd_ready, i + 1)
            dve.wait_ge(s.xnT_psum, KD * i)
            if last_read is not None:
                dve.wait_ge(*last_read)
            for t in range(TB):
                dve.tensor_scalar(xn[:, t, :], x_all[:, i * TB + t, :], mean_var[:, t, 0:1], rstd[:, t:t + 1],
                                  ALU.subtract, ALU.mult).then_inc(s.ln_ready, 1)

        def ln_stats(dve, order, i, t):
            order.mark(dve.bn_stats(stats[:, t, :], x_all[:, i * TB + t, :]))

        def ln_variance(dve, order, s):
            order.settle()
            dve.sem_inc(spare, 1)
            for t in range(TB):
                order.mark(dve.bn_aggr(mean_var[:, t, :], stats[:, t, :]))
            order.settle()
            dve.tensor_scalar(var_eps[:], mean_var[:, :, 1], LN_EPS, None, ALU.add).then_inc(s.var_ready, 1)

        def ln_apply(dve, s, i):
            dve.wait_ge(s.rstd_ready, i + 1)
            dve.wait_ge(s.xnT_psum, KD * i)
            for t in range(TB):
                dve.tensor_scalar(xn[:, t, :], x_all[:, i * TB + t, :], mean_var[:, t, 0:1], rstd[:, t:t + 1],
                                  ALU.subtract, ALU.mult).then_inc(s.ln_ready, 1)

        LN_MARKS = 2 * TB

        def stage_start(eng, s):
            eng.wait_ge(x_updated, s.x_before)
            if s.k >= 2:
                eng.wait_ge(sems_cleared, s.k - 1)
                eng.sem_inc(spare, 1)
            if s.k == 0:
                eng.wait_ge(ctx_ready, 2 * KD)
            if s.k > 0 and plans[s.k - 1].looks_ahead:
                eng.wait_ge(plans[s.k - 1].xnT_ready, KD * (B + 1))

        def pool_rstd(pool, s, i):
            pool.wait_ge(s.var_ready, i + 1)
            nc.gpsimd.tensor_tensor(rstd[:], var_eps[:], minus_half[:], ALU.pow).then_inc(s.rstd_ready, 1)

        def pe_transpose_xn(pe, s, i, banks=(0, 1), src=None, ready=None):
            src = xn if src is None else src
            for k in range(KD):
                for t in range(TB):
                    if k == 0:
                        pe.wait_ge(ready or s.ln_ready, TB * i + t + 1)
                    last = nc.tensor.transpose(PS[:, banks[k], t * P:(t + 1) * P], src[:, t, k * P:(k + 1) * P], ident)
                last.then_inc(s.xnT_psum, 1)

        def act_copy_xnT(act, s, i, banks=(0, 1)):
            for k in range(KD):
                act.wait_ge(s.xnT_psum, KD * i + k + 1)
                nc.scalar.activation(xnT[:, k, :], PS[:, banks[k], :], ACT.Copy).then_inc(s.xnT_ready, 1)

        env = Names()
        env.LN_MARKS, env.PS, env.act_copy_xnT, env.const, env.ctx2T, env.dve_layernorm = LN_MARKS, PS, act_copy_xnT, const, ctx2T, dve_layernorm
        env.ident, env.mean_var, env.minus_half, env.nc, env.ones_bf, env.out_stored = ident, mean_var, minus_half, nc, ones_bf, out_stored
        env.pe_transpose_xn, env.pool_rstd, env.rstd, env.spare, env.stage_start, env.stats = pe_transpose_xn, pool_rstd, rstd, spare, stage_start, stats
        env.var_eps, env.x_all, env.x_updated, env.xn, env.xnT, env.zeros_ready = var_eps, x_all, x_updated, xn, xnT, zeros_ready
        env.pool_order, env.ln_stats, env.ln_variance, env.ln_apply = pool_order, ln_stats, ln_variance, ln_apply

        @block.sync
        def _(sp):
            for k, s in enumerate(plans):
                if k > 0:
                    sp.wait_ge(x_updated, NT * k)
                if k >= 2:
                    for lo, hi in runs(numbers[k % 2]):
                        last = sp.sem_clear(range(lo, hi))
                    last.then_inc(sems_cleared, 1)
                if k == 0:
                    for b in range(B):
                        sp.dma_start(x_all[:, b * TB:(b + 1) * TB, :],
                                     T["x"][b].rearrange("(t p) d -> p t d", p=P)).then_inc(x_loaded, 16)
                for later in plans[k:k + 2] if k == 0 else plans[k + 1:k + 2]:
                    for dst, src in later.loads:
                        sp.dma_start(dst, src).then_inc(later.weights_loaded, 16)
                    if later.early_sync_program:
                        later.early_sync_program(sp, env, later)
                if s.sync_program:
                    s.sync_program(sp, env, s)
            for b in range(0 if plans[-1].stores else B):
                sp.wait_ge(x_updated, NT * (len(plans) - 1) + TB * (b + 1))
                sp.dma_start(out[b].rearrange("(t p) d -> p t d", p=P),
                             x_all[:, b * TB:(b + 1) * TB, :]).then_inc(out_stored, 16)
            if not plans[-1].stores:
                sp.wait_ge(out_stored, 16 * B)

        @block.gpsimd
        def _(pool):
            nc.gpsimd.memset(minus_half[:], -0.5).then_inc(pool_order, 1)
            pool.wait_ge(pool_order, 1)
            order = Order(pool, pool_order)
            order.k = 1
            for s in plans:
                stage_start(pool, s)
                s.pool(pool, order, env, s)

        @block.scalar
        def _(act):
            order = Order(act, act_order)
            act.dma_start(consts[:], T["consts"]).then_inc(consts_loaded, 16)
            ctx_v = T["ctx_1024"].rearrange("b s d -> (b s) d").rearrange("(t p) d -> p t d", p=P)
            act.dma_start(xn[:], ctx_v).then_inc(ctx_loaded, 16)
            act.dma_start(tg[:, 0:4], T["g_xattn"].rearrange("(a n) -> a n", a=1).broadcast_to([P, 4])).then_inc(gates_loaded, 16)
            act.dma_start(tg[:, 4:8], T["g_ffn"].rearrange("(a n) -> a n", a=1).broadcast_to([P, 4])).then_inc(gates_loaded, 16)
            act.wait_ge(gates_loaded, 32)
            nc.scalar.activation(tg[:], tg[:], ACT.Tanh).then_inc(gates_ready, 1)
            for k in range(KD):
                act.wait_ge(ctx_psum, k + 1)
                src = PS[:, k, :].rearrange("p (b s) -> p b s", s=SC)
                for e in range(2):
                    nc.scalar.activation(ctx2T[:, k, :, e * SC:(e + 1) * SC], src, ACT.Copy).then_inc(ctx_ready, 1)
            for s in plans:
                stage_start(act, s)
                s.act(act, order, env, s)

        @block.vector
        def _(dve):
            order = Order(dve, dve_order)
            order.mark(dve.memset(ones_bf[:], 1.0))
            order.mark(dve.memset(x_all[:, NT:NT + TB, :], 0.0))
            order.settle()
            dve.sem_inc(zeros_ready, 1)
            dve.wait_ge(consts_loaded, 16)
            dve.wait_ge(gates_ready, 1)
            dve.wait_ge(ctx_psum, KD)
            dve.wait_ge(x_loaded, 16 * B)
            for s in plans:
                stage_start(dve, s)
                s.dve(dve, order, env, s)

        @block.tensor
        def _(pe):
            pe.wait_ge(consts_loaded, 16)
            pe.wait_ge(ctx_loaded, 16)
            for k in range(KD):
                for t in range(B * SC // P):
                    last = nc.tensor.transpose(PS[:, k, t * P:(t + 1) * P], xn[:, t, k * P:(k + 1) * P], ident)
                last.then_inc(ctx_psum, 1)
            pe.wait_ge(ctx_ready, 2 * KD)
            for s in plans:
                stage_start(pe, s)
                s.pe(pe, env, s)


def plan_xattn(s, T, sem, small):
    L = s.name[:2]
    s.rope, s.masked = L == "L0", L in ("L0", "L1")
    take = s.w.take
    s.wq, s.wk, s.wv, s.wo = take(KD, D), take(KD, D), take(KD, D), take(KD, D)
    s.bq, s.bk, s.bv, s.bo = take(KD), take(KD), take(D), take(D)
    n = {c: T[f"{s.name}_{c}"] for c in ("wq", "wk", "wv", "wo", "bq", "bk")}
    for c, w in (("wq", s.wq), ("wk", s.wk), ("wv", s.wv), ("wo", s.wo)):
        s.loads.append((w, n[c].rearrange("p (k n) -> p k n", k=KD)))
    s.loads += [(s.bq, n["bq"]), (s.bk, n["bk"]),
                (s.bv, T[f"{s.name}_bv"].broadcast_to([P, D])), (s.bo, T[f"{s.name}_bo"].broadcast_to([P, D]))]
    if s.masked:
        s.mask = take(B * SC)
        mask = T["mask_L0" if s.rope else "mask_L1"].rearrange("a (b s) -> a b s", s=SC)
        s.mask_u8 = s.mask[:, 0:B * SC // 4].bitcast(U8)
        s.loads.append((s.mask_u8 if s.rope else s.mask, mask.rearrange("a b s -> a (b s)").broadcast_to([P, B * SC])))
    if s.rope:
        s.rotary = {n: take(w) for n, w in zip(ROTARY, (S, S, SC, SC))}
        s.loads += [(s.rotary[n], T["table_" + n]) for n in ROTARY]
    take = s.a.take
    s.kT = take(KD, B * SC)
    s.kbd = take(KD, HH, SC)
    s.vbd = take(B, KD * NP, 2 * VW)
    s.qT = take(KD, S)
    s.shifted, s.probs, s.probsT = take(2, S), take(2, S), take(2, S)
    s.o, s.oT = take(2, D), take(2, KD, P)
    s.recip = take(2, NH)
    s.gbo = take(D)
    s.maxes = take(2, HH)
    if s.masked:
        s.keep = take(B * SC)
        s.mask_row = take(B * SC // 2).bitcast(BF16)
    if s.rope:
        s.rot, s.rot2 = take(KD, S), take(KD, S)
    s.sems = {n: sem(f"{s.name}_{n}") for n in (
        "k_psum", "k_ready", "v_psum", "v_ready", "setup", "q_psum", "q_ready", "swap_psum", "swap_read", "q_roped", "kbd_ready",
        "scores", "shifted_ready", "exp_ready", "pT_psum", "pT_ready", "pv_psum", "o_ready", "oT_psum",
        "oT_ready", "y_psum", "biased")}
    s.pe, s.act, s.dve, s.pool = xattn_pe, xattn_act, xattn_dve, xattn_pool


AHEAD_TURN, AHEAD_Q, AHEAD_Q_ROPE, AHEAD_SWAP = 5, 8, 7, 9


def xattn_pe(pe, e, s):
    PS, nc = e.PS, e.nc
    pe.wait_ge(s.weights_loaded, 16 * len(s.loads))
    for f in range(KD):
        for k in range(KD):
            last = nc.tensor.matmul(PS[:, f, :], s.wk[:, k, f * P:(f + 1) * P], e.ctx2T[:, k, :, 0:SC],
                                    start=k == 0, stop=k == KD - 1)
        last.then_inc(s.sems["k_psum"], 1)
    if s.rope:
        pe.wait_ge(s.sems["k_ready"], KD)
        for f in range(KD):
            nc.tensor.matmul(PS[:, f, :], e.const("swap"), s.kT[:, f, :], start=True, stop=True)\
                .then_inc(s.sems["swap_psum"], 1)
    for b in range(B):
        if b >= 2:
            pe.wait_ge(s.sems["v_ready"], 2 * (b - 1))
        for k in range(KD):
            last = nc.tensor.matmul(PS[:, 2 + b % 2, 0:D], e.ctx2T[:, k, b, :], s.wv[:, k, :],
                                    start=k == 0, stop=k == KD - 1)
        last.then_inc(s.sems["v_psum"], 1)
    pe.wait_ge(s.sems["setup"], 1)
    qT = s.rot if s.rope else s.qT

    def turn_xn(i, k):
        for t in range(TB):
            if k == 0:
                pe.wait_ge(s.ln_ready, TB * i + t + 1)
        if k > 0:
            pe.wait_ge(s.xnT_ready, KD * i + k)
        for t in range(TB):
            last = nc.tensor.transpose(PS[:, 0, t * P:(t + 1) * P], e.xn[:, t, k * P:(k + 1) * P], e.ident)
        last.then_inc(s.xnT_psum, 1)

    def query(i, f):
        pe.wait_ge(s.xnT_ready, KD * (i + 1))
        if f > 0:
            pe.wait_ge(s.sems["q_ready"], KD * i + f)
        for k in range(KD):
            last = nc.tensor.matmul(PS[:, 0, :], s.wq[:, k, f * P:(f + 1) * P], e.xnT[:, k, :],
                                    start=k == 0, stop=k == KD - 1)
        last.then_inc(s.sems["q_psum"], 1)

    def partners(i, f):
        pe.wait_ge(s.sems["q_ready"], KD * (i + 1))
        if f > 0:
            pe.wait_ge(s.sems["swap_read"], KD * i + f)
        nc.tensor.matmul(PS[:, 0, :], e.const("swap"), s.qT[:, f, :], start=True, stop=True).then_inc(s.sems["swap_psum"], 1)

    def batch(i, ahead):
        n = 2 * TB * i
        if s.rope:
            pe.wait_ge(s.sems["q_roped"], i + 1)
        pe.wait_ge(s.sems["q_ready"], KD * (i + 1))
        pe.wait_ge(s.sems["kbd_ready"], KD * (i + 1))

        def scores(u):
            t, f = u // KD, u % KD
            pe.wait_ge(s.sems["shifted_ready"], n + max(u - 1, 0))
            last = nc.tensor.matmul(PS[:, 2 + u % 2, :], qT[:, f, t * P:(t + 1) * P],
                                    s.kbd[:, f, :, :], start=True, stop=not s.masked)
            if s.masked:
                row = s.mask_row[0:1, :].rearrange("a (o b s) -> a o b s", o=1, s=SC)[:, :, bass.ds(i, 1), :]
                last = nc.tensor.matmul(PS[:, 2 + u % 2, :], e.ones_bf[:],
                                        row.rearrange("a o b s -> a (o b) s").broadcast_to([1, HH, SC]), start=False, stop=True)
            last.then_inc(s.sems["scores"], 1)

        def transposes(u):
            pe.wait_ge(s.sems["exp_ready"], n + u + 1)
            pe.wait_ge(s.sems["pT_ready"], n + max(u - 1, 0))
            for j in range(NP):
                last = nc.tensor.transpose(PS[:, 4 + u % 2, j * P:(j + 1) * P],
                                           s.probs[:, u % 2, j * P:(j + 1) * P], e.ident)
            last.then_inc(s.sems["pT_psum"], 1)

        def values(u):
            t, f = u // KD, u % KD
            pe.wait_ge(s.sems["pT_ready"], n + u + 1)
            if f == 0:
                pe.wait_ge(s.sems["o_ready"], TB * i + max(t - 1, 0))
            for j in range(NP):
                at = (f * NP + j) * 2 * VW
                last = nc.tensor.matmul(PS[:, 6 + t % 2, at:at + 2 * VW], s.probsT[:, u % 2, j * P:(j + 1) * P],
                                        s.vbd[:, bass.ds(i, 1), f * NP + j, :], start=True, stop=True)
            last.then_inc(s.sems["pv_psum"], 1)

        for step in range(2 * TB + 4):
            if step >= 5 and step % 2 == 1:
                t = (step - 5) // 2
                pe.wait_ge(s.sems["oT_ready"], TB * i + t + 1)
                for k in range(KD):
                    last = nc.tensor.matmul(PS[:, 1, D:2 * D], s.oT[:, t % 2, k, :], s.wo[:, k, :],
                                            start=k == 0, stop=k == KD - 1)
                last.then_inc(s.sems["y_psum"], 1)
            if step < 2 * TB:
                scores(step)
            if 1 <= step < 2 * TB + 1:
                transposes(step - 1)
            if 2 <= step < 2 * TB + 2:
                values(step - 2)
            for f in range(KD if ahead else 0):
                if step == AHEAD_TURN + f:
                    turn_xn(i + 1, f)
                if step == (AHEAD_Q_ROPE if s.rope else AHEAD_Q) + f:
                    query(i + 1, f)
                if s.rope and step == AHEAD_SWAP + f:
                    partners(i + 1, f)
            if step >= 4 and step % 2 == 0:
                t = (step - 4) // 2
                pe.wait_ge(s.sems["o_ready"], TB * i + t + 1)
                pe.wait_ge(e.x_updated, s.x_before + TB * i + t)
                for k in range(KD):
                    last = nc.tensor.transpose(PS[:, 1, k * P:(k + 1) * P], s.o[:, t % 2, k * P:(k + 1) * P], e.ident)
                last.then_inc(s.sems["oT_psum"], 1)

    for f in range(KD):
        turn_xn(0, f)
    for f in range(KD):
        query(0, f)
    for f in range(KD if s.rope else 0):
        partners(0, f)
    with pe.Fori(0, B - 1) as i:
        batch(i, True)
    batch(B - 1, False)


def xattn_act(act, order, e, s):
    PS, nc = e.PS, e.nc
    act.wait_ge(s.weights_loaded, 16 * len(s.loads))
    for f in range(KD):
        act.wait_ge(s.sems["k_psum"], f + 1)
        nc.scalar.activation(s.kT[:, f, :], PS[:, f, :], ACT.Identity, bias=s.bk[:, f:f + 1]).then_inc(s.sems["k_ready"], 1)
    def copy_xnT(i, k):
        act.wait_ge(s.xnT_psum, KD * i + k + 1)
        nc.scalar.activation(e.xnT[:, k, :], PS[:, 0, :], ACT.Copy).then_inc(s.xnT_ready, 1)

    def query(i, f):
        act.wait_ge(s.sems["q_psum"], KD * i + f + 1)
        if s.rope:
            act.wait_ge(s.sems["q_roped"], i)
        nc.scalar.activation(s.qT[:, f, :], PS[:, 0, :], ACT.Identity, bias=s.bq[:, f:f + 1]).then_inc(s.sems["q_ready"], 1)

    def batch(i, ahead):
        n = 2 * TB * i
        for step in range(2 * TB + 4):
            if step < 2 * TB:
                u = step
                act.wait_ge(s.sems["shifted_ready"], n + u + 1)
                act.wait_ge(s.sems["pT_psum"], n + max(u - 1, 0))
                nc.scalar.activation(s.probs[:, u % 2, :], s.shifted[:, u % 2, :], ACT.Exp).then_inc(s.sems["exp_ready"], 1)
            if 1 <= step < 2 * TB + 1:
                u = step - 1
                act.wait_ge(s.sems["pT_psum"], n + u + 1)
                act.wait_ge(s.sems["pv_psum"], n + max(u - 1, 0))
                nc.scalar.activation(s.probsT[:, u % 2, :], PS[:, 4 + u % 2, :], ACT.Copy).then_inc(s.sems["pT_ready"], 1)
            for f in range(KD if ahead else 0):
                if step == AHEAD_TURN + f:
                    copy_xnT(i + 1, f)
                if step == (AHEAD_Q_ROPE if s.rope else AHEAD_Q) + f:
                    query(i + 1, f)
            if step >= 4 and step % 2 == 0:
                t = (step - 4) // 2
                act.wait_ge(s.sems["oT_psum"], TB * i + t + 1)
                act.wait_ge(s.sems["y_psum"], TB * i + max(t - 1, 0))
                nc.scalar.activation(s.oT[:, t % 2, :, :], PS[:, 1, 0:D].rearrange("p (k n) -> p k n", k=KD),
                                     ACT.Copy).then_inc(s.sems["oT_ready"], 1)

    for f in range(KD):
        copy_xnT(0, f)
    for f in range(KD):
        query(0, f)
    with act.Fori(0, B - 1) as i:
        batch(i, True)
    batch(B - 1, False)


def xattn_dve(dve, order, e, s):
    PS = e.PS
    dve.wait_ge(s.weights_loaded, 16 * len(s.loads))
    order.mark(dve.memset(s.vbd, 0.0))
    if s.masked:
        order.mark(dve.tensor_scalar(s.keep, s.mask_u8 if s.rope else s.mask, 0.0, None, ALU.not_equal))
    order.settle()
    order.mark(dve.memset(s.vbd.rearrange("p b j (e v) -> p (b j e) v", v=VW)[:, :, HD:VW], 1.0))
    if s.masked:
        order.mark(dve.tensor_scalar(s.mask_row[0:1, :], s.keep[0:1, :], 1.0, 3e38 if s.rope else 1e9,
                                     ALU.subtract, ALU.mult))
    order.settle()
    for h in range(2):
        order.mark(dve.memset(s.vbd.rearrange("p b j (e v) -> p (b j) e v", v=VW)[h * SC:(h + 1) * SC, :, 1 - h, HD:VW], 0.0))
    if s.rope:
        cos = s.rotary["cos_k"].rearrange("p (o s) -> p o s", o=1).broadcast_to([P, B, SC])
        sin = s.rotary["sin_k"].rearrange("p (o s) -> p o s", o=1).broadcast_to([P, B, SC])
        for f in range(KD):
            dve.wait_ge(s.sems["swap_psum"], f + 1)
            order.mark(dve.tensor_tensor(s.rot2[:, f, :].rearrange("p (b s) -> p b s", s=SC),
                                         PS[:, f, :].rearrange("p (b s) -> p b s", s=SC), sin, ALU.mult))
            kf = s.kT[:, f, :].rearrange("p (b s) -> p b s", s=SC)
            order.mark(dve.tensor_tensor(kf, kf, cos, ALU.mult))
        order.settle()
        order.mark(dve.tensor_tensor(s.kT, s.kT, s.rot2, ALU.add))
    elif s.masked:
        dve.wait_ge(s.sems["k_ready"], KD)
        for f in range(KD):
            order.mark(dve.tensor_tensor(s.kT[:, f, :], s.kT[:, f, :], s.keep, ALU.mult))
    bv = s.bv.rearrange("p (j e d) -> p j e d", e=2, d=HD)
    order.settle()
    for b in range(B):
        dve.wait_ge(s.sems["v_psum"], b + 1)
        src = PS[:, 2 + b % 2, 0:D].rearrange("p (j e d) -> p j e d", e=2, d=HD)
        dst = s.vbd[:, b, :, :].rearrange("p j (e v) -> p j e v", v=VW)
        for h in range(2):
            r = slice(h * SC, (h + 1) * SC)
            dve.tensor_tensor(dst[r, :, h, 0:HD], src[r, :, h, :], bv[r, :, h, :], ALU.add).then_inc(s.sems["v_ready"], 1)
    dve.wait_ge(s.sems["k_ready"], KD)
    dve.wait_ge(s.sems["v_ready"], 2 * B)
    dve.tensor_scalar(s.gbo, s.bo, s.gate, None, ALU.mult).then_inc(s.sems["setup"], 1)

    def rotate(i, part):
        if part == 0:
            dve.wait_ge(s.sems["q_ready"], KD * (i + 1))
            order.mark(dve.tensor_tensor(s.rot, s.qT, s.rotary["cos_q"].rearrange("p (o s) -> p o s", o=1).broadcast_to([P, KD, S]),
                                         ALU.mult))
        if part < KD:
            dve.wait_ge(s.sems["swap_psum"], KD * (i + 1) + part + 1)
            dve.tensor_tensor(s.rot2[:, part, :], PS[:, 0, :], s.rotary["sin_q"], ALU.mult).then_inc(s.sems["swap_read"], 1)
        if part == KD:
            order.settle()
            dve.wait_ge(s.sems["swap_read"], KD * (i + 1))
            dve.tensor_tensor(s.rot, s.rot, s.rot2, ALU.add).then_inc(s.sems["q_roped"], 1)

    def batch(i, ahead):
        n = 2 * TB * i
        for step in range(2 * TB + 6):
            if step < 2 * TB:
                u = step
                dve.wait_ge(s.sems["scores"], n + u + 1)
                bank = PS[:, 2 + u % 2, :].rearrange("p (h s) -> p h s", s=SC)
                order.mark(dve.tensor_reduce(s.maxes[:, u % 2, :], bank, AX_X, ALU.max))
                order.settle()
                dve.wait_ge(s.sems["exp_ready"], n + max(u - 1, 0))
                dve.tensor_tensor(s.shifted[:, u % 2, :].rearrange("p (h s) -> p h s", s=SC), bank,
                                  s.maxes[:, u % 2, :].rearrange("p (h o) -> p h o", o=1).broadcast_to([P, HH, SC]),
                                  ALU.subtract).then_inc(s.sems["shifted_ready"], 1)
            if 3 <= step < 2 * TB + 3 and step % 2 == 1:
                t = (step - 3) // 2
                dve.wait_ge(s.sems["pv_psum"], 2 * (TB * i + t + 1))
                o = PS[:, 6 + t % 2, 0:NH * VW].rearrange("p (h v) -> p h v", v=VW)
                dve.wait_ge(s.sems["o_ready"], TB * i + max(t - 1, 0))
                order.mark(dve.reciprocal(s.recip[:, t % 2, :], o[:, :, HD]))
                order.settle()
                dve.wait_ge(s.sems["oT_psum"], TB * i + max(t - 1, 0))
                dve.tensor_tensor(s.o[:, t % 2, :].rearrange("p (h d) -> p h d", d=HD), o[:, :, 0:HD],
                                  s.recip[:, t % 2, :].rearrange("p (h o) -> p h o", o=1).broadcast_to([P, NH, HD]),
                                  ALU.mult).then_inc(s.sems["o_ready"], 1)
            if step >= 6 and step % 2 == 0:
                t = (step - 6) // 2
                dve.wait_ge(s.sems["y_psum"], TB * i + t + 1)
                if t == 0:
                    dve.wait_ge(s.sems["biased"], i + 1)
                tile = e.x_all[:, i * TB + t, :]
                dve.scalar_tensor_tensor(tile, PS[:, 1, D:2 * D], s.gate, tile, ALU.mult, ALU.add)\
                    .then_inc(e.x_updated, 1)
            if ahead:
                if step < TB:
                    e.ln_stats(dve, order, i + 1, step)
                if step == TB:
                    e.ln_variance(dve, order, s)
                    e.ln_apply(dve, s, i + 1)
                if s.rope and step >= AHEAD_SWAP and step <= AHEAD_SWAP + KD:
                    rotate(i + 1, step - AHEAD_SWAP)

    marks = 3 * TB + (1 if s.rope else 0) + e.LN_MARKS
    for t in range(TB):
        e.ln_stats(dve, order, 0, t)
    e.ln_variance(dve, order, s)
    e.ln_apply(dve, s, 0)
    for part in range(KD + 1 if s.rope else 0):
        rotate(0, part)
    with dve.Fori(0, B - 1) as i:
        order.turn(i, marks)
        batch(i, True)
    order.end(B - 1)
    batch(B - 1, False)


def xattn_pool(pool, order, e, s):
    nc = e.nc
    mask16 = e.const("head8" if s.rope else "head4").rearrange("p (h o) -> p h o", o=1).broadcast_to([P, HH, SC])
    pool.wait_ge(s.sems["setup"], 1)

    def keys(i):
        pool.wait_ge(s.sems["scores"], 2 * TB * i)
        for f in range(KD):
            keys = s.kT[:, f, :].rearrange("p (b s) -> p b s", s=SC)[:, bass.ds(i, 1), :].broadcast_to([P, HH, SC])
            nc.gpsimd.tensor_tensor(s.kbd[:, f, :, :], keys, mask16, ALU.mult).then_inc(s.sems["kbd_ready"], 1)

    def bias(i):
        pool.wait_ge(s.ln_ready, TB * (i + 1))
        tiles = e.x_all[:, bass.ds(i * TB, TB), :]
        nc.gpsimd.tensor_tensor(tiles, tiles, s.gbo.rearrange("p (o d) -> p o d", o=1).broadcast_to([P, TB, D]),
                                ALU.add).then_inc(s.sems["biased"], 1)

    e.pool_rstd(pool, s, 0)
    keys(0)
    with pool.Fori(0, B - 1) as i:
        bias(i)
        e.pool_rstd(pool, s, i + 1)
        keys(i + 1)
    bias(B - 1)


FF = 1024
KF = FF // P


def plan_ffn1(s, T, sem, small):
    take = s.w.take
    s.w1, s.w2 = take(KD, FF), take(KF, D)
    s.sc1, s.sc2 = take(KD, FF), take(KF, D)
    s.b1, s.gamma, s.beta, s.b2 = take(KF), take(KD), take(KD), take(D)
    n = {c: T["L1_ffn_" + c] for c in ("q1", "q2", "sc1", "sc2", "b1", "gamma", "beta", "b2")}
    s.q1, s.q2 = s.w1.bitcast(I32), s.w2.bitcast(I32)
    s.loads += [(s.q1, n["q1"].rearrange("p (k n) -> p k n", k=KD)), (s.q2, n["q2"].rearrange("p (k n) -> p k n", k=KF)),
                (s.sc1.rearrange("p k n -> p (k n)"), n["sc1"].broadcast_to([P, KD * FF])),
                (s.sc2.rearrange("p k n -> p (k n)"), n["sc2"].broadcast_to([P, KF * D])),
                (s.b1, n["b1"]), (s.gamma, n["gamma"]), (s.beta, n["beta"]), (s.b2, n["b2"].broadcast_to([P, D]))]
    take = s.a.take
    s.hn = take(TB, D)
    s.hT = take(KD, S)
    s.yT = take(KF, S)
    s.xng = take(TB, D)
    s.gb2 = take(D)
    s.half_gate = take(1)
    s.sems = {n: sem(f"{s.name}_{n}") for n in (
        "setup", "var2_ready", "rstd2_ready", "hn_ready", "up_psum", "y_ready", "down_psum", "residual")}
    s.looks_ahead = True
    s.pe, s.act, s.dve, s.pool = ffn1_pe, ffn1_act, ffn1_dve, ffn1_pool


def ffn1_pe(pe, e, s):
    PS, nc = e.PS, e.nc
    pe.wait_ge(s.sems["setup"], 1)

    def front(i):
        e.pe_transpose_xn(pe, s, i, src=s.hn, ready=s.sems["hn_ready"])

    front(0)
    with pe.Fori(0, B) as i:
        pe.wait_ge(s.xnT_ready, KD * (i + 1))
        for n in range(KF):
            if n >= 4:
                pe.wait_ge(s.sems["y_ready"], KF * i + n - 3)
            for k in range(KD):
                last = nc.tensor.matmul(PS[:, 2 + n % 4, :], s.w1[:, k, n * P:(n + 1) * P], s.hT[:, k, :],
                                        start=k == 0, stop=k == KD - 1)
            last.then_inc(s.sems["up_psum"], 1)
        for t in range(TB):
            if t == TB - 1:
                front(i + 1)
            pe.wait_ge(e.x_updated, s.x_before + TB * i + max(t - 1, 0))
            pe.wait_ge(s.sems["y_ready"], KF * (i + 1))
            for n in range(KF):
                last = nc.tensor.matmul(PS[:, 6 + t % 2, 0:D], s.yT[:, n, t * P:(t + 1) * P], s.w2[:, n, :],
                                        start=n == 0, stop=n == KF - 1)
            last.then_inc(s.sems["down_psum"], 1)


def ffn1_act(act, order, e, s):
    PS, nc = e.PS, e.nc
    act.wait_ge(s.weights_loaded, 16 * len(s.loads))

    def front(i):
        for k in range(KD):
            act.wait_ge(s.xnT_psum, KD * i + k + 1)
            nc.scalar.activation(s.hT[:, k, :], PS[:, k, :], ACT.Identity, bias=s.beta[:, k:k + 1],
                                 scale=s.gamma[:, k:k + 1]).then_inc(s.xnT_ready, 1)

    front(0)
    with act.Fori(0, B) as i:
        for n in range(KF):
            act.wait_ge(s.sems["up_psum"], KF * i + n + 1)
            if n == 0:
                act.wait_ge(s.sems["down_psum"], TB * i)
            nc.scalar.activation(s.yT[:, n, :], PS[:, 2 + n % 4, :], ACT.Silu, bias=s.b1[:, n:n + 1]).then_inc(s.sems["y_ready"], 1)
        front(i + 1)


def ffn1_dve(dve, order, e, s):
    PS = e.PS
    dve.wait_ge(s.weights_loaded, 16 * len(s.loads))
    order.mark(dve.scalar_tensor_tensor(s.w1, s.q1, 128.0, s.sc1, ALU.subtract, ALU.mult))
    order.mark(dve.scalar_tensor_tensor(s.w2, s.q2, 128.0, s.sc2, ALU.subtract, ALU.mult))
    order.mark(dve.tensor_scalar(s.half_gate, s.gate, 0.5, None, ALU.mult))
    order.settle()
    dve.tensor_scalar(s.gb2, s.b2, s.half_gate, None, ALU.mult).then_inc(s.sems["setup"], 1)

    def front(i):
        e.dve_layernorm(dve, order, s, i, last_read=(s.sems["residual"], 2 * i))
        dve.wait_ge(s.ln_ready, TB * (i + 1))
        for t in range(TB):
            order.mark(dve.bn_stats(e.stats[:, t, :], e.xn[:, t, :]))
        order.settle()
        dve.sem_inc(e.spare, 1)
        for t in range(TB):
            order.mark(dve.bn_aggr(e.mean_var[:, t, :], e.stats[:, t, :]))
        order.settle()
        dve.tensor_scalar(e.var_eps[:], e.mean_var[:, :, 1], LN_EPS, None, ALU.add).then_inc(s.sems["var2_ready"], 1)
        dve.wait_ge(s.sems["rstd2_ready"], i + 1)
        for t in range(TB):
            dve.tensor_scalar(s.hn[:, t, :], e.xn[:, t, :], e.mean_var[:, t, 0:1], e.rstd[:, t:t + 1],
                              ALU.subtract, ALU.mult).then_inc(s.sems["hn_ready"], 1)

    front(0)
    with dve.Fori(0, B) as i:
        order.turn(i, 2 * e.LN_MARKS)
        front(i + 1)
        for t in range(TB):
            dve.wait_ge(s.sems["down_psum"], TB * i + t + 1)
            if t == 0:
                dve.wait_ge(s.sems["residual"], 2 * (i + 1))
            tile = e.x_all[:, i * TB + t, :]
            dve.scalar_tensor_tensor(tile, PS[:, 6 + t % 2, 0:D], s.half_gate, tile, ALU.mult, ALU.add)\
                .then_inc(e.x_updated, 1)
    order.end(B)


def ffn1_pool(pool, order, e, s):
    nc = e.nc
    pool.wait_ge(s.sems["setup"], 1)

    def front(i):
        e.pool_rstd(pool, s, i)
        pool.wait_ge(s.sems["var2_ready"], i + 1)
        nc.gpsimd.tensor_tensor(e.rstd[:], e.var_eps[:], e.minus_half[:], ALU.pow).then_inc(s.sems["rstd2_ready"], 1)

    front(0)
    gate = s.gate.rearrange("p (o d) -> p o d", o=1).broadcast_to([P, TB, D])
    bias = s.gb2.rearrange("p (o d) -> p o d", o=1).broadcast_to([P, TB, D])
    with pool.Fori(0, B) as i:
        order.turn(i, 1)
        tiles = e.x_all[:, bass.ds(i * TB, TB), :]
        pool.wait_ge(s.sems["hn_ready"], TB * (i + 1))
        nc.gpsimd.tensor_tensor(s.xng, e.xn[:], gate, ALU.mult).then_inc(s.sems["residual"], 1)
        pool.wait_ge(s.sems["residual"], 2 * i + 1)
        order.mark(nc.gpsimd.tensor_tensor(s.xng, s.xng, bias, ALU.add))
        order.settle()
        nc.gpsimd.tensor_tensor(tiles, tiles, s.xng, ALU.add).then_inc(s.sems["residual"], 1)
        front(i + 1)
    order.end(B)


def plan_xattn2(s, T, sem, small):
    take = s.w.take
    s.wq, s.wk, s.wv = take(KD, D), take(KD, D), take(KD, D)
    s.bq, s.bk, s.bv = take(KD), take(KD), take(D)
    s.mask = take(TB, SC)
    n = {c: T[f"{s.name}_{c}"] for c in ("wq", "wk", "wv", "bq", "bk", "bv")}
    for c, w in (("wq", s.wq), ("wk", s.wk), ("wv", s.wv)):
        s.loads.append((w, n[c].rearrange("p (k n) -> p k n", k=KD)))
    s.loads += [(s.bq, n["bq"]), (s.bk, n["bk"]), (s.bv, n["bv"].broadcast_to([P, D])),
                (s.mask.bitcast(I32), T["mask_L2"].rearrange("(t p) s -> p t s", p=P))]
    take = s.a.take
    s.keep, s.bias = take(TB, SC), take(TB, SC)
    s.kT = take(KD, B * SC)
    s.bq_wide = take(KD, P)
    s.qk = take(KD, B * SC)
    s.qk_bias = take(B * SC)
    s.v = take(B, D)
    s.sc, s.probs = take(TB, SC), take(TB, SC)
    s.maxes, s.sums, s.scale = take(TB), take(TB), take(TB)
    s.probsT = take(TB, P)
    s.sems = {n: sem(f"{s.name}_{n}") for n in (
        "k_psum", "k_ready", "qk_psum", "qk_ready", "v_psum", "v_ready", "setup", "scores", "shifted_ready",
        "exp_ready", "pT_psum", "pT_ready", "out_psum")}
    s.looks_ahead = True
    s.pe, s.act, s.dve, s.pool = xattn2_pe, xattn2_act, xattn2_dve, xattn2_pool


def xattn2_pe(pe, e, s):
    PS, nc = e.PS, e.nc
    pe.wait_ge(s.weights_loaded, 16 * len(s.loads))
    for f in range(KD):
        for k in range(KD):
            last = nc.tensor.matmul(PS[:, f, :], s.wk[:, k, f * P:(f + 1) * P], e.ctx2T[:, k, :, 0:SC],
                                    start=k == 0, stop=k == KD - 1)
        last.then_inc(s.sems["k_psum"], 1)
    pe.wait_ge(s.sems["k_ready"], KD + 1)
    for f in range(KD + 1):
        for k in range(KD):
            lhsT = s.wq[:, k, f * P:(f + 1) * P] if f < KD else s.bq_wide[:, k, :]
            last = nc.tensor.matmul(PS[:, 2 + f, :], lhsT, s.kT[:, k, :], start=k == 0, stop=k == KD - 1)
        last.then_inc(s.sems["qk_psum"], 1)
    for b in range(B):
        if b >= 2:
            pe.wait_ge(s.sems["v_ready"], b - 1)
        for k in range(KD):
            last = nc.tensor.matmul(PS[0:SC, 5 + b % 2, 0:D], e.ctx2T[:, k, b, 0:SC], s.wv[:, k, :],
                                    start=k == 0, stop=k == KD - 1)
        last.then_inc(s.sems["v_psum"], 1)
    pe.wait_ge(s.sems["setup"], 1)
    e.pe_transpose_xn(pe, s, 0)
    with pe.Fori(0, B) as i:
        pe.wait_ge(s.xnT_ready, KD * (i + 1))
        for t in range(TB):
            for k in range(KD):
                rhs = s.qk[:, k, :].rearrange("p (b s) -> p b s", s=SC)[:, bass.ds(i, 1), :]
                last = nc.tensor.matmul(PS[:, 2, t * SC:(t + 1) * SC], e.xnT[:, k, t * P:(t + 1) * P], rhs,
                                        start=k == 0, stop=k == KD - 1)
        last.then_inc(s.sems["scores"], 1)
        e.pe_transpose_xn(pe, s, i + 1)
        pe.wait_ge(s.sems["exp_ready"], i + 1)
        pe.sem_inc(e.spare, 1)
        for t in range(TB):
            last = nc.tensor.transpose(PS[0:SC, 3, t * P:(t + 1) * P], s.probs[:, t, :], e.ident)
        last.then_inc(s.sems["pT_psum"], 1)
        for t in range(TB):
            if t == 0:
                pe.wait_ge(s.sems["pT_ready"], i + 1)
                pe.sem_inc(e.spare, 1)
            if t >= 2:
                pe.wait_ge(e.x_updated, s.x_before + TB * i + t - 1)
                pe.sem_inc(e.spare, 1)
            nc.tensor.matmul(PS[:, 4 + t % 2, 0:D], s.probsT[0:SC, t, :], s.v[0:SC, bass.ds(i, 1), :],
                             start=True, stop=True).then_inc(s.sems["out_psum"], 1)


def xattn2_act(act, order, e, s):
    PS, nc = e.PS, e.nc
    act.wait_ge(s.weights_loaded, 16 * len(s.loads))
    for f in range(KD):
        act.wait_ge(s.sems["k_psum"], f + 1)
        nc.scalar.activation(s.kT[:, f, :], PS[:, f, :], ACT.Identity, bias=s.bk[:, f:f + 1]).then_inc(s.sems["k_ready"], 1)
    for f in range(KD + 1):
        act.wait_ge(s.sems["qk_psum"], f + 1)
        nc.scalar.activation(s.qk[:, f, :] if f < KD else s.qk_bias, PS[:, 2 + f, :], ACT.Copy).then_inc(s.sems["qk_ready"], 1)
    e.act_copy_xnT(act, s, 0)
    with act.Fori(0, B) as i:
        act.wait_ge(s.sems["scores"], i + 1)
        e.act_copy_xnT(act, s, i + 1)
        act.wait_ge(s.sems["shifted_ready"], i + 1)
        nc.scalar.activation(s.probs, s.sc, ACT.Exp).then_inc(s.sems["exp_ready"], 1)
        act.wait_ge(s.sems["pT_psum"], i + 1)
        nc.scalar.activation(s.probsT[0:SC, :, :], PS[0:SC, 3, :].rearrange("p (t n) -> p t n", n=P), ACT.Copy)\
            .then_inc(s.sems["pT_ready"], 1)


def xattn2_dve(dve, order, e, s):
    PS = e.PS
    dve.wait_ge(s.weights_loaded, 16 * len(s.loads))
    dve.tensor_copy(s.bq_wide, s.bq.rearrange("p (k o) -> p k o", o=1).broadcast_to([P, KD, P])).then_inc(s.sems["k_ready"], 1)
    order.mark(dve.tensor_scalar(s.keep, s.mask.bitcast(I32), 0.0, None, ALU.not_equal))
    order.settle()
    order.mark(dve.tensor_scalar(s.bias, s.keep, 1.0, 1e9, ALU.subtract, ALU.mult))
    for b in range(B):
        dve.wait_ge(s.sems["v_psum"], b + 1)
        dve.tensor_tensor(s.v[0:SC, b, :], PS[0:SC, 5 + b % 2, 0:D], s.bv[0:SC, :], ALU.add).then_inc(s.sems["v_ready"], 1)
    dve.wait_ge(s.sems["qk_ready"], KD + 1)
    dve.wait_ge(s.sems["v_ready"], B)
    dve.sem_inc(s.sems["setup"], 1)
    e.dve_layernorm(dve, order, s, 0)
    with dve.Fori(0, B) as i:
        order.turn(i, e.LN_MARKS + 7)
        dve.wait_ge(s.sems["scores"], i + 1)
        dve.wait_ge(s.sems["pT_psum"], i)
        qk_bias = s.qk_bias.rearrange("p (b s) -> p b s", s=SC)[:, bass.ds(i, 1), :].broadcast_to([P, TB, SC])
        order.mark(dve.tensor_tensor(s.sc, PS[:, 2, 0:TB * SC].rearrange("p (t s) -> p t s", s=SC), qk_bias, ALU.add))
        order.settle()
        order.mark(dve.tensor_tensor(s.sc, s.sc, s.keep, ALU.mult))
        order.settle()
        order.mark(dve.tensor_tensor(s.sc, s.sc, s.bias, ALU.add))
        order.settle()
        order.mark(dve.tensor_reduce(s.maxes, s.sc, AX_X, ALU.max))
        order.settle()
        dve.tensor_tensor(s.sc, s.sc, s.maxes.rearrange("p (t o) -> p t o", o=1).broadcast_to([P, TB, SC]), ALU.subtract)\
            .then_inc(s.sems["shifted_ready"], 1)
        e.dve_layernorm(dve, order, s, i + 1)
        dve.wait_ge(s.sems["exp_ready"], i + 1)
        order.mark(dve.tensor_reduce(s.sums, s.probs, AX_X, ALU.add))
        order.settle()
        order.mark(dve.reciprocal(s.scale, s.sums))
        order.settle()
        order.mark(dve.tensor_scalar(s.scale, s.scale, s.gate, None, ALU.mult))
        order.settle()
        for t in range(TB):
            dve.wait_ge(s.sems["out_psum"], TB * i + t + 1)
            tile = e.x_all[:, i * TB + t, :]
            dve.scalar_tensor_tensor(tile, PS[:, 4 + t % 2, 0:D], s.scale[:, t:t + 1], tile, ALU.mult, ALU.add)\
                .then_inc(e.x_updated, 1)
    order.end(B)


def xattn2_pool(pool, order, e, s):
    e.pool_rstd(pool, s, 0)
    with pool.Fori(0, B) as i:
        e.pool_rstd(pool, s, i + 1)


GATES = ("f", "i", "c")


def plan_ffn2(s, T, sem, small):
    take = s.w.take
    s.wx = [take(KD, D) for _ in GATES]
    s.wc = [take(KD, D) for _ in GATES]
    s.wo, s.uo = take(KD, D), take(KD, D)
    s.bg = take(3, KD)
    s.bo, s.c0 = take(D), take(KD)
    for g, n in enumerate(GATES):
        s.loads.append((s.wx[g], T[f"L2_ffn_w{n}"].rearrange("p (k n) -> p k n", k=KD)))
        s.loads.append((s.wc[g], T[f"L2_ffn_u{n}"].rearrange("p (k n) -> p k n", k=KD)))
        s.loads.append((s.bg[:, g, :], T[f"L2_ffn_b{n}"]))
    s.loads += [(s.wo, T["L2_ffn_wo"].rearrange("p (k n) -> p k n", k=KD)),
                (s.uo, T["L2_ffn_uo"].rearrange("p (k n) -> p k n", k=KD)),
                (s.bo, T["L2_ffn_bo"].broadcast_to([P, D])), (s.c0, T["L2_ffn_in_c"])]
    take = s.a.take
    s.cT = take(KD, S)
    s.gates = take(3, KD, S)
    s.own = take(NT, D)
    s.last = take(TB, D)
    s.sems = {n: sem(f"{s.name}_{n}") for n in (
        "added", "gate_psum", "gate_ready", "c_ready", "own_psum", "own_ready", "last_psum", "sum_ready", "tanh_ready")}
    s.looks_ahead = True
    s.pe, s.act, s.dve, s.pool = ffn2_pe, ffn2_act, ffn2_dve, ffn2_pool


def ffn2_pe(pe, e, s):
    PS, nc = e.PS, e.nc
    pe.wait_ge(s.weights_loaded, 16 * len(s.loads))
    NG = 3 * KD
    e.pe_transpose_xn(pe, s, 0)
    pe.wait_ge(s.sems["c_ready"], 1)
    with pe.Fori(0, B) as i:
        pe.wait_ge(s.xnT_ready, KD * (i + 1))
        for g in range(3):
            for m in range(KD):
                pe.wait_ge(s.sems["gate_ready"], NG * i)
                for k in range(KD):
                    nc.tensor.matmul(PS[:, 2 + KD * g + m, :], s.wx[g][:, k, m * P:(m + 1) * P], e.xnT[:, k, :],
                                     start=k == 0, stop=False)
        for t in range(TB):
            for k in range(KD):
                last = nc.tensor.matmul(PS[:, t // 2, (t % 2) * D:(t % 2 + 1) * D], e.xnT[:, k, t * P:(t + 1) * P],
                                        s.wo[:, k, :], start=k == 0, stop=k == KD - 1)
            last.then_inc(s.sems["own_psum"], 1)
        pe.wait_ge(s.sems["c_ready"], i + 1)
        for g in range(3):
            for m in range(KD):
                for k in range(KD):
                    last = nc.tensor.matmul(PS[:, 2 + KD * g + m, :], s.wc[g][:, k, m * P:(m + 1) * P], s.cT[:, k, :],
                                            start=False, stop=k == KD - 1)
                last.then_inc(s.sems["gate_psum"], 1)
        pe.wait_ge(s.sems["own_ready"], TB * (i + 1))
        e.pe_transpose_xn(pe, s, i + 1)
    pe.wait_ge(s.sems["c_ready"], B + 1)
    for t in range(TB):
        for k in range(KD):
            last = nc.tensor.matmul(PS[:, 2 + t // 2, (t % 2) * D:(t % 2 + 1) * D], s.cT[:, k, t * P:(t + 1) * P],
                                    s.uo[:, k, :], start=k == 0, stop=k == KD - 1)
    last.then_inc(s.sems["last_psum"], 1)


def ffn2_act(act, order, e, s):
    PS, nc = e.PS, e.nc
    act.wait_ge(s.weights_loaded, 16 * len(s.loads))
    e.act_copy_xnT(act, s, 0)
    NG = 3 * KD
    with act.Fori(0, B) as i:
        act.wait_ge(s.sems["c_ready"], i + 1)
        for g in range(3):
            for m in range(KD):
                act.wait_ge(s.sems["gate_psum"], NG * i + KD * g + m + 1)
                nc.scalar.activation(s.gates[:, g, m, :], PS[:, 2 + KD * g + m, :], ACT.Tanh if g == 2 else ACT.Sigmoid,
                                     bias=s.bg[:, g, m:m + 1]).then_inc(s.sems["gate_ready"], 1)
        e.act_copy_xnT(act, s, i + 1)
    with act.Fori(0, B) as i:
        act.wait_ge(s.sems["sum_ready"], i + 1)
        own = s.own[:, bass.ds(i * TB, TB), :]
        nc.scalar.activation(own, own, ACT.Tanh).then_inc(s.sems["tanh_ready"], 1)


def ffn2_dve(dve, order, e, s):
    PS = e.PS
    dve.wait_ge(s.weights_loaded, 16 * len(s.loads))
    NG = 3 * KD
    dve.tensor_copy(s.cT, s.c0.rearrange("p (k o) -> p k o", o=1).broadcast_to([P, KD, S])).then_inc(s.sems["c_ready"], 1)
    e.dve_layernorm(dve, order, s, 0)
    with dve.Fori(0, B) as i:
        order.turn(i, e.LN_MARKS + 2)
        for t in range(TB):
            dve.wait_ge(s.sems["own_psum"], TB * i + 2 * (t // 2) + 2)
            dve.tensor_tensor(s.own[:, i * TB + t, :], PS[:, t // 2, (t % 2) * D:(t % 2 + 1) * D], s.bo, ALU.add)\
                .then_inc(s.sems["own_ready"], 1)
        e.dve_layernorm(dve, order, s, i + 1)
        dve.wait_ge(s.sems["gate_ready"], NG * i + 2 * KD)
        dve.wait_ge(s.sems["c_ready"], i + 1)
        dve.wait_ge(s.sems["gate_psum"], NG * (i + 1))
        order.mark(dve.tensor_tensor(s.cT, s.cT, s.gates[:, 0, :, :], ALU.mult))
        dve.wait_ge(s.sems["gate_ready"], NG * (i + 1))
        order.mark(dve.tensor_tensor(s.gates[:, 1, :, :], s.gates[:, 1, :, :], s.gates[:, 2, :, :], ALU.mult))
        order.settle()
        dve.tensor_tensor(s.cT, s.cT, s.gates[:, 1, :, :], ALU.add).then_inc(s.sems["c_ready"], 1)
    order.end(B)
    dve.wait_ge(s.sems["own_ready"], NT)
    dve.wait_ge(s.sems["last_psum"], 1)
    order.mark(dve.tensor_copy(s.last, PS[:, 2:4, :].rearrange("p b (t d) -> p (b t) d", d=D)))
    order.settle()
    with dve.Fori(0, B) as i:
        own = s.own[:, bass.ds(i * TB, TB), :]
        dve.tensor_tensor(own, own, s.last, ALU.add).then_inc(s.sems["sum_ready"], 1)
    with dve.Fori(0, B) as i:
        dve.wait_ge(s.sems["tanh_ready"], i + 1)
        tiles = e.x_all[:, bass.ds(i * TB, TB), :]
        dve.scalar_tensor_tensor(tiles, s.own[:, bass.ds(i * TB, TB), :], s.gate, tiles, ALU.mult, ALU.add)\
            .then_inc(s.sems["added"], 1)
    dve.wait_ge(s.sems["added"], B)
    dve.sem_inc(e.x_updated, NT)


def ffn2_pool(pool, order, e, s):
    e.pool_rstd(pool, s, 0)
    with pool.Fori(0, B) as i:
        e.pool_rstd(pool, s, i + 1)


def plan_moe(s, T, sem, small):
    s.stores = True
    s.T = T
    first = W_N - 2 * E_N
    assert first >= 0 and first + NE * E_N <= 2 * W_N + A_N
    s.experts = s.mem[:, first:first + NE * E_N].rearrange("p (e n) -> p e n", e=NE)
    s.expert_loads = [(s.experts[:, (e + 2) % NE, :], T["L3_ffn_experts"][e]) for e in range(NE)]
    s.loads = s.expert_loads[:2]
    c = Carver(small, 0, MOE_N)
    s.gate_w, s.rms_w = c.take(KD, NE), c.take(D)
    s.small_loads = [(s.gate_w, T["L3_ffn_gate_w"].rearrange("p (k n) -> p k n", k=KD)),
                     (s.rms_w, T["L3_ffn_rms_w"].broadcast_to([P, D]))]
    s.mean_var, s.var_eps, s.rstd = c.take(NT, 2), c.take(NT), c.take(NT)
    s.ms, s.rrms, s.minus_half = c.take(NT), c.take(NT), c.take(NT)
    c2 = Carver(small, c.at, c.at + 2 * KE * P)
    s.hT = c.take(2, KE, P)
    s.logits, s.top = c2.take(NT, NE), c2.take(NT, 8)
    s.index = c2.take(NT, 8).bitcast(mybir.dt.uint32)
    s.pick = [c2.take(NT, NE), c2.take(NT, NE)]
    s.picked = c2.take(NT, NE)
    s.index_f = c.take(NT, 2)
    s.total, s.cum = c.take(NE, NT), c.take(NE, NT)
    s.count, s.pad, s.padcum, s.base = c.take(NE), c.take(NE), c.take(NE), c.take(NE)
    s.slot = c.take(2, NT)
    s.slot_u = c.take(2, NT).bitcast(mybir.dt.uint32)
    s.w = c.take(2, NT)
    s.tile_expert, s.tile_wrap = c.take(MOE_TILES), c.take(MOE_TILES)
    s.tile_slot = c.take(MOE_TILES).bitcast(I32)
    s.sems = {n: sem(f"{s.name}_{n}") for n in (
        "experts_loaded", "msq_ready", "rrms_ready", "y_ready", "y_kept", "logits_psum", "logits_kept",
        "residual", "residual_stored", "residual_loaded", "dispatch", "picked", "ranks_psum", "slots_ready", "exp2",
        "rowT_psum", "rowT_ready", "up_psum", "gate_psum", "silu_ready",
        "h_ready", "hT_psum", "hT_ready", "y_psum", "y_copied", "y_stored", "final")}
    s.row_loaded_s = [sem(f"{s.name}_row_loaded{n}") for n in range(2)]
    s.small_loaded_s, s.zeroed_s, s.row_scattered_s = [s.own_sem(f"{s.name}_{n}") for n in ("small_loaded", "zeroed", "row_scattered")]
    s.gathered_s = [s.own_sem(f"{s.name}_gathered{b}") for b in range(B)]
    s.early_sync_program, s.sync_program = moe_early_sync, moe_sync
    s.pe, s.act, s.dve, s.pool = moe_pe, moe_act, moe_dve, moe_pool


def moe_buffers(e, s):
    m = Names()
    flat = e.ctx2T[:, :, :, :].rearrange("p k b s -> p (k b s)")
    m.y = flat[:, 0:TB * D].rearrange("p (t d) -> p t d", d=D)
    m.residual = flat[:, TB * D:2 * TB * D].rearrange("p (t d) -> p t d", d=D)
    m.rowT = flat[:, 0:2 * D].rearrange("p (b k n) -> p b k n", k=KD, n=P)
    m.h = flat[:, 2 * D:2 * D + 2 * DE].rearrange("p (b n) -> p b n", n=DE)
    m.row, m.result = e.xn[:, 0:2, :], e.xn[:, 2:4, :]
    m.hT = s.hT
    m.gathered = s.mem[:, 0:2 * NT * D].rearrange("p (c t d) -> p c t d", c=2, d=D)
    return m


def moe_early_sync(sp, e, s):
    for dst, src in s.small_loads:
        sp.dma_start(dst, src).then_inc(s.small_loaded_s, 16)
    sp.wait_ge(e.zeros_ready, 1)
    slots = s.T["slots"].rearrange("(g t p) d -> g p t d", p=P, t=TB)
    for g in range(MOE_TILES // TB):
        sp.dma_start(slots[g], e.x_all[:, NT:NT + TB, :]).then_inc(s.zeroed_s, 16)


def moe_sync(sp, e, s):
    e.stage_start(sp, s)
    for dst, src in s.expert_loads[2:]:
        sp.dma_start(dst, src).then_inc(s.sems["experts_loaded"], 16)
    residual = s.T["residual"].rearrange("(b t p) d -> b p t d", p=P, t=TB)
    m = moe_buffers(e, s)
    with sp.Fori(0, B) as i:
        sp.wait_ge(s.sems["residual"], 2 * (i + 1))
        sp.dma_start(residual[bass.ds(i, 1)].rearrange("o p t d -> (o p) t d"), m.residual).then_inc(s.sems["residual_stored"], 16)
    sp.wait_ge(s.sems["residual_stored"], 16 * B)
    sp.wait_ge(s.row_scattered_s, 16 * 2 * NT)
    sp.dma_start(e.x_all[:, 0:NT, :], s.T["residual"].rearrange("(t p) d -> p t d", p=P)).then_inc(s.sems["residual_loaded"], 16)
    rows_in = s.T["slots"].rearrange("(j p) d -> j p d", p=P)

    def load(j, par):
        sp.dma_start(m.row[:, par, :], rows_in[bass.ds(j, 1)].rearrange("o p d -> (o p) d")).then_inc(s.row_loaded_s[par], 16)

    load(0, 0)
    load(1, 1)
    with sp.Fori(0, MOE_TILES // 2 - 1) as i:
        for par in range(2):
            j = 2 * i + 2 + par
            sp.wait_ge(s.sems["rowT_psum"], j - 1)
            load(j, par)
    out = s.T["out"].rearrange("b (t p) d -> b p t d", p=P)
    for b in range(B):
        sp.wait_ge(s.sems["final"], TB * (b + 1))
        sp.dma_start(out[b], e.x_all[:, b * TB:(b + 1) * TB, :]).then_inc(e.out_stored, 16)
    sp.wait_ge(e.out_stored, 16 * B)


def moe_pe(pe, e, s):
    PS, nc = e.PS, e.nc
    m = moe_buffers(e, s)
    pe.wait_ge(s.small_loaded_s, 32)
    with pe.Fori(0, B) as i:
        e.pe_transpose_xn(pe, s, i, src=m.y, ready=s.sems["y_ready"])
        pe.wait_ge(s.xnT_ready, KD * (i + 1))
        for t in range(TB):
            for k in range(KD):
                last = nc.tensor.matmul(PS[:, 2, t * NE:(t + 1) * NE], e.xnT[:, k, t * P:(t + 1) * P], s.gate_w[:, k, :],
                                        start=k == 0, stop=k == KD - 1)
        last.then_inc(s.sems["logits_psum"], 1)
    pe.wait_ge(s.sems["picked"], 1)
    picked = s.picked.rearrange("p t e -> p (t e)")
    nc.tensor.matmul(PS[:, 3, 0:NT * NE], e.const("before"), picked, start=True, stop=True)
    nc.tensor.matmul(PS[:, 4, 0:NT * NE], e.const("ones"), picked, start=True, stop=True).then_inc(s.sems["ranks_psum"], 1)
    pe.wait_ge(s.sems["slots_ready"], 1)
    pe.wait_ge(s.weights_loaded, 32)
    pe.wait_ge(s.sems["experts_loaded"], 16 * (NE - 2))

    def expert(j):
        return pe.value_load(s.tile_slot[0:1, bass.ds(j, 1)], min_val=0, max_val=NE - 1)

    def turn_rows(j, par, nth):
        pe.wait_ge(s.row_loaded_s[par], 16 * nth)
        pe.wait_ge(s.sems["rowT_ready"], j)
        for k in range(KD):
            last = nc.tensor.transpose(PS[:, 0, k * P:(k + 1) * P], m.row[:, par, k * P:(k + 1) * P], e.ident)
        last.then_inc(s.sems["rowT_psum"], 1)

    def widen(j, par):
        w = s.experts[:, bass.ds(expert(j), 1), :]
        pe.wait_ge(s.sems["rowT_ready"], j + 1)
        pe.wait_ge(s.sems["h_ready"], 2 * j)
        for g in range(2):
            for half in range(2):
                for k in range(KD):
                    at = (g * KD + k) * DE + half * HE
                    last = nc.tensor.matmul(PS[:, 1 + 2 * g + half, 0:HE], m.rowT[:, par, k, :], w[:, :, at:at + HE],
                                            start=k == 0, stop=k == KD - 1)
                last.then_inc(s.sems["gate_psum"] if g else s.sems["up_psum"], 1)

    def turn_hidden(j, par):
        pe.wait_ge(s.sems["h_ready"], 2 * (j + 1))
        pe.wait_ge(s.sems["hT_ready"], 2 * j)
        for n in range(KE):
            wide = min(P, DE - n * P)
            last = nc.tensor.transpose(PS[0:wide, 5 + n // 4, (n % 4) * P:(n % 4 + 1) * P],
                                       m.h[:, par, n * P:n * P + wide], e.ident)
            if n in (3, KE - 1):
                last.then_inc(s.sems["hT_psum"], 1)

    def narrow(j, par):
        w = s.experts[:, bass.ds(expert(j), 1), :]
        pe.wait_ge(s.sems["hT_ready"], 2 * (j + 1))
        pe.wait_ge(s.sems["y_copied"], j)
        for n in range(KE):
            at = 2 * KD * DE + n * D
            last = nc.tensor.matmul(PS[:, 7, 0:D], m.hT[:, par, n, :], w[:, :, at:at + D], start=n == 0, stop=n == KE - 1)
        last.then_inc(s.sems["y_psum"], 1)

    turn_rows(0, 0, 1)
    widen(0, 0)
    turn_rows(1, 1, 1)
    with pe.Fori(0, MOE_TILES // 2 - 1) as i:
        for par in (1, 0):
            j = 2 * i + (1 if par else 2)
            turn_hidden(j - 1, 1 - par)
            widen(j, par)
            turn_rows(j + 1, 1 - par, i + 2)
            narrow(j - 1, 1 - par)
    turn_hidden(MOE_TILES - 2, 0)
    widen(MOE_TILES - 1, 1)
    narrow(MOE_TILES - 2, 0)
    turn_hidden(MOE_TILES - 1, 1)
    narrow(MOE_TILES - 1, 1)


def moe_act(act, order, e, s):
    PS, nc = e.PS, e.nc
    m = moe_buffers(e, s)
    with act.Fori(0, B) as i:
        e.act_copy_xnT(act, s, i)
        act.wait_ge(s.sems["residual"], 2 * (i + 1))
        nc.scalar.activation(e.x_all[:, bass.ds(i * TB, TB), :], m.y, ACT.Copy).then_inc(s.sems["y_kept"], 1)
    act.wait_ge(s.sems["dispatch"], 1)
    nc.scalar.activation(s.w[:, 1, :], s.w[:, 1, :], ACT.Exp).then_inc(s.sems["exp2"], 1)
    act.wait_ge(s.sems["slots_ready"], 1)
    act.wait_ge(s.sems["residual_stored"], 16 * B)
    rows_out = s.T["results"].rearrange("(j p) d -> j p d", p=P)

    def copy_row(j, par):
        act.wait_ge(s.sems["rowT_psum"], j + 1)
        if not isinstance(j, int):
            act.wait_ge(s.sems["gate_psum"], 2 * (j - 1))
        nc.scalar.activation(m.rowT[:, par, :, :], PS[:, 0, 0:D].rearrange("p (k n) -> p k n", k=KD), ACT.Copy)\
            .then_inc(s.sems["rowT_ready"], 1)

    def silu(j, par):
        for half in range(2):
            act.wait_ge(s.sems["up_psum"], 2 * j + half + 1)
            if not (isinstance(j, int) and j < 2):
                act.wait_ge(s.sems["hT_psum"], 2 * (j - 1))
            nc.scalar.activation(m.h[:, par, half * HE:(half + 1) * HE], PS[:, 1 + half, 0:HE], ACT.Silu)\
                .then_inc(s.sems["silu_ready"], 1)

    def result(j, par):
        act.wait_ge(s.sems["y_psum"], j + 1)
        act.wait_ge(s.sems["y_stored"], 16 * j)
        nc.scalar.activation(m.result[:, par, :], PS[:, 7, 0:D], ACT.Copy).then_inc(s.sems["y_copied"], 1)
        act.wait_ge(s.sems["y_copied"], j + 1)
        act.dma_start(rows_out[bass.ds(j, 1)].rearrange("o p d -> (o p) d"), m.result[:, par, :]).then_inc(s.sems["y_stored"], 16)

    copy_row(0, 0)
    silu(0, 0)
    copy_row(1, 1)
    with act.Fori(0, MOE_TILES // 2 - 1) as i:
        for par in (1, 0):
            j = 2 * i + (1 if par else 2)
            silu(j, par)
            copy_row(j + 1, 1 - par)
            result(j - 1, 1 - par)
    silu(MOE_TILES - 1, 1)
    result(MOE_TILES - 2, 0)
    result(MOE_TILES - 1, 1)


def moe_dve(dve, order, e, s):
    PS = e.PS
    m = moe_buffers(e, s)
    dve.wait_ge(s.small_loaded_s, 32)
    with dve.Fori(0, B) as i:
        order.turn(i, 2 * TB + 1)
        for t in range(TB):
            order.mark(dve.bn_stats(e.stats[:, t, :], e.x_all[:, i * TB + t, :]))
        order.settle()
        dve.sem_inc(e.spare, 1)
        for t in range(TB):
            order.mark(dve.bn_aggr(e.mean_var[:, t, :], e.stats[:, t, :]))
        order.settle()
        order.mark(dve.tensor_copy(s.mean_var[:, bass.ds(i * TB, TB), :], e.mean_var[:]))
    order.end(B)
    order.settle()
    dve.tensor_scalar(s.var_eps, s.mean_var[:, :, 1], LN_EPS, None, ALU.add).then_inc(s.var_ready, 1)
    dve.wait_ge(s.rstd_ready, 1)
    order.mark(dve.tensor_tensor(s.ms, s.rstd, s.rstd, ALU.mult))
    order.settle()
    order.mark(dve.tensor_tensor(s.ms, s.ms, s.mean_var[:, :, 1], ALU.mult))
    order.settle()
    dve.tensor_scalar(s.ms, s.ms, 1e-6, None, ALU.add).then_inc(s.sems["msq_ready"], 1)
    dve.wait_ge(s.sems["rrms_ready"], 1)
    with dve.Fori(0, B) as i:
        dve.wait_ge(s.sems["residual"], 2 * i)
        for t in range(TB):
            at = i * TB + t
            dve.tensor_scalar(e.xn[:, t, :], e.x_all[:, at, :], s.mean_var[:, bass.ds(at, 1), 0], s.rstd[:, bass.ds(at, 1)],
                              ALU.subtract, ALU.mult).then_inc(s.ln_ready, 1)
        dve.wait_ge(s.ln_ready, TB * (i + 1))
        dve.wait_ge(s.sems["y_kept"], i)
        dve.wait_ge(s.xnT_psum, KD * i)
        dve.sem_inc(e.spare, 1)
        for t in range(TB):
            dve.scalar_tensor_tensor(m.y[:, t, :], e.xn[:, t, :], s.rrms[:, bass.ds(i * TB + t, 1)], s.rms_w, ALU.mult, ALU.mult)\
                .then_inc(s.sems["y_ready"], 1)
        dve.wait_ge(s.sems["logits_psum"], i + 1)
        dve.tensor_copy(s.logits[:, bass.ds(i * TB, TB), :], PS[:, 2, 0:TB * NE].rearrange("p (t e) -> p t e", e=NE))\
            .then_inc(s.sems["logits_kept"], 1)
    dve.wait_ge(s.sems["logits_kept"], B)

    def step(ins):
        order.mark(ins)
        order.settle()

    def wide(ap, axis, shape):
        return ap.rearrange("p (o a) -> p o a" if axis == 0 else "p (a o) -> p a o", o=1).broadcast_to(shape)

    for t in range(NT):
        order.mark(dve.max(s.top[:, t, :], s.logits[:, t, :]))
    order.settle()
    for t in range(NT):
        order.mark(dve.max_index(s.index[:, t, :], s.top[:, t, :], s.logits[:, t, :]))
    order.settle()
    dve.tensor_tensor(s.w[:, 1, :], s.top[:, :, 1], s.top[:, :, 0], ALU.subtract).then_inc(s.sems["dispatch"], 1)
    step(dve.tensor_copy(s.index_f, s.index[:, :, 0:2]))
    for c in range(2):
        step(dve.tensor_tensor(s.pick[c], wide(e.const("expert"), 0, [P, NT, NE]),
                               wide(s.index_f[:, :, c], 1, [P, NT, NE]), ALU.is_equal))
    dve.tensor_tensor(s.picked, s.pick[0], s.pick[1], ALU.add).then_inc(s.sems["picked"], 1)
    dve.wait_ge(s.sems["ranks_psum"], 1)
    step(dve.tensor_copy(s.total, PS[:, 4, 0:NT * NE].rearrange("p (t e) -> p e t", e=NE)))
    flat = s.total.rearrange("p e t -> p (e t)")
    step(dve.tensor_tensor_scan(s.cum.rearrange("p e t -> p (e t)"), flat, flat, 0.0, ALU.add, ALU.max))
    step(dve.tensor_tensor(s.count, s.cum[:, :, NT - 1], s.cum[:, :, 0], ALU.subtract))
    step(dve.tensor_tensor(s.count, s.count, s.total[:, :, 0], ALU.add))
    step(dve.tensor_tensor(s.cum, s.cum, s.total, ALU.subtract))
    step(dve.tensor_scalar(s.pad.bitcast(I32), s.count, P - 1.0, None, ALU.add))
    step(dve.tensor_scalar(s.pad.bitcast(I32), s.pad.bitcast(I32), 7, 7, ALU.logical_shift_right, ALU.logical_shift_left))
    step(dve.tensor_copy(s.count, s.pad.bitcast(I32)))
    step(dve.tensor_tensor_scan(s.padcum, s.count, s.count, 0.0, ALU.add, ALU.max))
    step(dve.tensor_tensor(s.base, s.padcum, s.count, ALU.subtract))
    step(dve.tensor_tensor(s.base, s.base, s.cum[:, :, 0], ALU.subtract))
    step(dve.tensor_tensor(s.cum, s.cum, wide(s.base, 1, [P, NE, NT]), ALU.add))
    step(dve.tensor_tensor(s.picked, PS[:, 3, 0:NT * NE].rearrange("p (t e) -> p t e", e=NE),
                           s.cum.rearrange("p e t -> p t e"), ALU.add))
    for c in range(2):
        step(dve.tensor_tensor(s.pick[c], s.pick[c], s.picked, ALU.mult))
        step(dve.tensor_reduce(s.slot[:, c, :], s.pick[c], AX_X, ALU.add))
    step(dve.tensor_copy(s.slot_u, s.slot))
    step(dve.memset(s.tile_expert, 0.0))
    for x in range(NE - 1):
        step(dve.scalar_tensor_tensor(s.tile_expert, e.const("slot_start"), s.padcum[:, x:x + 1], s.tile_expert,
                                      ALU.is_ge, ALU.add))
    step(dve.tensor_scalar(s.tile_wrap, s.tile_expert, NE - 2.0, -float(NE), ALU.is_ge, ALU.mult))
    step(dve.scalar_tensor_tensor(s.tile_expert, s.tile_expert, 2.0, s.tile_wrap, ALU.add, ALU.add))
    step(dve.tensor_copy(s.tile_slot, s.tile_expert))
    dve.wait_ge(s.sems["exp2"], 1)
    step(dve.tensor_scalar(s.w[:, 0, :], s.w[:, 1, :], 1.0, None, ALU.add))
    step(dve.reciprocal(s.w[:, 0, :], s.w[:, 0, :]))
    step(dve.tensor_tensor(s.w[:, 1, :], s.w[:, 1, :], s.w[:, 0, :], ALU.mult))
    step(dve.tensor_scalar(s.w, s.w, s.gate, None, ALU.mult))
    dve.memset(m.hT[DE % P:P, :, KE - 1, :], 0.0).then_inc(s.sems["slots_ready"], 1)

    def multiply(j, par):
        for half in range(2):
            dve.wait_ge(s.sems["gate_psum"], 2 * j + half + 1)
            dve.wait_ge(s.sems["silu_ready"], 2 * j + half + 1)
            h = m.h[:, par, half * HE:(half + 1) * HE]
            dve.tensor_tensor(h, PS[:, 3 + half, 0:HE], h, ALU.mult).then_inc(s.sems["h_ready"], 1)

    def copy_hidden(j, par):
        dve.wait_ge(s.sems["y_psum"], j)
        dve.wait_ge(s.sems["hT_psum"], 2 * j + 1)
        dve.tensor_copy(m.hT[:, par, 0:4, :], PS[:, 5, :].rearrange("p (n t) -> p n t", t=P)).then_inc(s.sems["hT_ready"], 1)
        dve.wait_ge(s.sems["hT_psum"], 2 * j + 2)
        dve.tensor_copy(m.hT[:, par, 4, :], PS[:, 6, 0:P]).then_inc(e.spare, 1)
        dve.tensor_copy(m.hT[0:DE % P, par, 5, :], PS[0:DE % P, 6, P:2 * P]).then_inc(s.sems["hT_ready"], 1)

    multiply(0, 0)
    with dve.Fori(0, MOE_TILES // 2 - 1) as i:
        for par in (1, 0):
            j = 2 * i + (1 if par else 2)
            copy_hidden(j - 1, 1 - par)
            multiply(j, par)
    copy_hidden(MOE_TILES - 2, 0)
    multiply(MOE_TILES - 1, 1)
    copy_hidden(MOE_TILES - 1, 1)

    dve.wait_ge(s.sems["residual_loaded"], 16)
    for b in range(B):
        dve.wait_ge(s.gathered_s[b], 16 * 2 * TB)
        for c in range(2):
            for t in range(b * TB, (b + 1) * TB):
                tile = e.x_all[:, t, :]
                ins = dve.scalar_tensor_tensor(tile, m.gathered[:, c, t, :], s.w[:, c, t:t + 1], tile, ALU.mult, ALU.add)
                if c == 0:
                    order.mark(ins)
                else:
                    ins.then_inc(s.sems["final"], 1)
            if c == 0:
                order.settle()


def moe_pool(pool, order, e, s):
    nc = e.nc
    m = moe_buffers(e, s)
    gate = s.gate.rearrange("p (o d) -> p o d", o=1).broadcast_to([P, TB, D])
    nc.gpsimd.memset(s.minus_half, -0.5).then_inc(e.pool_order, 1)
    order.k += 1
    order.settle()
    pool.wait_ge(s.var_ready, 1)
    nc.gpsimd.tensor_tensor(s.rstd, s.var_eps, s.minus_half, ALU.pow).then_inc(s.rstd_ready, 1)
    pool.wait_ge(s.sems["msq_ready"], 1)
    nc.gpsimd.tensor_tensor(s.rrms, s.ms, s.minus_half, ALU.pow).then_inc(s.sems["rrms_ready"], 1)
    with pool.Fori(0, B) as i:
        pool.wait_ge(s.ln_ready, TB * (i + 1))
        pool.wait_ge(s.sems["residual_stored"], 16 * i)
        nc.gpsimd.tensor_tensor(m.residual, e.xn[:], gate, ALU.mult).then_inc(s.sems["residual"], 1)
        pool.wait_ge(s.sems["residual"], 2 * i + 1)
        nc.gpsimd.tensor_tensor(m.residual, m.residual, e.x_all[:, bass.ds(i * TB, TB), :], ALU.add).then_inc(s.sems["residual"], 1)
    pool.wait_ge(s.sems["slots_ready"], 1)
    pool.wait_ge(s.sems["y_kept"], B)
    pool.wait_ge(s.zeroed_s, 16 * MOE_TILES // TB)
    for t in range(NT):
        for c in range(2):
            nc.gpsimd.indirect_dma_start(s.T["slots"], bass.IndirectOffsetOnAxis(s.slot_u[:, c, t:t + 1], 0),
                                         e.x_all[:, t, :], None).then_inc(s.row_scattered_s, 16)
    pool.wait_ge(s.sems["y_stored"], 16 * MOE_TILES)
    for t in range(NT):
        for c in range(2):
            nc.gpsimd.indirect_dma_start(m.gathered[:, c, t, :], None, s.T["results"],
                                         bass.IndirectOffsetOnAxis(s.slot_u[:, c, t:t + 1], 0))\
                .then_inc(s.gathered_s[t // TB], 16)


CH, CD = 8, 64
CT = CH * CD // P
CV = CD + 1
NQ = 256
QT = NQ // P
ROUTE_STEPS = 50
ROUTE_TURN = ROUTE_STEPS // (B // 2)
ROUTE_K = NQ * 9 / 8
NR = B * NQ


def plan_colt(s, T, sem, small):
    s.T = T
    take = s.w.take
    s.wq, s.wk, s.wv, s.wo, s.gamma = [], [], [], [], []
    for part in ("light", "heavy"):
        for lst, n in ((s.wq, "wq"), (s.wk, "wk"), (s.wv, "wv")):
            w = take(KD, CH * CD)
            lst.append(w)
            s.loads.append((w, T[f"L0_ffn_{n}_{part}"].rearrange("p (k n) -> p k n", k=KD)))
        w = take(CT, D)
        s.wo.append(w)
        s.loads.append((w, T[f"L0_ffn_wo_{part}"].rearrange("p (k n) -> p k n", k=CT)))
        g = take(KD)
        s.gamma.append(g)
        s.loads.append((g, T[f"L0_ffn_gamma_{part}"]))
    s.token = take(D)
    s.loads.append((s.token, T["L0_ffn_q_routing_token"].broadcast_to([P, D])))
    take = s.a.take
    s.kTz = take(CH, S)
    s.v = take(TB, CH, CV)
    at = s.a.at
    s.qT = take(CT, S)
    s.shifted, s.probs, s.probsT = take(2, S), take(2, S), take(2, S)
    s.o, s.oT = take(2, CH * CD), take(2, CT, P)
    c = Carver(s.mem, at, s.a.end)
    s.hq_rows, s.hxT = c.take(QT, D), c.take(KD, NQ)
    s.hqT = c.take(CT, NQ)
    s.hprobs, s.hprobsT = c.take(2, S), c.take(2, S)
    s.ho, s.hoT = c.take(QT, CH * CD), c.take(QT, CT, P)
    s.hy = c.take(QT, D)
    s.a.at = max(c.at, s.a.at)
    s.back = s.a.take(TB, D)
    s.earlier = s.a.take(TB, S)
    s.loads.append((s.earlier, T["table_earlier"].rearrange("p (t j) -> p t j", t=TB)))
    s.row_scores = s.mem[:, W_N - NT * P:W_N]
    s.forth = s.back, s.mem[:, W_N - NT * P - TB * D:W_N - NT * P].rearrange("p (t d) -> p t d", d=D)
    c = Carver(small, 0, MOE_N)
    s.mean_var, s.var_eps, s.rstd = c.take(NT, 2), c.take(NT), c.take(NT)
    s.sumsq, s.rnorm, s.scale, s.norm = c.take(NT), c.take(NT), c.take(NT), c.take(NT)
    s.minus_half = c.take(NT)
    s.dots, s.dots_of_pair = c.take(NT), c.take(2 * TB)
    s.s, s.e, s.e_min, s.per_k = c.take(S), c.take(S), c.take(S), c.take(1)
    s.shift, s.limit, s.low, s.raise_, s.log = c.take(1), c.take(2), c.take(1), c.take(1), c.take(1)
    s.score, s.rank, s.over = c.take(NT), c.take(NT), c.take(NT)
    s.to_u, s.from_u = c.take(NT).bitcast(mybir.dt.uint32), c.take(NT).bitcast(mybir.dt.uint32)
    s.from_f = c.take(NT)
    s.junk2 = c.take(2, S)
    s.junk4 = s.junk2.rearrange("p a (b d) -> p (a b) d", d=D)
    s.maxes, s.recip = c.take(2, CH), c.take(2, CH)
    s.sems = {n: sem(f"{s.name}_{n}") for n in (
        "setup", "sumsq_ready", "rnorm_ready", "unit_ready", "unit_stored0", "unit_stored1", "dots_ready", "cd_psum",
        "shifted", "cd_exp", "cd_final", "cd_log", "cd_u", "score_row", "score_psum", "score_ready", "score_stored", "scores_spread", "slots_ready",
        "forth_loaded0", "forth_loaded1", "zero_rows", "results_stored", "light_done", "light_x", "merged")}
    s.scattered_s = [s.own_sem(f"{s.name}_scattered{h}") for h in range(2)]
    s.gathered_s = s.own_sem(f"{s.name}_gathered")
    s.parts = []
    for part in ("light", "heavy"):
        heavy = part == "heavy"
        names = ("loaded", "xT_psum", "xT_ready", "proj_psum", "k_ready", "v_ready", "q_ready", "scores", "shifted_ready",
                  "exp_ready", "pT_psum", "pT_ready", "pv_psum", "o_ready", "oT_psum", "oT_ready", "y_psum")\
            + (("q_loaded", "qx_psum", "qx_ready", "y_ready") if heavy else ())
        p = Names()
        p.heavy, p.sems = heavy, {n: sem(f"{s.name}_{part}_{n}") for n in names}
        s.parts.append(p)
    s.sync_program = colt_sync
    s.pe, s.act, s.dve, s.pool = colt_pe, colt_act, colt_dve, colt_pool


AHEAD_KEYS = ((), (0,), (1,), (2, 3))


def unit_buffers(e):
    return e.xn[:], e.xnT[:].rearrange("p k s -> p (k s)").rearrange("p (t d) -> p t d", d=D)


def colt_sync(sp, e, s):
    units = s.T["unit_rows"].rearrange("(b t p) d -> b p t d", p=P, t=TB)
    light, heavy = s.parts
    e.stage_start(sp, s)
    with sp.Fori(0, B // 2) as j:
        for h, unit in enumerate(unit_buffers(e)):
            sp.wait_ge(s.sems["unit_ready"], TB * (2 * j + h + 1))
            sp.sem_inc(e.spare, 1)
            sp.dma_start(units[bass.ds(2 * j + h, 1)].rearrange("o p t d -> (o p) t d"), unit)\
                .then_inc(s.sems[f"unit_stored{h}"], 16)
    for h in range(2):
        sp.wait_ge(s.sems[f"unit_stored{h}"], 16 * B // 2)
    sp.wait_ge(s.sems["dots_ready"], 1)
    for r in range(NR // (TB * P)):
        sp.dma_start(s.T["routed_out"][r * TB * P:(r + 1) * TB * P, :].rearrange("(t p) d -> p t d", p=P),
                     e.x_all[:, NT:NT + TB, :]).then_inc(s.sems["zero_rows"], 16)
    sp.dma_start(s.T["routed_out"][NR:NR + P, :], e.x_all[:, NT, :]).then_inc(s.sems["zero_rows"], 16)

    def load_rows(p, batch):
        sp.dma_start(e.xn[:], units[bass.ds(batch, 1)].rearrange("o p t d -> (o p) t d")).then_inc(p.sems["loaded"], 16)

    with sp.Fori(0, B // 2 + 1) as i:
        sp.wait_ge(light.sems["xT_psum"], KD * i)
        load_rows(light, i)
    sp.wait_ge(s.sems["score_row"], 1)
    sp.dma_start(s.T["row_scores"].rearrange("(b n) -> b n", b=B), s.e_min[0:B, :]).then_inc(s.sems["score_stored"], 16)
    sp.wait_ge(s.sems["score_stored"], 16)
    sp.dma_start(s.row_scores, s.T["row_scores"].rearrange("(o n) -> o n", o=1).broadcast_to([P, B * S]))\
        .then_inc(s.sems["scores_spread"], 16)
    with sp.Fori(B // 2 + 1, B) as i:
        sp.wait_ge(light.sems["xT_psum"], KD * i)
        load_rows(light, i)
    routed = s.T["routed_in"].rearrange("(b t p) d -> b p t d", p=P, t=QT)
    out = s.T["routed_out"][0:NR, :].rearrange("(b t p) d -> b p t d", p=P, t=QT)

    def load_routed(batch):
        sp.dma_start(s.hq_rows, routed[bass.ds(batch, 1)].rearrange("o p t d -> (o p) t d")).then_inc(heavy.sems["q_loaded"], 16)

    def store(batch):
        sp.dma_start(out[bass.ds(batch, 1)].rearrange("o p t d -> (o p) t d"), s.hy).then_inc(s.sems["results_stored"], 16)

    for b in range(B):
        if b >= 2:
            sp.wait_ge(s.scattered_s[b % 2], 16 * TB * (b // 2))
        sp.dma_start(s.forth[b % 2], units[b]).then_inc(s.sems[f"forth_loaded{b % 2}"], 16)
    sp.wait_ge(light.sems["xT_psum"], KD * B)
    load_rows(heavy, B - 1)
    sp.wait_ge(s.sems["light_done"], 1)
    for h in range(2):
        sp.wait_ge(s.scattered_s[h], 16 * NT // 2)
    load_routed(B - 1)
    sp.wait_ge(s.sems["zero_rows"], 16 * (NR // (TB * P) + 1))
    with sp.Fori(0, B - 1) as i:
        sp.wait_ge(heavy.sems["xT_psum"], KD * (i + 1))
        sp.sem_inc(e.spare, 1)
        load_rows(heavy, B - 2 - i)
        sp.wait_ge(heavy.sems["qx_psum"], i + 1)
        sp.sem_inc(e.spare, 1)
        load_routed(B - 2 - i)
        sp.wait_ge(heavy.sems["y_ready"], QT * (i + 1))
        sp.sem_inc(e.spare, 1)
        store(B - 1 - i)
    sp.wait_ge(heavy.sems["y_ready"], QT * B)
    store(0)


def colt_pe(pe, e, s):
    PS, nc = e.PS, e.nc
    pe.wait_ge(s.sems["setup"], 1)
    light, heavy = s.parts

    def product(p, i, c):
        w, kind, n = (1 if p.heavy else 0), c // CT, c % CT
        if c >= 6:
            pe.wait_ge(p.sems["k_ready"] if c - 6 < CT else p.sems["v_ready"], CT * i + (c - 6) % CT + 1)
        if kind == 2 and n == 0 and p.heavy:
            pe.wait_ge(p.sems["qx_ready"], i + 1)
        for k in range(KD):
            if kind == 0:
                lhsT, rhs = s.wk[w][:, k, n * P:(n + 1) * P], e.xnT[:, k, :]
            elif kind == 1:
                lhsT, rhs = e.xnT[:, k, n * P:(n + 1) * P], s.wv[w][:, k, :]
            else:
                lhsT, rhs = s.wq[w][:, k, n * P:(n + 1) * P], (s.hxT if p.heavy else e.xnT)[:, k, :]
            wide = NQ if p.heavy and kind == 2 else S
            last = nc.tensor.matmul(PS[:, 2 + c % 6, 0:wide], lhsT, rhs, start=k == 0, stop=k == KD - 1)
        last.then_inc(p.sems["proj_psum"], 1)

    def project_first(p, i, after):
        if after == 0:
            pe.wait_ge(p.sems["loaded"], 16 * (i + 1))
            for k in range(KD):
                for t in range(TB):
                    last = nc.tensor.transpose(PS[:, 2 + k, t * P:(t + 1) * P], e.xn[:, t, k * P:(k + 1) * P], e.ident)
                last.then_inc(p.sems["xT_psum"], 1)
        if after == 1:
            pe.wait_ge(p.sems["xT_ready"], KD * (i + 1))
        for c in AHEAD_KEYS[after]:
            product(p, i, c)

    def project_rest(p, i):
        if p.heavy:
            pe.wait_ge(p.sems["oT_ready"], QT * i)
            pe.wait_ge(p.sems["y_ready"], QT * i)
            pe.wait_ge(p.sems["q_loaded"], 16 * (i + 1))
            for k in range(KD):
                for t in range(QT):
                    last = nc.tensor.transpose(PS[:, 0, (k * QT + t) * P:(k * QT + t + 1) * P],
                                               s.hq_rows[:, t, k * P:(k + 1) * P], e.ident)
            last.then_inc(p.sems["qx_psum"], 1)
        else:
            pe.wait_ge(p.sems["oT_ready"], TB * i)
            pe.wait_ge(s.sems["light_x"], TB * i)
        for c in range(CT, 3 * CT):
            product(p, i, c)
        pe.wait_ge(p.sems["q_ready"], CT * (i + 1))
        pe.wait_ge(p.sems["k_ready"], CT * (i + 1))
        pe.wait_ge(p.sems["v_ready"], TB * (i + 1))

    def turn_probs(p, n, u, probs):
        pe.wait_ge(p.sems["exp_ready"], n + u + 1)
        if u >= 2:
            pe.wait_ge(p.sems["pT_ready"], n + u - 1)
        for j in range(4):
            last = nc.tensor.transpose(PS[:, 4 + u % 2, j * P:(j + 1) * P], probs[:, u % 2, j * P:(j + 1) * P], e.ident)
        last.then_inc(p.sems["pT_psum"], 1)

    def project_out(p, n, t, o, oT, step):
        if step == 0:
            for k in range(CT):
                last = nc.tensor.transpose(PS[:, 0, k * P:(k + 1) * P], o[:, t % 2, k * P:(k + 1) * P], e.ident)
            last.then_inc(p.sems["oT_psum"], 1)
        else:
            pe.wait_ge(p.sems["oT_ready"], n + t + 1)
            for k in range(CT):
                last = nc.tensor.matmul(PS[:, 1, 0:D], oT[:, t % 2, k, :], s.wo[1 if p.heavy else 0][:, k, :],
                                        start=k == 0, stop=k == CT - 1)
            last.then_inc(p.sems["y_psum"], 1)

    def light_batch(i, ahead=True):
        p, n = light, 2 * TB * i
        project_rest(p, i)
        for step in range(2 * TB + 4):
            if step < 2 * TB:
                u, t, g = step, step // 2, step % 2
                if u >= 2:
                    pe.wait_ge(p.sems["shifted_ready"], n + u - 1)
                for j in range(4):
                    h = 4 * g + j
                    last = nc.tensor.matmul(PS[:, 2 + u % 2, j * P:(j + 1) * P], s.qT[:, h // 2, t * P:(t + 1) * P],
                                            s.kTz[:, h, t * P:(t + 1) * P], start=True, stop=True)
                last.then_inc(p.sems["scores"], 1)
            if 1 <= step < 2 * TB + 1:
                turn_probs(p, n, step - 1, s.probs)
            if 2 <= step < 2 * TB + 2:
                u = step - 2
                pe.wait_ge(p.sems["pT_ready"], n + u + 1)
                if u >= 2:
                    pe.wait_ge(p.sems["o_ready"], n + u - 1)
                for j in range(4):
                    last = nc.tensor.matmul(PS[:, 6 + u % 2, j * CV:(j + 1) * CV], s.probsT[:, u % 2, j * P:(j + 1) * P],
                                            s.v[:, u // 2, 4 * (u % 2) + j, :], start=True, stop=True)
                last.then_inc(p.sems["pv_psum"], 1)
            if step >= 4 and step % 2 == 0:
                t = (step - 4) // 2
                pe.wait_ge(p.sems["o_ready"], n + 2 * (t + 1))
                pe.wait_ge(p.sems["oT_ready"], TB * i + t)
                project_out(p, TB * i, t, s.o, s.oT, 0)
            if step >= 5 and step % 2 == 1:
                t = (step - 5) // 2
                pe.wait_ge(s.sems["light_x"], TB * i + t)
                project_out(p, TB * i, t, s.o, s.oT, 1)
            if ahead and step >= 2 * TB:
                project_first(p, i + 1, step - 2 * TB)

    pe.wait_ge(s.sems["dots_ready"], 1)
    for t in range(TB):
        last = nc.tensor.transpose(PS[0:B, 2, t * P:(t + 1) * P], s.dots.rearrange("p (b t) -> p t b", t=TB)[:, t, :], e.ident)
    last.then_inc(s.sems["cd_psum"], 1)
    pe.wait_ge(s.sems["shifted"], 1)
    for after in range(len(AHEAD_KEYS)):
        project_first(light, 0, after)
    with pe.Fori(0, B // 2) as i:
        light_batch(i)
    pe.wait_ge(s.sems["score_row"], 1)
    for t in range(TB):
        last = nc.tensor.transpose(PS[:, 7, t * B:(t + 1) * B], s.e_min[0:B, t * P:(t + 1) * P], e.ident[0:B, 0:B])
    last.then_inc(s.sems["score_psum"], 1)
    pe.wait_ge(s.sems["score_ready"], 1)
    with pe.Fori(B // 2, B - 1) as i:
        light_batch(i)
    light_batch(B - 1, ahead=False)
    pe.wait_ge(light.sems["o_ready"], 2 * TB * B)
    pe.wait_ge(s.sems["light_x"], NT)

    def heavy_batch(i, ahead=True):
        p, n = heavy, QT * CH * i
        project_rest(p, i)
        for step in range(QT * CH + 4):
            if step < QT * CH:
                u, t, h = step, step // CH, step % CH
                if u >= 2:
                    pe.wait_ge(p.sems["exp_ready"], n + u - 1)
                nc.tensor.matmul(PS[:, 2 + u % 2, :], s.hqT[:, h // 2, t * P:(t + 1) * P], s.kTz[:, h, :],
                                 start=True, stop=True).then_inc(p.sems["scores"], 1)
            if 1 <= step < QT * CH + 1:
                turn_probs(p, n, step - 1, s.hprobs)
            if 2 <= step < QT * CH + 2:
                u = step - 2
                t, h = u // CH, u % CH
                pe.wait_ge(p.sems["pT_ready"], n + u + 1)
                if h % 4 == 0:
                    pe.wait_ge(p.sems["o_ready"], (QT * i + t) * 2 + max(h // 4 - 1, 0) if t or h else QT * i * 2)
                for j in range(4):
                    last = nc.tensor.matmul(PS[:, 6 + h // 4, (h % 4) * CV:(h % 4 + 1) * CV],
                                            s.hprobsT[:, u % 2, j * P:(j + 1) * P], s.v[:, j, h, :], start=j == 0, stop=j == 3)
                last.then_inc(p.sems["pv_psum"], 1)
            for t in range(QT):
                if step == (t + 1) * CH + 2:
                    pe.wait_ge(p.sems["o_ready"], 2 * (QT * i + t + 1))
                    pe.wait_ge(p.sems["oT_ready"], QT * i + t)
                    project_out(p, QT * i, t, s.ho, s.hoT, 0)
                if step == (t + 1) * CH + 3:
                    pe.wait_ge(p.sems["y_ready"], QT * i + t)
                    project_out(p, QT * i, t, s.ho, s.hoT, 1)
            if ahead and step >= QT * CH:
                project_first(p, i + 1, step - QT * CH)

    for after in range(len(AHEAD_KEYS)):
        project_first(heavy, 0, after)
    with pe.Fori(0, B - 1) as i:
        heavy_batch(i)
    heavy_batch(B - 1, ahead=False)


def colt_act(act, order, e, s):
    PS, nc = e.PS, e.nc
    light, heavy = s.parts

    def copy_xT(p, i):
        for k in range(KD):
            act.wait_ge(p.sems["xT_psum"], KD * i + k + 1)
            nc.scalar.activation(e.xnT[:, k, :], PS[:, 2 + k, :], ACT.Copy).then_inc(p.sems["xT_ready"], 1)

    def project(p, i):
        if p.heavy:
            act.wait_ge(p.sems["qx_psum"], i + 1)
            nc.scalar.activation(s.hxT, PS[:, 0, :].rearrange("p (k n) -> p k n", k=KD), ACT.Copy).then_inc(p.sems["qx_ready"], 1)
        for t in range(TB):
            act.wait_ge(p.sems["proj_psum"], 3 * CT * i + CT + t + 1)
            nc.scalar.activation(s.v[:, t, :, 0:CD], PS[:, 2 + (CT + t) % 6, :].rearrange("p (h d) -> p h d", d=CD), ACT.Copy)\
                .then_inc(p.sems["v_ready"], 1)
        for m in range(CT):
            act.wait_ge(p.sems["proj_psum"], 3 * CT * i + 2 * CT + m + 1)
            q, wide = (s.hqT, NQ) if p.heavy else (s.qT, S)
            nc.scalar.activation(q[:, m, :], PS[:, 2 + (2 * CT + m) % 6, 0:wide], ACT.Copy).then_inc(p.sems["q_ready"], 1)

    def copy_oT(p, n, t, oT):
        act.wait_ge(p.sems["oT_psum"], n + t + 1)
        act.wait_ge(p.sems["y_psum"], n + max(t - 1, 0))
        nc.scalar.activation(oT[:, t % 2, :, :], PS[:, 0, :].rearrange("p (k n) -> p k n", k=CT), ACT.Copy).then_inc(p.sems["oT_ready"], 1)

    def shifted_exp(n):
        act.wait_ge(s.sems["shifted"], n)
        nc.scalar.activation(s.e[0:B, :], s.s[0:B, :], ACT.Exp, bias=s.shift[0:B, :]).then_inc(s.sems["cd_exp"], 1)

    shifted_exp(1)
    nc.scalar.activation(s.limit[0:B, 0:1], s.shift[0:B, :], ACT.Exp).then_inc(s.sems["cd_exp"], 1)

    def light_batch(i, routing, ahead=True):
        p, n = light, 2 * TB * i
        project(p, i)
        for step in range(2 * TB + 4):
            if routing and step % (ROUTE_TURN // 2 + 1) == 0:
                shifted_exp(2 * i + 2 + step // (ROUTE_TURN // 2 + 1))
            if step < 2 * TB:
                u = step
                act.wait_ge(p.sems["shifted_ready"], n + u + 1)
                if u >= 2:
                    act.wait_ge(p.sems["pT_psum"], n + u - 1)
                nc.scalar.activation(s.probs[:, u % 2, :], s.shifted[:, u % 2, :], ACT.Exp).then_inc(p.sems["exp_ready"], 1)
            if 1 <= step < 2 * TB + 1:
                u = step - 1
                act.wait_ge(p.sems["pT_psum"], n + u + 1)
                if u >= 2:
                    act.wait_ge(p.sems["pv_psum"], n + u - 1)
                nc.scalar.activation(s.probsT[:, u % 2, :], PS[:, 4 + u % 2, :], ACT.Copy).then_inc(p.sems["pT_ready"], 1)
            if step >= 4 and step % 2 == 0:
                copy_oT(p, TB * i, (step - 4) // 2, s.oT)
            if ahead and step == 2 * TB + 1:
                copy_xT(p, i + 1)

    copy_xT(light, 0)
    with act.Fori(0, B // 2) as i:
        light_batch(i, True)
    act.wait_ge(s.sems["cd_final"], 1)
    nc.scalar.activation(s.log[0:B, :], s.limit[0:B, 0:1], ACT.Ln).then_inc(s.sems["cd_log"], 1)
    act.wait_ge(s.sems["cd_u"], 1)
    nc.scalar.activation(s.e_min[0:B, :], s.e[0:B, :], ACT.Exp).then_inc(s.sems["score_row"], 1)
    with act.Fori(B // 2, B - 1) as i:
        light_batch(i, False)
    light_batch(B - 1, False, ahead=False)

    def heavy_batch(i, ahead=True):
        p, n = heavy, QT * CH * i
        project(p, i)
        for step in range(QT * CH + 4):
            if step < QT * CH:
                u = step
                act.wait_ge(p.sems["shifted_ready"], n + u + 1)
                if u >= 2:
                    act.wait_ge(p.sems["pT_psum"], n + u - 1)
                nc.scalar.activation(s.hprobs[:, u % 2, :], PS[:, 2 + u % 2, :], ACT.Exp, bias=s.maxes[:, 0, u % 2:u % 2 + 1])\
                    .then_inc(p.sems["exp_ready"], 1)
            for t in range(QT):
                if step == (t + 1) * CH + 2:
                    copy_oT(p, QT * i, t, s.hoT)
                if step == (t + 1) * CH + 3:
                    act.wait_ge(p.sems["y_psum"], QT * i + t + 1)
                    act.wait_ge(s.sems["results_stored"], 16 * i)
                    nc.scalar.activation(s.hy[:, t, :], PS[:, 1, 0:D], ACT.Copy, scale=s.gate).then_inc(p.sems["y_ready"], 1)
            if ahead and step == QT * CH + 1:
                copy_xT(p, i + 1)

    copy_xT(heavy, 0)
    with act.Fori(0, B - 1) as i:
        heavy_batch(i)
    heavy_batch(B - 1, ahead=False)


def colt_dve(dve, order, e, s):
    PS = e.PS
    light, heavy = s.parts
    dve.wait_ge(s.weights_loaded, 16 * len(s.loads))
    for w in range(2):
        for k in range(KD):
            g = s.gamma[w][:, k:k + 1]
            order.mark(dve.tensor_scalar(s.wk[w][:, k, :], s.wk[w][:, k, :], g, D ** 0.5, ALU.mult, ALU.mult))
            order.mark(dve.tensor_scalar(s.wv[w][:, k, :], s.wv[w][:, k, :], g, D ** 0.5, ALU.mult, ALU.mult))
            order.mark(dve.tensor_scalar(s.wq[w][:, k, :], s.wq[w][:, k, :], g, D ** 0.5 * CD ** -0.5, ALU.mult, ALU.mult))
    order.mark(dve.memset(s.kTz, 0.0))
    order.mark(dve.memset(s.v[:, :, :, CD:CV], 1.0))
    order.settle()
    dve.sem_inc(s.sems["setup"], 1)

    def step(ins):
        order.mark(ins)
        order.settle()

    with dve.Fori(0, B) as i:
        order.turn(i, 2 * TB + 1)
        for t in range(TB):
            order.mark(dve.bn_stats(e.stats[:, t, :], e.x_all[:, i * TB + t, :]))
        order.settle()
        dve.sem_inc(e.spare, 1)
        for t in range(TB):
            order.mark(dve.bn_aggr(e.mean_var[:, t, :], e.stats[:, t, :]))
        order.settle()
        order.mark(dve.tensor_copy(s.mean_var[:, bass.ds(i * TB, TB), :], e.mean_var[:]))
    order.end(B)
    order.settle()
    dve.tensor_scalar(s.var_eps, s.mean_var[:, :, 1], LN_EPS, None, ALU.add).then_inc(s.var_ready, 1)
    dve.wait_ge(s.rstd_ready, 1)
    step(dve.tensor_tensor(s.sumsq, s.rstd, s.rstd, ALU.mult))
    step(dve.tensor_tensor(s.sumsq, s.sumsq, s.mean_var[:, :, 1], ALU.mult))
    dve.tensor_scalar(s.sumsq, s.sumsq, float(D), 1e-24, ALU.mult, ALU.max).then_inc(s.sems["sumsq_ready"], 1)
    dve.wait_ge(s.sems["rnorm_ready"], 1)
    order.mark(dve.tensor_tensor(s.norm, s.sumsq, s.rnorm, ALU.mult))
    step(dve.tensor_tensor(s.scale, s.rstd, s.rnorm, ALU.mult))
    with dve.Fori(0, B // 2) as j:
        order.turn(j, 2 * TB + 1)
        for h, unit in enumerate(unit_buffers(e)):
            dve.wait_ge(s.sems[f"unit_stored{h}"], 16 * j)
            dve.sem_inc(e.spare, 1)
            for t in range(TB):
                at = (2 * j + h) * TB + t
                dve.tensor_scalar(unit[:, t, :], e.x_all[:, at, :], s.mean_var[:, bass.ds(at, 1), 0], s.scale[:, bass.ds(at, 1)],
                                  ALU.subtract, ALU.mult).then_inc(s.sems["unit_ready"], 1)
            dve.wait_ge(s.sems["unit_ready"], TB * (2 * j + h + 1))
            order.settle()
            for t in range(TB):
                order.mark(dve.tensor_tensor_reduce(s.junk4[:, t, :], unit[:, t, :], s.token, 1.0, 0.0, ALU.mult, ALU.add,
                                                    s.dots_of_pair[:, h * TB + t:h * TB + t + 1]))
        order.settle()
        order.mark(dve.tensor_copy(s.dots[:, bass.ds(2 * TB * j, 2 * TB)], s.dots_of_pair))
    order.end(B // 2)
    order.settle()
    dve.tensor_tensor(s.dots, s.dots, s.norm, ALU.mult).then_inc(s.sems["dots_ready"], 1)

    dve.wait_ge(s.sems["cd_psum"], 1)
    order.mark(dve.tensor_copy(s.s[0:B, :], PS[0:B, 2, :]))
    order.mark(dve.memset(s.per_k, 1.0 / ROUTE_K))
    step(dve.tensor_reduce(s.shift[0:B, :], PS[0:B, 2, :], AX_X, ALU.max, negate=True))
    dve.tensor_scalar(s.shift[0:B, :], s.shift[0:B, :], 0.0, None, ALU.max).then_inc(s.sems["shifted"], 1)
    dve.wait_ge(s.sems["cd_exp"], 2)
    step(dve.tensor_scalar(s.limit[0:B, 1:2], s.limit[0:B, 0:1], S / ROUTE_K, None, ALU.mult))

    def route_step(r):
        order.settle()
        order.mark(dve.scalar_tensor_tensor(s.e_min[0:B, :], s.e[0:B, :], s.limit[0:B, r % 2:r % 2 + 1], s.per_k[0:B, :].broadcast_to([B, S]),
                                            ALU.min, ALU.mult, accum_out=s.limit[0:B, 1 - r % 2:2 - r % 2]))

    def raise_shift():
        limit = s.limit[0:B, 0:1]
        order.settle()
        step(dve.tensor_scalar(s.low[0:B, :], limit, exp(-30.0), None, ALU.is_lt))
        order.mark(dve.tensor_scalar(s.raise_[0:B, :], s.low[0:B, :], exp(34.0) - 1.0, 1.0, ALU.mult, ALU.add))
        step(dve.scalar_tensor_tensor(s.shift[0:B, :], s.low[0:B, :], 34.0, s.shift[0:B, :], ALU.mult, ALU.add))
        dve.tensor_tensor(limit, limit, s.raise_[0:B, :], ALU.mult).then_inc(s.sems["shifted"], 1)

    def rank_tile(t):
        row = s.row_scores[:, t // TB * S:(t // TB + 1) * S]
        step(dve.scalar_tensor_tensor(s.junk2[:, 0, :], row, s.score[:, t:t + 1], s.earlier[:, t % TB, :], ALU.is_equal, ALU.mult))
        step(dve.scalar_tensor_tensor(s.junk2[:, 1, :], row, s.score[:, t:t + 1], s.junk2[:, 0, :], ALU.is_gt, ALU.add,
                                      accum_out=s.rank[:, t:t + 1]))

    def copy_keys(p, i, these=range(CT)):
        for m in these:
            dve.wait_ge(p.sems["proj_psum"], 3 * CT * i + m + 1)
            dve.tensor_copy(s.kTz[0:CD, 2 * m, :], PS[0:CD, 2 + m, :]).then_inc(e.spare, 1)
            dve.tensor_copy(s.kTz[CD:P, 2 * m + 1, :], PS[CD:P, 2 + m, :]).then_inc(p.sems["k_ready"], 1)

    def normalise(p, wait, bank, at, o, done, par):
        dve.wait_ge(p.sems["pv_psum"], wait)
        dve.wait_ge(p.sems["o_ready"], done)
        recip = s.recip[:, par, 0:4]
        src = PS[:, bank, 0:4 * CV].rearrange("p (h v) -> p h v", v=CV)
        order.mark(dve.reciprocal(recip, src[:, :, CD]))
        order.settle()
        dve.tensor_tensor(o[:, at:at + 4 * CD].rearrange("p (h d) -> p h d", d=CD), src[:, :, 0:CD],
                          recip.rearrange("p (h o) -> p h o", o=1).broadcast_to([P, 4, CD]), ALU.mult)\
            .then_inc(p.sems["o_ready"], 1)

    def light_batch(i, routing, ahead=True):
        p, n = light, 2 * TB * i
        for step_ in range(2 * TB + 6):
            if step_ < 2 * TB:
                u = step_
                dve.wait_ge(p.sems["scores"], n + u + 1)
                bank = PS[:, 2 + u % 2, :].rearrange("p (h s) -> p h s", s=P)
                order.mark(dve.tensor_reduce(s.maxes[:, u % 2, 0:4], bank, AX_X, ALU.max))
                order.settle()
                if u >= 2:
                    dve.wait_ge(p.sems["exp_ready"], n + u - 1)
                dve.tensor_tensor(s.shifted[:, u % 2, :].rearrange("p (h s) -> p h s", s=P), bank,
                                  s.maxes[:, u % 2, 0:4].rearrange("p (h o) -> p h o", o=1).broadcast_to([P, 4, P]),
                                  ALU.subtract).then_inc(p.sems["shifted_ready"], 1)
            if 3 <= step_ < 2 * TB + 3:
                u = step_ - 3
                if u >= 4 and u % 2 == 0:
                    dve.wait_ge(p.sems["oT_psum"], TB * i + u // 2 - 1)
                normalise(p, n + u + 1, 6 + u % 2, (u % 2) * 4 * CD, s.o[:, (u // 2) % 2, :], n + max(u - 1, 0), u % 2)
            if step_ >= 6 and step_ % 2 == 0:
                t = (step_ - 6) // 2
                dve.wait_ge(p.sems["y_psum"], TB * i + t + 1)
                tile = e.x_all[:, i * TB + t, :]
                dve.scalar_tensor_tensor(tile, PS[:, 1, 0:D], s.gate, tile, ALU.mult, ALU.add).then_inc(s.sems["light_x"], 1)
            if ahead and step_ >= 2 * TB + 3:
                copy_keys(p, i + 1, ((0,), (1,), (2, 3))[step_ - 2 * TB - 3])
            if routing and step_ % (ROUTE_TURN // 2 + 1) == 0:
                raise_shift()
            elif routing:
                if step_ % (ROUTE_TURN // 2 + 1) == 1:
                    dve.wait_ge(s.sems["shifted"], 2 * i + 2 + step_ // (ROUTE_TURN // 2 + 1))
                    dve.wait_ge(s.sems["cd_exp"], 2 * i + 3 + step_ // (ROUTE_TURN // 2 + 1))
                route_step(step_ % (ROUTE_TURN // 2 + 1) - 1)
            g = 0 if routing else (i - B // 2) * (2 * TB + 6) + step_ - 4
            if not routing and 0 <= g < NT:
                if g == 0:
                    dve.wait_ge(s.sems["scores_spread"], 16)
                rank_tile(g)
            if not routing and g == NT:
                slots()

    def slots():
        step(dve.tensor_scalar(s.over, s.rank, float(NQ), None, ALU.is_ge))
        step(dve.tensor_tensor(s.rank, s.rank, e.const("batch_slot"), ALU.add))
        step(dve.scalar_tensor_tensor(s.from_f, s.over, float(NR - NQ), s.rank, ALU.mult, ALU.add))
        step(dve.tensor_copy(s.to_u, s.from_f))
        step(dve.tensor_scalar(s.from_f, s.rank, -1.0, float(NR), ALU.mult, ALU.add))
        step(dve.tensor_tensor(s.from_f, s.from_f, s.over, ALU.mult))
        step(dve.tensor_tensor(s.from_f, s.from_f, s.rank, ALU.add))
        step(dve.tensor_copy(s.from_u, s.from_f))
        dve.sem_inc(s.sems["slots_ready"], 1)

    for r in range(1, ROUTE_STEPS % (B // 2)):
        route_step(r)
    copy_keys(light, 0)
    with dve.Fori(0, B // 2) as i:
        order.turn(i, 4 * TB + ROUTE_TURN + 2 * 3)
        light_batch(i, True)
    order.end(B // 2)
    order.settle()
    dve.sem_inc(s.sems["cd_final"], 1)
    dve.wait_ge(s.sems["cd_log"], 1)
    step(dve.tensor_tensor(s.log[0:B, :], s.shift[0:B, :], s.log[0:B, :], ALU.subtract))
    dve.tensor_scalar(s.e[0:B, :], s.s[0:B, :], s.log[0:B, :], 0.0, ALU.add, ALU.min).then_inc(s.sems["cd_u"], 1)
    dve.wait_ge(s.sems["score_psum"], 1)
    dve.tensor_copy(s.score.rearrange("p (b t) -> p t b", t=TB), PS[:, 7, 0:NT].rearrange("p (t b) -> p t b", b=B))\
        .then_inc(s.sems["score_ready"], 1)
    dve.wait_ge(s.sems["score_ready"], 1)
    for i in range(B // 2, B):
        light_batch(i, False, ahead=i < B - 1)
    dve.wait_ge(s.sems["light_x"], NT)
    order.settle()
    dve.sem_inc(s.sems["light_done"], 1)
    dve.wait_ge(s.scattered_s[0], 16 * NT // 2)
    step(dve.memset(s.back, 0.0))

    def add_back(at):
        for t in range(TB):
            dve.tensor_tensor(e.x_all[:, at + t, :], e.x_all[:, at + t, :], s.back[:, t, :], ALU.add).then_inc(s.sems["merged"], 1)

    def heavy_batch(i, ahead=True):
        p, n = heavy, QT * CH * i
        dve.wait_ge(s.gathered_s, 16 * TB * i)
        dve.sem_inc(e.spare, 1)
        add_back((B - i) * TB)
        for step_ in range(QT * CH + 4):
            if step_ < QT * CH:
                u = step_
                dve.wait_ge(p.sems["scores"], n + u + 1)
                if u >= 2:
                    dve.wait_ge(p.sems["exp_ready"], n + u - 1)
                dve.tensor_reduce(s.maxes[:, 0, u % 2:u % 2 + 1], PS[:, 2 + u % 2, :], AX_X, ALU.max, negate=True)\
                    .then_inc(p.sems["shifted_ready"], 1)
            if 1 <= step_ < QT * CH + 1:
                u = step_ - 1
                dve.wait_ge(p.sems["pT_psum"], n + u + 1)
                if u >= 2:
                    dve.wait_ge(p.sems["pv_psum"], n + u - 1)
                dve.tensor_copy(s.hprobsT[:, u % 2, :], PS[:, 4 + u % 2, :]).then_inc(p.sems["pT_ready"], 1)
            if step_ >= 6 and (step_ - 2) % 4 == 0:
                g = (step_ - 6) // 4
                if g % 2 == 0:
                    dve.wait_ge(p.sems["oT_psum"], QT * i)
                normalise(p, n + 4 * (g + 1), 6 + g % 2, (g % 2) * 4 * CD, s.ho[:, g // 2, :], 2 * QT * i + max(g - 1, 0), g % 2)
            if ahead and step_ == QT * CH + 3:
                copy_keys(p, i + 1)

    copy_keys(heavy, 0)
    with dve.Fori(0, B - 1) as i:
        order.turn(i, 2 * QT)
        heavy_batch(i)
    order.end(B - 1)
    heavy_batch(B - 1, ahead=False)

    dve.wait_ge(s.gathered_s, 16 * TB * B)
    add_back(0)
    dve.wait_ge(s.sems["merged"], TB * (B + 1))
    dve.sem_inc(e.x_updated, NT)


def colt_pool(pool, order, e, s):
    nc = e.nc
    nc.gpsimd.memset(s.minus_half, -0.5).then_inc(e.pool_order, 1)
    order.k += 1
    order.settle()
    pool.wait_ge(s.var_ready, 1)
    nc.gpsimd.tensor_tensor(s.rstd, s.var_eps, s.minus_half, ALU.pow).then_inc(s.rstd_ready, 1)
    pool.wait_ge(s.sems["sumsq_ready"], 1)
    nc.gpsimd.tensor_tensor(s.rnorm, s.sumsq, s.minus_half, ALU.pow).then_inc(s.sems["rnorm_ready"], 1)
    pool.wait_ge(s.sems["slots_ready"], 1)
    for b in range(B):
        pool.wait_ge(s.sems[f"forth_loaded{b % 2}"], 16 * (b // 2 + 1))
        for t in range(TB):
            nc.gpsimd.indirect_dma_start(s.T["routed_in"], bass.IndirectOffsetOnAxis(s.to_u[:, b * TB + t:b * TB + t + 1], 0),
                                         s.forth[b % 2][:, t, :], None).then_inc(s.scattered_s[b % 2], 16)
    for i in range(B):
        pool.wait_ge(s.sems["results_stored"], 16 * (i + 1))
        pool.wait_ge(s.sems["merged"], TB * (i + 1))
        for t in range(TB):
            at = (B - 1 - i) * TB + t
            nc.gpsimd.indirect_dma_start(s.back[:, t, :], None, s.T["routed_out"],
                                         bass.IndirectOffsetOnAxis(s.from_u[:, at:at + 1], 0)).then_inc(s.gathered_s, 16)


PLAN = {"L0_xattn": plan_xattn, "L1_xattn": plan_xattn, "L3_xattn": plan_xattn, "L1_ffn": plan_ffn1,
        "L2_xattn": plan_xattn2, "L2_ffn": plan_ffn2, "L3_ffn": plan_moe, "L0_ffn": plan_colt}


def rows(w):
    k, n = w.shape
    return np.ascontiguousarray(w.reshape(k // P, P, n).transpose(1, 0, 2).reshape(P, -1))


def cols(b):
    return np.ascontiguousarray(b.reshape(-1, P).T)


def lay_out(i):
    i = {k: np.asarray(v) for k, v in i.items()}
    t = {"x": i["x"], "ctx_1024": i["ctx_1024"], "g_xattn": i["g_xattn"], "g_ffn": i["g_ffn"]}
    t["consts"] = np.zeros((P, CONST_N), np.float32)
    for name, a in shape_constants().items():
        if name in OF_A_STAGE:
            t["table_" + name] = a
            continue
        at, n = CONST_AT[name]
        t["consts"][:, at:at + n] = a
    t["mask_L0"] = i["mask_BxS2_bf1"].view(np.uint8).reshape(1, -1)
    t["mask_L1"] = i["mask_Bx1x1xS2_ff1"].reshape(1, -1)
    wkv, bkv = i["L0_xattn_Wkv"], i["L0_xattn_bkv"]
    xa = {"L0": (i["L0_xattn_Wq"], wkv[:, :D], wkv[:, D:], i["L0_xattn_Wo"], i["L0_xattn_bq"], bkv[:D], bkv[D:], i["L0_xattn_bo"])}
    for L, q in (("L1", "W{} b{}"), ("L3", "w_{} b_{}")):
        wn, bn = q.split()
        up = (lambda c: c)
        xa[L] = tuple(i[f"{L}_xattn_{wn.format(c)}"].T for c in "qkvo") + tuple(i[f"{L}_xattn_{bn.format(c)}"] for c in "qkvo")
    for L, (wq, wk, wv, wo, bq, bk, bv, bo) in xa.items():
        for n, w in (("wq", wq), ("wk", wk), ("wv", wv), ("wo", wo)):
            t[f"{L}_xattn_{n}"] = rows(w)
        t[f"{L}_xattn_bq"], t[f"{L}_xattn_bk"] = cols(bq), cols(bk)
        t[f"{L}_xattn_bv"], t[f"{L}_xattn_bo"] = bv.reshape(1, -1), bo.reshape(1, -1)
    for part in ("light", "heavy"):
        wkv = i[f"L0_ffn_wkv_{part}"]
        if part == "light":
            wk, wv = wkv[:, :CH * CD], wkv[:, CH * CD:]
        else:
            heads = wkv.reshape(CH, 2, CD, D)
            wk, wv = heads[:, 0].reshape(CH * CD, D).T, heads[:, 1].reshape(CH * CD, D).T
        for n, w in (("wq", i[f"L0_ffn_wq_{part}"]), ("wk", wk), ("wv", wv), ("wo", i[f"L0_ffn_wo_{part}"])):
            t[f"L0_ffn_{n}_{part}"] = rows(w)
        t[f"L0_ffn_gamma_{part}"] = cols(i[f"L0_ffn_gamma_{part}"])
    t["L0_ffn_q_routing_token"] = i["L0_ffn_q_routing_token"].reshape(1, -1)
    t["L1_ffn_q1"], t["L1_ffn_q2"] = rows(i["L1_ffn_fc1_q"]), rows(i["L1_ffn_fc2_q"])
    t["L1_ffn_sc1"], t["L1_ffn_sc2"] = i["L1_ffn_fc1_scales"].reshape(1, -1), i["L1_ffn_fc2_scales"].reshape(1, -1)
    t["L1_ffn_b1"], t["L1_ffn_b2"] = cols(i["L1_ffn_fc1_bias"]), i["L1_ffn_fc2_bias"].reshape(1, -1)
    t["L1_ffn_gamma"], t["L1_ffn_beta"] = cols(i["L1_ffn_ln_gamma"]), cols(i["L1_ffn_ln_beta"])
    t["mask_L2"] = i["mask_SxS2_ik1"]
    t["L2_xattn_wq"] = rows(i["L2_xattn_Wq"])
    t["L2_xattn_wk"], t["L2_xattn_wv"] = rows(i["L2_xattn_Wk"].T), rows(i["L2_xattn_Wv"].T)
    t["L2_xattn_bq"], t["L2_xattn_bk"] = cols(i["L2_xattn_bq"]), cols(i["L2_xattn_bk"])
    t["L2_xattn_bv"] = i["L2_xattn_bv"].reshape(1, -1)
    for g in ("f", "i", "c", "o"):
        t[f"L2_ffn_w{g}"], t[f"L2_ffn_u{g}"] = rows(i[f"L2_ffn_w{g}"].T), rows(i[f"L2_ffn_u{g}"].T)
        t[f"L2_ffn_b{g}"] = i["L2_ffn_bo"].reshape(1, -1) if g == "o" else cols(i[f"L2_ffn_b{g}"])
    ex = np.zeros((NE, P, E_N), np.float32)
    for e in range(NE):
        ex[e, :, 0:KD * DE] = rows(i["L3_ffn_W1"][e].T)
        ex[e, :, KD * DE:2 * KD * DE] = rows(i["L3_ffn_W2"][e].T)
        down = np.zeros((KE * P, D), np.float32)
        down[:DE] = i["L3_ffn_W3"][e].T
        ex[e, :, 2 * KD * DE:] = rows(down)
    t["L3_ffn_experts"] = ex
    t["L3_ffn_gate_w"], t["L3_ffn_rms_w"] = rows(i["L3_ffn_gate_w"].T), i["L3_ffn_rms_w"].reshape(1, -1)
    t["L2_ffn_in_c"] = cols(i["L2_ffn_in_c"])
    return t


def declare_and_write(nc, tensors, stages):
    arrays = {f"in_{n}": np.ascontiguousarray(a) for n, a in tensors.items()}
    T = {n[3:]: nc.dram_tensor(n, a.shape, mybir.dt.from_np(a.dtype), kind="ExternalInput").ap() for n, a in arrays.items()}
    T["out"] = nc.dram_tensor("out_x", (B, S, D), F32, kind="ExternalOutput").ap()
    for n, shape in (("slots", (MOE_TILES * P, D)), ("results", (MOE_TILES * P, D)), ("unit_rows", (B * S, D)),
                     ("row_scores", (B * S,)), ("routed_in", (2 * NR, D)), ("routed_out", (NR + P, D)), ("residual", (B * S, D))):
        T[n] = nc.dram_tensor(n, shape, F32, kind="Internal").ap()
    flamingo_kernel(nc, T, T["out"], stages)
    return arrays


def kernel(**inputs):
    import concourse.bacc as bacc
    from concourse.bass_utils import run_bass_kernel_spmd as run

    nc = bacc.Bacc("TRN2", target_bir_lowering=False, num_devices=1)
    arrays = declare_and_write(nc, lay_out(inputs), STAGES)
    return run(nc, [arrays], core_ids=[0]).results[0]["out_x"]
```

```python
from contextlib import ExitStack
from math import exp

import concourse.bass as bass
from concourse import mybir
import numpy as np

F32 = mybir.dt.float32
BF16 = mybir.dt.bfloat16
I32 = mybir.dt.int32
U8 = mybir.dt.uint8
ALU = mybir.AluOpType
ACT = mybir.ActivationFunctionType
AX_X = mybir.AxisListType.X

P = 128
B, S, D = 8, 512, 256
TB = S // P
NT = B * TB
KD = D // P
SC = 64
NH, HD = 16, 16
HH = NH // KD
NP = HH // 2
VW = HD + 1
LN_EPS = 1e-5
STAGES = ["L0_xattn", "L0_ffn", "L1_xattn", "L1_ffn", "L2_xattn", "L2_ffn", "L3_xattn", "L3_ffn"]

NE, DE = 8, 704
KE = -(-DE // P)
HE = DE // 2
MOE_TILES = 2 * B * S // P + NE
E_N = 2 * KD * DE + KE * D
MOE_N = 3400



def shape_constants():
    p = np.arange(P)
    f = np.float32
    out = {"ident": np.eye(P, dtype=f)}
    for name, scale in (("head8", 64 ** -0.5), ("head4", 0.25)):
        out[name] = ((p[:, None] // HD) == np.arange(HH)[None, :]).astype(f) * f(scale)
    swap = np.zeros((P, P), f)
    swap[p[0::2] + 1, p[0::2]] = -1.0
    swap[p[0::2], p[0::2] + 1] = 1.0
    out["swap"] = swap
    inv = (f(1.0) / np.power(f(10000.0), np.arange(0, HD, 2, dtype=f) / f(HD))).astype(f)
    for name, n in (("q", S), ("k", SC)):
        pos = (f(10.0) * (np.arange(n, dtype=f) / f(n))).astype(f)
        ang = (inv[(p % HD) // 2][:, None] * pos[None, :]).astype(f)
        out["cos_" + name] = np.cos(ang).astype(f)
        out["sin_" + name] = np.sin(ang).astype(f)
    q = np.arange(P)
    tok = np.arange(TB)[None, :, None] * P + p[:, None, None]
    out["earlier"] = (np.arange(S)[None, None, :] < tok).astype(f).reshape(P, TB * S)
    out["expert"] = np.broadcast_to(np.arange(8, dtype=f)[None, :], (P, 8)).copy()
    out["before"] = (q[:, None] < q[None, :]).astype(f)
    out["ones"] = np.ones((P, P), f)
    out["batch_slot"] = np.broadcast_to((q[:NT] // TB * 256).astype(f)[None, :], (P, NT)).copy()
    out["slot_start"] = np.broadcast_to(P * np.arange(MOE_TILES, dtype=f)[None, :], (P, MOE_TILES)).copy()
    return out


ROTARY = ("cos_q", "sin_q", "cos_k", "sin_k")
OF_A_STAGE = ROTARY + ("earlier",)


def constant_columns():
    at, cols = 0, {}
    for name, a in shape_constants().items():
        if name in OF_A_STAGE:
            continue
        cols[name] = (at, a.shape[1])
        at += a.shape[1]
    return cols, at


CONST_AT, CONST_N = constant_columns()


W_N, A_N = 9216, 17100


def runs(numbers):
    out = []
    for n in sorted(numbers):
        if out and out[-1][1] == n:
            out[-1][1] = n + 1
        else:
            out.append([n, n + 1])
    return out


class Carver:

    def __init__(self, tensor, first, end):
        self.tensor, self.at, self.end = tensor, first, end

    def take(self, *shape):
        n = 1
        for s in shape:
            n *= s
        ap = self.tensor[:, self.at:self.at + n]
        self.at += n
        assert self.at <= self.end, (self.at, self.end)
        if len(shape) == 2:
            ap = ap.rearrange("p (a b) -> p a b", b=shape[1])
        elif len(shape) == 3:
            ap = ap.rearrange("p (a b c) -> p a b c", b=shape[1], c=shape[2])
        elif len(shape) == 4:
            ap = ap.rearrange("p (a b c d) -> p a b c d", b=shape[1], c=shape[2], d=shape[3])
        return ap


class Order:

    def __init__(self, eng, sem):
        self.eng, self.sem, self.base, self.k, self.i, self.per = eng, sem, 0, 0, None, 0

    def mark(self, ins):
        ins.then_inc(self.sem, 1)
        self.k += 1

    def turn(self, i, per):
        self.base, self.i, self.per, self.k = self.base + self.k, i, per, 0

    def end(self, turns):
        assert self.k == self.per, (self.k, self.per)
        self.base, self.i, self.k = self.base + turns * self.per, None, 0

    def settle(self, back=0):
        v = self.base + self.k - back
        self.eng.wait_ge(self.sem, v if self.i is None else self.i * self.per + v)


class Names:
    pass


def flamingo_kernel(nc, T, out, stages):
    ctx = ExitStack()
    with ctx:
        def sb(name, shape, dt=F32):
            return ctx.enter_context(nc.sbuf_tensor(name, shape, dt))

        def sem(name):
            return ctx.enter_context(nc.semaphore(name))

        numbers, handles = [[], []], [[], []]

        def stage_sems(k):
            for h in handles[k % 2]:
                nc.release_semaphore(h)
            handles[k % 2] = []
            used = iter(list(numbers[k % 2]))

            def take(name):
                num = next(used, None)
                h = nc.alloc_semaphore(name=name, num=num)
                if num is None:
                    numbers[k % 2].append(h.num)
                handles[k % 2].append(h)
                return h
            return take

        x_all = sb("x_all", [P, NT + TB, D])
        consts = sb("consts", [P, CONST_N])
        ctx2T = sb("ctx2T", [P, KD, B, 2 * SC])
        tg = sb("tg", [P, 8])
        minus_half = sb("minus_half", [P, TB])
        ones_bf = sb("ones_bf", [1, P], BF16)
        mem = sb("mem", [P, 2 * W_N + A_N])
        xn = sb("xn", [P, TB, D])
        xnT = sb("xnT", [P, KD, S])
        stats = sb("stats", [P, TB, 6])
        mean_var = sb("mean_var", [P, TB, 2])
        var_eps = sb("var_eps", [P, TB])
        rstd = sb("rstd", [P, TB])
        moe_small = sb("moe_small", [P, MOE_N])
        PS = ctx.enter_context(nc.psum_tensor("PS", [P, 8, 512], F32))

        def const(name, rows=P):
            at, n = CONST_AT[name]
            return consts[0:rows, at:at + n]

        ident = const("ident")

        x_loaded = sem("x_loaded")
        consts_loaded = sem("consts_loaded")
        ctx_loaded = sem("ctx_loaded")
        gates_loaded = sem("gates_loaded")
        gates_ready = sem("gates_ready")
        ctx_psum = sem("ctx_psum")
        ctx_ready = sem("ctx_ready")
        x_updated = sem("x_updated")
        out_stored = sem("out_stored")
        zeros_ready = sem("zeros_ready")
        sems_cleared = sem("sems_cleared")
        spare = sem("spare")
        dve_order = sem("dve_order")
        act_order = sem("act_order")
        pool_order = sem("pool_order")

        loaded = [sem(f"{name}_weights_loaded") for name in stages]
        plans = []
        for k, name in enumerate(stages):
            s = Names()
            s.name, s.k = name, k
            half = STAGES.index(name) % 2
            s.w = Carver(mem, half * W_N, (half + 1) * W_N)
            s.a = Carver(mem, 2 * W_N, 2 * W_N + A_N)
            s.mem = mem
            s.x_before = NT * k
            s.weights_loaded = loaded[k]
            s.looks_ahead = s.stores = False
            s.early_sync_program = s.sync_program = None
            s.loads = []
            s.gate = tg[:, STAGES.index(name) // 2 + 4 * (STAGES.index(name) % 2):][:, 0:1]
            stage, s.own_sem = stage_sems(k), sem
            s.var_ready, s.rstd_ready, s.ln_ready, s.xnT_psum, s.xnT_ready = (
                stage(f"{name}_{n}") for n in ("var_ready", "rstd_ready", "ln_ready", "xnT_psum", "xnT_ready"))
            PLAN[name](s, T, stage, moe_small)
            plans.append(s)

        block = ctx.enter_context(nc.Block())

        def dve_layernorm(dve, order, s, i, last_read=None):
            for t in range(TB):
                order.mark(dve.bn_stats(stats[:, t, :], x_all[:, i * TB + t, :]))
            order.settle()
            dve.sem_inc(spare, 1)
            for t in range(TB):
                order.mark(dve.bn_aggr(mean_var[:, t, :], stats[:, t, :]))
            order.settle()
            dve.tensor_scalar(var_eps[:], mean_var[:, :, 1], LN_EPS, None, ALU.add).then_inc(s.var_ready, 1)
            dve.wait_ge(s.rstd_ready, i + 1)
            dve.wait_ge(s.xnT_psum, KD * i)
            if last_read is not None:
                dve.wait_ge(*last_read)
            for t in range(TB):
                dve.tensor_scalar(xn[:, t, :], x_all[:, i * TB + t, :], mean_var[:, t, 0:1], rstd[:, t:t + 1],
                                  ALU.subtract, ALU.mult).then_inc(s.ln_ready, 1)

        def ln_stats(dve, order, i, t):
            order.mark(dve.bn_stats(stats[:, t, :], x_all[:, i * TB + t, :]))

        def ln_variance(dve, order, s):
            order.settle()
            dve.sem_inc(spare, 1)
            for t in range(TB):
                order.mark(dve.bn_aggr(mean_var[:, t, :], stats[:, t, :]))
            order.settle()
            dve.tensor_scalar(var_eps[:], mean_var[:, :, 1], LN_EPS, None, ALU.add).then_inc(s.var_ready, 1)

        def ln_apply(dve, s, i):
            dve.wait_ge(s.rstd_ready, i + 1)
            dve.wait_ge(s.xnT_psum, KD * i)
            for t in range(TB):
                dve.tensor_scalar(xn[:, t, :], x_all[:, i * TB + t, :], mean_var[:, t, 0:1], rstd[:, t:t + 1],
                                  ALU.subtract, ALU.mult).then_inc(s.ln_ready, 1)

        LN_MARKS = 2 * TB

        def stage_start(eng, s):
            eng.wait_ge(x_updated, s.x_before)
            if s.k >= 2:
                eng.wait_ge(sems_cleared, s.k - 1)
                eng.sem_inc(spare, 1)
            if s.k == 0:
                eng.wait_ge(ctx_ready, 2 * KD)
            if s.k > 0 and plans[s.k - 1].looks_ahead:
                eng.wait_ge(plans[s.k - 1].xnT_ready, KD * (B + 1))

        def pool_rstd(pool, s, i):
            pool.wait_ge(s.var_ready, i + 1)
            nc.gpsimd.tensor_tensor(rstd[:], var_eps[:], minus_half[:], ALU.pow).then_inc(s.rstd_ready, 1)

        def pe_transpose_xn(pe, s, i, banks=(0, 1), src=None, ready=None):
            src = xn if src is None else src
            for k in range(KD):
                for t in range(TB):
                    if k == 0:
                        pe.wait_ge(ready or s.ln_ready, TB * i + t + 1)
                    last = nc.tensor.transpose(PS[:, banks[k], t * P:(t + 1) * P], src[:, t, k * P:(k + 1) * P], ident)
                last.then_inc(s.xnT_psum, 1)

        def act_copy_xnT(act, s, i, banks=(0, 1)):
            for k in range(KD):
                act.wait_ge(s.xnT_psum, KD * i + k + 1)
                nc.scalar.activation(xnT[:, k, :], PS[:, banks[k], :], ACT.Copy).then_inc(s.xnT_ready, 1)

        env = Names()
        env.LN_MARKS, env.PS, env.act_copy_xnT, env.const = LN_MARKS, PS, act_copy_xnT, const
        env.ctx2T, env.dve_layernorm, env.ident, env.mean_var = ctx2T, dve_layernorm, ident, mean_var
        env.minus_half, env.nc, env.ones_bf, env.out_stored = minus_half, nc, ones_bf, out_stored
        env.pe_transpose_xn, env.pool_rstd, env.rstd, env.spare = pe_transpose_xn, pool_rstd, rstd, spare
        env.stage_start, env.stats, env.var_eps, env.x_all = stage_start, stats, var_eps, x_all
        env.x_updated, env.xn, env.xnT, env.zeros_ready = x_updated, xn, xnT, zeros_ready
        env.pool_order, env.ln_stats, env.ln_variance, env.ln_apply = pool_order, ln_stats, ln_variance, ln_apply

        @block.sync
        def _(sp):
            for k, s in enumerate(plans):
                if k > 0:
                    sp.wait_ge(x_updated, NT * k)
                if k >= 2:
                    for lo, hi in runs(numbers[k % 2]):
                        last = sp.sem_clear(range(lo, hi))
                    last.then_inc(sems_cleared, 1)
                if k == 0:
                    for b in range(B):
                        sp.dma_start(x_all[:, b * TB:(b + 1) * TB, :],
                                     T["x"][b].rearrange("(t p) d -> p t d", p=P)).then_inc(x_loaded, 16)
                for later in plans[k:k + 2] if k == 0 else plans[k + 1:k + 2]:
                    for dst, src in later.loads:
                        sp.dma_start(dst, src).then_inc(later.weights_loaded, 16)
                    if later.early_sync_program:
                        later.early_sync_program(sp, env, later)
                if s.sync_program:
                    s.sync_program(sp, env, s)
            for b in range(0 if plans[-1].stores else B):
                sp.wait_ge(x_updated, NT * (len(plans) - 1) + TB * (b + 1))
                sp.dma_start(out[b].rearrange("(t p) d -> p t d", p=P),
                             x_all[:, b * TB:(b + 1) * TB, :]).then_inc(out_stored, 16)
            if not plans[-1].stores:
                sp.wait_ge(out_stored, 16 * B)

        @block.gpsimd
        def _(pool):
            nc.gpsimd.memset(minus_half[:], -0.5).then_inc(pool_order, 1)
            pool.wait_ge(pool_order, 1)
            order = Order(pool, pool_order)
            order.k = 1
            for s in plans:
                stage_start(pool, s)
                s.pool(pool, order, env, s)

        @block.scalar
        def _(act):
            order = Order(act, act_order)
            act.dma_start(consts[:], T["consts"]).then_inc(consts_loaded, 16)
            ctx_v = T["ctx_1024"].rearrange("b s d -> (b s) d").rearrange("(t p) d -> p t d", p=P)
            act.dma_start(xn[:], ctx_v).then_inc(ctx_loaded, 16)
            act.dma_start(tg[:, 0:4], T["g_xattn"].rearrange("(a n) -> a n", a=1).broadcast_to([P, 4])).then_inc(gates_loaded, 16)
            act.dma_start(tg[:, 4:8], T["g_ffn"].rearrange("(a n) -> a n", a=1).broadcast_to([P, 4])).then_inc(gates_loaded, 16)
            act.wait_ge(gates_loaded, 32)
            nc.scalar.activation(tg[:], tg[:], ACT.Tanh).then_inc(gates_ready, 1)
            for k in range(KD):
                act.wait_ge(ctx_psum, k + 1)
                src = PS[:, k, :].rearrange("p (b s) -> p b s", s=SC)
                for e in range(2):
                    nc.scalar.activation(ctx2T[:, k, :, e * SC:(e + 1) * SC], src, ACT.Copy).then_inc(ctx_ready, 1)
            for s in plans:
                stage_start(act, s)
                s.act(act, order, env, s)

        @block.vector
        def _(dve):
            order = Order(dve, dve_order)
            order.mark(dve.memset(ones_bf[:], 1.0))
            order.mark(dve.memset(x_all[:, NT:NT + TB, :], 0.0))
            order.settle()
            dve.sem_inc(zeros_ready, 1)
            dve.wait_ge(consts_loaded, 16)
            dve.wait_ge(gates_ready, 1)
            dve.wait_ge(ctx_psum, KD)
            dve.wait_ge(x_loaded, 16 * B)
            for s in plans:
                stage_start(dve, s)
                s.dve(dve, order, env, s)

        @block.tensor
        def _(pe):
            pe.wait_ge(consts_loaded, 16)
            pe.wait_ge(ctx_loaded, 16)
            for k in range(KD):
                for t in range(B * SC // P):
                    last = nc.tensor.transpose(PS[:, k, t * P:(t + 1) * P], xn[:, t, k * P:(k + 1) * P], ident)
                last.then_inc(ctx_psum, 1)
            pe.wait_ge(ctx_ready, 2 * KD)
            for s in plans:
                stage_start(pe, s)
                s.pe(pe, env, s)


def plan_xattn(s, T, sem, small):
    L = s.name[:2]
    s.rope, s.masked = L == "L0", L in ("L0", "L1")
    take = s.w.take
    s.wq, s.wk, s.wv, s.wo = take(KD, D), take(KD, D), take(KD, D), take(KD, D)
    s.bq, s.bk, s.bv, s.bo = take(KD), take(KD), take(D), take(D)
    n = {c: T[f"{s.name}_{c}"] for c in ("wq", "wk", "wv", "wo", "bq", "bk")}
    for c, w in (("wq", s.wq), ("wk", s.wk), ("wv", s.wv), ("wo", s.wo)):
        s.loads.append((w, n[c].rearrange("p (k n) -> p k n", k=KD)))
    s.loads += [(s.bq, n["bq"]), (s.bk, n["bk"]),
                (s.bv, T[f"{s.name}_bv"].broadcast_to([P, D])), (s.bo, T[f"{s.name}_bo"].broadcast_to([P, D]))]
    if s.masked:
        s.mask = take(B * SC)
        mask = T["mask_L0" if s.rope else "mask_L1"].rearrange("a (b s) -> a b s", s=SC)
        s.mask_u8 = s.mask[:, 0:B * SC // 4].bitcast(U8)
        s.loads.append((s.mask_u8 if s.rope else s.mask, mask.rearrange("a b s -> a (b s)").broadcast_to([P, B * SC])))
    if s.rope:
        s.rotary = {n: take(w) for n, w in zip(ROTARY, (S, S, SC, SC))}
        s.loads += [(s.rotary[n], T["table_" + n]) for n in ROTARY]
    take = s.a.take
    s.kT = take(KD, B * SC)
    s.kbd = take(2, KD, HH * SC)
    s.vbd = take(B, KD * NP, 2 * VW)
    s.qT = take(1 if s.rope else 2, KD, S)
    s.shifted, s.probs, s.probsT = take(2, S), take(2, S), take(2, S)
    s.o, s.oT = take(2, D), take(2, KD, P)
    s.recip = take(2, NH)
    s.gbo = take(D)
    s.maxes = take(2, HH)
    if s.masked:
        s.keep = take(B * SC)
        s.mask_row = take(B * SC // 2).bitcast(BF16)
    if s.rope:
        s.rot, s.rot2 = take(2, KD, S), take(KD, S)
    s.sems = {n: sem(f"{s.name}_{n}") for n in (
        "k_psum", "k_ready", "v_psum", "v_ready", "setup", "q_psum", "q_ready", "swap_psum", "swap_read", "q_roped", "kbd_ready",
        "scores", "shifted_ready", "exp_ready", "pT_psum", "pT_ready", "pv_psum", "o_ready", "oT_psum",
        "oT_ready", "y_psum", "biased")}
    s.pe, s.act, s.dve, s.pool = xattn_pe, xattn_act, xattn_dve, xattn_pool


UNITS = 2 * TB
AHEAD_TURN, AHEAD_Q, AHEAD_SWAP = 2, 4, 6


def wait_for(eng, sem, value):
    if not (isinstance(value, int) and value <= 0):
        eng.wait_ge(sem, value)


def all_turns(eng, turn, order=None, marks=0):
    turn(0, 0, first=True)
    with eng.Fori(0, (B - 2) // 2) as j:
        if order is not None:
            order.turn(j, 2 * marks)
        turn(2 * j + 1, 1)
        turn(2 * j + 2, 0)
    if order is not None:
        order.end((B - 2) // 2)
    turn(B - 1, 1, ahead=False)
    turn(B, 0, ahead=False, drain=True)


def xattn_pe(pe, e, s):
    PS, nc = e.PS, e.nc
    pe.wait_ge(s.weights_loaded, 16 * len(s.loads))
    for f in range(KD):
        for k in range(KD):
            last = nc.tensor.matmul(PS[:, f, :], s.wk[:, k, f * P:(f + 1) * P], e.ctx2T[:, k, :, 0:SC],
                                    start=k == 0, stop=k == KD - 1)
        last.then_inc(s.sems["k_psum"], 1)
    if s.rope:
        pe.wait_ge(s.sems["k_ready"], KD)
        for f in range(KD):
            nc.tensor.matmul(PS[:, f, :], e.const("swap"), s.kT[:, f, :], start=True, stop=True)\
                .then_inc(s.sems["swap_psum"], 1)
    for b in range(B):
        if b >= 2:
            pe.wait_ge(s.sems["v_ready"], 2 * (b - 1))
        for k in range(KD):
            last = nc.tensor.matmul(PS[:, 2 + b % 2, 0:D], e.ctx2T[:, k, b, :], s.wv[:, k, :],
                                    start=k == 0, stop=k == KD - 1)
        last.then_inc(s.sems["v_psum"], 1)
    pe.wait_ge(s.sems["setup"], 1)
    def turn_xn(i, k):
        for t in range(TB):
            if k == 0:
                pe.wait_ge(s.ln_ready, TB * i + t + 1)
        if k > 0:
            pe.wait_ge(s.xnT_ready, KD * i + k)
        for t in range(TB):
            last = nc.tensor.transpose(PS[:, 0, t * P:(t + 1) * P], e.xn[:, t, k * P:(k + 1) * P], e.ident)
        last.then_inc(s.xnT_psum, 1)

    def query(i, f):
        pe.wait_ge(s.xnT_ready, KD * (i + 1))
        if f > 0:
            pe.wait_ge(s.sems["q_ready"], KD * i + f)
        for k in range(KD):
            last = nc.tensor.matmul(PS[:, 0, :], s.wq[:, k, f * P:(f + 1) * P], e.xnT[:, k, :],
                                    start=k == 0, stop=k == KD - 1)
        last.then_inc(s.sems["q_psum"], 1)

    def partners(i, f):
        pe.wait_ge(s.sems["q_ready"], KD * (i + 1))
        if f > 0:
            pe.wait_ge(s.sems["swap_read"], KD * i + f)
        nc.tensor.matmul(PS[:, 0, :], e.const("swap"), s.qT[:, 0, f, :], start=True, stop=True).then_inc(s.sems["swap_psum"], 1)

    def turn(i, par, first=False, ahead=True, drain=False):
        n = UNITS * i
        qT = (s.rot if s.rope else s.qT)[:, par, :, :]

        def scores(u):
            t, f = u // KD, u % KD
            if u == 0:
                pe.wait_ge(s.sems["q_roped"] if s.rope else s.sems["q_ready"], i + 1 if s.rope else KD * (i + 1))
                pe.wait_ge(s.sems["kbd_ready"], KD * (i + 1))
            wait_for(pe, s.sems["shifted_ready"], n + u - 1)
            keys = s.kbd[:, par, f, :].rearrange("p (h s) -> p h s", s=SC)
            last = nc.tensor.matmul(PS[:, 2 + u % 2, :], qT[:, f, t * P:(t + 1) * P], keys, start=True, stop=not s.masked)
            if s.masked:
                row = s.mask_row[0:1, :].rearrange("a (o b s) -> a o b s", o=1, s=SC)[:, :, bass.ds(i, 1), :]
                last = nc.tensor.matmul(PS[:, 2 + u % 2, :], e.ones_bf[:],
                                        row.rearrange("a o b s -> a (o b) s").broadcast_to([1, HH, SC]), start=False, stop=True)
            last.then_inc(s.sems["scores"], 1)

        def transposes(v):
            pe.wait_ge(s.sems["exp_ready"], n + v + 1)
            wait_for(pe, s.sems["pT_ready"], n + v - 1)
            for j in range(NP):
                last = nc.tensor.transpose(PS[:, 4 + v % 2, j * P:(j + 1) * P],
                                           s.probs[:, v % 2, j * P:(j + 1) * P], e.ident)
            last.then_inc(s.sems["pT_psum"], 1)

        def values(v):
            t, f = v // KD, v % KD
            pe.wait_ge(s.sems["pT_ready"], n + v + 1)
            if f == 0:
                wait_for(pe, s.sems["o_ready"], TB * i + t - 1)
            pe.sem_inc(e.spare, 1)
            batch = i - 1 if v < 0 else i
            for j in range(NP):
                at = (f * NP + j) * 2 * VW
                last = nc.tensor.matmul(PS[:, 6 + t % 2, at:at + 2 * VW], s.probsT[:, v % 2, j * P:(j + 1) * P],
                                        s.vbd[:, bass.ds(batch, 1), f * NP + j, :], start=True, stop=True)
            last.then_inc(s.sems["pv_psum"], 1)

        def turn_out(t):
            pe.wait_ge(s.sems["o_ready"], TB * i + t + 1)
            pe.wait_ge(e.x_updated, s.x_before + TB * i + t)
            for k in range(KD):
                last = nc.tensor.transpose(PS[:, 1, k * P:(k + 1) * P], s.o[:, t % 2, k * P:(k + 1) * P], e.ident)
            last.then_inc(s.sems["oT_psum"], 1)

        def project_out(t):
            pe.wait_ge(s.sems["oT_ready"], TB * i + t + 1)
            for k in range(KD):
                last = nc.tensor.matmul(PS[:, 1, D:2 * D], s.oT[:, t % 2, k, :], s.wo[:, k, :], start=k == 0, stop=k == KD - 1)
            last.then_inc(s.sems["y_psum"], 1)

        def due(v):
            return not drain if v >= 0 else not first

        for step in range(UNITS if not drain else 6):
            late = step == 0 and s.rope
            if due(step) and not late:
                scores(step)
            if due(step - 2):
                transposes(step - 2)
            if step % 2 == 1 and due(step - 7):
                project_out((step - 7) // 2)
            if due(step - 3):
                values(step - 3)
            for f in range(KD if ahead else 0):
                if step == AHEAD_TURN + f:
                    turn_xn(i + 1, f)
                if step == AHEAD_Q + f:
                    query(i + 1, f)
                if s.rope and step == AHEAD_SWAP + f:
                    partners(i + 1, f)
            if step % 2 == 0 and due(step - 6):
                turn_out((step - 6) // 2)
            if due(step) and late:
                scores(step)

    for f in range(KD):
        turn_xn(0, f)
    for f in range(KD):
        query(0, f)
    for f in range(KD if s.rope else 0):
        partners(0, f)
    all_turns(pe, turn)


def xattn_act(act, order, e, s):
    PS, nc = e.PS, e.nc
    act.wait_ge(s.weights_loaded, 16 * len(s.loads))
    for f in range(KD):
        act.wait_ge(s.sems["k_psum"], f + 1)
        nc.scalar.activation(s.kT[:, f, :], PS[:, f, :], ACT.Identity, bias=s.bk[:, f:f + 1]).then_inc(s.sems["k_ready"], 1)
    def copy_xnT(i, k):
        act.wait_ge(s.xnT_psum, KD * i + k + 1)
        nc.scalar.activation(e.xnT[:, k, :], PS[:, 0, :], ACT.Copy).then_inc(s.xnT_ready, 1)

    def query(i, par, f):
        act.wait_ge(s.sems["q_psum"], KD * i + f + 1)
        if s.rope:
            wait_for(act, s.sems["q_roped"], i)
        nc.scalar.activation(s.qT[:, 0 if s.rope else par, f, :], PS[:, 0, :], ACT.Identity, bias=s.bq[:, f:f + 1])\
            .then_inc(s.sems["q_ready"], 1)

    def turn(i, par, first=False, ahead=True, drain=False):
        n = UNITS * i
        for step in range(UNITS if not drain else 5):
            v = step - 2
            if not (first if v < 0 else drain):
                act.wait_ge(s.sems["pT_psum"], n + v + 1)
                wait_for(act, s.sems["pv_psum"], n + v - 1)
                nc.scalar.activation(s.probsT[:, v % 2, :], PS[:, 4 + v % 2, :], ACT.Copy).then_inc(s.sems["pT_ready"], 1)
            if not drain:
                u = step
                act.wait_ge(s.sems["shifted_ready"], n + u + 1)
                wait_for(act, s.sems["pT_psum"], n + u - 1)
                nc.scalar.activation(s.probs[:, u % 2, :], s.shifted[:, u % 2, :], ACT.Exp).then_inc(s.sems["exp_ready"], 1)
            for f in range(KD if ahead else 0):
                if step == AHEAD_TURN + f:
                    copy_xnT(i + 1, f)
                if step == AHEAD_Q + f:
                    query(i + 1, 1 - par, f)
            t = (step - 6) // 2
            if step % 2 == 0 and not (first if t < 0 else drain):
                act.wait_ge(s.sems["oT_psum"], TB * i + t + 1)
                wait_for(act, s.sems["y_psum"], TB * i + t - 1)
                nc.scalar.activation(s.oT[:, t % 2, :, :], PS[:, 1, 0:D].rearrange("p (k n) -> p k n", k=KD),
                                     ACT.Copy).then_inc(s.sems["oT_ready"], 1)

    for f in range(KD):
        copy_xnT(0, f)
    for f in range(KD):
        query(0, 0, f)
    all_turns(act, turn)


def xattn_dve(dve, order, e, s):
    PS = e.PS
    dve.wait_ge(s.weights_loaded, 16 * len(s.loads))
    order.mark(dve.memset(s.vbd, 0.0))
    if s.masked:
        order.mark(dve.tensor_scalar(s.keep, s.mask_u8 if s.rope else s.mask, 0.0, None, ALU.not_equal))
    order.settle()
    order.mark(dve.memset(s.vbd.rearrange("p b j (e v) -> p (b j e) v", v=VW)[:, :, HD:VW], 1.0))
    if s.masked:
        order.mark(dve.tensor_scalar(s.mask_row[0:1, :], s.keep[0:1, :], 1.0, 3e38 if s.rope else 1e9,
                                     ALU.subtract, ALU.mult))
    order.settle()
    for h in range(2):
        order.mark(dve.memset(s.vbd.rearrange("p b j (e v) -> p (b j) e v", v=VW)[h * SC:(h + 1) * SC, :, 1 - h, HD:VW], 0.0))
    if s.rope:
        cos = s.rotary["cos_k"].rearrange("p (o s) -> p o s", o=1).broadcast_to([P, B, SC])
        sin = s.rotary["sin_k"].rearrange("p (o s) -> p o s", o=1).broadcast_to([P, B, SC])
        for f in range(KD):
            dve.wait_ge(s.sems["swap_psum"], f + 1)
            order.mark(dve.tensor_tensor(s.rot2[:, f, :].rearrange("p (b s) -> p b s", s=SC),
                                         PS[:, f, :].rearrange("p (b s) -> p b s", s=SC), sin, ALU.mult))
            kf = s.kT[:, f, :].rearrange("p (b s) -> p b s", s=SC)
            order.mark(dve.tensor_tensor(kf, kf, cos, ALU.mult))
        order.settle()
        order.mark(dve.tensor_tensor(s.kT, s.kT, s.rot2, ALU.add))
    elif s.masked:
        dve.wait_ge(s.sems["k_ready"], KD)
        for f in range(KD):
            order.mark(dve.tensor_tensor(s.kT[:, f, :], s.kT[:, f, :], s.keep, ALU.mult))
    bv = s.bv.rearrange("p (j e d) -> p j e d", e=2, d=HD)
    order.settle()
    for b in range(B):
        dve.wait_ge(s.sems["v_psum"], b + 1)
        src = PS[:, 2 + b % 2, 0:D].rearrange("p (j e d) -> p j e d", e=2, d=HD)
        dst = s.vbd[:, b, :, :].rearrange("p j (e v) -> p j e v", v=VW)
        for h in range(2):
            r = slice(h * SC, (h + 1) * SC)
            dve.tensor_tensor(dst[r, :, h, 0:HD], src[r, :, h, :], bv[r, :, h, :], ALU.add).then_inc(s.sems["v_ready"], 1)
    dve.wait_ge(s.sems["k_ready"], KD)
    dve.wait_ge(s.sems["v_ready"], 2 * B)
    dve.tensor_scalar(s.gbo, s.bo, s.gate, None, ALU.mult).then_inc(s.sems["setup"], 1)

    def rotate(i, par, part):
        rot = s.rot[:, par, :, :]
        if part == 0:
            dve.wait_ge(s.sems["q_ready"], KD * (i + 1))
            order.mark(dve.tensor_tensor(rot, s.qT[:, 0, :, :],
                                         s.rotary["cos_q"].rearrange("p (o s) -> p o s", o=1).broadcast_to([P, KD, S]), ALU.mult))
        if part < KD:
            dve.wait_ge(s.sems["swap_psum"], KD * (i + 1) + part + 1)
            dve.tensor_tensor(s.rot2[:, part, :], PS[:, 0, :], s.rotary["sin_q"], ALU.mult).then_inc(s.sems["swap_read"], 1)
        if part == KD - 1:
            order.settle()
            dve.wait_ge(s.sems["swap_read"], KD * (i + 1))
            dve.tensor_tensor(rot, rot, s.rot2, ALU.add).then_inc(s.sems["q_roped"], 1)

    def turn(i, par, first=False, ahead=True, drain=False):
        n = UNITS * i
        for step in range(UNITS if not drain else 7):
            t = (step - 8) // 2
            if step % 2 == 0 and not (first if t < 0 else drain):
                dve.wait_ge(s.sems["y_psum"], TB * i + t + 1)
                if t == -TB:
                    dve.wait_ge(s.sems["biased"], i)
                tile = e.x_all[:, i * TB + t, :]
                dve.scalar_tensor_tensor(tile, PS[:, 1, D:2 * D], s.gate, tile, ALU.mult, ALU.add)\
                    .then_inc(e.x_updated, 1)
            if not drain:
                u = step
                dve.wait_ge(s.sems["scores"], n + u + 1)
                bank = PS[:, 2 + u % 2, :].rearrange("p (h s) -> p h s", s=SC)
                order.mark(dve.tensor_reduce(s.maxes[:, u % 2, :], bank, AX_X, ALU.max))
                order.settle()
                wait_for(dve, s.sems["exp_ready"], n + u - 1)
                dve.tensor_tensor(s.shifted[:, u % 2, :].rearrange("p (h s) -> p h s", s=SC), bank,
                                  s.maxes[:, u % 2, :].rearrange("p (h o) -> p h o", o=1).broadcast_to([P, HH, SC]),
                                  ALU.subtract).then_inc(s.sems["shifted_ready"], 1)
            t = (step - 5) // 2
            if step % 2 == 1 and not (first if t < 0 else drain):
                dve.wait_ge(s.sems["pv_psum"], 2 * (TB * i + t + 1))
                o = PS[:, 6 + t % 2, 0:NH * VW].rearrange("p (h v) -> p h v", v=VW)
                wait_for(dve, s.sems["o_ready"], TB * i + t - 1)
                order.mark(dve.reciprocal(s.recip[:, t % 2, :], o[:, :, HD]))
                order.settle()
                wait_for(dve, s.sems["oT_psum"], TB * i + t - 1)
                dve.tensor_tensor(s.o[:, t % 2, :].rearrange("p (h d) -> p h d", d=HD), o[:, :, 0:HD],
                                  s.recip[:, t % 2, :].rearrange("p (h o) -> p h o", o=1).broadcast_to([P, NH, HD]),
                                  ALU.mult).then_inc(s.sems["o_ready"], 1)
            if ahead:
                if step == 0:
                    for t in range(TB):
                        e.ln_stats(dve, order, i + 1, t)
                    e.ln_variance(dve, order, s)
                if step == 1:
                    e.ln_apply(dve, s, i + 1)
                if s.rope and step >= AHEAD_SWAP:
                    rotate(i + 1, 1 - par, step - AHEAD_SWAP)

    for t in range(TB):
        e.ln_stats(dve, order, 0, t)
    e.ln_variance(dve, order, s)
    e.ln_apply(dve, s, 0)
    for part in range(KD if s.rope else 0):
        rotate(0, 0, part)
    all_turns(dve, turn, order, 3 * TB + (1 if s.rope else 0) + e.LN_MARKS)


def xattn_pool(pool, order, e, s):
    nc = e.nc
    mask16 = e.const("head8" if s.rope else "head4").rearrange("p (h o) -> p h o", o=1).broadcast_to([P, HH, SC])
    pool.wait_ge(s.sems["setup"], 1)

    def keys(i, par):
        wait_for(pool, s.sems["scores"], UNITS * (i - 1))
        for f in range(KD):
            keys = s.kT[:, f, :].rearrange("p (b s) -> p b s", s=SC)[:, bass.ds(i, 1), :].broadcast_to([P, HH, SC])
            nc.gpsimd.tensor_tensor(s.kbd[:, par, f, :].rearrange("p (h s) -> p h s", s=SC), keys, mask16, ALU.mult)\
                .then_inc(s.sems["kbd_ready"], 1)

    def turn(i, par, first=False, ahead=True, drain=False):
        if ahead:
            e.pool_rstd(pool, s, i + 1)
        if not drain:
            pool.wait_ge(s.ln_ready, TB * (i + 1))
            tiles = e.x_all[:, bass.ds(i * TB, TB), :]
            nc.gpsimd.tensor_tensor(tiles, tiles, s.gbo.rearrange("p (o d) -> p o d", o=1).broadcast_to([P, TB, D]),
                                    ALU.add).then_inc(s.sems["biased"], 1)
        if ahead:
            keys(i + 1, 1 - par)

    e.pool_rstd(pool, s, 0)
    keys(0, 0)
    all_turns(pool, turn)


FF = 1024
KF = FF // P


def plan_ffn1(s, T, sem, small):
    take = s.w.take
    s.w1, s.w2 = take(KD, FF), take(KF, D)
    s.sc1, s.sc2 = take(KD, FF), take(KF, D)
    s.b1, s.gamma, s.beta, s.b2 = take(KF), take(KD), take(KD), take(D)
    n = {c: T["L1_ffn_" + c] for c in ("q1", "q2", "sc1", "sc2", "b1", "gamma", "beta", "b2")}
    s.q1, s.q2 = s.w1.bitcast(I32), s.w2.bitcast(I32)
    s.loads += [(s.q1, n["q1"].rearrange("p (k n) -> p k n", k=KD)), (s.q2, n["q2"].rearrange("p (k n) -> p k n", k=KF)),
                (s.sc1.rearrange("p k n -> p (k n)"), n["sc1"].broadcast_to([P, KD * FF])),
                (s.sc2.rearrange("p k n -> p (k n)"), n["sc2"].broadcast_to([P, KF * D])),
                (s.b1, n["b1"]), (s.gamma, n["gamma"]), (s.beta, n["beta"]), (s.b2, n["b2"].broadcast_to([P, D]))]
    take = s.a.take
    s.hn = take(TB, D)
    s.hT = take(KD, S)
    s.yT = take(KF, S)
    s.xng = take(TB, D)
    s.gb2 = take(D)
    s.half_gate = take(1)
    s.sems = {n: sem(f"{s.name}_{n}") for n in (
        "setup", "var2_ready", "rstd2_ready", "hn_ready", "up_psum", "y_ready", "down_psum", "residual")}
    s.looks_ahead = True
    s.pe, s.act, s.dve, s.pool = ffn1_pe, ffn1_act, ffn1_dve, ffn1_pool


def ffn1_pe(pe, e, s):
    PS, nc = e.PS, e.nc
    pe.wait_ge(s.sems["setup"], 1)

    def front(i):
        e.pe_transpose_xn(pe, s, i, src=s.hn, ready=s.sems["hn_ready"])

    front(0)
    with pe.Fori(0, B) as i:
        pe.wait_ge(s.xnT_ready, KD * (i + 1))
        for n in range(KF):
            if n >= 4:
                pe.wait_ge(s.sems["y_ready"], KF * i + n - 3)
            for k in range(KD):
                last = nc.tensor.matmul(PS[:, 2 + n % 4, :], s.w1[:, k, n * P:(n + 1) * P], s.hT[:, k, :],
                                        start=k == 0, stop=k == KD - 1)
            last.then_inc(s.sems["up_psum"], 1)
        for t in range(TB):
            if t == TB - 1:
                front(i + 1)
            pe.wait_ge(e.x_updated, s.x_before + TB * i + max(t - 1, 0))
            pe.wait_ge(s.sems["y_ready"], KF * (i + 1))
            for n in range(KF):
                last = nc.tensor.matmul(PS[:, 6 + t % 2, 0:D], s.yT[:, n, t * P:(t + 1) * P], s.w2[:, n, :],
                                        start=n == 0, stop=n == KF - 1)
            last.then_inc(s.sems["down_psum"], 1)


def ffn1_act(act, order, e, s):
    PS, nc = e.PS, e.nc
    act.wait_ge(s.weights_loaded, 16 * len(s.loads))

    def front(i):
        for k in range(KD):
            act.wait_ge(s.xnT_psum, KD * i + k + 1)
            nc.scalar.activation(s.hT[:, k, :], PS[:, k, :], ACT.Identity, bias=s.beta[:, k:k + 1],
                                 scale=s.gamma[:, k:k + 1]).then_inc(s.xnT_ready, 1)

    front(0)
    with act.Fori(0, B) as i:
        for n in range(KF):
            act.wait_ge(s.sems["up_psum"], KF * i + n + 1)
            if n == 0:
                act.wait_ge(s.sems["down_psum"], TB * i)
            nc.scalar.activation(s.yT[:, n, :], PS[:, 2 + n % 4, :], ACT.Silu, bias=s.b1[:, n:n + 1]).then_inc(s.sems["y_ready"], 1)
        front(i + 1)


def ffn1_dve(dve, order, e, s):
    PS = e.PS
    dve.wait_ge(s.weights_loaded, 16 * len(s.loads))
    order.mark(dve.scalar_tensor_tensor(s.w1, s.q1, 128.0, s.sc1, ALU.subtract, ALU.mult))
    order.mark(dve.scalar_tensor_tensor(s.w2, s.q2, 128.0, s.sc2, ALU.subtract, ALU.mult))
    order.mark(dve.tensor_scalar(s.half_gate, s.gate, 0.5, None, ALU.mult))
    order.settle()
    dve.tensor_scalar(s.gb2, s.b2, s.half_gate, None, ALU.mult).then_inc(s.sems["setup"], 1)

    def front(i):
        e.dve_layernorm(dve, order, s, i, last_read=(s.sems["residual"], 2 * i))
        dve.wait_ge(s.ln_ready, TB * (i + 1))
        for t in range(TB):
            order.mark(dve.bn_stats(e.stats[:, t, :], e.xn[:, t, :]))
        order.settle()
        dve.sem_inc(e.spare, 1)
        for t in range(TB):
            order.mark(dve.bn_aggr(e.mean_var[:, t, :], e.stats[:, t, :]))
        order.settle()
        dve.tensor_scalar(e.var_eps[:], e.mean_var[:, :, 1], LN_EPS, None, ALU.add).then_inc(s.sems["var2_ready"], 1)
        dve.wait_ge(s.sems["rstd2_ready"], i + 1)
        for t in range(TB):
            dve.tensor_scalar(s.hn[:, t, :], e.xn[:, t, :], e.mean_var[:, t, 0:1], e.rstd[:, t:t + 1],
                              ALU.subtract, ALU.mult).then_inc(s.sems["hn_ready"], 1)

    front(0)
    with dve.Fori(0, B) as i:
        order.turn(i, 2 * e.LN_MARKS)
        front(i + 1)
        for t in range(TB):
            dve.wait_ge(s.sems["down_psum"], TB * i + t + 1)
            if t == 0:
                dve.wait_ge(s.sems["residual"], 2 * (i + 1))
            tile = e.x_all[:, i * TB + t, :]
            dve.scalar_tensor_tensor(tile, PS[:, 6 + t % 2, 0:D], s.half_gate, tile, ALU.mult, ALU.add)\
                .then_inc(e.x_updated, 1)
    order.end(B)


def ffn1_pool(pool, order, e, s):
    nc = e.nc
    pool.wait_ge(s.sems["setup"], 1)

    def front(i):
        e.pool_rstd(pool, s, i)
        pool.wait_ge(s.sems["var2_ready"], i + 1)
        nc.gpsimd.tensor_tensor(e.rstd[:], e.var_eps[:], e.minus_half[:], ALU.pow).then_inc(s.sems["rstd2_ready"], 1)

    front(0)
    gate = s.gate.rearrange("p (o d) -> p o d", o=1).broadcast_to([P, TB, D])
    bias = s.gb2.rearrange("p (o d) -> p o d", o=1).broadcast_to([P, TB, D])
    with pool.Fori(0, B) as i:
        order.turn(i, 1)
        tiles = e.x_all[:, bass.ds(i * TB, TB), :]
        pool.wait_ge(s.sems["hn_ready"], TB * (i + 1))
        nc.gpsimd.tensor_tensor(s.xng, e.xn[:], gate, ALU.mult).then_inc(s.sems["residual"], 1)
        pool.wait_ge(s.sems["residual"], 2 * i + 1)
        order.mark(nc.gpsimd.tensor_tensor(s.xng, s.xng, bias, ALU.add))
        order.settle()
        nc.gpsimd.tensor_tensor(tiles, tiles, s.xng, ALU.add).then_inc(s.sems["residual"], 1)
        front(i + 1)
    order.end(B)


def plan_xattn2(s, T, sem, small):
    take = s.w.take
    s.wq, s.wk, s.wv = take(KD, D), take(KD, D), take(KD, D)
    s.bq, s.bk, s.bv = take(KD), take(KD), take(D)
    s.mask = take(TB, SC)
    n = {c: T[f"{s.name}_{c}"] for c in ("wq", "wk", "wv", "bq", "bk", "bv")}
    for c, w in (("wq", s.wq), ("wk", s.wk), ("wv", s.wv)):
        s.loads.append((w, n[c].rearrange("p (k n) -> p k n", k=KD)))
    s.loads += [(s.bq, n["bq"]), (s.bk, n["bk"]), (s.bv, n["bv"].broadcast_to([P, D])),
                (s.mask.bitcast(I32), T["mask_L2"].rearrange("(t p) s -> p t s", p=P))]
    take = s.a.take
    s.keep, s.bias = take(TB, SC), take(TB, SC)
    s.kT = take(KD, B * SC)
    s.bq_wide = take(KD, P)
    s.qk = take(KD, B * SC)
    s.qk_bias = take(B * SC)
    s.v = take(B, D)
    s.sc, s.probs = take(2, TB, SC), take(2, TB, SC)
    s.maxes, s.sums, s.scale = take(TB), take(TB), take(TB)
    s.probsT = take(TB, P)
    s.sems = {n: sem(f"{s.name}_{n}") for n in (
        "k_psum", "k_ready", "qk_psum", "qk_ready", "v_psum", "v_ready", "setup", "scores", "shifted_ready",
        "exp_ready", "pT_psum", "pT_ready", "out_psum", "scaled")}
    s.pe, s.act, s.dve, s.pool = xattn2_pe, xattn2_act, xattn2_dve, xattn2_pool


def xattn2_pe(pe, e, s):
    PS, nc = e.PS, e.nc
    pe.wait_ge(s.weights_loaded, 16 * len(s.loads))
    for f in range(KD):
        for k in range(KD):
            last = nc.tensor.matmul(PS[:, f, :], s.wk[:, k, f * P:(f + 1) * P], e.ctx2T[:, k, :, 0:SC],
                                    start=k == 0, stop=k == KD - 1)
        last.then_inc(s.sems["k_psum"], 1)
    pe.wait_ge(s.sems["k_ready"], KD + 1)
    for f in range(KD + 1):
        for k in range(KD):
            lhsT = s.wq[:, k, f * P:(f + 1) * P] if f < KD else s.bq_wide[:, k, :]
            last = nc.tensor.matmul(PS[:, 2 + f, :], lhsT, s.kT[:, k, :], start=k == 0, stop=k == KD - 1)
        last.then_inc(s.sems["qk_psum"], 1)
    for b in range(B):
        if b >= 2:
            pe.wait_ge(s.sems["v_ready"], b - 1)
        for k in range(KD):
            last = nc.tensor.matmul(PS[0:SC, 5 + b % 2, 0:D], e.ctx2T[:, k, b, 0:SC], s.wv[:, k, :],
                                    start=k == 0, stop=k == KD - 1)
        last.then_inc(s.sems["v_psum"], 1)
    pe.wait_ge(s.sems["setup"], 1)
    e.pe_transpose_xn(pe, s, 0)

    def turn(i, par, first=False, ahead=True, drain=False):
        if not drain:
            pe.wait_ge(s.xnT_ready, KD * (i + 1))
            wait_for(pe, s.sems["shifted_ready"], i - 1)
            for t in range(TB):
                for k in range(KD):
                    rhs = s.qk[:, k, :].rearrange("p (b s) -> p b s", s=SC)[:, bass.ds(i, 1), :]
                    last = nc.tensor.matmul(PS[:, 2 + par, t * SC:(t + 1) * SC], e.xnT[:, k, t * P:(t + 1) * P], rhs,
                                            start=k == 0, stop=k == KD - 1)
            last.then_inc(s.sems["scores"], 1)
        if not first:
            pe.wait_ge(s.sems["exp_ready"], i)
            pe.sem_inc(e.spare, 1)
            for t in range(TB):
                last = nc.tensor.transpose(PS[0:SC, 4, t * P:(t + 1) * P], s.probs[:, 1 - par, t, :], e.ident)
            last.then_inc(s.sems["pT_psum"], 1)
        if ahead:
            e.pe_transpose_xn(pe, s, i + 1)
        if not first:
            pe.wait_ge(s.sems["pT_ready"], i)
            pe.wait_ge(e.x_updated, s.x_before + TB * (i - 1))
            pe.sem_inc(e.spare, 1)
            for t in range(TB):
                last = nc.tensor.matmul(PS[:, 5 + t // 2, t % 2 * D:(t % 2 + 1) * D], s.probsT[0:SC, t, :],
                                        s.v[0:SC, bass.ds(i - 1, 1), :], start=True, stop=True)
                if t % 2 == 1:
                    last.then_inc(s.sems["out_psum"], 1)

    all_turns(pe, turn)


def xattn2_act(act, order, e, s):
    PS, nc = e.PS, e.nc
    act.wait_ge(s.weights_loaded, 16 * len(s.loads))
    for f in range(KD):
        act.wait_ge(s.sems["k_psum"], f + 1)
        nc.scalar.activation(s.kT[:, f, :], PS[:, f, :], ACT.Identity, bias=s.bk[:, f:f + 1]).then_inc(s.sems["k_ready"], 1)
    for f in range(KD + 1):
        act.wait_ge(s.sems["qk_psum"], f + 1)
        nc.scalar.activation(s.qk[:, f, :] if f < KD else s.qk_bias, PS[:, 2 + f, :], ACT.Copy).then_inc(s.sems["qk_ready"], 1)
    e.act_copy_xnT(act, s, 0)

    def turn(i, par, first=False, ahead=True, drain=False):
        if not first:
            act.wait_ge(s.sems["pT_psum"], i)
            nc.scalar.activation(s.probsT[0:SC, :, :], PS[0:SC, 4, :].rearrange("p (t n) -> p t n", n=P), ACT.Copy)\
                .then_inc(s.sems["pT_ready"], 1)
        if ahead:
            act.wait_ge(s.sems["scores"], i + 1)
            e.act_copy_xnT(act, s, i + 1)
        if not drain:
            act.wait_ge(s.sems["shifted_ready"], i + 1)
            wait_for(act, s.sems["scaled"], i - 1)
            nc.scalar.activation(s.probs[:, par, :, :], s.sc[:, par, :, :], ACT.Exp).then_inc(s.sems["exp_ready"], 1)

    all_turns(act, turn)


def xattn2_dve(dve, order, e, s):
    PS = e.PS
    dve.wait_ge(s.weights_loaded, 16 * len(s.loads))
    dve.tensor_copy(s.bq_wide, s.bq.rearrange("p (k o) -> p k o", o=1).broadcast_to([P, KD, P])).then_inc(s.sems["k_ready"], 1)
    order.mark(dve.tensor_scalar(s.keep, s.mask.bitcast(I32), 0.0, None, ALU.not_equal))
    order.settle()
    order.mark(dve.tensor_scalar(s.bias, s.keep, 1.0, 1e9, ALU.subtract, ALU.mult))
    for b in range(B):
        dve.wait_ge(s.sems["v_psum"], b + 1)
        dve.tensor_tensor(s.v[0:SC, b, :], PS[0:SC, 5 + b % 2, 0:D], s.bv[0:SC, :], ALU.add).then_inc(s.sems["v_ready"], 1)
    dve.wait_ge(s.sems["qk_ready"], KD + 1)
    dve.wait_ge(s.sems["v_ready"], B)
    dve.sem_inc(s.sems["setup"], 1)
    e.dve_layernorm(dve, order, s, 0)

    def turn(i, par, first=False, ahead=True, drain=False):
        if ahead:
            e.dve_layernorm(dve, order, s, i + 1)
        if not drain:
            dve.wait_ge(s.sems["scores"], i + 1)
            wait_for(dve, s.sems["exp_ready"], i - 1)
            wait_for(dve, s.sems["shifted_ready"], i)
            sc = s.sc[:, par, :, :]
            qk_bias = s.qk_bias.rearrange("p (b s) -> p b s", s=SC)[:, bass.ds(i, 1), :].broadcast_to([P, TB, SC])
            order.mark(dve.tensor_tensor(sc, PS[:, 2 + par, 0:TB * SC].rearrange("p (t s) -> p t s", s=SC), qk_bias, ALU.add))
            order.settle()
            order.mark(dve.tensor_tensor(sc, sc, s.keep, ALU.mult))
            order.settle()
            order.mark(dve.tensor_tensor(sc, sc, s.bias, ALU.add))
            order.settle()
            order.mark(dve.tensor_reduce(s.maxes, sc, AX_X, ALU.max))
            order.settle()
            dve.tensor_tensor(sc, sc, s.maxes.rearrange("p (t o) -> p t o", o=1).broadcast_to([P, TB, SC]), ALU.subtract)\
                .then_inc(s.sems["shifted_ready"], 1)
        if not first:
            dve.wait_ge(s.sems["exp_ready"], i)
            dve.wait_ge(e.x_updated, s.x_before + TB * (i - 1))
            order.mark(dve.tensor_reduce(s.sums, s.probs[:, 1 - par, :, :], AX_X, ALU.add))
            order.settle()
            order.mark(dve.reciprocal(s.scale, s.sums))
            order.settle()
            dve.sem_inc(s.sems["scaled"], 1)
            order.mark(dve.tensor_scalar(s.scale, s.scale, s.gate, None, ALU.mult))
            order.settle()
            for t in range(TB):
                dve.wait_ge(s.sems["out_psum"], 2 * (i - 1) + t // 2 + 1)
                tile = e.x_all[:, (i - 1) * TB + t, :]
                dve.scalar_tensor_tensor(tile, PS[:, 5 + t // 2, t % 2 * D:(t % 2 + 1) * D], s.scale[:, t:t + 1], tile,
                                         ALU.mult, ALU.add).then_inc(e.x_updated, 1)

    all_turns(dve, turn, order, e.LN_MARKS + 7)


def xattn2_pool(pool, order, e, s):
    e.pool_rstd(pool, s, 0)

    def turn(i, par, first=False, ahead=True, drain=False):
        if ahead:
            e.pool_rstd(pool, s, i + 1)

    all_turns(pool, turn)


GATES = ("f", "i", "c")


def plan_ffn2(s, T, sem, small):
    take = s.w.take
    s.wx = [take(KD, D) for _ in GATES]
    s.wc = [take(KD, D) for _ in GATES]
    s.wo, s.uo = take(KD, D), take(KD, D)
    s.bg = take(3, KD)
    s.bo, s.c0 = take(D), take(KD)
    for g, n in enumerate(GATES):
        s.loads.append((s.wx[g], T[f"L2_ffn_w{n}"].rearrange("p (k n) -> p k n", k=KD)))
        s.loads.append((s.wc[g], T[f"L2_ffn_u{n}"].rearrange("p (k n) -> p k n", k=KD)))
        s.loads.append((s.bg[:, g, :], T[f"L2_ffn_b{n}"]))
    s.loads += [(s.wo, T["L2_ffn_wo"].rearrange("p (k n) -> p k n", k=KD)),
                (s.uo, T["L2_ffn_uo"].rearrange("p (k n) -> p k n", k=KD)),
                (s.bo, T["L2_ffn_bo"].broadcast_to([P, D])), (s.c0, T["L2_ffn_in_c"])]
    take = s.a.take
    s.cT = take(KD, S)
    s.gates = take(3, KD, S)
    s.own = take(NT, D)
    s.last = take(TB, D)
    s.sems = {n: sem(f"{s.name}_{n}") for n in (
        "added", "gate_psum", "gate_ready", "c_ready", "own_psum", "own_ready", "last_psum", "sum_ready", "tanh_ready")}
    s.looks_ahead = True
    s.pe, s.act, s.dve, s.pool = ffn2_pe, ffn2_act, ffn2_dve, ffn2_pool


def ffn2_pe(pe, e, s):
    PS, nc = e.PS, e.nc
    pe.wait_ge(s.weights_loaded, 16 * len(s.loads))
    NG = 3 * KD
    e.pe_transpose_xn(pe, s, 0)
    pe.wait_ge(s.sems["c_ready"], 1)
    with pe.Fori(0, B) as i:
        pe.wait_ge(s.xnT_ready, KD * (i + 1))
        for g in range(3):
            for m in range(KD):
                pe.wait_ge(s.sems["gate_ready"], NG * i)
                for k in range(KD):
                    nc.tensor.matmul(PS[:, 2 + KD * g + m, :], s.wx[g][:, k, m * P:(m + 1) * P], e.xnT[:, k, :],
                                     start=k == 0, stop=False)
        for t in range(TB):
            for k in range(KD):
                last = nc.tensor.matmul(PS[:, t // 2, (t % 2) * D:(t % 2 + 1) * D], e.xnT[:, k, t * P:(t + 1) * P],
                                        s.wo[:, k, :], start=k == 0, stop=k == KD - 1)
            last.then_inc(s.sems["own_psum"], 1)
        pe.wait_ge(s.sems["c_ready"], i + 1)
        for g in range(3):
            for m in range(KD):
                for k in range(KD):
                    last = nc.tensor.matmul(PS[:, 2 + KD * g + m, :], s.wc[g][:, k, m * P:(m + 1) * P], s.cT[:, k, :],
                                            start=False, stop=k == KD - 1)
                last.then_inc(s.sems["gate_psum"], 1)
        pe.wait_ge(s.sems["own_ready"], TB * (i + 1))
        e.pe_transpose_xn(pe, s, i + 1)
    pe.wait_ge(s.sems["c_ready"], B + 1)
    for t in range(TB):
        for k in range(KD):
            last = nc.tensor.matmul(PS[:, 2 + t // 2, (t % 2) * D:(t % 2 + 1) * D], s.cT[:, k, t * P:(t + 1) * P],
                                    s.uo[:, k, :], start=k == 0, stop=k == KD - 1)
    last.then_inc(s.sems["last_psum"], 1)


def ffn2_act(act, order, e, s):
    PS, nc = e.PS, e.nc
    act.wait_ge(s.weights_loaded, 16 * len(s.loads))
    e.act_copy_xnT(act, s, 0)
    NG = 3 * KD
    with act.Fori(0, B) as i:
        act.wait_ge(s.sems["c_ready"], i + 1)
        for g in range(3):
            for m in range(KD):
                act.wait_ge(s.sems["gate_psum"], NG * i + KD * g + m + 1)
                nc.scalar.activation(s.gates[:, g, m, :], PS[:, 2 + KD * g + m, :], ACT.Tanh if g == 2 else ACT.Sigmoid,
                                     bias=s.bg[:, g, m:m + 1]).then_inc(s.sems["gate_ready"], 1)
        e.act_copy_xnT(act, s, i + 1)
    with act.Fori(0, B) as i:
        act.wait_ge(s.sems["sum_ready"], i + 1)
        own = s.own[:, bass.ds(i * TB, TB), :]
        nc.scalar.activation(own, own, ACT.Tanh).then_inc(s.sems["tanh_ready"], 1)


def ffn2_dve(dve, order, e, s):
    PS = e.PS
    dve.wait_ge(s.weights_loaded, 16 * len(s.loads))
    NG = 3 * KD
    dve.tensor_copy(s.cT, s.c0.rearrange("p (k o) -> p k o", o=1).broadcast_to([P, KD, S])).then_inc(s.sems["c_ready"], 1)
    e.dve_layernorm(dve, order, s, 0)
    with dve.Fori(0, B) as i:
        order.turn(i, e.LN_MARKS + 2)
        for t in range(TB):
            dve.wait_ge(s.sems["own_psum"], TB * i + 2 * (t // 2) + 2)
            dve.tensor_tensor(s.own[:, i * TB + t, :], PS[:, t // 2, (t % 2) * D:(t % 2 + 1) * D], s.bo, ALU.add)\
                .then_inc(s.sems["own_ready"], 1)
        e.dve_layernorm(dve, order, s, i + 1)
        dve.wait_ge(s.sems["gate_ready"], NG * i + 2 * KD)
        dve.wait_ge(s.sems["c_ready"], i + 1)
        dve.wait_ge(s.sems["gate_psum"], NG * (i + 1))
        order.mark(dve.tensor_tensor(s.cT, s.cT, s.gates[:, 0, :, :], ALU.mult))
        dve.wait_ge(s.sems["gate_ready"], NG * (i + 1))
        order.mark(dve.tensor_tensor(s.gates[:, 1, :, :], s.gates[:, 1, :, :], s.gates[:, 2, :, :], ALU.mult))
        order.settle()
        dve.tensor_tensor(s.cT, s.cT, s.gates[:, 1, :, :], ALU.add).then_inc(s.sems["c_ready"], 1)
    order.end(B)
    dve.wait_ge(s.sems["own_ready"], NT)
    dve.wait_ge(s.sems["last_psum"], 1)
    order.mark(dve.tensor_copy(s.last, PS[:, 2:4, :].rearrange("p b (t d) -> p (b t) d", d=D)))
    order.settle()
    with dve.Fori(0, B) as i:
        own = s.own[:, bass.ds(i * TB, TB), :]
        dve.tensor_tensor(own, own, s.last, ALU.add).then_inc(s.sems["sum_ready"], 1)
    with dve.Fori(0, B) as i:
        dve.wait_ge(s.sems["tanh_ready"], i + 1)
        tiles = e.x_all[:, bass.ds(i * TB, TB), :]
        dve.scalar_tensor_tensor(tiles, s.own[:, bass.ds(i * TB, TB), :], s.gate, tiles, ALU.mult, ALU.add)\
            .then_inc(s.sems["added"], 1)
    dve.wait_ge(s.sems["added"], B)
    dve.sem_inc(e.x_updated, NT)


def ffn2_pool(pool, order, e, s):
    e.pool_rstd(pool, s, 0)
    with pool.Fori(0, B) as i:
        e.pool_rstd(pool, s, i + 1)


def plan_moe(s, T, sem, small):
    s.stores = True
    s.T = T
    first = W_N - 2 * E_N
    assert first >= 0 and first + NE * E_N <= 2 * W_N + A_N
    s.experts = s.mem[:, first:first + NE * E_N].rearrange("p (e n) -> p e n", e=NE)
    s.expert_loads = [(s.experts[:, (e + 2) % NE, :], T["L3_ffn_experts"][e]) for e in range(NE)]
    s.loads = s.expert_loads[:2]
    c = Carver(small, 0, MOE_N)
    s.gate_w, s.rms_w = c.take(KD, NE), c.take(D)
    s.small_loads = [(s.gate_w, T["L3_ffn_gate_w"].rearrange("p (k n) -> p k n", k=KD)),
                     (s.rms_w, T["L3_ffn_rms_w"].broadcast_to([P, D]))]
    s.mean_var, s.var_eps, s.rstd = c.take(NT, 2), c.take(NT), c.take(NT)
    s.ms, s.rrms, s.minus_half = c.take(NT), c.take(NT), c.take(NT)
    c2 = Carver(small, c.at, c.at + 2 * KE * P)
    s.hT = c.take(2, KE, P)
    s.logits, s.top = c2.take(NT, NE), c2.take(NT, 8)
    s.index = c2.take(NT, 8).bitcast(mybir.dt.uint32)
    s.pick = [c2.take(NT, NE), c2.take(NT, NE)]
    s.picked = c2.take(NT, NE)
    s.index_f = c.take(NT, 2)
    s.total, s.cum = c.take(NE, NT), c.take(NE, NT)
    s.count, s.pad, s.padcum, s.base = c.take(NE), c.take(NE), c.take(NE), c.take(NE)
    s.slot = c.take(2, NT)
    s.slot_u = c.take(2, NT).bitcast(mybir.dt.uint32)
    s.w = c.take(2, NT)
    s.tile_expert, s.tile_wrap = c.take(MOE_TILES), c.take(MOE_TILES)
    s.tile_slot = c.take(MOE_TILES).bitcast(I32)
    s.sems = {n: sem(f"{s.name}_{n}") for n in (
        "experts_loaded", "msq_ready", "rrms_ready", "y_ready", "y_kept", "logits_psum", "logits_kept",
        "residual", "residual_stored0", "residual_stored1", "residual_loaded", "dispatch", "picked", "ranks_psum", "rows_placed", "slots_ready", "exp2",
        "rowT_psum", "rowT_ready", "up_psum", "gate_psum", "silu_ready",
        "h_ready", "hT_psum", "hT_ready", "y_psum", "y_copied", "y_stored", "final")}
    s.row_loaded_s = [sem(f"{s.name}_row_loaded{n}") for n in range(2)]
    s.small_loaded_s, s.zeroed_s, s.row_scattered_s = [s.own_sem(f"{s.name}_{n}") for n in ("small_loaded", "zeroed", "row_scattered")]
    s.gathered_s = [s.own_sem(f"{s.name}_gathered{b}") for b in range(B)]
    s.early_sync_program, s.sync_program = moe_early_sync, moe_sync
    s.pe, s.act, s.dve, s.pool = moe_pe, moe_act, moe_dve, moe_pool


def moe_buffers(e, s):
    m = Names()
    flat = e.ctx2T[:, :, :, :].rearrange("p k b s -> p (k b s)")
    m.y = flat[:, 0:TB * D].rearrange("p (t d) -> p t d", d=D)
    m.residual = flat[:, TB * D:2 * TB * D].rearrange("p (t d) -> p t d", d=D)
    m.rowT = flat[:, 0:2 * D].rearrange("p (b k n) -> p b k n", k=KD, n=P)
    m.h = flat[:, 2 * D:2 * D + 2 * DE].rearrange("p (b n) -> p b n", n=DE)
    m.row, m.result = e.xn[:, 0:2, :], e.xn[:, 2:4, :]
    m.hT = s.hT
    m.gathered = s.mem[:, 0:2 * NT * D].rearrange("p (c t d) -> p c t d", c=2, d=D)
    return m


def moe_early_sync(sp, e, s):
    for dst, src in s.small_loads:
        sp.dma_start(dst, src).then_inc(s.small_loaded_s, 16)
    sp.wait_ge(e.zeros_ready, 1)
    slots = s.T["slots"].rearrange("(g t p) d -> g p t d", p=P, t=TB)
    for g in range(MOE_TILES // TB):
        sp.dma_start(slots[g], e.x_all[:, NT:NT + TB, :]).then_inc(s.zeroed_s, 16)


def moe_sync(sp, e, s):
    e.stage_start(sp, s)
    for dst, src in s.expert_loads[2:]:
        sp.dma_start(dst, src).then_inc(s.sems["experts_loaded"], 16)
    residual = s.T["residual"].rearrange("(b t p) d -> b p t d", p=P, t=TB)
    m = moe_buffers(e, s)
    with sp.Fori(0, B // 2) as j:
        for h, part in enumerate((e.xn[:], m.residual)):
            sp.wait_ge(s.sems["residual"], 2 * j + h + 1)
            sp.sem_inc(e.spare, 1)
            sp.dma_start(residual[bass.ds(2 * j + h, 1)].rearrange("o p t d -> (o p) t d"), part)\
                .then_inc(s.sems[f"residual_stored{h}"], 16)
    for h in range(2):
        sp.wait_ge(s.sems[f"residual_stored{h}"], 16 * B // 2)
    sp.wait_ge(s.row_scattered_s, 16 * 2 * NT)
    sp.dma_start(e.x_all[:, 0:NT, :], s.T["residual"].rearrange("(t p) d -> p t d", p=P)).then_inc(s.sems["residual_loaded"], 16)
    rows_in = s.T["slots"].rearrange("(j p) d -> j p d", p=P)

    def load(j, par):
        sp.dma_start(m.row[:, par, :], rows_in[bass.ds(j, 1)].rearrange("o p d -> (o p) d")).then_inc(s.row_loaded_s[par], 16)

    load(0, 0)
    load(1, 1)
    with sp.Fori(0, MOE_TILES // 2 - 1) as i:
        for par in range(2):
            j = 2 * i + 2 + par
            sp.wait_ge(s.sems["rowT_psum"], j - 1)
            load(j, par)
    out = s.T["out"].rearrange("b (t p) d -> b p t d", p=P)
    for b in range(B):
        sp.wait_ge(s.sems["final"], TB * (b + 1))
        sp.dma_start(out[b], e.x_all[:, b * TB:(b + 1) * TB, :]).then_inc(e.out_stored, 16)
    sp.wait_ge(e.out_stored, 16 * B)


def moe_pe(pe, e, s):
    PS, nc = e.PS, e.nc
    m = moe_buffers(e, s)
    pe.wait_ge(s.small_loaded_s, 32)
    with pe.Fori(0, B) as i:
        e.pe_transpose_xn(pe, s, i, src=m.y, ready=s.sems["y_ready"])
        pe.wait_ge(s.xnT_ready, KD * (i + 1))
        pe.wait_ge(s.sems["logits_kept"], i)
        for t in range(TB):
            for k in range(KD):
                last = nc.tensor.matmul(PS[:, 2, t * NE:(t + 1) * NE], e.xnT[:, k, t * P:(t + 1) * P], s.gate_w[:, k, :],
                                        start=k == 0, stop=k == KD - 1)
        last.then_inc(s.sems["logits_psum"], 1)
    pe.wait_ge(s.sems["picked"], 1)
    picked = s.picked.rearrange("p t e -> p (t e)")
    nc.tensor.matmul(PS[:, 3, 0:NT * NE], e.const("before"), picked, start=True, stop=True)
    nc.tensor.matmul(PS[:, 4, 0:NT * NE], e.const("ones"), picked, start=True, stop=True).then_inc(s.sems["ranks_psum"], 1)
    pe.wait_ge(s.sems["slots_ready"], 1)
    pe.wait_ge(s.weights_loaded, 32)
    pe.wait_ge(s.sems["experts_loaded"], 16 * (NE - 2))

    def expert(j):
        return pe.value_load(s.tile_slot[0:1, bass.ds(j, 1)], min_val=0, max_val=NE - 1)

    def turn_rows(j, par, nth):
        pe.wait_ge(s.row_loaded_s[par], 16 * nth)
        pe.wait_ge(s.sems["rowT_ready"], j)
        for k in range(KD):
            last = nc.tensor.transpose(PS[:, 0, k * P:(k + 1) * P], m.row[:, par, k * P:(k + 1) * P], e.ident)
        last.then_inc(s.sems["rowT_psum"], 1)

    def widen(j, par):
        w = s.experts[:, bass.ds(expert(j), 1), :]
        pe.wait_ge(s.sems["rowT_ready"], j + 1)
        pe.wait_ge(s.sems["h_ready"], 2 * j)
        for g in range(2):
            for half in range(2):
                for k in range(KD):
                    at = (g * KD + k) * DE + half * HE
                    last = nc.tensor.matmul(PS[:, 1 + 2 * g + half, 0:HE], m.rowT[:, par, k, :], w[:, :, at:at + HE],
                                            start=k == 0, stop=k == KD - 1)
                last.then_inc(s.sems["gate_psum"] if g else s.sems["up_psum"], 1)

    def turn_hidden(j, par):
        pe.wait_ge(s.sems["h_ready"], 2 * (j + 1))
        pe.wait_ge(s.sems["hT_ready"], 2 * j)
        for n in range(KE):
            wide = min(P, DE - n * P)
            last = nc.tensor.transpose(PS[0:wide, 5 + n // 4, (n % 4) * P:(n % 4 + 1) * P],
                                       m.h[:, par, n * P:n * P + wide], e.ident)
            if n in (3, KE - 1):
                last.then_inc(s.sems["hT_psum"], 1)

    def narrow(j, par):
        w = s.experts[:, bass.ds(expert(j), 1), :]
        pe.wait_ge(s.sems["hT_ready"], 2 * (j + 1))
        pe.wait_ge(s.sems["y_copied"], j)
        for n in range(KE):
            at = 2 * KD * DE + n * D
            last = nc.tensor.matmul(PS[:, 7, 0:D], m.hT[:, par, n, :], w[:, :, at:at + D], start=n == 0, stop=n == KE - 1)
        last.then_inc(s.sems["y_psum"], 1)

    turn_rows(0, 0, 1)
    widen(0, 0)
    turn_rows(1, 1, 1)
    with pe.Fori(0, MOE_TILES // 2 - 1) as i:
        for par in (1, 0):
            j = 2 * i + (1 if par else 2)
            turn_hidden(j - 1, 1 - par)
            widen(j, par)
            turn_rows(j + 1, 1 - par, i + 2)
            narrow(j - 1, 1 - par)
    turn_hidden(MOE_TILES - 2, 0)
    widen(MOE_TILES - 1, 1)
    narrow(MOE_TILES - 2, 0)
    turn_hidden(MOE_TILES - 1, 1)
    narrow(MOE_TILES - 1, 1)


def moe_act(act, order, e, s):
    PS, nc = e.PS, e.nc
    m = moe_buffers(e, s)
    with act.Fori(0, B) as i:
        e.act_copy_xnT(act, s, i)
        act.wait_ge(s.sems["residual"], i + 1)
        nc.scalar.activation(e.x_all[:, bass.ds(i * TB, TB), :], m.y, ACT.Copy).then_inc(s.sems["y_kept"], 1)
        act.wait_ge(s.sems["logits_psum"], i + 1)
        nc.scalar.activation(s.logits[:, bass.ds(i * TB, TB), :], PS[:, 2, 0:TB * NE].rearrange("p (t e) -> p t e", e=NE), ACT.Copy)\
            .then_inc(s.sems["logits_kept"], 1)
    act.wait_ge(s.sems["dispatch"], 1)
    nc.scalar.activation(s.w[:, 1, :], s.w[:, 1, :], ACT.Exp).then_inc(s.sems["exp2"], 1)
    act.wait_ge(s.sems["slots_ready"], 1)
    for h in range(2):
        act.wait_ge(s.sems[f"residual_stored{h}"], 16 * B // 2)
    rows_out = s.T["results"].rearrange("(j p) d -> j p d", p=P)

    def copy_row(j, par):
        act.wait_ge(s.sems["rowT_psum"], j + 1)
        if not isinstance(j, int):
            act.wait_ge(s.sems["gate_psum"], 2 * (j - 1))
        nc.scalar.activation(m.rowT[:, par, :, :], PS[:, 0, 0:D].rearrange("p (k n) -> p k n", k=KD), ACT.Copy)\
            .then_inc(s.sems["rowT_ready"], 1)

    def silu(j, par):
        for half in range(2):
            act.wait_ge(s.sems["up_psum"], 2 * j + half + 1)
            if not (isinstance(j, int) and j < 2):
                act.wait_ge(s.sems["hT_psum"], 2 * (j - 1))
            nc.scalar.activation(m.h[:, par, half * HE:(half + 1) * HE], PS[:, 1 + half, 0:HE], ACT.Silu)\
                .then_inc(s.sems["silu_ready"], 1)

    def result(j, par):
        act.wait_ge(s.sems["y_psum"], j + 1)
        act.wait_ge(s.sems["y_stored"], 16 * j)
        nc.scalar.activation(m.result[:, par, :], PS[:, 7, 0:D], ACT.Copy).then_inc(s.sems["y_copied"], 1)
        act.wait_ge(s.sems["y_copied"], j + 1)
        act.dma_start(rows_out[bass.ds(j, 1)].rearrange("o p d -> (o p) d"), m.result[:, par, :]).then_inc(s.sems["y_stored"], 16)

    copy_row(0, 0)
    silu(0, 0)
    copy_row(1, 1)
    with act.Fori(0, MOE_TILES // 2 - 1) as i:
        for par in (1, 0):
            j = 2 * i + (1 if par else 2)
            silu(j, par)
            copy_row(j + 1, 1 - par)
            result(j - 1, 1 - par)
    silu(MOE_TILES - 1, 1)
    result(MOE_TILES - 2, 0)
    result(MOE_TILES - 1, 1)


def moe_dve(dve, order, e, s):
    PS = e.PS
    m = moe_buffers(e, s)
    dve.wait_ge(s.small_loaded_s, 32)
    with dve.Fori(0, B) as i:
        order.turn(i, 2 * TB + 1)
        for t in range(TB):
            order.mark(dve.bn_stats(e.stats[:, t, :], e.x_all[:, i * TB + t, :]))
        order.settle()
        dve.sem_inc(e.spare, 1)
        for t in range(TB):
            order.mark(dve.bn_aggr(e.mean_var[:, t, :], e.stats[:, t, :]))
        order.settle()
        order.mark(dve.tensor_copy(s.mean_var[:, bass.ds(i * TB, TB), :], e.mean_var[:]))
    order.end(B)
    order.settle()
    dve.tensor_scalar(s.var_eps, s.mean_var[:, :, 1], LN_EPS, None, ALU.add).then_inc(s.var_ready, 1)
    dve.wait_ge(s.rstd_ready, 1)
    order.mark(dve.tensor_tensor(s.ms, s.rstd, s.rstd, ALU.mult))
    order.settle()
    order.mark(dve.tensor_tensor(s.ms, s.ms, s.mean_var[:, :, 1], ALU.mult))
    order.settle()
    dve.tensor_scalar(s.ms, s.ms, 1e-6, None, ALU.add).then_inc(s.sems["msq_ready"], 1)
    dve.wait_ge(s.sems["rrms_ready"], 1)
    with dve.Fori(0, B // 2) as j:
        for h, xn in enumerate((e.xn[:], m.residual)):
            i = 2 * j + h
            dve.wait_ge(s.sems[f"residual_stored{h}"], 16 * j)
            dve.sem_inc(e.spare, 1)
            for t in range(TB):
                at = i * TB + t
                dve.tensor_scalar(xn[:, t, :], e.x_all[:, at, :], s.mean_var[:, bass.ds(at, 1), 0], s.rstd[:, bass.ds(at, 1)],
                                  ALU.subtract, ALU.mult).then_inc(s.ln_ready, 1)
            dve.wait_ge(s.ln_ready, TB * (i + 1))
            dve.wait_ge(s.sems["y_kept"], i)
            dve.wait_ge(s.xnT_psum, KD * i)
            dve.sem_inc(e.spare, 1)
            for t in range(TB):
                dve.scalar_tensor_tensor(m.y[:, t, :], xn[:, t, :], s.rrms[:, bass.ds(i * TB + t, 1)], s.rms_w,
                                         ALU.mult, ALU.mult).then_inc(s.sems["y_ready"], 1)
            dve.wait_ge(s.sems["y_ready"], TB * (i + 1))
            dve.scalar_tensor_tensor(xn, xn, s.gate, e.x_all[:, bass.ds(i * TB, TB), :], ALU.mult, ALU.add)\
                .then_inc(s.sems["residual"], 1)
    dve.wait_ge(s.sems["logits_kept"], B)

    def step(ins):
        order.mark(ins)
        order.settle()

    def wide(ap, axis, shape):
        return ap.rearrange("p (o a) -> p o a" if axis == 0 else "p (a o) -> p a o", o=1).broadcast_to(shape)

    for t in range(NT):
        order.mark(dve.max(s.top[:, t, :], s.logits[:, t, :]))
    order.settle()
    for t in range(NT):
        order.mark(dve.max_index(s.index[:, t, :], s.top[:, t, :], s.logits[:, t, :]))
    order.settle()
    dve.tensor_tensor(s.w[:, 1, :], s.top[:, :, 1], s.top[:, :, 0], ALU.subtract).then_inc(s.sems["dispatch"], 1)
    step(dve.tensor_copy(s.index_f, s.index[:, :, 0:2]))
    for c in range(2):
        step(dve.tensor_tensor(s.pick[c], wide(e.const("expert"), 0, [P, NT, NE]),
                               wide(s.index_f[:, :, c], 1, [P, NT, NE]), ALU.is_equal))
    dve.tensor_tensor(s.picked, s.pick[0], s.pick[1], ALU.add).then_inc(s.sems["picked"], 1)
    dve.wait_ge(s.sems["ranks_psum"], 1)
    step(dve.tensor_copy(s.total, PS[:, 4, 0:NT * NE].rearrange("p (t e) -> p e t", e=NE)))
    flat = s.total.rearrange("p e t -> p (e t)")
    step(dve.tensor_tensor_scan(s.cum.rearrange("p e t -> p (e t)"), flat, flat, 0.0, ALU.add, ALU.max))
    step(dve.tensor_tensor(s.count, s.cum[:, :, NT - 1], s.cum[:, :, 0], ALU.subtract))
    step(dve.tensor_tensor(s.count, s.count, s.total[:, :, 0], ALU.add))
    step(dve.tensor_tensor(s.cum, s.cum, s.total, ALU.subtract))
    step(dve.tensor_scalar(s.pad.bitcast(I32), s.count, P - 1.0, None, ALU.add))
    step(dve.tensor_scalar(s.pad.bitcast(I32), s.pad.bitcast(I32), 7, 7, ALU.logical_shift_right, ALU.logical_shift_left))
    step(dve.tensor_copy(s.count, s.pad.bitcast(I32)))
    step(dve.tensor_tensor_scan(s.padcum, s.count, s.count, 0.0, ALU.add, ALU.max))
    step(dve.tensor_tensor(s.base, s.padcum, s.count, ALU.subtract))
    step(dve.tensor_tensor(s.base, s.base, s.cum[:, :, 0], ALU.subtract))
    step(dve.tensor_tensor(s.cum, s.cum, wide(s.base, 1, [P, NE, NT]), ALU.add))
    step(dve.tensor_tensor(s.picked, PS[:, 3, 0:NT * NE].rearrange("p (t e) -> p t e", e=NE),
                           s.cum.rearrange("p e t -> p t e"), ALU.add))
    for c in range(2):
        step(dve.tensor_tensor(s.pick[c], s.pick[c], s.picked, ALU.mult))
        step(dve.tensor_reduce(s.slot[:, c, :], s.pick[c], AX_X, ALU.add))
    step(dve.tensor_copy(s.slot_u, s.slot))
    dve.sem_inc(s.sems["rows_placed"], 1)
    step(dve.memset(s.tile_expert, 0.0))
    for x in range(NE - 1):
        step(dve.scalar_tensor_tensor(s.tile_expert, e.const("slot_start"), s.padcum[:, x:x + 1], s.tile_expert,
                                      ALU.is_ge, ALU.add))
    step(dve.tensor_scalar(s.tile_wrap, s.tile_expert, NE - 2.0, -float(NE), ALU.is_ge, ALU.mult))
    step(dve.scalar_tensor_tensor(s.tile_expert, s.tile_expert, 2.0, s.tile_wrap, ALU.add, ALU.add))
    step(dve.tensor_copy(s.tile_slot, s.tile_expert))
    dve.wait_ge(s.sems["exp2"], 1)
    step(dve.tensor_scalar(s.w[:, 0, :], s.w[:, 1, :], 1.0, None, ALU.add))
    step(dve.reciprocal(s.w[:, 0, :], s.w[:, 0, :]))
    step(dve.tensor_tensor(s.w[:, 1, :], s.w[:, 1, :], s.w[:, 0, :], ALU.mult))
    step(dve.tensor_scalar(s.w, s.w, s.gate, None, ALU.mult))
    dve.memset(m.hT[DE % P:P, :, KE - 1, :], 0.0).then_inc(s.sems["slots_ready"], 1)

    def multiply(j, par):
        for half in range(2):
            dve.wait_ge(s.sems["gate_psum"], 2 * j + half + 1)
            dve.wait_ge(s.sems["silu_ready"], 2 * j + half + 1)
            h = m.h[:, par, half * HE:(half + 1) * HE]
            dve.tensor_tensor(h, PS[:, 3 + half, 0:HE], h, ALU.mult).then_inc(s.sems["h_ready"], 1)

    def copy_hidden(j, par):
        dve.wait_ge(s.sems["y_psum"], j)
        dve.wait_ge(s.sems["hT_psum"], 2 * j + 1)
        dve.tensor_copy(m.hT[:, par, 0:4, :], PS[:, 5, :].rearrange("p (n t) -> p n t", t=P)).then_inc(s.sems["hT_ready"], 1)
        dve.wait_ge(s.sems["hT_psum"], 2 * j + 2)
        dve.tensor_copy(m.hT[:, par, 4, :], PS[:, 6, 0:P]).then_inc(e.spare, 1)
        dve.tensor_copy(m.hT[0:DE % P, par, 5, :], PS[0:DE % P, 6, P:2 * P]).then_inc(s.sems["hT_ready"], 1)

    multiply(0, 0)
    with dve.Fori(0, MOE_TILES // 2 - 1) as i:
        for par in (1, 0):
            j = 2 * i + (1 if par else 2)
            copy_hidden(j - 1, 1 - par)
            multiply(j, par)
    copy_hidden(MOE_TILES - 2, 0)
    multiply(MOE_TILES - 1, 1)
    copy_hidden(MOE_TILES - 1, 1)

    dve.wait_ge(s.sems["residual_loaded"], 16)
    for b in range(B):
        dve.wait_ge(s.gathered_s[b], 16 * 2 * TB)
        for c in range(2):
            for t in range(b * TB, (b + 1) * TB):
                tile = e.x_all[:, t, :]
                ins = dve.scalar_tensor_tensor(tile, m.gathered[:, c, t, :], s.w[:, c, t:t + 1], tile, ALU.mult, ALU.add)
                if c == 0:
                    order.mark(ins)
                else:
                    ins.then_inc(s.sems["final"], 1)
            if c == 0:
                order.settle()


def moe_pool(pool, order, e, s):
    nc = e.nc
    m = moe_buffers(e, s)
    nc.gpsimd.memset(s.minus_half, -0.5).then_inc(e.pool_order, 1)
    order.k += 1
    order.settle()
    pool.wait_ge(s.var_ready, 1)
    nc.gpsimd.tensor_tensor(s.rstd, s.var_eps, s.minus_half, ALU.pow).then_inc(s.rstd_ready, 1)
    pool.wait_ge(s.sems["msq_ready"], 1)
    nc.gpsimd.tensor_tensor(s.rrms, s.ms, s.minus_half, ALU.pow).then_inc(s.sems["rrms_ready"], 1)
    pool.wait_ge(s.sems["rows_placed"], 1)
    pool.wait_ge(s.sems["y_kept"], B)
    pool.wait_ge(s.zeroed_s, 16 * MOE_TILES // TB)
    for t in range(NT):
        for c in range(2):
            nc.gpsimd.indirect_dma_start(s.T["slots"], bass.IndirectOffsetOnAxis(s.slot_u[:, c, t:t + 1], 0),
                                         e.x_all[:, t, :], None).then_inc(s.row_scattered_s, 16)
    pool.wait_ge(s.sems["y_stored"], 16 * MOE_TILES)
    for t in range(NT):
        for c in range(2):
            nc.gpsimd.indirect_dma_start(m.gathered[:, c, t, :], None, s.T["results"],
                                         bass.IndirectOffsetOnAxis(s.slot_u[:, c, t:t + 1], 0))\
                .then_inc(s.gathered_s[t // TB], 16)


CH, CD = 8, 64
CT = CH * CD // P
CV = CD + 1
NQ = 256
QT = NQ // P
ROUTE_STEPS = 50
ROUTE_TURN = ROUTE_STEPS // (B // 2)
ROUTE_K = NQ * 9 / 8
NR = B * NQ


def plan_colt(s, T, sem, small):
    s.T = T
    take = s.w.take
    s.wq, s.wk, s.wv, s.wo, s.gamma = [], [], [], [], []
    for part in ("light", "heavy"):
        for lst, n in ((s.wq, "wq"), (s.wk, "wk"), (s.wv, "wv")):
            w = take(KD, CH * CD)
            lst.append(w)
            s.loads.append((w, T[f"L0_ffn_{n}_{part}"].rearrange("p (k n) -> p k n", k=KD)))
        w = take(CT, D)
        s.wo.append(w)
        s.loads.append((w, T[f"L0_ffn_wo_{part}"].rearrange("p (k n) -> p k n", k=CT)))
        g = take(KD)
        s.gamma.append(g)
        s.loads.append((g, T[f"L0_ffn_gamma_{part}"]))
    s.token = take(D)
    s.loads.append((s.token, T["L0_ffn_q_routing_token"].broadcast_to([P, D])))
    take = s.a.take
    s.kTz = take(CH, S)
    s.v = take(TB, CH, CV)
    at = s.a.at
    s.qT = take(CT, S)
    s.shifted, s.probs, s.probsT = take(2, S), take(2, S), take(2, S)
    s.o, s.oT = take(2, CH * CD), take(2, CT, P)
    c = Carver(s.mem, at, s.a.end)
    s.hq_rows, s.hxT = c.take(QT, D), c.take(KD, NQ)
    s.hqT = c.take(CT, NQ)
    s.hprobs, s.hprobsT = c.take(2, S), c.take(2, S)
    s.ho, s.hoT = c.take(QT, CH * CD), c.take(QT, CT, P)
    s.hy = c.take(QT, D)
    s.a.at = max(c.at, s.a.at)
    s.back = s.a.take(TB, D)
    assert s.a.at <= s.a.end - TB * S
    s.a.at = s.a.end - TB * S
    s.earlier = s.a.take(TB, S)
    s.loads.append((s.earlier, T["table_earlier"].rearrange("p (t j) -> p t j", t=TB)))
    s.row_scores = s.mem[:, W_N - NT * P:W_N]
    s.forth = s.back, s.mem[:, W_N - NT * P - TB * D:W_N - NT * P].rearrange("p (t d) -> p t d", d=D)
    c = Carver(small, 0, MOE_N)
    s.mean_var, s.var_eps, s.rstd = c.take(NT, 2), c.take(NT), c.take(NT)
    s.sumsq, s.rnorm, s.scale, s.norm = c.take(NT), c.take(NT), c.take(NT), c.take(NT)
    s.minus_half = c.take(NT)
    s.dots, s.dots_of_pair = c.take(NT), c.take(2 * TB)
    s.s, s.e, s.e_min, s.per_k = c.take(S), c.take(S), c.take(S), c.take(1)
    s.shift, s.limit, s.low, s.raise_, s.log = c.take(1), c.take(2), c.take(1), c.take(1), c.take(1)
    s.score, s.rank, s.over = c.take(NT), c.take(NT), c.take(NT)
    s.to_u, s.from_u = c.take(NT).bitcast(mybir.dt.uint32), c.take(NT).bitcast(mybir.dt.uint32)
    s.from_f = c.take(NT)
    s.junk2 = c.take(2, S)
    s.junk4 = s.junk2.rearrange("p a (b d) -> p (a b) d", d=D)
    s.maxes, s.recip = c.take(2, CH), c.take(2, CH)
    s.sems = {n: sem(f"{s.name}_{n}") for n in (
        "setup", "sumsq_ready", "rnorm_ready", "unit_ready", "unit_stored0", "unit_stored1", "dots_ready", "cd_psum",
        "shifted", "cd_exp", "cd_final", "cd_log", "cd_u", "score_row", "score_psum", "score_ready", "score_stored",
        "scores_spread", "slots_ready",
        "forth_loaded0", "forth_loaded1", "zero_rows", "results_stored", "light_done", "light_x", "merged")}
    s.scattered_s = [s.own_sem(f"{s.name}_scattered{h}") for h in range(2)]
    s.gathered_s = s.own_sem(f"{s.name}_gathered")
    s.parts = []
    for part in ("light", "heavy"):
        heavy = part == "heavy"
        names = ("loaded", "xT_psum", "xT_ready", "proj_psum", "k_ready", "v_ready", "q_ready", "scores", "shifted_ready",
                  "exp_ready", "pT_psum", "pT_ready", "pv_psum", "o_ready", "oT_psum", "oT_ready", "y_psum")\
            + (("q_loaded", "qx_psum", "qx_ready", "y_ready") if heavy else ())
        p = Names()
        p.heavy, p.sems = heavy, {n: sem(f"{s.name}_{part}_{n}") for n in names}
        s.parts.append(p)
    s.sync_program = colt_sync
    s.pe, s.act, s.dve, s.pool = colt_pe, colt_act, colt_dve, colt_pool


RANKED = ((0, 5), (5, 14), (14, 23), (23, NT))
AHEAD_KEYS = ((), (0,), (1,), (2, 3))


def unit_buffers(e):
    return e.xn[:], e.xnT[:].rearrange("p k s -> p (k s)").rearrange("p (t d) -> p t d", d=D)


def colt_sync(sp, e, s):
    units = s.T["unit_rows"].rearrange("(b t p) d -> b p t d", p=P, t=TB)
    light, heavy = s.parts
    e.stage_start(sp, s)
    with sp.Fori(0, B // 2) as j:
        for h, unit in enumerate(unit_buffers(e)):
            sp.wait_ge(s.sems["unit_ready"], TB * (2 * j + h + 1))
            sp.sem_inc(e.spare, 1)
            sp.dma_start(units[bass.ds(2 * j + h, 1)].rearrange("o p t d -> (o p) t d"), unit)\
                .then_inc(s.sems[f"unit_stored{h}"], 16)
    for h in range(2):
        sp.wait_ge(s.sems[f"unit_stored{h}"], 16 * B // 2)
    sp.wait_ge(s.sems["dots_ready"], 1)
    for r in range(NR // (TB * P)):
        sp.dma_start(s.T["routed_out"][r * TB * P:(r + 1) * TB * P, :].rearrange("(t p) d -> p t d", p=P),
                     e.x_all[:, NT:NT + TB, :]).then_inc(s.sems["zero_rows"], 16)
    sp.dma_start(s.T["routed_out"][NR:NR + P, :], e.x_all[:, NT, :]).then_inc(s.sems["zero_rows"], 16)

    def load_rows(p, batch):
        sp.dma_start(e.xn[:], units[bass.ds(batch, 1)].rearrange("o p t d -> (o p) t d")).then_inc(p.sems["loaded"], 16)

    with sp.Fori(0, B // 2 + 1) as i:
        sp.wait_ge(light.sems["xT_psum"], KD * i)
        load_rows(light, i)
    sp.wait_ge(s.sems["score_row"], 1)
    sp.dma_start(s.T["row_scores"].rearrange("(b n) -> b n", b=B), s.e_min[0:B, :]).then_inc(s.sems["score_stored"], 16)
    sp.wait_ge(s.sems["score_stored"], 16)
    sp.dma_start(s.row_scores, s.T["row_scores"].rearrange("(o n) -> o n", o=1).broadcast_to([P, B * S]))\
        .then_inc(s.sems["scores_spread"], 16)
    with sp.Fori(B // 2 + 1, B) as i:
        sp.wait_ge(light.sems["xT_psum"], KD * i)
        load_rows(light, i)
    routed = s.T["routed_in"].rearrange("(b t p) d -> b p t d", p=P, t=QT)
    out = s.T["routed_out"][0:NR, :].rearrange("(b t p) d -> b p t d", p=P, t=QT)

    def load_routed(batch):
        sp.dma_start(s.hq_rows, routed[bass.ds(batch, 1)].rearrange("o p t d -> (o p) t d")).then_inc(heavy.sems["q_loaded"], 16)

    def store(batch):
        sp.dma_start(out[bass.ds(batch, 1)].rearrange("o p t d -> (o p) t d"), s.hy).then_inc(s.sems["results_stored"], 16)

    for b in range(B):
        if b >= 2:
            sp.wait_ge(s.scattered_s[b % 2], 16 * TB * (b // 2))
        sp.dma_start(s.forth[b % 2], units[b]).then_inc(s.sems[f"forth_loaded{b % 2}"], 16)
    sp.wait_ge(light.sems["xT_psum"], KD * B)
    load_rows(heavy, B - 1)
    sp.wait_ge(s.sems["light_done"], 1)
    for h in range(2):
        sp.wait_ge(s.scattered_s[h], 16 * NT // 2)
    load_routed(B - 1)
    sp.wait_ge(s.sems["zero_rows"], 16 * (NR // (TB * P) + 1))
    with sp.Fori(0, B - 1) as i:
        sp.wait_ge(heavy.sems["xT_psum"], KD * (i + 1))
        sp.sem_inc(e.spare, 1)
        load_rows(heavy, B - 2 - i)
        sp.wait_ge(heavy.sems["qx_psum"], i + 1)
        sp.sem_inc(e.spare, 1)
        load_routed(B - 2 - i)
        sp.wait_ge(heavy.sems["y_ready"], QT * (i + 1))
        sp.sem_inc(e.spare, 1)
        store(B - 1 - i)
    sp.wait_ge(heavy.sems["y_ready"], QT * B)
    store(0)


def colt_pe(pe, e, s):
    PS, nc = e.PS, e.nc
    pe.wait_ge(s.sems["setup"], 1)
    light, heavy = s.parts

    def product(p, i, c):
        w, kind, n = (1 if p.heavy else 0), c // CT, c % CT
        if c >= 6:
            pe.wait_ge(p.sems["k_ready"] if c - 6 < CT else p.sems["v_ready"], CT * i + (c - 6) % CT + 1)
        if kind == 2 and n == 0 and p.heavy:
            pe.wait_ge(p.sems["qx_ready"], i + 1)
        for k in range(KD):
            if kind == 0:
                lhsT, rhs = s.wk[w][:, k, n * P:(n + 1) * P], e.xnT[:, k, :]
            elif kind == 1:
                lhsT, rhs = e.xnT[:, k, n * P:(n + 1) * P], s.wv[w][:, k, :]
            else:
                lhsT, rhs = s.wq[w][:, k, n * P:(n + 1) * P], (s.hxT if p.heavy else e.xnT)[:, k, :]
            wide = NQ if p.heavy and kind == 2 else S
            last = nc.tensor.matmul(PS[:, 2 + c % 6, 0:wide], lhsT, rhs, start=k == 0, stop=k == KD - 1)
        last.then_inc(p.sems["proj_psum"], 1)

    def project_first(p, i, after):
        if after == 0:
            pe.wait_ge(p.sems["loaded"], 16 * (i + 1))
            for k in range(KD):
                for t in range(TB):
                    last = nc.tensor.transpose(PS[:, 2 + k, t * P:(t + 1) * P], e.xn[:, t, k * P:(k + 1) * P], e.ident)
                last.then_inc(p.sems["xT_psum"], 1)
        if after == 1:
            pe.wait_ge(p.sems["xT_ready"], KD * (i + 1))
        for c in AHEAD_KEYS[after]:
            product(p, i, c)

    def project_rest(p, i):
        if p.heavy:
            pe.wait_ge(p.sems["oT_ready"], QT * i)
            pe.wait_ge(p.sems["y_ready"], QT * i)
            pe.wait_ge(p.sems["q_loaded"], 16 * (i + 1))
            for k in range(KD):
                for t in range(QT):
                    last = nc.tensor.transpose(PS[:, 0, (k * QT + t) * P:(k * QT + t + 1) * P],
                                               s.hq_rows[:, t, k * P:(k + 1) * P], e.ident)
            last.then_inc(p.sems["qx_psum"], 1)
        else:
            pe.wait_ge(p.sems["oT_ready"], TB * i)
            pe.wait_ge(s.sems["light_x"], TB * i)
        for c in range(CT, 3 * CT):
            product(p, i, c)
        pe.wait_ge(p.sems["q_ready"], CT * (i + 1))
        pe.wait_ge(p.sems["k_ready"], CT * (i + 1))
        pe.wait_ge(p.sems["v_ready"], TB * (i + 1))

    def turn_probs(p, n, u, probs):
        pe.wait_ge(p.sems["exp_ready"], n + u + 1)
        if u >= 2:
            pe.wait_ge(p.sems["pT_ready"], n + u - 1)
        for j in range(4):
            last = nc.tensor.transpose(PS[:, 4 + u % 2, j * P:(j + 1) * P], probs[:, u % 2, j * P:(j + 1) * P], e.ident)
        last.then_inc(p.sems["pT_psum"], 1)

    def project_out(p, n, t, o, oT, step):
        if step == 0:
            for k in range(CT):
                last = nc.tensor.transpose(PS[:, 0, k * P:(k + 1) * P], o[:, t % 2, k * P:(k + 1) * P], e.ident)
            last.then_inc(p.sems["oT_psum"], 1)
        else:
            pe.wait_ge(p.sems["oT_ready"], n + t + 1)
            for k in range(CT):
                last = nc.tensor.matmul(PS[:, 1, 0:D], oT[:, t % 2, k, :], s.wo[1 if p.heavy else 0][:, k, :],
                                        start=k == 0, stop=k == CT - 1)
            last.then_inc(p.sems["y_psum"], 1)

    def light_batch(i, ahead=True):
        p, n = light, 2 * TB * i
        project_rest(p, i)
        for step in range(2 * TB + 6):
            if step < 2 * TB:
                u, t, g = step, step // 2, step % 2
                if u >= 2:
                    pe.wait_ge(p.sems["shifted_ready"], n + u - 1)
                for j in range(4):
                    h = 4 * g + j
                    last = nc.tensor.matmul(PS[:, 2 + u % 2, j * P:(j + 1) * P], s.qT[:, h // 2, t * P:(t + 1) * P],
                                            s.kTz[:, h, t * P:(t + 1) * P], start=True, stop=True)
                last.then_inc(p.sems["scores"], 1)
            if 2 <= step < 2 * TB + 2:
                turn_probs(p, n, step - 2, s.probs)
            if 3 <= step < 2 * TB + 3:
                u = step - 3
                pe.wait_ge(p.sems["pT_ready"], n + u + 1)
                if u >= 2:
                    pe.wait_ge(p.sems["o_ready"], n + u - 1)
                for j in range(4):
                    last = nc.tensor.matmul(PS[:, 6 + u % 2, j * CV:(j + 1) * CV], s.probsT[:, u % 2, j * P:(j + 1) * P],
                                            s.v[:, u // 2, 4 * (u % 2) + j, :], start=True, stop=True)
                last.then_inc(p.sems["pv_psum"], 1)
            if step >= 6 and step % 2 == 0:
                t = (step - 6) // 2
                pe.wait_ge(p.sems["o_ready"], n + 2 * (t + 1))
                pe.wait_ge(p.sems["oT_ready"], TB * i + t)
                project_out(p, TB * i, t, s.o, s.oT, 0)
            if step >= 7 and step % 2 == 1:
                t = (step - 7) // 2
                pe.wait_ge(s.sems["light_x"], TB * i + t)
                project_out(p, TB * i, t, s.o, s.oT, 1)
            if ahead and step >= 2 * TB + 2:
                project_first(p, i + 1, step - 2 * TB - 2)

    pe.wait_ge(s.sems["dots_ready"], 1)
    for t in range(TB):
        last = nc.tensor.transpose(PS[0:B, 2, t * P:(t + 1) * P], s.dots.rearrange("p (b t) -> p t b", t=TB)[:, t, :], e.ident)
    last.then_inc(s.sems["cd_psum"], 1)
    pe.wait_ge(s.sems["shifted"], 1)
    for after in range(len(AHEAD_KEYS)):
        project_first(light, 0, after)
    with pe.Fori(0, B // 2) as i:
        light_batch(i)
    pe.wait_ge(s.sems["score_row"], 1)
    for t in range(TB):
        last = nc.tensor.transpose(PS[:, 7, t * B:(t + 1) * B], s.e_min[0:B, t * P:(t + 1) * P], e.ident[0:B, 0:B])
    last.then_inc(s.sems["score_psum"], 1)
    pe.wait_ge(s.sems["score_ready"], 1)
    with pe.Fori(B // 2, B - 1) as i:
        light_batch(i)
    light_batch(B - 1, ahead=False)
    pe.wait_ge(light.sems["o_ready"], 2 * TB * B)
    pe.wait_ge(s.sems["light_x"], NT)

    def heavy_batch(i, ahead=True):
        p, n = heavy, QT * CH * i
        project_rest(p, i)
        for step in range(QT * CH + 4):
            if step < QT * CH:
                u, t, h = step, step // CH, step % CH
                if u >= 2:
                    pe.wait_ge(p.sems["exp_ready"], n + u - 1)
                nc.tensor.matmul(PS[:, 2 + u % 2, :], s.hqT[:, h // 2, t * P:(t + 1) * P], s.kTz[:, h, :],
                                 start=True, stop=True).then_inc(p.sems["scores"], 1)
            if 1 <= step < QT * CH + 1:
                turn_probs(p, n, step - 1, s.hprobs)
            if 2 <= step < QT * CH + 2:
                u = step - 2
                t, h = u // CH, u % CH
                pe.wait_ge(p.sems["pT_ready"], n + u + 1)
                if h % 4 == 0:
                    pe.wait_ge(p.sems["o_ready"], (QT * i + t) * 2 + max(h // 4 - 1, 0) if t or h else QT * i * 2)
                for j in range(4):
                    last = nc.tensor.matmul(PS[:, 6 + h // 4, (h % 4) * CV:(h % 4 + 1) * CV],
                                            s.hprobsT[:, u % 2, j * P:(j + 1) * P], s.v[:, j, h, :], start=j == 0, stop=j == 3)
                last.then_inc(p.sems["pv_psum"], 1)
            for t in range(QT):
                if step == (t + 1) * CH + 2:
                    pe.wait_ge(p.sems["o_ready"], 2 * (QT * i + t + 1))
                    pe.wait_ge(p.sems["oT_ready"], QT * i + t)
                    project_out(p, QT * i, t, s.ho, s.hoT, 0)
                if step == (t + 1) * CH + 3:
                    pe.wait_ge(p.sems["y_ready"], QT * i + t)
                    project_out(p, QT * i, t, s.ho, s.hoT, 1)
            if ahead and step >= QT * CH:
                project_first(p, i + 1, step - QT * CH)

    for after in range(len(AHEAD_KEYS)):
        project_first(heavy, 0, after)
    with pe.Fori(0, B - 1) as i:
        heavy_batch(i)
    heavy_batch(B - 1, ahead=False)


def colt_act(act, order, e, s):
    PS, nc = e.PS, e.nc
    light, heavy = s.parts

    def copy_xT(p, i):
        for k in range(KD):
            act.wait_ge(p.sems["xT_psum"], KD * i + k + 1)
            nc.scalar.activation(e.xnT[:, k, :], PS[:, 2 + k, :], ACT.Copy).then_inc(p.sems["xT_ready"], 1)

    def copy_values(p, i):
        for t in range(TB):
            act.wait_ge(p.sems["proj_psum"], 3 * CT * i + CT + t + 1)
            nc.scalar.activation(s.v[:, t, :, 0:CD], PS[:, 2 + (CT + t) % 6, :].rearrange("p (h d) -> p h d", d=CD), ACT.Copy)\
                .then_inc(p.sems["v_ready"], 1)

    def copy_queries(p, i):
        for m in range(CT):
            act.wait_ge(p.sems["proj_psum"], 3 * CT * i + 2 * CT + m + 1)
            q, wide = (s.hqT, NQ) if p.heavy else (s.qT, S)
            nc.scalar.activation(q[:, m, :], PS[:, 2 + (2 * CT + m) % 6, 0:wide], ACT.Copy).then_inc(p.sems["q_ready"], 1)

    def copy_oT(p, n, t, oT):
        act.wait_ge(p.sems["oT_psum"], n + t + 1)
        act.wait_ge(p.sems["y_psum"], n + max(t - 1, 0))
        nc.scalar.activation(oT[:, t % 2, :, :], PS[:, 0, :].rearrange("p (k n) -> p k n", k=CT), ACT.Copy).then_inc(p.sems["oT_ready"], 1)

    def shifted_exp(n):
        act.wait_ge(s.sems["shifted"], n)
        nc.scalar.activation(s.e[0:B, :], s.s[0:B, :], ACT.Exp, bias=s.shift[0:B, :]).then_inc(s.sems["cd_exp"], 1)

    shifted_exp(1)
    nc.scalar.activation(s.limit[0:B, 0:1], s.shift[0:B, :], ACT.Exp).then_inc(s.sems["cd_exp"], 1)

    def light_batch(i, routing, ahead=True):
        p, n = light, 2 * TB * i
        if routing:
            shifted_exp(2 * i + 2)
        copy_values(p, i)
        if routing:
            shifted_exp(2 * i + 3)
        copy_queries(p, i)
        for step in range(2 * TB + 6):
            if step < 2 * TB:
                u = step
                act.wait_ge(p.sems["shifted_ready"], n + u + 1)
                if u >= 2:
                    act.wait_ge(p.sems["pT_psum"], n + u - 1)
                nc.scalar.activation(s.probs[:, u % 2, :], s.shifted[:, u % 2, :], ACT.Exp).then_inc(p.sems["exp_ready"], 1)
            if 2 <= step < 2 * TB + 2:
                u = step - 2
                act.wait_ge(p.sems["pT_psum"], n + u + 1)
                if u >= 2:
                    act.wait_ge(p.sems["pv_psum"], n + u - 1)
                nc.scalar.activation(s.probsT[:, u % 2, :], PS[:, 4 + u % 2, :], ACT.Copy).then_inc(p.sems["pT_ready"], 1)
            if step >= 6 and step % 2 == 0:
                copy_oT(p, TB * i, (step - 6) // 2, s.oT)
            if ahead and step == 2 * TB + 3:
                copy_xT(p, i + 1)

    copy_xT(light, 0)
    with act.Fori(0, B // 2) as i:
        light_batch(i, True)
    act.wait_ge(s.sems["cd_final"], 1)
    nc.scalar.activation(s.log[0:B, :], s.limit[0:B, 0:1], ACT.Ln).then_inc(s.sems["cd_log"], 1)
    act.wait_ge(s.sems["cd_u"], 1)
    nc.scalar.activation(s.e_min[0:B, :], s.e[0:B, :], ACT.Exp).then_inc(s.sems["score_row"], 1)
    with act.Fori(B // 2, B - 1) as i:
        light_batch(i, False)
    light_batch(B - 1, False, ahead=False)

    def heavy_batch(i, ahead=True):
        p, n = heavy, QT * CH * i
        act.wait_ge(p.sems["qx_psum"], i + 1)
        nc.scalar.activation(s.hxT, PS[:, 0, :].rearrange("p (k n) -> p k n", k=KD), ACT.Copy).then_inc(p.sems["qx_ready"], 1)
        copy_values(p, i)
        copy_queries(p, i)
        for step in range(QT * CH + 4):
            if step < QT * CH:
                u = step
                act.wait_ge(p.sems["shifted_ready"], n + u + 1)
                if u >= 2:
                    act.wait_ge(p.sems["pT_psum"], n + u - 1)
                nc.scalar.activation(s.hprobs[:, u % 2, :], PS[:, 2 + u % 2, :], ACT.Exp, bias=s.maxes[:, 0, u % 2:u % 2 + 1])\
                    .then_inc(p.sems["exp_ready"], 1)
            for t in range(QT):
                if step == (t + 1) * CH + 2:
                    copy_oT(p, QT * i, t, s.hoT)
                if step == (t + 1) * CH + 3:
                    act.wait_ge(p.sems["y_psum"], QT * i + t + 1)
                    act.wait_ge(s.sems["results_stored"], 16 * i)
                    nc.scalar.activation(s.hy[:, t, :], PS[:, 1, 0:D], ACT.Copy, scale=s.gate).then_inc(p.sems["y_ready"], 1)
            if ahead and step == QT * CH + 1:
                copy_xT(p, i + 1)

    copy_xT(heavy, 0)
    with act.Fori(0, B - 1) as i:
        heavy_batch(i)
    heavy_batch(B - 1, ahead=False)


def colt_dve(dve, order, e, s):
    PS = e.PS
    light, heavy = s.parts
    dve.wait_ge(s.weights_loaded, 16 * len(s.loads))
    for w in range(2):
        for k in range(KD):
            g = s.gamma[w][:, k:k + 1]
            order.mark(dve.tensor_scalar(s.wk[w][:, k, :], s.wk[w][:, k, :], g, D ** 0.5, ALU.mult, ALU.mult))
            order.mark(dve.tensor_scalar(s.wv[w][:, k, :], s.wv[w][:, k, :], g, D ** 0.5, ALU.mult, ALU.mult))
            order.mark(dve.tensor_scalar(s.wq[w][:, k, :], s.wq[w][:, k, :], g, D ** 0.5 * CD ** -0.5, ALU.mult, ALU.mult))
    order.mark(dve.memset(s.kTz, 0.0))
    order.mark(dve.memset(s.v[:, :, :, CD:CV], 1.0))
    order.settle()
    dve.sem_inc(s.sems["setup"], 1)

    def step(ins):
        order.mark(ins)
        order.settle()

    with dve.Fori(0, B) as i:
        order.turn(i, 2 * TB + 1)
        for t in range(TB):
            order.mark(dve.bn_stats(e.stats[:, t, :], e.x_all[:, i * TB + t, :]))
        order.settle()
        dve.sem_inc(e.spare, 1)
        for t in range(TB):
            order.mark(dve.bn_aggr(e.mean_var[:, t, :], e.stats[:, t, :]))
        order.settle()
        order.mark(dve.tensor_copy(s.mean_var[:, bass.ds(i * TB, TB), :], e.mean_var[:]))
    order.end(B)
    order.settle()
    dve.tensor_scalar(s.var_eps, s.mean_var[:, :, 1], LN_EPS, None, ALU.add).then_inc(s.var_ready, 1)
    dve.wait_ge(s.rstd_ready, 1)
    step(dve.tensor_tensor(s.sumsq, s.rstd, s.rstd, ALU.mult))
    step(dve.tensor_tensor(s.sumsq, s.sumsq, s.mean_var[:, :, 1], ALU.mult))
    dve.tensor_scalar(s.sumsq, s.sumsq, float(D), 1e-24, ALU.mult, ALU.max).then_inc(s.sems["sumsq_ready"], 1)
    dve.wait_ge(s.sems["rnorm_ready"], 1)
    order.mark(dve.tensor_tensor(s.norm, s.sumsq, s.rnorm, ALU.mult))
    step(dve.tensor_tensor(s.scale, s.rstd, s.rnorm, ALU.mult))
    with dve.Fori(0, B // 2) as j:
        order.turn(j, 2 * TB + 1)
        for h, unit in enumerate(unit_buffers(e)):
            dve.wait_ge(s.sems[f"unit_stored{h}"], 16 * j)
            dve.sem_inc(e.spare, 1)
            for t in range(TB):
                at = (2 * j + h) * TB + t
                dve.tensor_scalar(unit[:, t, :], e.x_all[:, at, :], s.mean_var[:, bass.ds(at, 1), 0], s.scale[:, bass.ds(at, 1)],
                                  ALU.subtract, ALU.mult).then_inc(s.sems["unit_ready"], 1)
            dve.wait_ge(s.sems["unit_ready"], TB * (2 * j + h + 1))
            order.settle()
            for t in range(TB):
                order.mark(dve.tensor_tensor_reduce(s.junk4[:, t, :], unit[:, t, :], s.token, 1.0, 0.0, ALU.mult, ALU.add,
                                                    s.dots_of_pair[:, h * TB + t:h * TB + t + 1]))
        order.settle()
        order.mark(dve.tensor_copy(s.dots[:, bass.ds(2 * TB * j, 2 * TB)], s.dots_of_pair))
    order.end(B // 2)
    order.settle()
    dve.tensor_tensor(s.dots, s.dots, s.norm, ALU.mult).then_inc(s.sems["dots_ready"], 1)

    dve.wait_ge(s.sems["cd_psum"], 1)
    order.mark(dve.tensor_copy(s.s[0:B, :], PS[0:B, 2, :]))
    order.mark(dve.memset(s.per_k, 1.0 / ROUTE_K))
    step(dve.tensor_reduce(s.shift[0:B, :], PS[0:B, 2, :], AX_X, ALU.max, negate=True))
    dve.tensor_scalar(s.shift[0:B, :], s.shift[0:B, :], 0.0, None, ALU.max).then_inc(s.sems["shifted"], 1)
    dve.wait_ge(s.sems["cd_exp"], 2)
    step(dve.tensor_scalar(s.limit[0:B, 1:2], s.limit[0:B, 0:1], S / ROUTE_K, None, ALU.mult))

    def route_step(r):
        order.settle()
        order.mark(dve.scalar_tensor_tensor(s.e_min[0:B, :], s.e[0:B, :], s.limit[0:B, r % 2:r % 2 + 1], s.per_k[0:B, :].broadcast_to([B, S]),
                                            ALU.min, ALU.mult, accum_out=s.limit[0:B, 1 - r % 2:2 - r % 2]))

    def raise_shift():
        limit = s.limit[0:B, 0:1]
        order.settle()
        step(dve.tensor_scalar(s.low[0:B, :], limit, exp(-30.0), None, ALU.is_lt))
        order.mark(dve.tensor_scalar(s.raise_[0:B, :], s.low[0:B, :], exp(34.0) - 1.0, 1.0, ALU.mult, ALU.add))
        step(dve.scalar_tensor_tensor(s.shift[0:B, :], s.low[0:B, :], 34.0, s.shift[0:B, :], ALU.mult, ALU.add))
        dve.tensor_tensor(limit, limit, s.raise_[0:B, :], ALU.mult).then_inc(s.sems["shifted"], 1)

    def rank_tile(t):
        row = s.row_scores[:, t // TB * S:(t // TB + 1) * S]
        step(dve.scalar_tensor_tensor(s.junk2[:, 0, :], row, s.score[:, t:t + 1], s.earlier[:, t % TB, :], ALU.is_equal, ALU.mult))
        step(dve.scalar_tensor_tensor(s.junk2[:, 1, :], row, s.score[:, t:t + 1], s.junk2[:, 0, :], ALU.is_gt, ALU.add,
                                      accum_out=s.rank[:, t:t + 1]))

    def copy_keys(p, i, these=range(CT)):
        for m in these:
            dve.wait_ge(p.sems["proj_psum"], 3 * CT * i + m + 1)
            dve.tensor_copy(s.kTz[0:CD, 2 * m, :], PS[0:CD, 2 + m, :]).then_inc(e.spare, 1)
            dve.tensor_copy(s.kTz[CD:P, 2 * m + 1, :], PS[CD:P, 2 + m, :]).then_inc(p.sems["k_ready"], 1)

    def normalise(p, wait, bank, at, o, done, par):
        dve.wait_ge(p.sems["pv_psum"], wait)
        dve.wait_ge(p.sems["o_ready"], done)
        recip = s.recip[:, par, 0:4]
        src = PS[:, bank, 0:4 * CV].rearrange("p (h v) -> p h v", v=CV)
        order.mark(dve.reciprocal(recip, src[:, :, CD]))
        order.settle()
        dve.tensor_tensor(o[:, at:at + 4 * CD].rearrange("p (h d) -> p h d", d=CD), src[:, :, 0:CD],
                          recip.rearrange("p (h o) -> p h o", o=1).broadcast_to([P, 4, CD]), ALU.mult)\
            .then_inc(p.sems["o_ready"], 1)

    def light_batch(i, routing, ahead=True):
        p, n = light, 2 * TB * i
        if routing:
            for part in range(2):
                raise_shift()
                dve.wait_ge(s.sems["shifted"], 2 * i + 2 + part)
                dve.wait_ge(s.sems["cd_exp"], 2 * i + 3 + part)
                for r in range(ROUTE_TURN // 2):
                    route_step(r)
        else:
            for t in range(*RANKED[i - B // 2]):
                rank_tile(t)
            if i == B - 1:
                slots()
        for step_ in range(2 * TB + 8):
            if step_ < 2 * TB:
                u = step_
                dve.wait_ge(p.sems["scores"], n + u + 1)
                bank = PS[:, 2 + u % 2, :].rearrange("p (h s) -> p h s", s=P)
                order.mark(dve.tensor_reduce(s.maxes[:, u % 2, 0:4], bank, AX_X, ALU.max))
                order.settle()
                if u >= 2:
                    dve.wait_ge(p.sems["exp_ready"], n + u - 1)
                dve.tensor_tensor(s.shifted[:, u % 2, :].rearrange("p (h s) -> p h s", s=P), bank,
                                  s.maxes[:, u % 2, 0:4].rearrange("p (h o) -> p h o", o=1).broadcast_to([P, 4, P]),
                                  ALU.subtract).then_inc(p.sems["shifted_ready"], 1)
            if 4 <= step_ < 2 * TB + 4:
                u = step_ - 4
                if u >= 4 and u % 2 == 0:
                    dve.wait_ge(p.sems["oT_psum"], TB * i + u // 2 - 1)
                normalise(p, n + u + 1, 6 + u % 2, (u % 2) * 4 * CD, s.o[:, (u // 2) % 2, :], n + max(u - 1, 0), u % 2)
            if step_ >= 8 and step_ % 2 == 0:
                t = (step_ - 8) // 2
                dve.wait_ge(p.sems["y_psum"], TB * i + t + 1)
                tile = e.x_all[:, i * TB + t, :]
                dve.scalar_tensor_tensor(tile, PS[:, 1, 0:D], s.gate, tile, ALU.mult, ALU.add).then_inc(s.sems["light_x"], 1)
            if ahead and step_ >= 2 * TB + 5:
                copy_keys(p, i + 1, ((0,), (1,), (2, 3))[step_ - 2 * TB - 5])
    def slots():
        step(dve.tensor_scalar(s.over, s.rank, float(NQ), None, ALU.is_ge))
        step(dve.tensor_tensor(s.rank, s.rank, e.const("batch_slot"), ALU.add))
        step(dve.scalar_tensor_tensor(s.from_f, s.over, float(NR - NQ), s.rank, ALU.mult, ALU.add))
        step(dve.tensor_copy(s.to_u, s.from_f))
        step(dve.tensor_scalar(s.from_f, s.rank, -1.0, float(NR), ALU.mult, ALU.add))
        step(dve.tensor_tensor(s.from_f, s.from_f, s.over, ALU.mult))
        step(dve.tensor_tensor(s.from_f, s.from_f, s.rank, ALU.add))
        step(dve.tensor_copy(s.from_u, s.from_f))
        dve.sem_inc(s.sems["slots_ready"], 1)

    for r in range(1, ROUTE_STEPS % (B // 2)):
        route_step(r)
    copy_keys(light, 0)
    with dve.Fori(0, B // 2) as i:
        order.turn(i, 4 * TB + ROUTE_TURN + 2 * 3)
        light_batch(i, True)
    order.end(B // 2)
    order.settle()
    dve.sem_inc(s.sems["cd_final"], 1)
    dve.wait_ge(s.sems["cd_log"], 1)
    step(dve.tensor_tensor(s.log[0:B, :], s.shift[0:B, :], s.log[0:B, :], ALU.subtract))
    dve.tensor_scalar(s.e[0:B, :], s.s[0:B, :], s.log[0:B, :], 0.0, ALU.add, ALU.min).then_inc(s.sems["cd_u"], 1)
    dve.wait_ge(s.sems["score_psum"], 1)
    dve.tensor_copy(s.score.rearrange("p (b t) -> p t b", t=TB), PS[:, 7, 0:NT].rearrange("p (t b) -> p t b", b=B))\
        .then_inc(s.sems["score_ready"], 1)
    dve.wait_ge(s.sems["score_ready"], 1)
    dve.wait_ge(s.sems["scores_spread"], 16)
    for i in range(B // 2, B):
        light_batch(i, False, ahead=i < B - 1)
    dve.wait_ge(s.sems["light_x"], NT)
    order.settle()
    dve.sem_inc(s.sems["light_done"], 1)
    dve.wait_ge(s.scattered_s[0], 16 * NT // 2)
    step(dve.memset(s.back, 0.0))

    def add_back(at):
        for t in range(TB):
            dve.tensor_tensor(e.x_all[:, at + t, :], e.x_all[:, at + t, :], s.back[:, t, :], ALU.add).then_inc(s.sems["merged"], 1)

    def heavy_batch(i, ahead=True):
        p, n = heavy, QT * CH * i
        dve.wait_ge(s.gathered_s, 16 * TB * i)
        dve.sem_inc(e.spare, 1)
        add_back((B - i) * TB)
        for step_ in range(QT * CH + 4):
            if step_ < QT * CH:
                u = step_
                dve.wait_ge(p.sems["scores"], n + u + 1)
                if u >= 2:
                    dve.wait_ge(p.sems["exp_ready"], n + u - 1)
                dve.tensor_reduce(s.maxes[:, 0, u % 2:u % 2 + 1], PS[:, 2 + u % 2, :], AX_X, ALU.max, negate=True)\
                    .then_inc(p.sems["shifted_ready"], 1)
            if 1 <= step_ < QT * CH + 1:
                u = step_ - 1
                dve.wait_ge(p.sems["pT_psum"], n + u + 1)
                if u >= 2:
                    dve.wait_ge(p.sems["pv_psum"], n + u - 1)
                dve.tensor_copy(s.hprobsT[:, u % 2, :], PS[:, 4 + u % 2, :]).then_inc(p.sems["pT_ready"], 1)
            if step_ >= 6 and (step_ - 2) % 4 == 0:
                g = (step_ - 6) // 4
                if g % 2 == 0:
                    dve.wait_ge(p.sems["oT_psum"], QT * i)
                normalise(p, n + 4 * (g + 1), 6 + g % 2, (g % 2) * 4 * CD, s.ho[:, g // 2, :], 2 * QT * i + max(g - 1, 0), g % 2)
            if ahead and step_ == QT * CH + 3:
                copy_keys(p, i + 1)

    copy_keys(heavy, 0)
    with dve.Fori(0, B - 1) as i:
        order.turn(i, 2 * QT)
        heavy_batch(i)
    order.end(B - 1)
    heavy_batch(B - 1, ahead=False)

    dve.wait_ge(s.gathered_s, 16 * TB * B)
    add_back(0)
    dve.wait_ge(s.sems["merged"], TB * (B + 1))
    dve.sem_inc(e.x_updated, NT)


def colt_pool(pool, order, e, s):
    nc = e.nc
    nc.gpsimd.memset(s.minus_half, -0.5).then_inc(e.pool_order, 1)
    order.k += 1
    order.settle()
    pool.wait_ge(s.var_ready, 1)
    nc.gpsimd.tensor_tensor(s.rstd, s.var_eps, s.minus_half, ALU.pow).then_inc(s.rstd_ready, 1)
    pool.wait_ge(s.sems["sumsq_ready"], 1)
    nc.gpsimd.tensor_tensor(s.rnorm, s.sumsq, s.minus_half, ALU.pow).then_inc(s.sems["rnorm_ready"], 1)
    pool.wait_ge(s.sems["slots_ready"], 1)
    for b in range(B):
        pool.wait_ge(s.sems[f"forth_loaded{b % 2}"], 16 * (b // 2 + 1))
        for t in range(TB):
            nc.gpsimd.indirect_dma_start(s.T["routed_in"], bass.IndirectOffsetOnAxis(s.to_u[:, b * TB + t:b * TB + t + 1], 0),
                                         s.forth[b % 2][:, t, :], None).then_inc(s.scattered_s[b % 2], 16)
    for i in range(B):
        pool.wait_ge(s.sems["results_stored"], 16 * (i + 1))
        pool.wait_ge(s.sems["merged"], TB * (i + 1))
        for t in range(TB):
            at = (B - 1 - i) * TB + t
            nc.gpsimd.indirect_dma_start(s.back[:, t, :], None, s.T["routed_out"],
                                         bass.IndirectOffsetOnAxis(s.from_u[:, at:at + 1], 0)).then_inc(s.gathered_s, 16)


PLAN = {"L0_xattn": plan_xattn, "L1_xattn": plan_xattn, "L3_xattn": plan_xattn, "L1_ffn": plan_ffn1,
        "L2_xattn": plan_xattn2, "L2_ffn": plan_ffn2, "L3_ffn": plan_moe, "L0_ffn": plan_colt}


def rows(w):
    k, n = w.shape
    return np.ascontiguousarray(w.reshape(k // P, P, n).transpose(1, 0, 2).reshape(P, -1))


def cols(b):
    return np.ascontiguousarray(b.reshape(-1, P).T)


def lay_out(i):
    i = {k: np.asarray(v) for k, v in i.items()}
    t = {"x": i["x"], "ctx_1024": i["ctx_1024"], "g_xattn": i["g_xattn"], "g_ffn": i["g_ffn"]}
    t["consts"] = np.zeros((P, CONST_N), np.float32)
    for name, a in shape_constants().items():
        if name in OF_A_STAGE:
            t["table_" + name] = a
            continue
        at, n = CONST_AT[name]
        t["consts"][:, at:at + n] = a
    t["mask_L0"] = i["mask_BxS2_bf1"].view(np.uint8).reshape(1, -1)
    t["mask_L1"] = i["mask_Bx1x1xS2_ff1"].reshape(1, -1)
    wkv, bkv = i["L0_xattn_Wkv"], i["L0_xattn_bkv"]
    xa = {"L0": (i["L0_xattn_Wq"], wkv[:, :D], wkv[:, D:], i["L0_xattn_Wo"], i["L0_xattn_bq"], bkv[:D], bkv[D:], i["L0_xattn_bo"])}
    for L, q in (("L1", "W{} b{}"), ("L3", "w_{} b_{}")):
        wn, bn = q.split()
        xa[L] = tuple(i[f"{L}_xattn_{wn.format(c)}"].T for c in "qkvo") + tuple(i[f"{L}_xattn_{bn.format(c)}"] for c in "qkvo")
    for L, (wq, wk, wv, wo, bq, bk, bv, bo) in xa.items():
        for n, w in (("wq", wq), ("wk", wk), ("wv", wv), ("wo", wo)):
            t[f"{L}_xattn_{n}"] = rows(w)
        t[f"{L}_xattn_bq"], t[f"{L}_xattn_bk"] = cols(bq), cols(bk)
        t[f"{L}_xattn_bv"], t[f"{L}_xattn_bo"] = bv.reshape(1, -1), bo.reshape(1, -1)
    for part in ("light", "heavy"):
        wkv = i[f"L0_ffn_wkv_{part}"]
        if part == "light":
            wk, wv = wkv[:, :CH * CD], wkv[:, CH * CD:]
        else:
            heads = wkv.reshape(CH, 2, CD, D)
            wk, wv = heads[:, 0].reshape(CH * CD, D).T, heads[:, 1].reshape(CH * CD, D).T
        for n, w in (("wq", i[f"L0_ffn_wq_{part}"]), ("wk", wk), ("wv", wv), ("wo", i[f"L0_ffn_wo_{part}"])):
            t[f"L0_ffn_{n}_{part}"] = rows(w)
        t[f"L0_ffn_gamma_{part}"] = cols(i[f"L0_ffn_gamma_{part}"])
    t["L0_ffn_q_routing_token"] = i["L0_ffn_q_routing_token"].reshape(1, -1)
    t["L1_ffn_q1"], t["L1_ffn_q2"] = rows(i["L1_ffn_fc1_q"]), rows(i["L1_ffn_fc2_q"])
    t["L1_ffn_sc1"], t["L1_ffn_sc2"] = i["L1_ffn_fc1_scales"].reshape(1, -1), i["L1_ffn_fc2_scales"].reshape(1, -1)
    t["L1_ffn_b1"], t["L1_ffn_b2"] = cols(i["L1_ffn_fc1_bias"]), i["L1_ffn_fc2_bias"].reshape(1, -1)
    t["L1_ffn_gamma"], t["L1_ffn_beta"] = cols(i["L1_ffn_ln_gamma"]), cols(i["L1_ffn_ln_beta"])
    t["mask_L2"] = i["mask_SxS2_ik1"]
    t["L2_xattn_wq"] = rows(i["L2_xattn_Wq"])
    t["L2_xattn_wk"], t["L2_xattn_wv"] = rows(i["L2_xattn_Wk"].T), rows(i["L2_xattn_Wv"].T)
    t["L2_xattn_bq"], t["L2_xattn_bk"] = cols(i["L2_xattn_bq"]), cols(i["L2_xattn_bk"])
    t["L2_xattn_bv"] = i["L2_xattn_bv"].reshape(1, -1)
    for g in ("f", "i", "c", "o"):
        t[f"L2_ffn_w{g}"], t[f"L2_ffn_u{g}"] = rows(i[f"L2_ffn_w{g}"].T), rows(i[f"L2_ffn_u{g}"].T)
        t[f"L2_ffn_b{g}"] = i["L2_ffn_bo"].reshape(1, -1) if g == "o" else cols(i[f"L2_ffn_b{g}"])
    ex = np.zeros((NE, P, E_N), np.float32)
    for e in range(NE):
        ex[e, :, 0:KD * DE] = rows(i["L3_ffn_W1"][e].T)
        ex[e, :, KD * DE:2 * KD * DE] = rows(i["L3_ffn_W2"][e].T)
        down = np.zeros((KE * P, D), np.float32)
        down[:DE] = i["L3_ffn_W3"][e].T
        ex[e, :, 2 * KD * DE:] = rows(down)
    t["L3_ffn_experts"] = ex
    t["L3_ffn_gate_w"], t["L3_ffn_rms_w"] = rows(i["L3_ffn_gate_w"].T), i["L3_ffn_rms_w"].reshape(1, -1)
    t["L2_ffn_in_c"] = cols(i["L2_ffn_in_c"])
    return t


def declare_and_write(nc, tensors, stages):
    arrays = {f"in_{n}": np.ascontiguousarray(a) for n, a in tensors.items()}
    T = {n[3:]: nc.dram_tensor(n, a.shape, mybir.dt.from_np(a.dtype), kind="ExternalInput").ap() for n, a in arrays.items()}
    T["out"] = nc.dram_tensor("out_x", (B, S, D), F32, kind="ExternalOutput").ap()
    for n, shape in (("slots", (MOE_TILES * P, D)), ("results", (MOE_TILES * P, D)), ("unit_rows", (B * S, D)),
                     ("row_scores", (B * S,)), ("routed_in", (2 * NR, D)), ("routed_out", (NR + P, D)), ("residual", (B * S, D))):
        T[n] = nc.dram_tensor(n, shape, F32, kind="Internal").ap()
    flamingo_kernel(nc, T, T["out"], stages)
    return arrays


def kernel(**inputs):
    import concourse.bacc as bacc
    from concourse.bass_utils import run_bass_kernel_spmd as run

    nc = bacc.Bacc("TRN2", target_bir_lowering=False, num_devices=1)
    arrays = declare_and_write(nc, lay_out(inputs), STAGES)
    return run(nc, [arrays], core_ids=[0]).results[0]["out_x"]
```
